# Optimizing a Trainium2 kernel written in Bass

```python
import numpy as np
import jax
import jax.numpy as jnp

def _softmax(x, axis=-1):
    return jax.nn.softmax(x, axis=axis)

def _gelu(x):
    return jax.nn.gelu(x, approximate=True)

def _silu(x):
    return jax.nn.silu(x)

def _sigmoid(x):
    return jax.nn.sigmoid(x)

def _layernorm(x, axis=-1, eps=1e-05):
    m = jnp.mean(x, axis=axis, keepdims=True)
    v = jnp.var(x, axis=axis, keepdims=True)
    return (x - m) / jnp.sqrt(v + eps)

def _scatter_add(tgt, idx, src, axis=0):
    return tgt.at[idx].add(src)

def _segment_sum(src, seg, n):
    return jax.ops.segment_sum(src, seg, n)
kernel_name = 'mk_prb_d4_jaxref_r8_1e7329'

def setup_inputs(seed: int=0):
    np.random.seed(seed)
    _w = jnp.asarray

    def _L0_attn_setup():
        import jax, jax.numpy as jnp
        import numpy as np
        from functools import partial
        B, S, D, H, DK, DV, DFF = (4, 256, 128, 8, 128, 128, 512)
        EPS = 1e-06

        def rms_norm(x):
            return x * jax.lax.rsqrt(jnp.mean(x * x, axis=-1, keepdims=True) + EPS)

        def l2norm(x):
            return x * jax.lax.rsqrt(jnp.sum(x * x, axis=-1, keepdims=True) + EPS)

        def gated_delta_net(h, Wq, Wk, Wv, Wb, Wa, A_log, dt_bias, Wg, o_norm_w, Wo):
            b, s, _ = h.shape
            q = l2norm(jax.nn.silu(h @ Wq).reshape(b, s, H, DK))
            k = l2norm(jax.nn.silu(h @ Wk).reshape(b, s, H, DK))
            v = jax.nn.silu(h @ Wv).reshape(b, s, H, DV)
            beta = jax.nn.sigmoid(h @ Wb)
            g = -jnp.exp(A_log) * jax.nn.softplus(h @ Wa + dt_bias)
            alpha = jnp.exp(g)
            scale = DK ** (-0.5)
            tm = lambda a: jnp.moveaxis(a, 1, 0)
            qs, ks_, vs, als, bts = (tm(q), tm(k), tm(v), tm(alpha), tm(beta))

            def step(Sst, inp):
                q_t, k_t, v_t, a_t, b_t = inp
                Sst = Sst * a_t[..., None, None]
                kv = jnp.einsum('bhd,bhde->bhe', k_t, Sst)
                delta = (v_t - kv) * b_t[..., None]
                Sst = Sst + jnp.einsum('bhd,bhe->bhde', k_t, delta)
                o_t = jnp.einsum('bhd,bhde->bhe', q_t, Sst) * scale
                return (Sst, o_t)
            S0 = jnp.zeros((b, H, DK, DV), dtype=h.dtype)
            _, o = jax.lax.scan(step, S0, (qs, ks_, vs, als, bts))
            o = jnp.moveaxis(o, 0, 1)
            gate = (h @ Wg).reshape(b, s, H, DV)
            o = rms_norm(o) * o_norm_w * jax.nn.silu(gate)
            return o.reshape(b, s, H * DV) @ Wo
        key = jax.random.key(seed)
        ks = jax.random.split(key, 16)
        w = lambda k, shp: jax.random.normal(k, shp, dtype=jnp.float32) * 0.02
        return {'x': jax.random.normal(ks[0], (B, S, D), dtype=jnp.float32), 'Wq': w(ks[1], (D, H * DK)), 'Wk': w(ks[2], (D, H * DK)), 'Wv': w(ks[3], (D, H * DV)), 'Wb': w(ks[4], (D, H)), 'Wa': w(ks[5], (D, H)), 'A_log': jnp.log(jnp.linspace(1.0, 8.0, H).astype(jnp.float32)), 'dt_bias': jax.random.normal(ks[6], (H,), dtype=jnp.float32) * 0.1, 'Wg': w(ks[7], (D, H * DV)), 'o_norm_w': jnp.ones((DV,), dtype=jnp.float32), 'Wo': w(ks[8], (H * DV, D)), 'W_fc': w(ks[9], (D, DFF)), 'W_proj': w(ks[10], (DFF, D))}
    _L0_attn_in = _L0_attn_setup()

    def _L0_ffn_setup():
        import jax, jax.numpy as jnp
        import numpy as np
        GROUP = 16
        EPS = 1e-05

        def _dequant(q, scale):
            w = q.astype(jnp.float32) / 7.5 - 1.0
            return w * jnp.repeat(scale, GROUP, axis=1)

        def _qlora_linear(x, q, scale, bias, la, lb):
            w = _dequant(q, scale)
            base = jnp.einsum('btd,od->bto', x, w) + bias
            lora = jnp.einsum('btr,or->bto', jnp.einsum('btd,rd->btr', x, la), lb)
            return base + lora

        def _layernorm(x, g, b):
            mu = jnp.mean(x, axis=-1, keepdims=True)
            var = jnp.mean(jnp.square(x - mu), axis=-1, keepdims=True)
            return (x - mu) * jax.lax.rsqrt(var + EPS) * g + b
        key = jax.random.key(seed)
        ks = jax.random.split(key, 6)
        D, R, B, T = (128, 32, 8, 512)
        x = jax.random.normal(ks[0], (B, T, D), dtype=jnp.float32)
        qweights = jax.random.randint(ks[1], (6, D, D), 0, 16, dtype=jnp.int32)
        scales = jax.random.uniform(ks[2], (6, D, D // GROUP), dtype=jnp.float32)
        biases = jax.random.normal(ks[3], (6, D), dtype=jnp.float32) * 0.02
        lora_a = jax.random.normal(ks[4], (6, R, D), dtype=jnp.float32) * 0.02
        lora_b = jax.random.normal(ks[5], (6, D, R), dtype=jnp.float32) * 0.02
        ln_gamma = jnp.ones((3, D), dtype=jnp.float32)
        ln_beta = jnp.zeros((3, D), dtype=jnp.float32)
        return {'x': x, 'qweights': qweights, 'scales': scales, 'biases': biases, 'lora_a': lora_a, 'lora_b': lora_b, 'ln_gamma': ln_gamma, 'ln_beta': ln_beta}
    _L0_ffn_in = _L0_ffn_setup()

    def _L1_attn_setup():
        import jax, jax.numpy as jnp
        import numpy as np
        import math
        D_MODEL = 128
        NUM_HEADS = 16
        HEAD_DIM = D_MODEL // NUM_HEADS
        ROPE_THETA = 10000.0

        def _rope_tables(seq_len, dim, theta=ROPE_THETA):
            inv = 1.0 / theta ** (jnp.arange(0, dim, 2, dtype=jnp.float32) / dim)
            t = jnp.arange(seq_len, dtype=jnp.float32)
            f = jnp.outer(t, inv)
            cos = jnp.repeat(jnp.cos(f), 2, axis=-1)
            sin = jnp.repeat(jnp.sin(f), 2, axis=-1)
            return (cos, sin)

        def _rotate_half(x):
            x1 = x[..., ::2]
            x2 = x[..., 1::2]
            return jnp.stack((-x2, x1), axis=-1).reshape(x.shape)
        key = jax.random.key(seed)
        ks = jax.random.split(key, 5)
        scale = 1.0 / math.sqrt(D_MODEL)
        return {'x': jax.random.normal(ks[0], (2, 256, D_MODEL), dtype=jnp.float32), 'W_Q': jax.random.normal(ks[1], (D_MODEL, D_MODEL), dtype=jnp.float32) * scale, 'W_K': jax.random.normal(ks[2], (D_MODEL, D_MODEL), dtype=jnp.float32) * scale, 'W_V': jax.random.normal(ks[3], (D_MODEL, D_MODEL), dtype=jnp.float32) * scale, 'W_O': jax.random.normal(ks[4], (D_MODEL, D_MODEL), dtype=jnp.float32) * scale}
    _L1_attn_in = _L1_attn_setup()

    def _L1_ffn_setup():
        import jax, jax.numpy as jnp
        import numpy as np
        B, S, D, F, E = (2, 256, 128, 512, 8)
        LN_EPS = 1e-05

        def _layer_norm(x, gamma, beta):
            mu = jnp.mean(x, axis=-1, keepdims=True)
            var = jnp.mean(jnp.square(x - mu), axis=-1, keepdims=True)
            return (x - mu) * jax.lax.rsqrt(var + LN_EPS) * gamma + beta
        key = jax.random.key(seed)
        ks = jax.random.split(key, 8)

        def xavier(k, shape):
            fan_in, fan_out = (shape[-1], shape[-2])
            a = jnp.sqrt(6.0 / (fan_in + fan_out))
            return jax.random.uniform(k, shape, jnp.float32, -a, a)
        return {'tgt': jax.random.normal(ks[0], (B, S, D), jnp.float32), 'Wr': xavier(ks[1], (E, D)), 'br': jnp.zeros((E,), jnp.float32), 'W1': xavier(ks[2], (E, F, D)), 'b1': jnp.zeros((E, F), jnp.float32), 'W2': xavier(ks[3], (E, D, F)), 'b2': jnp.zeros((E, D), jnp.float32), 'gamma': jnp.ones((D,), jnp.float32), 'beta': jnp.zeros((D,), jnp.float32)}
    _L1_ffn_in = _L1_ffn_setup()

    def _L2_attn_setup():
        import jax, jax.numpy as jnp
        import numpy as np
        EPS = float(np.finfo(np.float32).eps)
        B, S, F_, E, H = (8, 512, 128, 128, 16)
        HD = E // H
        LAYER = 1
        LAMBDA_INIT = 0.8 - 0.6 * float(np.exp(-0.3 * (LAYER - 1)))
        SCALE = 1.0 / float(np.sqrt(E // 2))

        def _rms(x, g):
            return x * jax.lax.rsqrt(jnp.mean(x * x, axis=-1, keepdims=True) + EPS) * g
        key = jax.random.key(seed)
        ks = jax.random.split(key, 7)
        x = jax.random.normal(ks[0], (B, S, F_), jnp.float32)
        s = 0.02
        Wq = jax.random.normal(ks[1], (E, F_), jnp.float32) * s
        Wk = jax.random.normal(ks[2], (E, F_), jnp.float32) * s
        Wv = jax.random.normal(ks[3], (E, F_), jnp.float32) * s
        W1 = jax.random.normal(ks[4], (E, E), jnp.float32) * s
        W2 = jax.random.normal(ks[5], (E, E), jnp.float32) * s
        lambda_params = jnp.full((4,), 0.8, jnp.float32)
        g1 = jnp.ones((F_,), jnp.float32)
        g2 = jnp.ones((HD,), jnp.float32)
        g3 = jnp.ones((E,), jnp.float32)
        return dict(x=x, Wq=Wq, Wk=Wk, Wv=Wv, lambda_params=lambda_params, g1=g1, g2=g2, g3=g3, W1=W1, W2=W2)
    _L2_attn_in = _L2_attn_setup()

    def _L2_ffn_setup():
        import jax, jax.numpy as jnp
        import numpy as np
        NUM_EXPERTS = 64
        TOP_K = 2
        B, S, EMB, MLP = (4, 256, 128, 256)
        key = jax.random.key(seed)
        k1, k2, k3, k4, k5 = jax.random.split(key, 5)
        inputs = jax.random.normal(k1, (B, S, EMB), dtype=jnp.float32)
        gate_kernel = jax.random.normal(k2, (EMB, NUM_EXPERTS), dtype=jnp.float32) / np.sqrt(EMB)
        w0 = jax.random.normal(k3, (NUM_EXPERTS, EMB, MLP), dtype=jnp.float32) / np.sqrt(EMB)
        w1 = jax.random.normal(k4, (NUM_EXPERTS, EMB, MLP), dtype=jnp.float32) / np.sqrt(EMB)
        wo = jax.random.normal(k5, (NUM_EXPERTS, MLP, EMB), dtype=jnp.float32) / np.sqrt(MLP)
        return {'inputs': inputs, 'gate_kernel': gate_kernel, 'w0': w0, 'w1': w1, 'wo': wo}
    _L2_ffn_in = _L2_ffn_setup()

    def _L3_attn_setup():
        import jax, jax.numpy as jnp
        import numpy as np
        HID = 128
        NH = 16
        HD = HID // NH
        RANK = 16
        B, L = (2, 256)
        key = jax.random.key(seed)
        ks = jax.random.split(key, 9)
        s = 0.02
        return {'x': jax.random.normal(ks[0], (B, L, HID), dtype=jnp.float32), 'Wq': jax.random.normal(ks[1], (HID, HID), dtype=jnp.float32) * s, 'Wk': jax.random.normal(ks[2], (HID, HID), dtype=jnp.float32) * s, 'Wv': jax.random.normal(ks[3], (HID, HID), dtype=jnp.float32) * s, 'Wg': jax.random.normal(ks[4], (HID, HID), dtype=jnp.float32) * s, 'Wgk1': jax.random.normal(ks[5], (HID, RANK), dtype=jnp.float32) * s, 'Wgk2': jax.random.normal(ks[6], (RANK, HID), dtype=jnp.float32) * s, 'bgk2': jnp.zeros((HID,), dtype=jnp.float32), 'gamma': jnp.ones((HID,), dtype=jnp.float32), 'beta': jnp.zeros((HID,), dtype=jnp.float32), 'Wout': jax.random.normal(ks[7], (HID, HID), dtype=jnp.float32) * s}
    _L3_attn_in = _L3_attn_setup()

    def _L3_ffn_setup():
        import jax, jax.numpy as jnp
        import numpy as np

        def _binarize(w):
            alpha = jax.lax.stop_gradient(jnp.mean(jnp.abs(w), axis=1, keepdims=True))
            bw = alpha * jnp.sign(w)
            return w + jax.lax.stop_gradient(bw - w)
        key = jax.random.key(seed)
        k1, k2, k3, k4, k5 = jax.random.split(key, 5)
        D, H = (128, 512)
        x = jax.random.normal(k1, (64, 196, D), dtype=jnp.float32)
        w1 = jax.random.normal(k2, (H, D), dtype=jnp.float32) * 0.02
        b1 = jax.random.normal(k3, (H,), dtype=jnp.float32) * 0.02
        w2 = jax.random.normal(k4, (D, H), dtype=jnp.float32) * 0.02
        b2 = jax.random.normal(k5, (D,), dtype=jnp.float32) * 0.02
        return {'x': x, 'w1': w1, 'b1': b1, 'w2': w2, 'b2': b2}
    _L3_ffn_in = _L3_ffn_setup()
    _d = {'L0_attn_x': _L0_attn_in['x'], 'L0_attn_Wq': _L0_attn_in['Wq'], 'L0_attn_Wk': _L0_attn_in['Wk'], 'L0_attn_Wv': _L0_attn_in['Wv'], 'L0_attn_Wb': _L0_attn_in['Wb'], 'L0_attn_Wa': _L0_attn_in['Wa'], 'L0_attn_A_log': _L0_attn_in['A_log'], 'L0_attn_dt_bias': _L0_attn_in['dt_bias'], 'L0_attn_Wg': _L0_attn_in['Wg'], 'L0_attn_o_norm_w': _L0_attn_in['o_norm_w'], 'L0_attn_Wo': _L0_attn_in['Wo'], 'L0_attn_W_fc': _L0_attn_in['W_fc'], 'L0_attn_W_proj': _L0_attn_in['W_proj'], 'L0_ffn_qweights': _L0_ffn_in['qweights'], 'L0_ffn_scales': _L0_ffn_in['scales'], 'L0_ffn_biases': _L0_ffn_in['biases'], 'L0_ffn_lora_a': _L0_ffn_in['lora_a'], 'L0_ffn_lora_b': _L0_ffn_in['lora_b'], 'L0_ffn_ln_gamma': _L0_ffn_in['ln_gamma'], 'L0_ffn_ln_beta': _L0_ffn_in['ln_beta'], 'L1_attn_W_Q': _L1_attn_in['W_Q'], 'L1_attn_W_K': _L1_attn_in['W_K'], 'L1_attn_W_V': _L1_attn_in['W_V'], 'L1_attn_W_O': _L1_attn_in['W_O'], 'L1_ffn_Wr': _L1_ffn_in['Wr'], 'L1_ffn_br': _L1_ffn_in['br'], 'L1_ffn_W1': _L1_ffn_in['W1'], 'L1_ffn_b1': _L1_ffn_in['b1'], 'L1_ffn_W2': _L1_ffn_in['W2'], 'L1_ffn_b2': _L1_ffn_in['b2'], 'L1_ffn_gamma': _L1_ffn_in['gamma'], 'L1_ffn_beta': _L1_ffn_in['beta'], 'L2_attn_Wq': _L2_attn_in['Wq'], 'L2_attn_Wk': _L2_attn_in['Wk'], 'L2_attn_Wv': _L2_attn_in['Wv'], 'L2_attn_lambda_params': _L2_attn_in['lambda_params'], 'L2_attn_g1': _L2_attn_in['g1'], 'L2_attn_g2': _L2_attn_in['g2'], 'L2_attn_g3': _L2_attn_in['g3'], 'L2_attn_W1': _L2_attn_in['W1'], 'L2_attn_W2': _L2_attn_in['W2'], 'L2_ffn_gate_kernel': _L2_ffn_in['gate_kernel'], 'L2_ffn_w0': _L2_ffn_in['w0'], 'L2_ffn_w1': _L2_ffn_in['w1'], 'L2_ffn_wo': _L2_ffn_in['wo'], 'L3_attn_Wq': _L3_attn_in['Wq'], 'L3_attn_Wk': _L3_attn_in['Wk'], 'L3_attn_Wv': _L3_attn_in['Wv'], 'L3_attn_Wg': _L3_attn_in['Wg'], 'L3_attn_Wgk1': _L3_attn_in['Wgk1'], 'L3_attn_Wgk2': _L3_attn_in['Wgk2'], 'L3_attn_bgk2': _L3_attn_in['bgk2'], 'L3_attn_gamma': _L3_attn_in['gamma'], 'L3_attn_beta': _L3_attn_in['beta'], 'L3_attn_Wout': _L3_attn_in['Wout'], 'L3_ffn_w1': _L3_ffn_in['w1'], 'L3_ffn_b1': _L3_ffn_in['b1'], 'L3_ffn_w2': _L3_ffn_in['w2'], 'L3_ffn_b2': _L3_ffn_in['b2']}
    _x0 = _d['L0_attn_x']
    _d['L0_attn_x'] = jax.random.normal(jax.random.fold_in(jax.random.key(seed), 1), (4, 1024, 128), dtype=_x0.dtype)
    del _x0
    return _d

def reference(L0_attn_x, L0_attn_Wq, L0_attn_Wk, L0_attn_Wv, L0_attn_Wb, L0_attn_Wa, L0_attn_A_log, L0_attn_dt_bias, L0_attn_Wg, L0_attn_o_norm_w, L0_attn_Wo, L0_attn_W_fc, L0_attn_W_proj, L0_ffn_qweights, L0_ffn_scales, L0_ffn_biases, L0_ffn_lora_a, L0_ffn_lora_b, L0_ffn_ln_gamma, L0_ffn_ln_beta, L1_attn_W_Q, L1_attn_W_K, L1_attn_W_V, L1_attn_W_O, L1_ffn_Wr, L1_ffn_br, L1_ffn_W1, L1_ffn_b1, L1_ffn_W2, L1_ffn_b2, L1_ffn_gamma, L1_ffn_beta, L2_attn_Wq, L2_attn_Wk, L2_attn_Wv, L2_attn_lambda_params, L2_attn_g1, L2_attn_g2, L2_attn_g3, L2_attn_W1, L2_attn_W2, L2_ffn_gate_kernel, L2_ffn_w0, L2_ffn_w1, L2_ffn_wo, L3_attn_Wq, L3_attn_Wk, L3_attn_Wv, L3_attn_Wg, L3_attn_Wgk1, L3_attn_Wgk2, L3_attn_bgk2, L3_attn_gamma, L3_attn_beta, L3_attn_Wout, L3_ffn_w1, L3_ffn_b1, L3_ffn_w2, L3_ffn_b2):

    def _L0_attn_ref(x, Wq, Wk, Wv, Wb, Wa, A_log, dt_bias, Wg, o_norm_w, Wo, W_fc, W_proj):
        import jax, jax.numpy as jnp
        import numpy as np
        from functools import partial
        B, S, D, H, DK, DV, DFF = (4, 256, 128, 8, 128, 128, 512)
        EPS = 1e-06

        def rms_norm(x):
            return x * jax.lax.rsqrt(jnp.mean(x * x, axis=-1, keepdims=True) + EPS)

        def l2norm(x):
            return x * jax.lax.rsqrt(jnp.sum(x * x, axis=-1, keepdims=True) + EPS)

        def gated_delta_net(h, Wq, Wk, Wv, Wb, Wa, A_log, dt_bias, Wg, o_norm_w, Wo):
            b, s, _ = h.shape
            q = l2norm(jax.nn.silu(h @ Wq).reshape(b, s, H, DK))
            k = l2norm(jax.nn.silu(h @ Wk).reshape(b, s, H, DK))
            v = jax.nn.silu(h @ Wv).reshape(b, s, H, DV)
            beta = jax.nn.sigmoid(h @ Wb)
            g = -jnp.exp(A_log) * jax.nn.softplus(h @ Wa + dt_bias)
            alpha = jnp.exp(g)
            scale = DK ** (-0.5)
            tm = lambda a: jnp.moveaxis(a, 1, 0)
            qs, ks_, vs, als, bts = (tm(q), tm(k), tm(v), tm(alpha), tm(beta))

            def step(Sst, inp):
                q_t, k_t, v_t, a_t, b_t = inp
                Sst = Sst * a_t[..., None, None]
                kv = jnp.einsum('bhd,bhde->bhe', k_t, Sst)
                delta = (v_t - kv) * b_t[..., None]
                Sst = Sst + jnp.einsum('bhd,bhe->bhde', k_t, delta)
                o_t = jnp.einsum('bhd,bhde->bhe', q_t, Sst) * scale
                return (Sst, o_t)
            S0 = jnp.zeros((b, H, DK, DV), dtype=h.dtype)
            _, o = jax.lax.scan(step, S0, (qs, ks_, vs, als, bts))
            o = jnp.moveaxis(o, 0, 1)
            gate = (h @ Wg).reshape(b, s, H, DV)
            o = rms_norm(o) * o_norm_w * jax.nn.silu(gate)
            return o.reshape(b, s, H * DV) @ Wo
        ln_scale = 1.0
        h = gated_delta_net(ln_scale * rms_norm(x), Wq, Wk, Wv, Wb, Wa, A_log, dt_bias, Wg, o_norm_w, Wo)
        x = x + h
        m = ln_scale * rms_norm(x)
        y = jnp.square(jax.nn.relu(m @ W_fc)) @ W_proj
        return x + y

    def _L0_ffn_ref(x, qweights, scales, biases, lora_a, lora_b, ln_gamma, ln_beta):
        import jax, jax.numpy as jnp
        import numpy as np
        GROUP = 16
        EPS = 1e-05

        def _dequant(q, scale):
            w = q.astype(jnp.float32) / 7.5 - 1.0
            return w * jnp.repeat(scale, GROUP, axis=1)

        def _qlora_linear(x, q, scale, bias, la, lb):
            w = _dequant(q, scale)
            base = jnp.einsum('btd,od->bto', x, w) + bias
            lora = jnp.einsum('btr,or->bto', jnp.einsum('btd,rd->btr', x, la), lb)
            return base + lora

        def _layernorm(x, g, b):
            mu = jnp.mean(x, axis=-1, keepdims=True)
            var = jnp.mean(jnp.square(x - mu), axis=-1, keepdims=True)
            return (x - mu) * jax.lax.rsqrt(var + EPS) * g + b
        h = x
        for blk in range(3):
            i0, i1 = (2 * blk, 2 * blk + 1)
            y = _qlora_linear(h, qweights[i0], scales[i0], biases[i0], lora_a[i0], lora_b[i0])
            y = _layernorm(y, ln_gamma[blk], ln_beta[blk])
            y = jax.nn.gelu(y, approximate=False)
            y = _qlora_linear(y, qweights[i1], scales[i1], biases[i1], lora_a[i1], lora_b[i1])
            h = y + h
        return h

    def _L1_attn_ref(x, W_Q, W_K, W_V, W_O):
        import jax, jax.numpy as jnp
        import numpy as np
        import math
        D_MODEL = 128
        NUM_HEADS = 16
        HEAD_DIM = D_MODEL // NUM_HEADS
        ROPE_THETA = 10000.0

        def _rope_tables(seq_len, dim, theta=ROPE_THETA):
            inv = 1.0 / theta ** (jnp.arange(0, dim, 2, dtype=jnp.float32) / dim)
            t = jnp.arange(seq_len, dtype=jnp.float32)
            f = jnp.outer(t, inv)
            cos = jnp.repeat(jnp.cos(f), 2, axis=-1)
            sin = jnp.repeat(jnp.sin(f), 2, axis=-1)
            return (cos, sin)

        def _rotate_half(x):
            x1 = x[..., ::2]
            x2 = x[..., 1::2]
            return jnp.stack((-x2, x1), axis=-1).reshape(x.shape)
        B, L, _ = x.shape

        def proj(W):
            return jnp.einsum('bld,ed->ble', x, W).reshape(B, L, NUM_HEADS, HEAD_DIM).transpose(0, 2, 1, 3)
        q, k, v = (proj(W_Q), proj(W_K), proj(W_V))
        cos, sin = _rope_tables(L, HEAD_DIM)
        cos = cos[None, None].astype(x.dtype)
        sin = sin[None, None].astype(x.dtype)
        q = q * cos + _rotate_half(q) * sin
        k = k * cos + _rotate_half(k) * sin
        scores = jnp.einsum('bhqd,bhkd->bhqk', q, k) / math.sqrt(HEAD_DIM)
        attn = jax.nn.softmax(scores, axis=-1)
        ctx = jnp.einsum('bhqk,bhkd->bhqd', attn, v)
        ctx = ctx.transpose(0, 2, 1, 3).reshape(B, L, D_MODEL)
        return jnp.einsum('bld,ed->ble', ctx, W_O)

    def _L1_ffn_ref(tgt, Wr, br, W1, b1, W2, b2, gamma, beta):
        import jax, jax.numpy as jnp
        import numpy as np
        B, S, D, F, E = (2, 256, 128, 512, 8)
        LN_EPS = 1e-05

        def _layer_norm(x, gamma, beta):
            mu = jnp.mean(x, axis=-1, keepdims=True)
            var = jnp.mean(jnp.square(x - mu), axis=-1, keepdims=True)
            return (x - mu) * jax.lax.rsqrt(var + LN_EPS) * gamma + beta
        logits = jnp.einsum('bsd,ed->bse', tgt, Wr) + br
        top_v, top_i = jax.lax.top_k(logits, 2)
        top_w = jax.nn.softmax(top_v, axis=-1)
        n_exp = logits.shape[-1]
        router_w = jnp.sum(jax.nn.one_hot(top_i, n_exp, dtype=top_w.dtype) * top_w[..., None], axis=-2)
        h = jnp.einsum('bsd,efd->bsef', tgt, W1) + b1
        h = jax.nn.relu(h)
        o = jnp.einsum('bsef,edf->bsed', h, W2) + b2
        tgt2 = jnp.einsum('bsed,bse->bsd', o, router_w)
        return _layer_norm(tgt + tgt2, gamma, beta)

    def _L2_attn_ref(x, Wq, Wk, Wv, lambda_params, g1, g2, g3, W1, W2):
        import jax, jax.numpy as jnp
        import numpy as np
        EPS = float(np.finfo(np.float32).eps)
        B, S, F_, E, H = (8, 512, 128, 128, 16)
        HD = E // H
        LAYER = 1
        LAMBDA_INIT = 0.8 - 0.6 * float(np.exp(-0.3 * (LAYER - 1)))
        SCALE = 1.0 / float(np.sqrt(E // 2))

        def _rms(x, g):
            return x * jax.lax.rsqrt(jnp.mean(x * x, axis=-1, keepdims=True) + EPS) * g
        b, s_len, _ = x.shape
        xn = _rms(x, g1)
        Q = jnp.einsum('bsf,ef->bse', xn, Wq).reshape(b, s_len, H, HD)
        K = jnp.einsum('bsf,ef->bse', xn, Wk).reshape(b, s_len, H, HD)
        V = jnp.einsum('bsf,ef->bse', xn, Wv).reshape(b, s_len, H, HD)
        pQ = jax.nn.elu(Q)
        pK = jax.nn.elu(K)
        Q1, Q2 = jnp.split(pQ, 2, axis=-1)
        K1, K2 = jnp.split(pK, 2, axis=-1)
        kv1 = jnp.einsum('bshe,bshd->bsed', K1, V) * SCALE
        kv2 = jnp.einsum('bshe,bshd->bsed', K2, V) * SCALE
        w1 = jnp.einsum('bshe,bsed->bshd', Q1, kv1)
        w2 = jnp.einsum('bshe,bsed->bshd', Q2, kv2)
        lmb = jnp.exp(lambda_params[0] * lambda_params[1]) - jnp.exp(lambda_params[2] * lambda_params[3]) + LAMBDA_INIT
        attn = w1 - lmb * w2
        attn = (1.0 - LAMBDA_INIT) * _rms(attn, g2)
        attn = attn.reshape(b, s_len, E)
        attn = _rms(attn, g3) + attn
        h = jax.nn.gelu(jnp.einsum('bse,fe->bsf', attn, W1), approximate=False)
        out = jnp.einsum('bsf,ef->bse', h, W2) + attn
        return out

    def _L2_ffn_ref(inputs, gate_kernel, w0, w1, wo):
        import jax, jax.numpy as jnp
        import numpy as np
        NUM_EXPERTS = 64
        TOP_K = 2
        B, S, EMB, MLP = (4, 256, 128, 256)
        b, s, e = inputs.shape
        x = inputs.reshape(b * s, e)
        gate_logits = jnp.einsum('te,ex->tx', x, gate_kernel)
        weights, selected = jax.lax.top_k(gate_logits, TOP_K)
        weights = jax.nn.softmax(weights.astype(jnp.float32), axis=-1)
        flat_experts = selected.reshape(-1)
        sort_idx = jnp.argsort(flat_experts)
        token_idx = sort_idx // TOP_K
        sorted_x = jnp.take(x, token_idx, axis=0)
        group_sizes = jnp.bincount(flat_experts, length=NUM_EXPERTS).astype(jnp.int32)
        h0 = jax.lax.ragged_dot(sorted_x, w0, group_sizes)
        h1 = jax.lax.ragged_dot(sorted_x, w1, group_sizes)
        inter = jax.nn.silu(h0) * h1
        out_sorted = jax.lax.ragged_dot(inter, wo, group_sizes)
        unsorted = jnp.take(out_sorted, jnp.argsort(sort_idx), axis=0)
        per_tok = unsorted.reshape(b * s, TOP_K, e)
        out = jnp.einsum('BKE,BK->BE', per_tok.astype(jnp.float32), weights)
        return out.reshape(b, s, e)

    def _L3_attn_ref(x, Wq, Wk, Wv, Wg, Wgk1, Wgk2, bgk2, gamma, beta, Wout):
        import jax, jax.numpy as jnp
        import numpy as np
        HID = 128
        NH = 16
        HD = HID // NH
        RANK = 16
        B, L = (2, 256)
        Bb, Ll, Hid = x.shape
        H, Dh = (NH, HD)
        q = (x @ Wq).reshape(Bb, Ll, H, Dh)
        k = (x @ Wk).reshape(Bb, Ll, H, Dh)
        v = (x @ Wv).reshape(Bb, Ll, H, Dh)
        gk = (jax.nn.log_sigmoid(x @ Wgk1 @ Wgk2 + bgk2) / 16.0).reshape(Bb, Ll, H, Dh)
        qT = jnp.transpose(q, (1, 0, 2, 3))
        kT = jnp.transpose(k, (1, 0, 2, 3))
        vT = jnp.transpose(v, (1, 0, 2, 3))
        gT = jnp.transpose(gk, (1, 0, 2, 3))

        def step(state, inp):
            qt, kt, vt, gt = inp
            gate = jnp.exp(gt)
            state = state * gate[..., None] + vt[..., None] * kt[..., None, :]
            out_t = jnp.einsum('bhvk,bhk->bhv', state, qt)
            return (state, out_t)
        state0 = jnp.zeros((Bb, H, Dh, Dh), dtype=x.dtype)
        _, outs = jax.lax.scan(step, state0, (qT, kT, vT, gT))
        out = jnp.transpose(outs, (1, 0, 2, 3)).reshape(Bb, Ll, Hid)
        mu = out.mean(-1, keepdims=True)
        var = out.var(-1, keepdims=True)
        out = (out - mu) / jnp.sqrt(var + 1e-05) * gamma + beta
        out = out * jax.nn.silu(x @ Wg)
        return out @ Wout

    def _L3_ffn_ref(x, w1, b1, w2, b2):
        import jax, jax.numpy as jnp
        import numpy as np

        def _binarize(w):
            alpha = jax.lax.stop_gradient(jnp.mean(jnp.abs(w), axis=1, keepdims=True))
            bw = alpha * jnp.sign(w)
            return w + jax.lax.stop_gradient(bw - w)
        bw1 = _binarize(w1)
        h = jnp.einsum('bsd,hd->bsh', x, bw1) + b1
        h = jax.nn.gelu(h, approximate=False)
        bw2 = _binarize(w2)
        out = jnp.einsum('bsh,dh->bsd', h, bw2) + b2
        return out
    x = L0_attn_x
    xn = _layernorm(x, axis=-1)
    x = x + _L0_attn_ref(xn, L0_attn_Wq, L0_attn_Wk, L0_attn_Wv, L0_attn_Wb, L0_attn_Wa, L0_attn_A_log, L0_attn_dt_bias, L0_attn_Wg, L0_attn_o_norm_w, L0_attn_Wo, L0_attn_W_fc, L0_attn_W_proj) + _L0_ffn_ref(xn, L0_ffn_qweights, L0_ffn_scales, L0_ffn_biases, L0_ffn_lora_a, L0_ffn_lora_b, L0_ffn_ln_gamma, L0_ffn_ln_beta)
    xn = _layernorm(x, axis=-1)
    x = x + _L1_attn_ref(xn, L1_attn_W_Q, L1_attn_W_K, L1_attn_W_V, L1_attn_W_O) + _L1_ffn_ref(xn, L1_ffn_Wr, L1_ffn_br, L1_ffn_W1, L1_ffn_b1, L1_ffn_W2, L1_ffn_b2, L1_ffn_gamma, L1_ffn_beta)
    xn = _layernorm(x, axis=-1)
    x = x + _L2_attn_ref(xn, L2_attn_Wq, L2_attn_Wk, L2_attn_Wv, L2_attn_lambda_params, L2_attn_g1, L2_attn_g2, L2_attn_g3, L2_attn_W1, L2_attn_W2) + _L2_ffn_ref(xn, L2_ffn_gate_kernel, L2_ffn_w0, L2_ffn_w1, L2_ffn_wo)
    xn = _layernorm(x, axis=-1)
    x = x + _L3_attn_ref(xn, L3_attn_Wq, L3_attn_Wk, L3_attn_Wv, L3_attn_Wg, L3_attn_Wgk1, L3_attn_Wgk2, L3_attn_bgk2, L3_attn_gamma, L3_attn_beta, L3_attn_Wout) + _L3_ffn_ref(xn, L3_ffn_w1, L3_ffn_b1, L3_ffn_w2, L3_ffn_b2)
    return x

_drawn_inputs = setup_inputs


def setup_inputs(seed=0):
    import zlib

    import numpy as np

    out = dict(_drawn_inputs(seed))
    spreads = {'L0_attn_o_norm_w': (1.0, 0.6),
     'L0_ffn_ln_gamma': (1.0, 0.2),
     'L0_ffn_ln_beta': (0.0, 0.1),
     'L1_ffn_br': (0.0, 2.0),
     'L1_ffn_b1': (0.0, 2.0),
     'L1_ffn_b2': (0.0, 1.741),
     'L1_ffn_gamma': (1.0, 0.6),
     'L1_ffn_beta': (0.0, 0.43),
     'L2_attn_lambda_params': (0.800000011920929, 0.2),
     'L2_attn_g1': (1.0, 0.2),
     'L2_attn_g2': (1.0, 0.2),
     'L2_attn_g3': (1.0, 0.542),
     'L3_attn_bgk2': (0.0, 0.8),
     'L3_attn_gamma': (1.0, 0.6),
     'L3_attn_beta': (0.0, 0.8)}
    factors = {'L0_attn_Wq': 7.436,
     'L0_attn_Wk': 7.556,
     'L0_attn_Wv': 7.387,
     'L0_attn_Wb': 8.0,
     'L0_attn_Wa': 8.0,
     'L0_attn_A_log': 8.0,
     'L0_attn_dt_bias': 8.0,
     'L0_attn_Wg': 7.716,
     'L0_attn_Wo': 7.241,
     'L0_attn_W_fc': 7.762,
     'L0_attn_W_proj': 7.748,
     'L0_ffn_biases': 11.961,
     'L0_ffn_lora_a': 4.177,
     'L0_ffn_lora_b': 4.201,
     'L1_attn_W_Q': 4.494,
     'L1_attn_W_K': 4.486,
     'L2_attn_W1': 7.522,
     'L2_attn_W2': 7.292,
     'L3_attn_Wq': 8.0,
     'L3_attn_Wk': 8.0,
     'L3_attn_Wv': 8.0,
     'L3_attn_Wg': 8.0,
     'L3_attn_Wgk1': 8.0,
     'L3_attn_Wgk2': 8.0,
     'L3_attn_Wout': 8.0,
     'L3_ffn_w1': 8.0,
     'L3_ffn_b1': 23.381,
     'L3_ffn_w2': 8.0,
     'L3_ffn_b2': 49.775,
     'L1_ffn_W1': 2.734}
    for name, (base, spread) in spreads.items():
        noise = np.random.default_rng([zlib.crc32(name.encode()), seed]).standard_normal(out[name].shape)
        drawn = base * np.exp(spread * noise) if base else spread * noise
        out[name] = jnp.asarray(drawn.astype(out[name].dtype))
    for name, factor in factors.items():
        out[name] = (out[name] * factor).astype(out[name].dtype)
    return out
```

```python
from contextlib import ExitStack

import numpy as np

import concourse.bass as bass
from concourse import mybir

F32 = mybir.dt.float32
BF16 = mybir.dt.bfloat16
I32 = mybir.dt.int32
U32 = mybir.dt.uint32
ALU = mybir.AluOpType
ACT = mybir.ActivationFunctionType
AX = mybir.AxisListType.X

P = 128
BATCH, SEQ, D = 4, 1024, 128
TOK = BATCH * SEQ
GRP = 512
GROUPS = TOK // GRP
CHUNK = 128
CHUNKS = TOK // CHUNK

class Steps:

    def __init__(self, sem, names):
        self.sem, self.names, self.next = sem, names.split(), 0

    def does(self, name):
        assert self.names[self.next] == name, (self.names[self.next], name)
        self.next = (self.next + 1) % len(self.names)
        return self.sem, 1

    def did(self, tile, name):
        return self.sem, tile * len(self.names) + (self.names.index(name) + 1)

class Loads:

    def __init__(self, sem):
        self.sem, self.count = sem, 0

    def one(self):
        self.count += 16
        return self.sem, 16

    def all(self):
        return self.sem, self.count

def tiles(eng, n, depth, body):
    for i in range(depth):
        body(i, i, False)
    with eng.Fori(1, n // depth) as turn:
        for s in range(depth):
            body(turn * depth + s, s, True)

class Space:

    def __init__(self, nc, prefix, stack):
        self.nc, self.prefix, self.stack = nc, prefix, stack

    def sb(self, name, shape, dt=F32):
        return self.stack.enter_context(self.nc.sbuf_tensor(self.prefix + name, shape, dt))

    def ps(self, name, shape=(P, 512), dt=F32):
        return self.stack.enter_context(self.nc.psum_tensor(self.prefix + name, list(shape), dt))

    def sem(self, name):
        return self.stack.enter_context(self.nc.semaphore(self.prefix + name))

def over_heads(ap, n):
    return ap.unsqueeze(1).to_broadcast([P, n, ap.shape[1]])

def along(ap, n):
    return ap.unsqueeze(2).to_broadcast([P, ap.shape[1], n])

def on_all_partitions(ap):
    flat = ap.rearrange("(a n) -> a n", a=1)
    return flat.to_broadcast([P, flat.shape[1]])

def rsqrt_names(k):
    return f"ln{k} rs{k} r2{k}", f"vr{k} nt{k} rn{k}"

def rsqrt_act(nc, eng, act, g, k, v, eps, ln, rs, r2):
    nc.scalar.activation(ln, v, ACT.Ln, bias=eps).then_inc(*act.does(f"ln{k}"))
    eng.wait_ge(*act.did(g, f"ln{k}"))
    nc.scalar.activation(rs, ln, ACT.Exp, scale=-0.5).then_inc(*act.does(f"rs{k}"))
    eng.wait_ge(*act.did(g, f"rs{k}"))
    nc.scalar.activation(r2, rs, ACT.Square).then_inc(*act.does(f"r2{k}"))

def rsqrt_dve(nc, eng, act, dve, g, k, v, eps, rs, r2):
    eng.wait_ge(*act.did(g, f"r2{k}"))
    nc.vector.scalar_tensor_tensor(r2, v, eps, r2, ALU.add, ALU.mult).then_inc(*dve.does(f"vr{k}"))
    eng.wait_ge(*dve.did(g, f"vr{k}"))
    nc.vector.tensor_scalar(r2, r2, -0.5, 1.5, ALU.mult, ALU.add).then_inc(*dve.does(f"nt{k}"))
    eng.wait_ge(*dve.did(g, f"nt{k}"))
    nc.vector.tensor_tensor(rs, rs, r2, ALU.mult).then_inc(*dve.does(f"rn{k}"))
    eng.wait_ge(*dve.did(g, f"rn{k}"))

def norm_stage(nc, name, XT, XN, ones_mean, rms=None):
    with ExitStack() as stack:
        m = Space(nc, name, stack)
        xc = m.sb("xc", [P, 2, GRP])
        sq = m.sb("sq", [P, 2, GRP])
        ln = m.sb("ln", [P, 2, GRP])
        rs = m.sb("rs", [P, 2, GRP])
        r2 = m.sb("r2", [P, 2, GRP])
        eps = m.sb("eps", [P, 2])
        mean = [m.ps(f"mean{s}") for s in range(2)]
        var = [m.ps(f"var{s}") for s in range(2)]
        pe_names, act_names, dve_names = "mean var", "sq " + rsqrt_names("v")[0], "xc " + rsqrt_names("v")[1] + " xn"
        if rms:
            HT, Wba, GL = rms
            hs = m.sb("hs", [P, 2, GRP])
            ms = [m.ps(f"ms{s}") for s in range(2)]
            gl = [m.ps(f"gl{s}") for s in range(2)]
            pe_names, act_names, dve_names = pe_names + " ms gl", act_names + " sq2 " + rsqrt_names("m")[0] + " ht", dve_names + " " + rsqrt_names("m")[1] + " hs gl"
        pe, act, dve = Steps(m.sem("pe"), pe_names), Steps(m.sem("act"), act_names), Steps(m.sem("dve"), dve_names)
        ready = m.sem("ready")

        def at(t, g):
            return t[:, bass.ds(g * GRP, GRP)]

        with nc.Block() as block:
            @block.tensor
            def _(eng):
                def body(g, s, again):
                    if again:
                        eng.wait_ge(*dve.did(g - 2, "xn"))
                    nc.tensor.matmul(mean[s][:], ones_mean[:], at(XT, g), start=True, stop=True).then_inc(*pe.does("mean"))
                    eng.wait_ge(*act.did(g, "sq"))
                    nc.tensor.matmul(var[s][:], ones_mean[:], sq[:, s], start=True, stop=True).then_inc(*pe.does("var"))
                    if rms:
                        eng.wait_ge(*act.did(g, "sq2"))
                        nc.tensor.matmul(ms[s][:], ones_mean[:], sq[:, s], start=True, stop=True).then_inc(*pe.does("ms"))
                        eng.wait_ge(*dve.did(g, "hs"))
                        if again:
                            eng.wait_ge(*dve.did(g - 2, "gl"))
                        for t in range(4):
                            last = nc.tensor.matmul(gl[s][:, t * 16:t * 16 + 16], hs[:, s, t * P:t * P + P], Wba[:], start=True, stop=True)
                        last.then_inc(*pe.does("gl"))
                tiles(eng, GROUPS, 2, body)

            @block.scalar
            def _(eng):
                nc.scalar.preload_act_table_set("natural_log_exp_and_others")
                eng.wait_ge(ready, 2)
                def body(g, s, again):
                    eng.wait_ge(*dve.did(g, "xc"))
                    nc.scalar.activation(sq[:, s], xc[:, s], ACT.Square).then_inc(*act.does("sq"))
                    eng.wait_ge(*pe.did(g, "var"))
                    rsqrt_act(nc, eng, act, g, "v", var[s][:], eps[:, 0:1], ln[:, s], rs[:, s], r2[:, s])
                    if rms:
                        eng.wait_ge(*dve.did(g, "xn"))
                        nc.scalar.activation(sq[:, s], at(XN, g), ACT.Square).then_inc(*act.does("sq2"))
                        eng.wait_ge(*pe.did(g, "ms"))
                        rsqrt_act(nc, eng, act, g, "m", ms[s][:], eps[:, 1:2], ln[:, s], rs[:, s], r2[:, s])
                        eng.wait_ge(*dve.did(g, "hs"))
                        nc.scalar.activation(at(HT, g), hs[:, s], ACT.Copy).then_inc(*act.does("ht"))
                tiles(eng, GROUPS, 2, body)

            @block.vector
            def _(eng):
                nc.vector.memset(eps[:, 0:1], 1e-5).then_inc(ready, 1)
                nc.vector.memset(eps[:, 1:2], 1e-6).then_inc(ready, 1)
                def body(g, s, again):
                    eng.wait_ge(*pe.did(g, "mean"))
                    nc.vector.tensor_tensor(xc[:, s], at(XT, g), mean[s][:], ALU.subtract).then_inc(*dve.does("xc"))
                    rsqrt_dve(nc, eng, act, dve, g, "v", var[s][:], 1e-5, rs[:, s], r2[:, s])
                    nc.vector.tensor_tensor(at(XN, g), xc[:, s], rs[:, s], ALU.mult).then_inc(*dve.does("xn"))
                    if rms:
                        rsqrt_dve(nc, eng, act, dve, g, "m", ms[s][:], 1e-6, rs[:, s], r2[:, s])
                        if again:
                            eng.wait_ge(*act.did(g - 2, "ht"))
                        nc.vector.tensor_tensor(hs[:, s], at(XN, g), rs[:, s], ALU.mult).then_inc(*dve.does("hs"))
                        eng.wait_ge(*pe.did(g, "gl"))
                        nc.vector.tensor_copy(GL[:, bass.ds(g * 64, 64)], gl[s][:, 0:64]).then_inc(*dve.does("gl"))
                tiles(eng, GROUPS, 2, body)

HEADS, DK = 8, 128
PAIR = 4 * P
SC = 48

def delta_gates(nc, name, GL, SCAL, A_log, dt_bias, masks):
    N = CHUNKS * HEADS
    with ExitStack() as stack:
        m = Space(nc, name, stack)
        la = m.sb("la", [P, HEADS])
        db = m.sb("db", [P, HEADS])
        ea = m.sb("ea", [P, HEADS])
        a, y, u, d, lu, g, eb = (m.sb(n, [P, N]) for n in "a y u d lu g eb".split())
        psum = [m.ps(f"sum{k}") for k in range(3)]
        loaded, act, dve, pe = Loads(m.sem("loaded")), Steps(m.sem("act"), "ea y lu eb e0 e1 e2"), \
            Steps(m.sem("dve"), "a na u d dm rd w1 is0 w2 w sp g ps b1 b2 b zero zc neg"), Steps(m.sem("pe"), "sums")
        before_incl, everyone, after = masks["row_le_col"], masks["ones"], masks["row_gt_col"]
        gl = GL[:].rearrange("p (c k) -> p c k", k=16)
        sc = SCAL[:].rearrange("p (c k) -> p c k", k=SC)

        def v3(t):
            return t[:].rearrange("p (c h) -> p c h", h=HEADS)

        def chunks(t):
            return t[:].unsqueeze(1).to_broadcast([P, CHUNKS, HEADS])

        with nc.Block() as block:
            @block.sync
            def _(eng):
                eng.dma_start(la[:], on_all_partitions(A_log)).then_inc(*loaded.one())
                eng.dma_start(db[:], on_all_partitions(dt_bias)).then_inc(*loaded.one())
                eng.wait_ge(*loaded.all())

            @block.scalar
            def _(eng):
                nc.scalar.preload_act_table_set("natural_log_exp_and_others")
                eng.wait_ge(*loaded.all())
                nc.scalar.activation(ea[:], la[:], ACT.Exp).then_inc(*act.does("ea"))
                eng.wait_ge(*dve.did(0, "na"))
                nc.scalar.activation(y[:], y[:], ACT.Exp).then_inc(*act.does("y"))
                eng.wait_ge(*dve.did(0, "u"))
                nc.scalar.activation(lu[:], u[:], ACT.Ln).then_inc(*act.does("lu"))
                nc.scalar.activation(v3(eb), gl[:, :, 0:HEADS], ACT.Exp, scale=-1.0).then_inc(*act.does("eb"))
                eng.wait_ge(*pe.did(0, "sums"))
                for k in range(3):
                    lo = (16, 32, 40)[k]
                    nc.scalar.activation(sc[:, :, lo:lo + HEADS], psum[k][:, 0:N].rearrange("p (c h) -> p c h", h=HEADS), ACT.Exp).then_inc(*act.does(f"e{k}"))

            @block.vector
            def _(eng):
                def step(ins, name_):
                    ins.then_inc(*dve.does(name_))
                    eng.wait_ge(*dve.did(0, name_))
                eng.wait_ge(*loaded.all())
                step(nc.vector.tensor_tensor(v3(a), gl[:, :, HEADS:16], chunks(db), ALU.add), "a")
                step(nc.vector.scalar_tensor_tensor(y[:], a[:], -1.0, a[:], ALU.mult, ALU.min), "na")
                eng.wait_ge(*act.did(0, "y"))
                step(nc.vector.tensor_scalar(u[:], y[:], 1.0, None, ALU.add), "u")
                step(nc.vector.tensor_scalar(d[:], u[:], -1.0, None, ALU.add), "d")
                step(nc.vector.tensor_scalar(g[:], d[:], 1e-30, None, ALU.max), "dm")
                step(nc.vector.reciprocal(g[:], g[:]), "rd")
                step(nc.vector.tensor_tensor(g[:], g[:], y[:], ALU.mult), "w1")
                step(nc.vector.tensor_scalar(d[:], d[:], 0.0, None, ALU.is_equal), "is0")
                eng.wait_ge(*act.did(0, "lu"))
                step(nc.vector.tensor_tensor(g[:], g[:], lu[:], ALU.mult), "w2")
                step(nc.vector.tensor_tensor(d[:], d[:], y[:], ALU.mult), "w")
                step(nc.vector.scalar_tensor_tensor(d[:], a[:], 0.0, d[:], ALU.max, ALU.add), "sp")
                step(nc.vector.tensor_tensor(g[:], g[:], d[:], ALU.add), "g")
                eng.wait_ge(*act.did(0, "ea"))
                step(nc.vector.scalar_tensor_tensor(sc[:, :, 0:HEADS], v3(g), -1.0, chunks(ea), ALU.mult, ALU.mult), "ps")
                eng.wait_ge(*act.did(0, "eb"))
                step(nc.vector.tensor_scalar(eb[:], eb[:], 1.0, None, ALU.add), "b1")
                step(nc.vector.reciprocal(eb[:], eb[:]), "b2")
                step(nc.vector.tensor_copy(sc[:, :, 8:16], v3(eb)), "b")
                eng.wait_ge(*act.did(0, "e2"))
                first = SCAL[:].rearrange("p (b c k) -> p b c k", b=BATCH, k=SC)[:, :, 0, :]
                step(nc.vector.memset(first[:, :, 16:24], 0.0), "zero")
                step(nc.vector.memset(first[:, :, 32:40], 0.0), "zc")
                step(nc.vector.scalar_tensor_tensor(sc[:, :, 24:32], sc[:, :, 16:24], -1.0, sc[:, :, 8:16], ALU.mult, ALU.mult), "neg")

            @block.tensor
            def _(eng):
                eng.wait_ge(*dve.did(0, "ps"))
                for k, who in enumerate((before_incl, everyone, after)):
                    last = nc.tensor.matmul(psum[k][:, 0:N].rearrange("p (c h) -> p c h", h=HEADS), who[:], sc[:, :, 0:HEADS], start=True, stop=True)
                last.then_inc(*pe.does("sums"))

def delta_stage(nc, name, HT, XN, X1, SCAL, w, masks):
    with ExitStack() as stack:
        m = Space(nc, name, stack)

        def heads(n):
            return m.sb(n, [P, HEADS, P])

        hc = m.sb("hc", [P, P])
        q, k, v, sg, kd = map(heads, "q k v sg kd".split())
        E, Em, Gm, kT, qT, An, PT = map(heads, "E Em Gm kT qT An PT".split())
        U, T, W, r, dl, oP, o, S = map(heads, "U T W r dl oP o S".split())
        Es = E
        sqs = Gm
        Pn = W
        osq, oT = r, oP
        ss = m.sb("ss", [P, 16])
        rr = m.sb("rr", [P, 16])
        os_ = m.sb("os", [P, 8])
        ro = m.sb("ro", [P, 8])
        half = m.sb("half", [P, 16])
        sc = m.sb("sc", [P, SC])
        nb = m.sb("nb", [P, HEADS])
        A = [m.ps(f"A{j}") for j in range(2)]
        B = [m.ps(f"B{j}") for j in range(2)]
        C = [m.ps(f"C{j}") for j in range(2)]
        Y = m.ps("Y")
        LEVELS = 7

        inv_pe = "z00 z01 t00 t01 " + " ".join(f"z{l}0 z{l}1 u{l}0 t{l}0 u{l}1 t{l}1" for l in range(1, LEVELS - 1)) + " z60 z61 u60 u61"
        inv_act = "t00 t01 " + " ".join(f"u{l}0 t{l}0 u{l}1 t{l}1" for l in range(1, LEVELS - 1)) + " u60 u61"
        pe = Steps(m.sem("pe"), "Q0 Q1 K0 K1 V0 V1 G0 G1 D0 D1 kT0 kT1 qT0 qT1 KK0 KK1 QK0 QK1 PT0 PT1 " + inv_pe +
                   " KS0 KS1 QS0 QS1 dl0 dl1 PD0 PD1 KD0 KD1 oT0 oT1 Y")
        act = Steps(m.sem("act"), "h sc q0 q1 k0 k1 v0 v1 g0 g1 E0 E1 kT0 kT1 qT0 qT1 PT0 PT1 " + inv_act + " dl0 dl1 oP0 oP1 oT0 oT1")
        dve = Steps(m.sem("dve"), "nb ssq ssk se sq qn0 qn1 kn0 kn1 A0 A1 P0 P1 " + " ".join(f"w{l}0 w{l}1" for l in range(LEVELS)) +
                    " r0 r1 o0 o1 S0 S1 os0 os1 oe on0 on1 og0 og1 x1")
        pool = Steps(m.sem("pool"), "qq kk rr bv Gm kd Em0 Es0 Em1 Es1 osq0 osq1 ro")
        cleared, half_set = m.sem("cleared"), m.sem("half_set")
        hs = [slice(4 * j, 4 * j + 4) for j in range(2)]

        def bank(t):
            return t[:].rearrange("p (h n) -> p h n", h=4)

        def tok(t, i):
            return t[:, bass.ds(i * CHUNK, CHUNK)]

        with nc.Block() as block:
            @block.tensor
            def _(eng):
                def mm(out, lhsT, rhs):
                    return nc.tensor.matmul(out, lhsT, rhs, start=True, stop=True)

                def body(i, _, again):
                    def prev(who, step):
                        if again:
                            eng.wait_ge(*who.did(i - 1, step))
                    eng.wait_ge(*act.did(i, "h"))
                    prev(act, "oT1")
                    prev(dve, "S1")
                    for n, bk in (("q", A), ("k", B), ("v", C), ("g", A)):
                        for j in range(2):
                            if n == "g":
                                eng.wait_ge(*act.did(i, f"q{j}"))
                            mm(bk[j][:], hc[:], w[n][:, j * PAIR:(j + 1) * PAIR]).then_inc(*pe.does(f"{n.upper()}{j}"))
                    eng.wait_ge(*pool.did(i, "Gm"))
                    for j in range(2):
                        eng.wait_ge(*act.did(i, f"k{j}"))
                        mm(B[j][:], masks["row_le_col"][:], Gm[:, hs[j], :].rearrange("p h n -> p (h n)")).then_inc(*pe.does(f"D{j}"))
                    for n, src, dst, before in (("kT", k, C, "v"), ("qT", q, A, "g")):
                        for j in range(2):
                            eng.wait_ge(*act.did(i, f"{before}{j}"))
                            eng.wait_ge(*dve.did(i, f"{n[0]}n{j}"))
                            for h in range(4):
                                last = nc.tensor.transpose(bank(dst[j])[:, h, :], src[:, 4 * j + h, :], masks["eye"][:])
                            last.then_inc(*pe.does(f"{n}{j}"))
                    for j in range(2):
                        eng.wait_ge(*act.did(i, f"E{j}"))
                        eng.wait_ge(*act.did(i, f"kT{j}"))
                        for h in range(4 * j, 4 * j + 4):
                            last = mm(bank(B[j])[:, h % 4, :], kT[:, h, :], kT[:, h, :])
                        last.then_inc(*pe.does(f"KK{j}"))
                    for j in range(2):
                        eng.wait_ge(*act.did(i, f"qT{j}"))
                        for h in range(4 * j, 4 * j + 4):
                            last = mm(bank(C[j])[:, h % 4, :], qT[:, h, :], kT[:, h, :])
                        last.then_inc(*pe.does(f"QK{j}"))
                    for j in range(2):
                        eng.wait_ge(*dve.did(i, f"P{j}"))
                        for h in range(4 * j, 4 * j + 4):
                            last = nc.tensor.transpose(bank(A[j])[:, h % 4, :], Pn[:, h, :], masks["eye"][:])
                        last.then_inc(*pe.does(f"PT{j}"))
                    for l in range(LEVELS):
                        for j in range(2):
                            eng.wait_ge(*dve.did(i, f"w{l - 1}{j}" if l else f"A{j}"))
                            if l:
                                eng.wait_ge(*(act.did(i, f"u{l - 1}{j}") if l > 1 else dve.did(i, f"w0{j}")))
                            for h in range(4 * j, 4 * j + 4):
                                nc.tensor.matmul(bank(B[j])[:, h % 4, :], masks["eye16"][:], masks["eye16"][:], start=True, stop=False)
                                last = nc.tensor.matmul(bank(B[j])[:, h % 4, :], An[:, h, :], U[:, h, :] if l else masks["eye"][:], start=False, stop=True)
                            last.then_inc(*pe.does(f"z{l}{j}"))
                        for j in range(2):
                            eng.wait_ge(*dve.did(i, f"w{l}{j}"))
                            if l:
                                eng.wait_ge(*(act.did(i, f"t{l - 1}{j}")))
                                if l == 1:
                                    eng.wait_ge(*dve.did(i, f"P{j}"))
                                for h in range(4 * j, 4 * j + 4):
                                    last = mm(bank(C[j])[:, h % 4, :], T[:, h, :], W[:, h, :])
                                last.then_inc(*pe.does(f"u{l}{j}"))
                            if l < LEVELS - 1:
                                if l == 0:
                                    eng.wait_ge(*act.did(i, f"PT{j}"))
                                for h in range(4 * j, 4 * j + 4):
                                    if l:
                                        last = mm(bank(A[j])[:, h % 4, :], W[:, h, :], T[:, h, :])
                                    else:
                                        last = mm(bank(A[j])[:, h % 4, :], U[:, h, :], masks["eye"][:])
                                last.then_inc(*pe.does(f"t{l}{j}"))
                    eng.wait_ge(cleared, 1)
                    for n, src, bk in (("KS", kT, B), ("QS", qT, A)):
                        for j in range(2):
                            prev(dve, f"S{j}")
                            for h in range(4 * j, 4 * j + 4):
                                last = mm(bank(bk[j])[:, h % 4, :], src[:, h, :], S[:, h, :])
                            last.then_inc(*pe.does(f"{n}{j}"))
                    for j in range(2):
                        eng.wait_ge(*dve.did(i, f"r{j}"))
                        eng.wait_ge(*act.did(i, f"u6{j}"))
                        for h in range(4 * j, 4 * j + 4):
                            last = mm(bank(C[j])[:, h % 4, :], U[:, h, :], r[:, h, :])
                        last.then_inc(*pe.does(f"dl{j}"))
                    for n, src, bk in (("PD", PT, B), ("KD", kd, C)):
                        for j in range(2):
                            eng.wait_ge(*act.did(i, f"dl{j}"))
                            if n == "KD" and j == 0:
                                eng.wait_ge(*pool.did(i, "kd"))
                            for h in range(4 * j, 4 * j + 4):
                                last = mm(bank(bk[j])[:, h % 4, :], src[:, h, :], dl[:, h, :])
                            last.then_inc(*pe.does(f"{n}{j}"))
                    for j in range(2):
                        eng.wait_ge(*dve.did(i, f"og{j}"))
                        for h in range(4 * j, 4 * j + 4):
                            last = nc.tensor.transpose(bank(A[j])[:, h % 4, :], o[:, h, :], masks["eye"][:])
                        last.then_inc(*pe.does(f"oT{j}"))
                    eng.wait_ge(*act.did(i, "oT1"))
                    prev(dve, "x1")
                    for h in range(HEADS):
                        last = nc.tensor.matmul(Y[:, 0:P], w["o"][:, h * P:(h + 1) * P], oT[:, h, :], start=(h == 0), stop=(h == HEADS - 1))
                    last.then_inc(*pe.does("Y"))
                tiles(eng, CHUNKS, 1, body)

            @block.scalar
            def _(eng):
                def body(i, _, again):
                    def prev(who, step):
                        if again:
                            eng.wait_ge(*who.did(i - 1, step))
                    prev(pe, "G1")
                    nc.scalar.activation(hc[:], tok(HT, i), ACT.Copy).then_inc(*act.does("h"))
                    prev(dve, "S1")
                    prev(pool, "kd")
                    nc.scalar.activation(sc[:], SCAL[:, bass.ds(i * SC, SC)], ACT.Copy).then_inc(*act.does("sc"))
                    for n, dst, bk, free in (("q", q, A, "qT1"), ("k", k, B, "KD1"), ("v", v, C, None), ("g", sg, A, None)):
                        for j in range(2):
                            eng.wait_ge(*pe.did(i, f"{n.upper()}{j}"))
                            if free:
                                prev(pe, free)
                            elif n == "v":
                                prev(dve, f"r{j}")
                            else:
                                prev(dve, f"og{j}")
                            nc.scalar.activation(dst[:, hs[j], :], bank(bk[j]), ACT.Silu).then_inc(*act.does(f"{n}{j}"))
                    for j in range(2):
                        eng.wait_ge(*pe.did(i, f"D{j}"))
                        prev(dve, f"A{j}")
                        nc.scalar.activation(E[:, hs[j], :], bank(B[j]), ACT.Exp).then_inc(*act.does(f"E{j}"))
                    for n, dst, bk in (("kT", kT, C), ("qT", qT, A), ("PT", PT, A)):
                        for j in range(2):
                            eng.wait_ge(*pe.did(i, f"{n}{j}"))
                            nc.scalar.activation(dst[:, hs[j], :], bank(bk[j]), ACT.Copy).then_inc(*act.does(f"{n}{j}"))
                    for l in range(LEVELS):
                        for j in range(2):
                            if l:
                                eng.wait_ge(*pe.did(i, f"u{l}{j}"))
                                nc.scalar.activation(U[:, hs[j], :], bank(C[j]), ACT.Copy).then_inc(*act.does(f"u{l}{j}"))
                            if l < LEVELS - 1:
                                eng.wait_ge(*pe.did(i, f"t{l}{j}"))
                                nc.scalar.activation(T[:, hs[j], :], bank(A[j]), ACT.Copy).then_inc(*act.does(f"t{l}{j}"))
                    for j in range(2):
                        eng.wait_ge(*pe.did(i, f"dl{j}"))
                        nc.scalar.activation(dl[:, hs[j], :], bank(C[j]), ACT.Copy).then_inc(*act.does(f"dl{j}"))
                    for j in range(2):
                        eng.wait_ge(*pe.did(i, f"PD{j}"))
                        nc.scalar.activation(oP[:, hs[j], :], bank(B[j]), ACT.Copy).then_inc(*act.does(f"oP{j}"))
                    for j in range(2):
                        eng.wait_ge(*pe.did(i, f"oT{j}"))
                        nc.scalar.activation(oT[:, hs[j], :], bank(A[j]), ACT.Copy).then_inc(*act.does(f"oT{j}"))
                tiles(eng, CHUNKS, 1, body)

            @block.vector
            def _(eng):
                nc.vector.memset(S[:], 0.0).then_inc(cleared, 1)

                def body(i, _, again):
                    def prev(who, step):
                        if again:
                            eng.wait_ge(*who.did(i - 1, step))
                    eng.wait_ge(*act.did(i, "sc"))
                    nc.vector.tensor_scalar(nb[:], sc[:, 8:16], -1.0, None, ALU.mult).then_inc(*dve.does("nb"))
                    eng.wait_ge(*pool.did(i, "qq"))
                    nc.vector.tensor_reduce(ss[:, 0:8], Gm[:], AX, ALU.add).then_inc(*dve.does("ssq"))
                    eng.wait_ge(*pool.did(i, "kk"))
                    nc.vector.tensor_reduce(ss[:, 8:16], Em[:], AX, ALU.add).then_inc(*dve.does("ssk"))
                    eng.wait_ge(*dve.did(i, "ssk"))
                    nc.vector.tensor_scalar(ss[:], ss[:], 1e-6, None, ALU.add).then_inc(*dve.does("se"))
                    eng.wait_ge(*pool.did(i, "rr"))
                    nc.vector.tensor_scalar(rr[:, 0:8], rr[:, 0:8], float(DK) ** -0.5, None, ALU.mult).then_inc(*dve.does("sq"))
                    eng.wait_ge(*dve.did(i, "sq"))
                    for n, t, lo in (("q", q, 0), ("k", k, 8)):
                        for j in range(2):
                            nc.vector.tensor_tensor(t[:, hs[j], :], t[:, hs[j], :], along(rr[:, lo + 4 * j:lo + 4 * j + 4], P), ALU.mult).then_inc(*dve.does(f"{n}n{j}"))
                    for j in range(2):
                        eng.wait_ge(*pe.did(i, f"KK{j}"))
                        eng.wait_ge(*pool.did(i, f"Es{j}"))
                        for h in range(4 * j, 4 * j + 4):
                            last = nc.vector.scalar_tensor_tensor(An[:, h, :], bank(B[j])[:, h % 4, :], nb[:, h:h + 1], Es[:, h, :], ALU.mult, ALU.mult)
                        last.then_inc(*dve.does(f"A{j}"))
                    for j in range(2):
                        eng.wait_ge(*pe.did(i, f"QK{j}"))
                        nc.vector.tensor_tensor(Pn[:, hs[j], :], bank(C[j]), Em[:, hs[j], :], ALU.mult).then_inc(*dve.does(f"P{j}"))
                    for l in range(LEVELS):
                        dst = W if l else U
                        for j in range(2):
                            eng.wait_ge(*pe.did(i, f"z{l}{j}"))
                            nc.vector.tensor_tensor(dst[:, hs[j], :], bank(B[j]), over_heads(masks["level"][:, l * P:(l + 1) * P], 4), ALU.mult).then_inc(*dve.does(f"w{l}{j}"))
                    for j in range(2):
                        eng.wait_ge(*pe.did(i, f"KS{j}"))
                        eng.wait_ge(*pool.did(i, "bv"))
                        for h in range(4 * j, 4 * j + 4):
                            last = nc.vector.scalar_tensor_tensor(r[:, h, :], bank(B[j])[:, h % 4, :], sc[:, 24 + h:25 + h], v[:, h, :], ALU.mult, ALU.add)
                        last.then_inc(*dve.does(f"r{j}"))
                    for j in range(2):
                        eng.wait_ge(*pe.did(i, f"QS{j}"))
                        eng.wait_ge(*act.did(i, f"oP{j}"))
                        for h in range(4 * j, 4 * j + 4):
                            last = nc.vector.scalar_tensor_tensor(o[:, h, :], bank(A[j])[:, h % 4, :], sc[:, 16 + h:17 + h], oP[:, h, :], ALU.mult, ALU.add)
                        last.then_inc(*dve.does(f"o{j}"))
                    for j in range(2):
                        eng.wait_ge(*pe.did(i, f"KD{j}"))
                        for h in range(4 * j, 4 * j + 4):
                            last = nc.vector.scalar_tensor_tensor(S[:, h, :], S[:, h, :], sc[:, 32 + h:33 + h], bank(C[j])[:, h % 4, :], ALU.mult, ALU.add)
                        last.then_inc(*dve.does(f"S{j}"))
                    for j in range(2):
                        eng.wait_ge(*pool.did(i, f"osq{j}"))
                        nc.vector.tensor_reduce(os_[:, 4 * j:4 * j + 4], osq[:, hs[j], :], AX, ALU.add).then_inc(*dve.does(f"os{j}"))
                    eng.wait_ge(*dve.did(i, "os1"))
                    nc.vector.tensor_scalar(os_[:], os_[:], 1.0 / DK, 1e-6, ALU.mult, ALU.add).then_inc(*dve.does("oe"))
                    eng.wait_ge(*pool.did(i, "ro"))
                    for j in range(2):
                        nc.vector.tensor_tensor(o[:, hs[j], :], o[:, hs[j], :], along(ro[:, 4 * j:4 * j + 4], P), ALU.mult).then_inc(*dve.does(f"on{j}"))
                    for j in range(2):
                        eng.wait_ge(*dve.did(i, f"on{j}"))
                        nc.vector.tensor_tensor(o[:, hs[j], :], o[:, hs[j], :], sg[:, hs[j], :], ALU.mult).then_inc(*dve.does(f"og{j}"))
                    eng.wait_ge(*pe.did(i, "Y"))
                    nc.vector.tensor_tensor(tok(X1, i), Y[:, 0:P], tok(XN, i), ALU.add).then_inc(*dve.does("x1"))
                tiles(eng, CHUNKS, 1, body)

            @block.gpsimd
            def _(eng):
                nc.gpsimd.memset(half[:], -0.5).then_inc(half_set, 1)
                eng.wait_ge(half_set, 1)

                def body(i, _, again):
                    def prev(who, step):
                        if again:
                            eng.wait_ge(*who.did(i - 1, step))
                    eng.wait_ge(*act.did(i, "q1"))
                    prev(pe, "D1")
                    nc.gpsimd.tensor_tensor(Gm[:], q[:], q[:], ALU.mult).then_inc(*pool.does("qq"))
                    eng.wait_ge(*act.did(i, "k1"))
                    prev(dve, "P1")
                    nc.gpsimd.tensor_tensor(Em[:], k[:], k[:], ALU.mult).then_inc(*pool.does("kk"))
                    eng.wait_ge(*dve.did(i, "se"))
                    nc.gpsimd.tensor_tensor(rr[:], ss[:], half[:], ALU.pow).then_inc(*pool.does("rr"))
                    eng.wait_ge(*act.did(i, "v1"))
                    nc.gpsimd.tensor_tensor(v[:], v[:], along(sc[:, 8:16], P), ALU.mult).then_inc(*pool.does("bv"))
                    nc.gpsimd.tensor_tensor(Gm[:], over_heads(masks["row_gt_col"][:], HEADS), along(sc[:, 0:8], P), ALU.mult).then_inc(*pool.does("Gm"))
                    eng.wait_ge(*dve.did(i, "kn1"))
                    prev(pe, "KD1")
                    nc.gpsimd.tensor_tensor(kd[:], k[:], along(sc[:, 40:48], P), ALU.mult).then_inc(*pool.does("kd"))
                    for j in range(2):
                        eng.wait_ge(*act.did(i, f"E{j}"))
                        nc.gpsimd.tensor_tensor(Em[:, hs[j], :], E[:, hs[j], :], over_heads(masks["row_ge_col"][:], 4), ALU.mult).then_inc(*pool.does(f"Em{j}"))
                        eng.wait_ge(*pool.did(i, f"Em{j}"))
                        nc.gpsimd.tensor_tensor(Es[:, hs[j], :], E[:, hs[j], :], over_heads(masks["row_gt_col"][:], 4), ALU.mult).then_inc(*pool.does(f"Es{j}"))
                    for j in range(2):
                        eng.wait_ge(*dve.did(i, f"o{j}"))
                        nc.gpsimd.tensor_tensor(osq[:, hs[j], :], o[:, hs[j], :], o[:, hs[j], :], ALU.mult).then_inc(*pool.does(f"osq{j}"))
                    eng.wait_ge(*dve.did(i, "oe"))
                    nc.gpsimd.tensor_tensor(ro[:], os_[:], half[:, 0:8], ALU.pow).then_inc(*pool.does("ro"))
                tiles(eng, CHUNKS, 1, body)

def at_group(t, g):
    return t[:, bass.ds(g * GRP, GRP)]

def relu_mlp_stage(nc, name, XT, X1, w_up, w_down, ones_mean):
    F = w_up.shape[1] // P
    with ExitStack() as stack:
        m = Space(nc, name, stack)
        sq, ln, rs, r2, xm = (m.sb(n, [P, 2, GRP]) for n in "sq ln rs r2 xm".split())
        r = m.sb("r", [P, F, GRP])
        hid = m.sb("hid", [P, F, GRP])
        xs = m.sb("xs", [P, 2, GRP])
        eps = m.sb("eps", [P, 1])
        ms = m.ps("ms")
        up = [m.ps(f"up{c}") for c in range(F)]
        down = m.ps("down")
        pe = Steps(m.sem("pe"), "ms " + " ".join(f"up{c}" for c in range(F)) + " down")
        act = Steps(m.sem("act"), "sq " + rsqrt_names("m")[0] + " " + " ".join(f"r{c}" for c in range(F)))
        dve = Steps(m.sem("dve"), rsqrt_names("m")[1] + " xm xs " + " ".join(f"hid{c}" for c in range(F)) + " out")
        ready = m.sem("ready")
        with nc.Block() as block:
            @block.tensor
            def _(eng):
                def body(g, s, again):
                    eng.wait_ge(*act.did(g, "sq"))
                    if s or again:
                        eng.wait_ge(*dve.did(g - 1, "xm"))
                    nc.tensor.matmul(ms[:], ones_mean[:], sq[:, s], start=True, stop=True).then_inc(*pe.does("ms"))
                    eng.wait_ge(*dve.did(g, "xm"))
                    for c in range(F):
                        if s or again:
                            eng.wait_ge(*dve.did(g - 1, f"hid{c}"))
                        nc.tensor.matmul(up[c][:], w_up[:, c * P:(c + 1) * P], xm[:, s], start=True, stop=True).then_inc(*pe.does(f"up{c}"))
                    if s or again:
                        eng.wait_ge(*dve.did(g - 1, "out"))
                    for c in range(F):
                        eng.wait_ge(*dve.did(g, f"hid{c}"))
                        last = nc.tensor.matmul(down[:], w_down[:, c * P:(c + 1) * P], hid[:, c], start=(c == 0), stop=(c == F - 1))
                    last.then_inc(*pe.does("down"))
                tiles(eng, GROUPS, 2, body)

            @block.scalar
            def _(eng):
                nc.scalar.preload_act_table_set("natural_log_exp_and_others")
                eng.wait_ge(ready, 1)
                def body(g, s, again):
                    nc.scalar.activation(sq[:, s], at_group(X1, g), ACT.Square).then_inc(*act.does("sq"))
                    eng.wait_ge(*pe.did(g, "ms"))
                    rsqrt_act(nc, eng, act, g, "m", ms[:], eps[:], ln[:, s], rs[:, s], r2[:, s])
                    for c in range(F):
                        eng.wait_ge(*pe.did(g, f"up{c}"))
                        if s or again:
                            eng.wait_ge(*dve.did(g - 1, f"hid{c}"))
                        nc.scalar.activation(r[:, c], up[c][:], ACT.Relu).then_inc(*act.does(f"r{c}"))
                tiles(eng, GROUPS, 2, body)

            @block.vector
            def _(eng):
                nc.vector.memset(eps[:], 1e-6).then_inc(ready, 1)
                def body(g, s, again):
                    rsqrt_dve(nc, eng, act, dve, g, "m", ms[:], 1e-6, rs[:, s], r2[:, s])
                    nc.vector.tensor_tensor(xm[:, s], at_group(X1, g), rs[:, s], ALU.mult).then_inc(*dve.does("xm"))
                    nc.vector.tensor_tensor(xs[:, s], at_group(XT, g), at_group(X1, g), ALU.add).then_inc(*dve.does("xs"))
                    for c in range(F):
                        eng.wait_ge(*act.did(g, f"r{c}"))
                        if s or again:
                            eng.wait_ge(*pe.did(g - 1, "down"))
                        nc.vector.scalar_tensor_tensor(hid[:, c], up[c][:], 0.0, r[:, c], ALU.max, ALU.mult).then_inc(*dve.does(f"hid{c}"))
                    eng.wait_ge(*pe.did(g, "down"))
                    eng.wait_ge(*dve.did(g, "xs"))
                    nc.vector.tensor_tensor(at_group(XT, g), down[:], xs[:, s], ALU.add).then_inc(*dve.does("out"))
                tiles(eng, GROUPS, 2, body)

def gelu_mlp_stage(nc, name, XT, XN, w1, w2, bias1, bias2):
    F = w1.shape[1] // P
    with ExitStack() as stack:
        m = Space(nc, name, stack)
        hid = m.sb("hid", [P, 2, F, GRP])
        up = [m.ps(f"up{c}") for c in range(F)]
        down = [m.ps(f"down{s}") for s in range(2)]
        pe = Steps(m.sem("pe"), " ".join(f"up{c}" for c in range(F)) + " down")
        act = Steps(m.sem("act"), " ".join(f"hid{c}" for c in range(F)))
        dve = Steps(m.sem("dve"), "out")
        with nc.Block() as block:
            @block.tensor
            def _(eng):
                def body(g, s, again):
                    for c in range(F):
                        if s or again:
                            eng.wait_ge(*act.did(g - 1, f"hid{c}"))
                        nc.tensor.matmul(up[c][:], w1[:, c * P:(c + 1) * P], at_group(XN, g), start=True, stop=True).then_inc(*pe.does(f"up{c}"))
                    if again:
                        eng.wait_ge(*dve.did(g - 2, "out"))
                    for c in range(F):
                        eng.wait_ge(*act.did(g, f"hid{c}"))
                        last = nc.tensor.matmul(down[s][:], w2[:, c * P:(c + 1) * P], hid[:, s, c], start=(c == 0), stop=(c == F - 1))
                    last.then_inc(*pe.does("down"))
                tiles(eng, GROUPS, 2, body)

            @block.scalar
            def _(eng):
                def body(g, s, again):
                    if again:
                        eng.wait_ge(*pe.did(g - 2, "down"))
                    for c in range(F):
                        eng.wait_ge(*pe.did(g, f"up{c}"))
                        nc.scalar.activation(hid[:, s, c], up[c][:], ACT.Gelu, bias=bias1[:, c:c + 1]).then_inc(*act.does(f"hid{c}"))
                tiles(eng, GROUPS, 2, body)

            @block.vector
            def _(eng):
                def body(g, s, again):
                    eng.wait_ge(*pe.did(g, "down"))
                    nc.vector.scalar_tensor_tensor(at_group(XT, g), down[s][:], bias2[:, 0:1], at_group(XT, g), ALU.add, ALU.add).then_inc(*dve.does("out"))
                tiles(eng, GROUPS, 2, body)

def binary_weights(nc, name, w1_in, w2_in, w1, w2, eye):
    H = w1_in.shape[0]
    F = H // P
    with ExitStack() as stack:
        m = Space(nc, name, stack)
        raw = m.sb("raw", [P, 2, F, P])
        mag = m.sb("mag", [P, 2, F, P])
        sign = m.sb("sign", [P, 2, F, P])
        al = m.sb("al", [P, 2, F])
        turned = [m.ps(f"turned{k}") for k in range(2)]
        loaded = Loads(m.sem("loaded"))
        act, dve, pe = Steps(m.sem("act"), "mag sign w0 w1"), Steps(m.sem("dve"), "sum1 sum2 mean1 mean2 a1 a2 diff w"), Steps(m.sem("pe"), "t0 t1")
        with nc.Block() as block:
            @block.sync
            def _(eng):
                eng.dma_start(raw[:, 0], w1_in.rearrange("(c p) d -> p c d", p=P)).then_inc(*loaded.one())
                eng.dma_start(raw[:, 1], w2_in.rearrange("d (c p) -> d c p", p=P)).then_inc(*loaded.one())

            @block.scalar
            def _(eng):
                eng.wait_ge(*loaded.all())
                nc.scalar.activation(mag[:], raw[:], ACT.Abs).then_inc(*act.does("mag"))
                nc.scalar.activation(sign[:], raw[:], ACT.Sign).then_inc(*act.does("sign"))
                for k, dst in enumerate((w1, w2)):
                    eng.wait_ge(*pe.did(0, f"t{k}"))
                    nc.scalar.activation(dst[:], turned[k][:], ACT.Copy).then_inc(*act.does(f"w{k}"))

            @block.vector
            def _(eng):
                def step(ins, name_):
                    ins.then_inc(*dve.does(name_))
                    eng.wait_ge(*dve.did(0, name_))
                eng.wait_ge(*act.did(0, "mag"))
                step(nc.vector.tensor_reduce(al[:, 0], mag[:, 0], AX, ALU.add), "sum1")
                step(nc.vector.tensor_reduce(al[:, 1, 0:1], mag[:, 1].rearrange("p c n -> p (c n)"), AX, ALU.add), "sum2")
                step(nc.vector.tensor_scalar(al[:, 0], al[:, 0], 1.0 / P, None, ALU.mult), "mean1")
                step(nc.vector.tensor_scalar(al[:, 1, 0:1], al[:, 1, 0:1], 1.0 / H, None, ALU.mult), "mean2")
                eng.wait_ge(*act.did(0, "sign"))
                step(nc.vector.tensor_tensor(mag[:, 0], sign[:, 0], along(al[:, 0], P), ALU.mult), "a1")
                step(nc.vector.tensor_scalar(mag[:, 1], sign[:, 1], al[:, 1, 0:1], None, ALU.mult), "a2")
                step(nc.vector.tensor_tensor(mag[:], mag[:], raw[:], ALU.subtract), "diff")
                step(nc.vector.tensor_tensor(mag[:], mag[:], raw[:], ALU.add), "w")

            @block.tensor
            def _(eng):
                eng.wait_ge(*dve.did(0, "w"))
                for k in range(2):
                    for c in range(F):
                        last = nc.tensor.transpose(turned[k][:, c * P:(c + 1) * P], mag[:, k, c], eye[:])
                    last.then_inc(*pe.does(f"t{k}"))

def qlora_weights(nc, name, q_in, scales, lora_a, lora_bT, WQ, eye):
    L, GROUP = q_in.shape[0], 16
    R = lora_a.shape[1]
    with ExitStack() as stack:
        m = Space(nc, name, stack)
        qi = m.sb("qi", [P, L, P], q_in.dtype)
        wf = m.sb("wf", [P, L, P])
        sc = m.sb("sc", [P, L, P // GROUP])
        la = m.sb("la", [R, L, P])
        lb = m.sb("lb", [R, L, P])
        low = [m.ps(f"low{k}") for k in range(2)]
        turned = [m.ps(f"turned{k}") for k in range(2)]
        loaded = Loads(m.sem("loaded"))
        pe, dve = Steps(m.sem("pe"), "low turned"), Steps(m.sem("dve"), "float affine scaled sum0 sum1 w0 w1")
        parts = [slice(0, 4), slice(4, L)]

        def bank(t, n):
            return t[:, 0:n * P].rearrange("p (l n) -> p l n", n=P)
        with nc.Block() as block:
            @block.sync
            def _(eng):
                eng.dma_start(qi[:], q_in.rearrange("l o i -> o l i")).then_inc(*loaded.one())
                eng.dma_start(sc[:], scales.rearrange("l o g -> o l g")).then_inc(*loaded.one())
                eng.dma_start(la[:], lora_a.rearrange("l r i -> r l i")).then_inc(*loaded.one())
                eng.dma_start(lb[:], lora_bT.rearrange("l r o -> r l o")).then_inc(*loaded.one())

            @block.tensor
            def _(eng):
                eng.wait_ge(*loaded.all())
                for l in range(L):
                    last = nc.tensor.matmul(bank(low[l // 4], 4)[:, l % 4, :], lb[:, l], la[:, l], start=True, stop=True)
                last.then_inc(*pe.does("low"))
                eng.wait_ge(*dve.did(0, "sum1"))
                for l in range(L):
                    last = nc.tensor.transpose(bank(turned[l // 4], 4)[:, l % 4, :], wf[:, l], eye[:])
                last.then_inc(*pe.does("turned"))

            @block.vector
            def _(eng):
                def step(ins, name_):
                    ins.then_inc(*dve.does(name_))
                    eng.wait_ge(*dve.did(0, name_))
                eng.wait_ge(*loaded.all())
                step(nc.vector.tensor_copy(wf[:], qi[:]), "float")
                step(nc.vector.tensor_scalar(wf[:], wf[:], 1.0 / 7.5, -1.0, ALU.mult, ALU.add), "affine")
                w4 = wf[:].rearrange("p l (g k) -> p (l g) k", k=GROUP)
                step(nc.vector.tensor_tensor(w4, w4, along(sc[:].rearrange("p l g -> p (l g)"), GROUP), ALU.mult), "scaled")
                eng.wait_ge(*pe.did(0, "low"))
                for k, part in enumerate(parts):
                    step(nc.vector.tensor_tensor(wf[:, part], wf[:, part], bank(low[k], part.stop - part.start), ALU.add), f"sum{k}")
                eng.wait_ge(*pe.did(0, "turned"))
                for k, part in enumerate(parts):
                    nc.vector.tensor_copy(WQ[:, part], bank(turned[k], part.stop - part.start)).then_inc(*dve.does(f"w{k}"))

def qlora_stage(nc, name, XT, XN, WQ, biasT, bias_rows, gammaT, betaT, eye):
    with ExitStack() as stack:
        m = Space(nc, name, stack)
        h = m.sb("h", [P, 2, GRP])
        y = m.sb("y", [P, 2, 4, P])
        z = m.sb("z", [P, 2, 4, P])
        yT = m.sb("yT", [P, 2, GRP])
        st = m.sb("st", [P, 2, 4, 6])
        ag = m.sb("ag", [P, 2, 4, 2])
        rs = m.sb("rs", [P, 2, 4])
        ve = m.sb("ve", [P, 2, 4])
        half = m.sb("half", [P, 4])
        carrier = m.sb("carrier", [P, 2])
        lin = [m.ps(f"lin{s}") for s in range(2)]
        turned = [m.ps(f"turned{s}") for s in range(2)]
        back = [m.ps(f"back{s}") for s in range(2)]
        N = 3
        per = lambda names: " ".join(f"{n}{b}" for b in range(N) for n in names.split())
        def pairs(names):
            return " ".join(f"{n}{b}{s}" for b in range(N) for n in names.split() for s in range(2))
        pe = Steps(m.sem("pe"), pairs("lin turned back"))
        act = Steps(m.sem("act"), "h0 h1 " + pairs("gelu"))
        dve = Steps(m.sem("dve"), " ".join(f"y{b}0 y{b}1 st{b}0 st{b}1 cr{b}0 ag{b}0 cr{b}1 ag{b}1 ve{b}0 ve{b}1 z{b}0 z{b}1 h{b}0 h{b}1" for b in range(N)) + " out0 out1")
        pool = Steps(m.sem("pool"), pairs("rs"))
        half_set = m.sem("half_set")

        with nc.Block() as block:
            @block.tensor
            def _(eng):
                def body(i, _, again):
                    for b in range(N):
                        for s in range(2):
                            if b == 0:
                                eng.wait_ge(*act.did(i, f"h{s}"))
                                if again:
                                    eng.wait_ge(*dve.did(i - 1, f"y{N - 1}{s}"))
                            else:
                                eng.wait_ge(*dve.did(i, f"h{b - 1}{s}"))
                            for t in range(4):
                                last = nc.tensor.matmul(lin[s][:, t * P:(t + 1) * P], h[:, s, t * P:(t + 1) * P], WQ[:, 2 * b], start=True, stop=True)
                            last.then_inc(*pe.does(f"lin{b}{s}"))
                        for s in range(2):
                            eng.wait_ge(*dve.did(i, f"z{b}{s}"))
                            for t in range(4):
                                last = nc.tensor.transpose(turned[s][:, t * P:(t + 1) * P], z[:, s, t], eye[:])
                            last.then_inc(*pe.does(f"turned{b}{s}"))
                        for s in range(2):
                            eng.wait_ge(*act.did(i, f"gelu{b}{s}"))
                            nc.tensor.matmul(back[s][:], WQ[:, 2 * b + 1], yT[:, s], start=True, stop=True).then_inc(*pe.does(f"back{b}{s}"))
                tiles(eng, GROUPS // 2, 1, body)

            @block.scalar
            def _(eng):
                def body(i, _, again):
                    for s in range(2):
                        if again:
                            eng.wait_ge(*dve.did(i - 1, f"out{s}"))
                        nc.scalar.activation(h[:, s], at_group(XN, i * 2 + s), ACT.Copy).then_inc(*act.does(f"h{s}"))
                    for b in range(N):
                        for s in range(2):
                            eng.wait_ge(*pe.did(i, f"turned{b}{s}"))
                            nc.scalar.activation(yT[:, s], turned[s][:], ACT.Gelu, scale=gammaT[:, b:b + 1], bias=betaT[:, b:b + 1]).then_inc(*act.does(f"gelu{b}{s}"))
                tiles(eng, GROUPS // 2, 1, body)

            @block.vector
            def _(eng):
                def body(i, _, again):
                    for b in range(N):
                        for s in range(2):
                            eng.wait_ge(*pe.did(i, f"lin{b}{s}"))
                            nc.vector.tensor_tensor(y[:, s], lin[s][:].rearrange("p (t n) -> p t n", n=P), over_heads(bias_rows[:, b], 4), ALU.add).then_inc(*dve.does(f"y{b}{s}"))
                        for s in range(2):
                            eng.wait_ge(*dve.did(i, f"y{b}{s}"))
                            for t in range(4):
                                last = nc.vector.bn_stats(st[:, s, t], y[:, s, t])
                            last.then_inc(*dve.does(f"st{b}{s}"))
                        for s in range(2):
                            eng.wait_ge(*dve.did(i, f"st{b}{s}"))
                            nc.vector.memset(carrier[:, s:s + 1], 0.0).then_inc(*dve.does(f"cr{b}{s}"))
                            for t in range(4):
                                last = nc.vector.bn_aggr(ag[:, s, t], st[:, s, t])
                            last.then_inc(*dve.does(f"ag{b}{s}"))
                        for s in range(2):
                            eng.wait_ge(*dve.did(i, f"ag{b}{s}"))
                            nc.vector.tensor_scalar(ve[:, s], ag[:, s, :, 1], 1e-5, None, ALU.add).then_inc(*dve.does(f"ve{b}{s}"))
                        for s in range(2):
                            eng.wait_ge(*pool.did(i, f"rs{b}{s}"))
                            for t in range(4):
                                last = nc.vector.tensor_scalar(z[:, s, t], y[:, s, t], ag[:, s, t, 0:1], rs[:, s, t:t + 1], ALU.subtract, ALU.mult)
                            last.then_inc(*dve.does(f"z{b}{s}"))
                        for s in range(2):
                            eng.wait_ge(*pe.did(i, f"back{b}{s}"))
                            nc.vector.scalar_tensor_tensor(h[:, s], back[s][:], biasT[:, b:b + 1], h[:, s], ALU.add, ALU.add).then_inc(*dve.does(f"h{b}{s}"))
                    for s in range(2):
                        eng.wait_ge(*dve.did(i, f"h{N - 1}{s}"))
                        nc.vector.tensor_tensor(at_group(XT, i * 2 + s), at_group(XT, i * 2 + s), h[:, s], ALU.add).then_inc(*dve.does(f"out{s}"))
                tiles(eng, GROUPS // 2, 1, body)

            @block.gpsimd
            def _(eng):
                nc.gpsimd.memset(half[:], -0.5).then_inc(half_set, 1)
                eng.wait_ge(half_set, 1)
                def body(i, _, again):
                    for b in range(N):
                        for s in range(2):
                            eng.wait_ge(*dve.did(i, f"ve{b}{s}"))
                            nc.gpsimd.tensor_tensor(rs[:, s], ve[:, s], half[:], ALU.pow).then_inc(*pool.does(f"rs{b}{s}"))
                tiles(eng, GROUPS // 2, 1, body)

AH, AD = 16, 8
AN = BATCH * AH
PARTS = 3
STACK = PARTS * PARTS * AD
QT = SEQ // P
SHIFT = 96
VW = AD + 1

def attn_project(nc, name, XN, Vh, q_dram, k_dram, w, wv, cos, sin):
    with ExitStack() as stack:
        m = Space(nc, name, stack)
        xs = m.sb("xs", [P, GRP])
        a = m.sb("a", [P, 2, GRP])
        b = m.sb("b", [P, 2, GRP])
        part = m.sb("part", [P, 2, PARTS, GRP], BF16)
        banks = [m.ps(f"w{k}") for k in range(4)]
        vb = m.ps("vb")
        pe = Steps(m.sem("pe"), "w0 w1 w2 w3 v")
        act = Steps(m.sem("act"), "xs v " + " ".join(f"c{p}{k}" for p in range(PARTS) for k in range(2)))
        dve = Steps(m.sem("dve"), "c0 s0 c1 s1")
        pool = Steps(m.sem("pool"), "r0 r1 d10 d11 d20 d21")
        ones_set, stored = m.sem("ones"), m.sem("stored")
        vh = Vh[:].rearrange("p (b h t e) -> p b h t e", b=BATCH, h=AH, e=VW)

        def both(eng, body):
            body(0, 0, False)
            body(0, 1, True)
            with eng.Fori(1, BATCH) as seq:
                body(seq, 0, True)
                body(seq, 1, True)

        with nc.Block() as block:
            @block.tensor
            def _(eng):
                def body(seq, s, again):
                    g = seq * 2 + s
                    for k in range(4):
                        if again:
                            eng.wait_ge(*dve.did(g - 1, f"{'cs'[k % 2]}{k // 2}"))
                        nc.tensor.matmul(banks[k][:], w[k][:], at_group(XN, g), start=True, stop=True).then_inc(*pe.does(f"w{k}"))
                    eng.wait_ge(*act.did(g, "xs"))
                    if again:
                        eng.wait_ge(*act.did(g - 1, "v"))
                    for t in range(4):
                        last = nc.tensor.matmul(vb[:, t * P:(t + 1) * P], xs[:, t * P:(t + 1) * P], wv[:], start=True, stop=True)
                    last.then_inc(*pe.does("v"))
                both(eng, body)

            @block.scalar
            def _(eng):
                eng.wait_ge(ones_set, 1)
                def body(seq, s, again):
                    g = seq * 2 + s
                    if again:
                        eng.wait_ge(*pe.did(g - 1, "v"))
                    nc.scalar.activation(xs[:], at_group(XN, g), ACT.Copy).then_inc(*act.does("xs"))
                    eng.wait_ge(*pe.did(g, "v"))
                    for t in range(4):
                        last = nc.scalar.activation(vh[:, bass.ds(seq, 1), :, 4 * s + t, 0:AD].rearrange("p o h e -> p (o h) e"),
                                                    vb[:, t * P:(t + 1) * P].rearrange("p (h e) -> p h e", e=AD), ACT.Copy)
                    last.then_inc(*act.does("v"))
                    for p in range(PARTS):
                        for k in range(2):
                            eng.wait_ge(*pool.did(g, f"d{p}{k}" if p else f"r{k}"))
                            if again:
                                eng.wait_ge(stored, g * (5 + 3) * 16)
                            nc.scalar.activation(part[:, k, p], a[:, k], ACT.Copy).then_inc(*act.does(f"c{p}{k}"))
                both(eng, body)

            @block.vector
            def _(eng):
                def body(seq, s, again):
                    g = seq * 2 + s
                    for k in range(2):
                        if again:
                            eng.wait_ge(*act.did(g - 1, f"c{PARTS - 1}{k}"))
                        for n, dst, table in ((0, a, cos), (1, b, sin)):
                            eng.wait_ge(*pe.did(g, f"w{2 * k + n}"))
                            nc.vector.tensor_tensor(dst[:, k], banks[2 * k + n][:], table[:, s * GRP:(s + 1) * GRP], ALU.mult).then_inc(*dve.does(f"{'cs'[n]}{k}"))
                both(eng, body)

            @block.gpsimd
            def _(eng):
                nc.gpsimd.memset(Vh[:], 1.0).then_inc(ones_set, 1)
                def body(seq, s, again):
                    g = seq * 2 + s
                    for k in range(2):
                        eng.wait_ge(*dve.did(g, f"s{k}"))
                        nc.gpsimd.tensor_tensor(a[:, k], a[:, k], b[:, k], ALU.add).then_inc(*pool.does(f"r{k}"))
                    for p in range(1, PARTS):
                        for k in range(2):
                            eng.wait_ge(*act.did(g, f"c{p - 1}{k}"))
                            nc.gpsimd.tensor_tensor(a[:, k], a[:, k], part[:, k, p - 1], ALU.subtract).then_inc(*pool.does(f"d{p}{k}"))
                both(eng, body)

            @block.sync
            def _(eng):
                def body(seq, s, again):
                    g = seq * 2 + s
                    for p in range(PARTS):
                        for k, dram in enumerate((q_dram, k_dram)):
                            eng.wait_ge(*act.did(g, f"c{p}{k}"))
                            for row in [p] + ([p + PARTS] if k and p < 2 else []):
                                dst = dram.rearrange("(b h) r d t -> b h r d t", h=AH)[bass.ds(seq, 1), :, row, :, s * GRP:(s + 1) * GRP]
                                eng.dma_start(dst.rearrange("o h d t -> (o h) d t"), part[:, k, p]).then_inc(stored, 16)
                both(eng, body)
                eng.wait_ge(stored, GROUPS * 8 * 16)

def attn_heads(nc, name, Vh, CTX, q_dram, k_dram, eye16):
    BANKS = 3
    UNITS = 2 * QT
    PLAN = [3, 3, 3, 3, 2, 2, 0, 0]
    with ExitStack() as stack:
        m = Space(nc, name, stack)
        qs = [m.sb(f"qs{s}", [P, SEQ], BF16) for s in range(2)]
        ks = [m.sb(f"ks{s}", [P, SEQ], BF16) for s in range(2)]
        pt = m.sb("pt", [P, 2, SEQ])
        mx = m.sb("mx", [P, QT, 2])
        nm = m.sb("nm", [P, QT])
        d1 = m.sb("d1", [P, QT])
        d2 = m.sb("d2", [P, QT])
        mp = m.sb("mp", [P, QT, PARTS], BF16)
        rec = m.sb("rec", [P, QT])
        first = [m.ps(f"first{k}") for k in range(BANKS)]
        second = [m.ps(f"second{k}", [P, 2, GRP]) for k in range(2)]
        O = m.ps("O")
        loaded = [m.sem(f"loaded{s}") for s in range(2)]
        ready = m.sem("ready")
        a_pe = Steps(m.sem("ape"), " ".join(f"n{u}" for u in range(UNITS)) + " row0 row1")
        b_pe = Steps(m.sem("bpe"), "s0 " + " ".join(f"s{t} v{t - 1}" for t in range(1, QT)) + f" v{QT - 1}")
        a_dve = Steps(m.sem("adve"), " ".join(f"m{u}" for u in range(UNITS)) + " nm p1 d1 p2 d2 p3")
        b_dve = Steps(m.sem("bdve"), "rec ctx")
        a_act = Steps(m.sem("aact"), "row0 row1")
        b_act = Steps(m.sem("bact"), " ".join(f"e{t}" for t in range(QT)))
        LOADS = 6

        def run(eng, maxima, weights):
            def turn(n, s, wt, mx_, again2, again3):
                units = maxima(n, s, again2) if mx_ else iter(())

                def step(t):
                    todo = PLAN[t] if t < QT else UNITS + 2
                    for _ in range(todo):
                        if next(units, None) is None:
                            return
                if wt:
                    weights(n - 1, 1 - s, again3, step)
                else:
                    step(QT)
            turn(0, 0, False, True, False, False)
            turn(1, 1, True, True, False, False)
            turn(2, 0, True, True, True, True)
            with eng.Fori(0, (AN - 4) // 2) as k:
                turn(k * 2 + 3, 1, True, True, True, True)
                turn(k * 2 + 4, 0, True, True, True, True)
            turn(AN - 1, 1, True, True, True, True)
            turn(AN, 0, True, False, True, True)

        with nc.Block() as block:
            @block.sync
            def _(eng):
                eng.wait_ge(ready, 6)
                def load(n, s, again):
                    if again:
                        eng.wait_ge(*b_pe.did(n - 2, f"s{QT - 1}"))
                    for r in range(PARTS):
                        rows = slice(r * 24, r * 24 + 24)
                        eng.dma_start(qs[s][rows, :], q_dram[bass.ds(n, 1)].rearrange("o r d t -> (o r d) t")).then_inc(loaded[s], 16)
                        eng.dma_start(ks[s][rows, :], k_dram[bass.ds(n, 1), r:r + 3].rearrange("o r d t -> (o r d) t")).then_inc(loaded[s], 16)
                tiles(eng, AN, 2, load)

            @block.gpsimd
            def _(eng):
                fills = [(t[lo:hi, :], x) for s in range(2) for t, lo, hi, x in ((qs[s], 64, P, 0.0), (ks[s], 64, SHIFT, 0.0), (ks[s], SHIFT, P, 1.0))]
                for n, (rows, x) in enumerate(fills):
                    nc.gpsimd.memset(rows, x).then_inc(ready, 1)
                    eng.wait_ge(ready, n + 1)

            @block.tensor
            def _(eng):
                def maxima(n, s, again):
                    eng.wait_ge(loaded[s], (n // 2 + 1) * LOADS * 16 if isinstance(n, int) else (n - s) * (LOADS * 8) + LOADS * 16)
                    for u in range(UNITS):
                        k = u % BANKS
                        if u >= BANKS:
                            eng.wait_ge(*a_dve.did(n, f"m{u - BANKS}"))
                        elif again or (isinstance(n, int) and n):
                            if k:
                                eng.wait_ge(*a_act.did(n - 1, f"row{k - 1}"))
                        qt, half = divmod(u, 2)
                        nc.tensor.matmul(first[k][:], qs[s][0:STACK, qt * P:(qt + 1) * P], ks[s][0:STACK, half * GRP:(half + 1) * GRP],
                                         start=True, stop=True).then_inc(*a_pe.does(f"n{u}"))
                        yield True
                    eng.wait_ge(*a_dve.did(n, "p3"))
                    for half in range(2):
                        for t in range(4):
                            last = nc.tensor.matmul(first[1 + half][SHIFT:SHIFT + PARTS, t * P:(t + 1) * P], mp[:, 4 * half + t, :], eye16[:],
                                                    start=True, stop=True)
                        last.then_inc(*a_pe.does(f"row{half}"))
                    yield True

                def weights(n, s, again, step):
                    eng.wait_ge(*a_act.did(n, "row1"))

                    def values(t):
                        eng.wait_ge(*b_act.did(n, f"e{t}"))
                        if t == 0 and again:
                            eng.wait_ge(*b_dve.did(n - 1, "ctx"))
                        for q in range(QT):
                            last = nc.tensor.matmul(O[:, q * VW:(q + 1) * VW], pt[:, t % 2, q * P:(q + 1) * P], Vh[:, bass.ds(n * (QT * VW) + t * VW, VW)],
                                                    start=(t == 0 and q == 0), stop=(t == QT - 1 and q == QT - 1), skip_group_check=True)
                        last.then_inc(*b_pe.does(f"v{t}"))
                    for t in range(QT):
                        step(t)
                        if t >= 2:
                            eng.wait_ge(*b_act.did(n, f"e{t - 2}"))
                        elif again:
                            eng.wait_ge(*b_act.did(n - 1, f"e{QT - 2 + t}"))
                        for half in range(2):
                            last = nc.tensor.matmul(second[t % 2][:, half], ks[s][0:SHIFT + PARTS, t * P:(t + 1) * P], qs[s][0:SHIFT + PARTS, half * GRP:(half + 1) * GRP],
                                                    start=True, stop=True)
                        last.then_inc(*b_pe.does(f"s{t}"))
                        if t:
                            values(t - 1)
                    step(QT)
                    values(QT - 1)
                run(eng, maxima, weights)

            @block.scalar
            def _(eng):
                nc.scalar.preload_act_table_set("exp_and_others")
                eng.wait_ge(ready, 6)
                def maxima(n, s, again):
                    for u in range(UNITS):
                        yield True
                    for half in range(2):
                        eng.wait_ge(*a_pe.did(n, f"row{half}"))
                        if again:
                            eng.wait_ge(*b_pe.did(n - 2, f"s{QT - 1}"))
                        nc.scalar.activation(qs[s][SHIFT:SHIFT + PARTS, half * GRP:(half + 1) * GRP], first[1 + half][SHIFT:SHIFT + PARTS, :],
                                             ACT.Copy).then_inc(*a_act.does(f"row{half}"))
                    yield True

                def weights(n, s, again, step):
                    for t in range(QT):
                        step(t)
                        eng.wait_ge(*b_pe.did(n, f"s{t}"))
                        if t >= 2:
                            eng.wait_ge(*b_pe.did(n, f"v{t - 2}"))
                        elif again:
                            eng.wait_ge(*b_pe.did(n - 1, f"v{QT - 2 + t}"))
                        nc.scalar.activation(pt[:, t % 2].rearrange("p (a b) -> p a b", a=2), second[t % 2][:], ACT.Exp, scale=float(AD) ** -0.5).then_inc(*b_act.does(f"e{t}"))
                    step(QT)
                run(eng, maxima, weights)

            @block.vector
            def _(eng):
                def maxima(n, s, again):
                    for u in range(UNITS):
                        eng.wait_ge(*a_pe.did(n, f"n{u}"))
                        nc.vector.tensor_reduce(mx[:, u // 2, u % 2:u % 2 + 1], first[u % BANKS][:], AX, ALU.max).then_inc(*a_dve.does(f"m{u}"))
                        yield True

                    def small(ins, name_):
                        ins.then_inc(*a_dve.does(name_))
                        eng.wait_ge(*a_dve.did(n, name_))
                    eng.wait_ge(*a_dve.did(n, f"m{UNITS - 1}"))
                    small(nc.vector.tensor_reduce(nm[:], mx[:], AX, ALU.max), "nm")
                    if again or (isinstance(n, int) and n):
                        eng.wait_ge(*a_pe.did(n - 1, "row1"))
                    small(nc.vector.tensor_scalar(mp[:, :, 0], nm[:], -1.0, None, ALU.mult), "p1")
                    small(nc.vector.scalar_tensor_tensor(d1[:], nm[:], -1.0, mp[:, :, 0], ALU.mult, ALU.subtract), "d1")
                    small(nc.vector.tensor_copy(mp[:, :, 1], d1[:]), "p2")
                    small(nc.vector.tensor_tensor(d2[:], d1[:], mp[:, :, 1], ALU.subtract), "d2")
                    small(nc.vector.tensor_copy(mp[:, :, 2], d2[:]), "p3")
                    yield True

                def weights(n, s, again, step):
                    for t in range(QT):
                        step(t)
                    step(QT)
                    out = O[:, 0:QT * VW].rearrange("p (q e) -> p q e", e=VW)
                    eng.wait_ge(*b_pe.did(n, f"v{QT - 1}"))
                    nc.vector.reciprocal(rec[:], out[:, :, AD]).then_inc(*b_dve.does("rec"))
                    eng.wait_ge(*b_dve.did(n, "rec"))
                    nc.vector.tensor_tensor(CTX[:, bass.ds(n * (QT * AD), QT * AD)].rearrange("p (q e) -> p q e", e=AD), out[:, :, 0:AD],
                                            along(rec[:], AD), ALU.mult).then_inc(*b_dve.does("ctx"))
                run(eng, maxima, weights)

def attn_output(nc, name, CTX, XT, w_out, eye):
    with ExitStack() as stack:
        m = Space(nc, name, stack)
        c = m.sb("c", [P, 2, 4, P])
        cT = m.sb("cT", [P, 2, GRP])
        turned = [m.ps(f"turned{s}") for s in range(2)]
        out = [m.ps(f"out{s}") for s in range(2)]
        pe, act, dve = Steps(m.sem("pe"), "t0 t1 o0 o1"), Steps(m.sem("act"), "c0 c1"), Steps(m.sem("dve"), "x0 x1")
        pool = Steps(m.sem("pool"), "c0 c1")
        ctx = CTX[:].rearrange("p (b h t e) -> p b h t e", b=BATCH, h=AH, e=AD)
        with nc.Block() as block:
            @block.gpsimd
            def _(eng):
                def body(seq, _, again):
                    for s in range(2):
                        if again:
                            eng.wait_ge(*pe.did(seq - 1, f"t{s}"))
                        for t in range(4):
                            last = nc.gpsimd.tensor_copy(c[:, s, t].rearrange("p (h e) -> p h e", e=AD), ctx[:, bass.ds(seq, 1), :, 4 * s + t].rearrange("p o h e -> p (o h) e"))
                        last.then_inc(*pool.does(f"c{s}"))
                tiles(eng, BATCH, 1, body)

            @block.tensor
            def _(eng):
                def body(seq, _, again):
                    for s in range(2):
                        eng.wait_ge(*pool.did(seq, f"c{s}"))
                        if again:
                            eng.wait_ge(*act.did(seq - 1, f"c{s}"))
                        for t in range(4):
                            last = nc.tensor.transpose(turned[s][:, t * P:(t + 1) * P], c[:, s, t], eye[:])
                        last.then_inc(*pe.does(f"t{s}"))
                    for s in range(2):
                        eng.wait_ge(*act.did(seq, f"c{s}"))
                        if again:
                            eng.wait_ge(*dve.did(seq - 1, f"x{s}"))
                        nc.tensor.matmul(out[s][:], w_out[:], cT[:, s], start=True, stop=True).then_inc(*pe.does(f"o{s}"))
                tiles(eng, BATCH, 1, body)

            @block.scalar
            def _(eng):
                def body(seq, _, again):
                    for s in range(2):
                        eng.wait_ge(*pe.did(seq, f"t{s}"))
                        if again:
                            eng.wait_ge(*pe.did(seq - 1, f"o{s}"))
                        nc.scalar.activation(cT[:, s], turned[s][:], ACT.Copy).then_inc(*act.does(f"c{s}"))
                tiles(eng, BATCH, 1, body)

            @block.vector
            def _(eng):
                def body(seq, _, again):
                    for s in range(2):
                        eng.wait_ge(*pe.did(seq, f"o{s}"))
                        nc.vector.tensor_tensor(at_group(XT, seq * 2 + s), at_group(XT, seq * 2 + s), out[s][:], ALU.add).then_inc(*dve.does(f"x{s}"))
                tiles(eng, BATCH, 1, body)

def router_small(nc, name, XN, RW, w_router, bias_row, iota, E_):
    with ExitStack() as stack:
        m = Space(nc, name, stack)
        xs = m.sb("xs", [P, 2, GRP])
        lg = m.sb("lg", [P, 2, 4, E_])
        top = m.sb("top", [P, CHUNKS, 8])
        top4 = m.sb("top4", [P, 2, 4, 8])
        idx4 = m.sb("idx4", [P, 2, 4, 8], U32)
        fi8 = m.sb("fi8", [P, CHUNKS, 8])
        carrier = m.sb("carrier", [P, 2])
        fi = m.sb("fi", [P, 2, CHUNKS])
        ex = m.sb("ex", [P, CHUNKS])
        den = m.sb("den", [P, CHUNKS])
        wt = m.sb("wt", [P, 2, CHUNKS])
        hot = m.sb("hot", [P, 2, CHUNKS, E_])
        lp = [m.ps(f"lp{s}") for s in range(2)]
        pe, act = Steps(m.sem("pe"), "lg"), Steps(m.sem("act"), "xs")
        dve = Steps(m.sem("dve"), "lg cr0 max cr1 at top idx")
        end = Steps(m.sem("end"), "f0 f1 d den rec w1 h0 h1 s0 s1 rw")
        exped = m.sem("exped")
        with nc.Block() as block:
            @block.scalar
            def _(eng):
                def body(g, s, again):
                    if again:
                        eng.wait_ge(*pe.did(g - 2, "lg"))
                    nc.scalar.activation(xs[:, s], at_group(XN, g), ACT.Copy).then_inc(*act.does("xs"))
                tiles(eng, GROUPS, 2, body)
                eng.wait_ge(*end.did(0, "d"))
                nc.scalar.activation(ex[:], ex[:], ACT.Exp).then_inc(exped, 1)

            @block.tensor
            def _(eng):
                def body(g, s, again):
                    eng.wait_ge(*act.did(g, "xs"))
                    if again:
                        eng.wait_ge(*dve.did(g - 2, "lg"))
                    for t in range(4):
                        last = nc.tensor.matmul(lp[s][:, t * E_:(t + 1) * E_], xs[:, s, t * P:(t + 1) * P], w_router[:], start=True, stop=True)
                    last.then_inc(*pe.does("lg"))
                tiles(eng, GROUPS, 2, body)

            @block.vector
            def _(eng):
                def body(g, s, again):
                    eng.wait_ge(*pe.did(g, "lg"))
                    src = lp[s][:, 0:4 * E_].rearrange("p (t e) -> p t e", e=E_)
                    nc.vector.tensor_tensor(lg[:, s], src, over_heads(bias_row[:], 4), ALU.add).then_inc(*dve.does("lg"))
                    eng.wait_ge(*dve.did(g, "lg"))
                    nc.vector.memset(carrier[:, 0:1], 0.0).then_inc(*dve.does("cr0"))
                    for t in range(4):
                        last = nc.vector.max(top4[:, s, t], lg[:, s, t])
                    last.then_inc(*dve.does("max"))
                    eng.wait_ge(*dve.did(g, "max"))
                    nc.vector.memset(carrier[:, 1:2], 0.0).then_inc(*dve.does("cr1"))
                    for t in range(4):
                        last = nc.vector.max_index(idx4[:, s, t], top4[:, s, t], lg[:, s, t])
                    last.then_inc(*dve.does("at"))
                    nc.vector.tensor_copy(top[:, bass.ds(g * 4, 4), :], top4[:, s]).then_inc(*dve.does("top"))
                    eng.wait_ge(*dve.did(g, "at"))
                    nc.vector.tensor_copy(fi8[:, bass.ds(g * 4, 4), :], idx4[:, s]).then_inc(*dve.does("idx"))
                tiles(eng, GROUPS, 2, body)

                def step(ins, name_):
                    ins.then_inc(*end.does(name_))
                    eng.wait_ge(*end.did(0, name_))
                eng.wait_ge(*dve.did(GROUPS - 1, "idx"))
                for k in range(2):
                    step(nc.vector.tensor_copy(fi[:, k], fi8[:, :, k]), f"f{k}")
                step(nc.vector.tensor_tensor(ex[:], top[:, :, 1], top[:, :, 0], ALU.subtract), "d")
                eng.wait_ge(exped, 1)
                step(nc.vector.tensor_scalar(den[:], ex[:], 1.0, None, ALU.add), "den")
                step(nc.vector.reciprocal(wt[:, 0], den[:]), "rec")
                step(nc.vector.tensor_tensor(wt[:, 1], wt[:, 0], ex[:], ALU.mult), "w1")
                for k in range(2):
                    step(nc.vector.tensor_tensor(hot[:, k], iota[:, 0:E_].unsqueeze(1).to_broadcast([P, CHUNKS, E_]), along(fi[:, k], E_), ALU.is_equal), f"h{k}")
                for k in range(2):
                    step(nc.vector.tensor_tensor(hot[:, k], hot[:, k], along(wt[:, k], E_), ALU.mult), f"s{k}")
                step(nc.vector.tensor_tensor(RW[:].rearrange("p (c e) -> p c e", e=E_), hot[:, 0], hot[:, 1], ALU.add), "rw")

def dense_moe(nc, name, XN, XT, RW, W1, B1, W2, b2, gammaT, betaT, eye, E_):
    F = 4
    with ExitStack() as stack:
        m = Space(nc, name, stack)
        xs = m.sb("xs", [P, GRP])
        rw = m.sb("rw", [P, 4, E_])
        rwT = m.sb("rwT", [E_, GRP])
        hid = m.sb("hid", [P, 2, F, GRP])
        acc = m.sb("acc", [P, 4, P])
        z = m.sb("z", [P, 4, P])
        zT = m.sb("zT", [P, GRP])
        st, ag, rs, ve = m.sb("st", [P, 4, 6]), m.sb("ag", [P, 4, 2]), m.sb("rs", [P, 4]), m.sb("ve", [P, 4])
        half, carrier = m.sb("half", [P, 4]), m.sb("carrier", [P, 1])
        up = [m.ps(f"up{c}") for c in range(F)]
        down = [m.ps(f"down{k}") for k in range(2)]
        side = m.ps("side")
        small = m.ps("small")
        pe = Steps(m.sem("pe"), "rwT init " + " ".join(f"up{e}{c}" for e in range(1) for c in range(F)) + " " +
                   " ".join(" ".join(f"up{e + 1}{c}" for c in range(F) if e + 1 < E_) + f" down{e}" for e in range(E_)) + " zT")
        act = Steps(m.sem("act"), "xs rw rwT init " + " ".join(f"hid{e}{c}" for e in range(E_) for c in range(F)) + " zT")
        dve = Steps(m.sem("dve"), " ".join(f"acc{e}" for e in range(E_)) + " st cr ag ve z out")
        pool = Steps(m.sem("pool"), "rs")
        half_set = m.sem("half_set")

        def tiles4(t):
            return t[:].rearrange("p (t n) -> p t n", n=P)
        with nc.Block() as block:
            @block.tensor
            def _(eng):
                def body(g, _, again):
                    def prev(who, step):
                        if again:
                            eng.wait_ge(*who.did(g - 1, step))
                    eng.wait_ge(*act.did(g, "rw"))
                    prev(act, "zT")
                    prev(act, "rwT")
                    for t in range(4):
                        last = nc.tensor.transpose(small[0:E_, t * P:(t + 1) * P], rw[:, t], eye[:])
                    last.then_inc(*pe.does("rwT"))
                    eng.wait_ge(*act.did(g, "rwT"))
                    for t in range(4):
                        nc.tensor.matmul(side[:, t * P:(t + 1) * P], xs[:, t * P:(t + 1) * P], eye[:], start=True, stop=False)
                        last = nc.tensor.matmul(side[:, t * P:(t + 1) * P], rwT[:, t * P:(t + 1) * P], b2[:], start=False, stop=True)
                    last.then_inc(*pe.does("init"))

                    def hidden(e):
                        for c in range(F):
                            if e:
                                eng.wait_ge(*act.did(g, f"hid{e - 1}{c}"))
                            elif again:
                                eng.wait_ge(*act.did(g - 1, f"hid{E_ - 1}{c}"))
                            nc.tensor.matmul(up[c][:], W1[:, e, c * P:(c + 1) * P], xs[:], start=True, stop=True).then_inc(*pe.does(f"up{e}{c}"))
                    hidden(0)
                    for e in range(E_):
                        if e + 1 < E_:
                            hidden(e + 1)
                        if e >= 2:
                            eng.wait_ge(*dve.did(g, f"acc{e - 2}"))
                        else:
                            prev(dve, f"acc{E_ - 2 + e}")
                        for t in range(4):
                            for c in range(F):
                                eng.wait_ge(*act.did(g, f"hid{e}{c}")) if t == 0 else None
                                last = nc.tensor.matmul(down[e % 2][:, t * P:(t + 1) * P], hid[:, e % 2, c, t * P:(t + 1) * P], W2[:, e, c], start=(c == 0), stop=(c == F - 1))
                        last.then_inc(*pe.does(f"down{e}"))
                    eng.wait_ge(*dve.did(g, "z"))
                    for t in range(4):
                        last = nc.tensor.transpose(side[:, t * P:(t + 1) * P], z[:, t], eye[:])
                    last.then_inc(*pe.does("zT"))
                tiles(eng, GROUPS, 1, body)

            @block.scalar
            def _(eng):
                def body(g, _, again):
                    def prev(who, step):
                        if again:
                            eng.wait_ge(*who.did(g - 1, step))
                    prev(pe, f"up{E_ - 1}{F - 1}")
                    nc.scalar.activation(xs[:], at_group(XN, g), ACT.Copy).then_inc(*act.does("xs"))
                    prev(dve, f"acc{E_ - 1}")
                    nc.scalar.activation(rw[:].rearrange("p t e -> p (t e)"), RW[:, bass.ds(g * (4 * E_), 4 * E_)], ACT.Copy).then_inc(*act.does("rw"))
                    eng.wait_ge(*pe.did(g, "rwT"))
                    nc.scalar.activation(rwT[:], small[0:E_, :], ACT.Copy).then_inc(*act.does("rwT"))
                    eng.wait_ge(*pe.did(g, "init"))
                    prev(dve, "z")
                    nc.scalar.activation(acc[:], tiles4(side), ACT.Copy).then_inc(*act.does("init"))
                    for e in range(E_):
                        for c in range(F):
                            eng.wait_ge(*pe.did(g, f"up{e}{c}"))
                            if c == 0:
                                if e >= 2:
                                    eng.wait_ge(*pe.did(g, f"down{e - 2}"))
                                else:
                                    prev(pe, f"down{E_ - 2 + e}")
                            nc.scalar.activation(hid[:, e % 2, c], up[c][:], ACT.Relu, bias=B1[:, e, c:c + 1]).then_inc(*act.does(f"hid{e}{c}"))
                    eng.wait_ge(*pe.did(g, "zT"))
                    prev(dve, "out")
                    nc.scalar.activation(zT[:], side[:], ACT.Identity, scale=gammaT[:, 0:1], bias=betaT[:, 0:1]).then_inc(*act.does("zT"))
                tiles(eng, GROUPS, 1, body)

            @block.vector
            def _(eng):
                def body(g, _, again):
                    for e in range(E_):
                        eng.wait_ge(*pe.did(g, f"down{e}"))
                        eng.wait_ge(*act.did(g, "init")) if e == 0 else eng.wait_ge(*dve.did(g, f"acc{e - 1}"))
                        for t in range(4):
                            last = nc.vector.scalar_tensor_tensor(acc[:, t], tiles4(down[e % 2])[:, t], rw[:, t, e:e + 1], acc[:, t], ALU.mult, ALU.add)
                        last.then_inc(*dve.does(f"acc{e}"))
                    eng.wait_ge(*dve.did(g, f"acc{E_ - 1}"))
                    for t in range(4):
                        last = nc.vector.bn_stats(st[:, t], acc[:, t])
                    last.then_inc(*dve.does("st"))
                    eng.wait_ge(*dve.did(g, "st"))
                    nc.vector.memset(carrier[:], 0.0).then_inc(*dve.does("cr"))
                    for t in range(4):
                        last = nc.vector.bn_aggr(ag[:, t], st[:, t])
                    last.then_inc(*dve.does("ag"))
                    eng.wait_ge(*dve.did(g, "ag"))
                    nc.vector.tensor_scalar(ve[:], ag[:, :, 1], 1e-5, None, ALU.add).then_inc(*dve.does("ve"))
                    eng.wait_ge(*pool.did(g, "rs"))
                    for t in range(4):
                        last = nc.vector.tensor_scalar(z[:, t], acc[:, t], ag[:, t, 0:1], rs[:, t:t + 1], ALU.subtract, ALU.mult)
                    last.then_inc(*dve.does("z"))
                    eng.wait_ge(*act.did(g, "zT"))
                    nc.vector.tensor_tensor(at_group(XT, g), at_group(XT, g), zT[:], ALU.add).then_inc(*dve.does("out"))
                tiles(eng, GROUPS, 1, body)

            @block.gpsimd
            def _(eng):
                nc.gpsimd.memset(half[:], -0.5).then_inc(half_set, 1)
                eng.wait_ge(half_set, 1)
                def body(g, _, again):
                    eng.wait_ge(*dve.did(g, "ve"))
                    nc.gpsimd.tensor_tensor(rs[:], ve[:], half[:], ALU.pow).then_inc(*pool.does("rs"))
                tiles(eng, GROUPS, 1, body)

GH, GD = 16, 8
STATES = GH * GD * GD
RT = STATES // P

def gla_gates(nc, name, XN, GT, w1, w2, bias):
    with ExitStack() as stack:
        m = Space(nc, name, stack)
        R = w1.shape[1]
        lo = m.sb("lo", [R, 2, GRP])
        z, y, u, d, lu, c = (m.sb(n, [P, 2, GRP]) for n in "z y u d lu c".split())
        lp = [m.ps(f"lp{s}") for s in range(2)]
        zp = [m.ps(f"zp{s}") for s in range(2)]
        pe, act = Steps(m.sem("pe"), "lo z"), Steps(m.sem("act"), "lo y lu gate")
        dve = Steps(m.sem("dve"), "z na u d m ls")
        with nc.Block() as block:
            @block.tensor
            def _(eng):
                def body(g, s, again):
                    if again:
                        eng.wait_ge(*act.did(g - 2, "lo"))
                    nc.tensor.matmul(lp[s][0:R, :], w1[:], at_group(XN, g), start=True, stop=True).then_inc(*pe.does("lo"))
                    eng.wait_ge(*act.did(g, "lo"))
                    if again:
                        eng.wait_ge(*dve.did(g - 2, "z"))
                    nc.tensor.matmul(zp[s][:], w2[:], lo[:, s], start=True, stop=True).then_inc(*pe.does("z"))
                tiles(eng, GROUPS, 2, body)

            @block.scalar
            def _(eng):
                nc.scalar.preload_act_table_set("natural_log_exp_and_others")
                def body(g, s, again):
                    eng.wait_ge(*pe.did(g, "lo"))
                    if again:
                        eng.wait_ge(*pe.did(g - 2, "z"))
                    nc.scalar.activation(lo[:, s], lp[s][0:R, :], ACT.Copy).then_inc(*act.does("lo"))
                    eng.wait_ge(*dve.did(g, "na"))
                    nc.scalar.activation(y[:, s], y[:, s], ACT.Exp).then_inc(*act.does("y"))
                    eng.wait_ge(*dve.did(g, "u"))
                    nc.scalar.activation(lu[:, s], u[:, s], ACT.Ln).then_inc(*act.does("lu"))
                    eng.wait_ge(*dve.did(g, "ls"))
                    nc.scalar.activation(at_group(GT, g), d[:, s], ACT.Exp, scale=1.0 / 16).then_inc(*act.does("gate"))
                tiles(eng, GROUPS, 2, body)

            @block.vector
            def _(eng):
                def body(g, s, again):
                    def chain(name_):
                        eng.wait_ge(*dve.did(g, name_))
                    eng.wait_ge(*pe.did(g, "z"))
                    nc.vector.tensor_scalar(z[:, s], zp[s][:], bias[:, 0:1], None, ALU.add).then_inc(*dve.does("z"))
                    chain("z")
                    nc.vector.scalar_tensor_tensor(y[:, s], z[:, s], -1.0, z[:, s], ALU.mult, ALU.min).then_inc(*dve.does("na"))
                    eng.wait_ge(*act.did(g, "y"))
                    nc.vector.tensor_scalar(u[:, s], y[:, s], 1.0, None, ALU.add).then_inc(*dve.does("u"))
                    chain("u")
                    if again:
                        eng.wait_ge(*act.did(g - 2, "gate"))
                    nc.vector.scalar_tensor_tensor(d[:, s], u[:, s], -1.0, y[:, s], ALU.add, ALU.subtract).then_inc(*dve.does("d"))
                    chain("d")
                    nc.vector.scalar_tensor_tensor(c[:, s], z[:, s], 0.0, d[:, s], ALU.min, ALU.add).then_inc(*dve.does("m"))
                    eng.wait_ge(*act.did(g, "lu"))
                    chain("m")
                    nc.vector.tensor_tensor(d[:, s], c[:, s], lu[:, s], ALU.subtract).then_inc(*dve.does("ls"))
                tiles(eng, GROUPS, 2, body)

def gla_states(nc, name, XN, GT, OT, wq, wk, wv, pick, fold):
    with ExitStack() as stack:
        m = Space(nc, name, stack)
        k_sb = m.sb("k", [P, 2, GRP])
        kv = m.sb("kv", [P, 2, GRP])
        st = m.sb("st", [P, 2, GRP])
        y = m.sb("y", [P, 2, GRP])
        carry = m.sb("carry", [P, RT])
        K, V, G, Q = (m.ps(n) for n in "KVGQ")
        out = [m.ps(f"out{s}") for s in range(2)]
        pe = Steps(m.sem("pe"), "K0 V0 G0 Q0 " + " ".join(f"K{r} V{r} G{r} Q{r} f{r - 1}" for r in range(1, RT)) + f" f{RT - 1}")
        act = Steps(m.sem("act"), " ".join(f"k{r}" for r in range(RT)) + " o")
        dve = Steps(m.sem("dve"), " ".join(f"kv{r} st{r} ca{r} y{r}" for r in range(RT)))

        def halves(eng, body):
            body(0, 0, False)
            body(0, 1, True)
            with eng.Fori(1, BATCH) as seq:
                body(seq, 0, True)
                body(seq, 1, True)

        with nc.Block() as block:
            @block.tensor
            def _(eng):
                def body(seq, s, again):
                    g = seq * 2 + s

                    def prev(who, kind, r):
                        if r:
                            eng.wait_ge(*who.did(g, f"{kind}{r - 1}"))
                        elif again:
                            eng.wait_ge(*who.did(g - 1, f"{kind}{RT - 1}"))

                    def fold_rows(r):
                        eng.wait_ge(*dve.did(g, f"y{r}"))
                        if r == 0 and not isinstance(seq, int):
                            eng.wait_ge(*act.did(g - 2, "o"))
                        nc.tensor.matmul(out[s][:], fold[:, r * P:(r + 1) * P], y[:, r % 2], start=(r == 0), stop=(r == RT - 1)).then_inc(*pe.does(f"f{r}"))
                    for r in range(RT):
                        for n, bk, w, src, who, kind in (("K", K, wk, XN, act, "k"), ("V", V, wv, XN, dve, "kv"), ("G", G, pick, GT, dve, "st"), ("Q", Q, wq, XN, dve, "y")):
                            prev(who, kind, r)
                            nc.tensor.matmul(bk[:], w[:, r * P:(r + 1) * P], at_group(src, g), start=True, stop=True).then_inc(*pe.does(f"{n}{r}"))
                        if r:
                            fold_rows(r - 1)
                    fold_rows(RT - 1)
                halves(eng, body)

            @block.scalar
            def _(eng):
                def body(seq, s, again):
                    g = seq * 2 + s
                    for r in range(RT):
                        eng.wait_ge(*pe.did(g, f"K{r}"))
                        if r >= 2:
                            eng.wait_ge(*dve.did(g, f"kv{r - 2}"))
                        elif again:
                            eng.wait_ge(*dve.did(g - 1, f"kv{RT - 2 + r}"))
                        nc.scalar.activation(k_sb[:, r % 2], K[:], ACT.Copy).then_inc(*act.does(f"k{r}"))
                    eng.wait_ge(*pe.did(g, f"f{RT - 1}"))
                    nc.scalar.activation(at_group(OT, g), out[s][:], ACT.Copy).then_inc(*act.does("o"))
                halves(eng, body)

            @block.vector
            def _(eng):
                def body(seq, s, again):
                    g = seq * 2 + s
                    for r in range(RT):
                        eng.wait_ge(*pe.did(g, f"V{r}"))
                        eng.wait_ge(*act.did(g, f"k{r}"))
                        nc.vector.tensor_tensor(kv[:, r % 2], V[:], k_sb[:, r % 2], ALU.mult).then_inc(*dve.does(f"kv{r}"))
                        eng.wait_ge(*pe.did(g, f"G{r}"))
                        eng.wait_ge(*dve.did(g, f"kv{r}"))
                        nc.vector.tensor_tensor_scan(st[:, r % 2], G[:], kv[:, r % 2], carry[:, r:r + 1] if s else 0.0, ALU.mult, ALU.add).then_inc(*dve.does(f"st{r}"))
                        eng.wait_ge(*dve.did(g, f"st{r}"))
                        nc.vector.tensor_copy(carry[:, r:r + 1], st[:, r % 2, GRP - 1:GRP]).then_inc(*dve.does(f"ca{r}"))
                        eng.wait_ge(*pe.did(g, f"Q{r}"))
                        if r >= 2:
                            eng.wait_ge(*pe.did(g, f"f{r - 2}"))
                        elif again:
                            eng.wait_ge(*pe.did(g - 1, f"f{RT - 2 + r}"))
                        nc.vector.tensor_tensor(y[:, r % 2], Q[:], st[:, r % 2], ALU.mult).then_inc(*dve.does(f"y{r}"))
                halves(eng, body)

def gla_output(nc, name, XN, OT, XT, w_gate, w_out, gammaT, betaT, ones_mean):
    with ExitStack() as stack:
        m = Space(nc, name, stack)
        xc, sq, ln, rs, r2, on, sg, og = (m.sb(n, [P, 2, GRP]) for n in "xc sq ln rs r2 on sg og".split())
        eps = m.sb("eps", [P, 1])
        mean = [m.ps(f"mean{s}") for s in range(2)]
        var = [m.ps(f"var{s}") for s in range(2)]
        gate = [m.ps(f"gate{s}") for s in range(2)]
        out = [m.ps(f"out{s}") for s in range(2)]
        an, dn = rsqrt_names("v")
        pe, act = Steps(m.sem("pe"), "mean gate var out"), Steps(m.sem("act"), "sq " + an + " sg")
        dve, ready = Steps(m.sem("dve"), "xc " + dn + " on af og xt"), m.sem("ready")
        with nc.Block() as block:
            @block.tensor
            def _(eng):
                def body(g, s, again):
                    if again:
                        eng.wait_ge(*dve.did(g - 2, "xt"))
                    nc.tensor.matmul(mean[s][:], ones_mean[:], at_group(OT, g), start=True, stop=True).then_inc(*pe.does("mean"))
                    nc.tensor.matmul(gate[s][:], w_gate[:], at_group(XN, g), start=True, stop=True).then_inc(*pe.does("gate"))
                    eng.wait_ge(*act.did(g, "sq"))
                    nc.tensor.matmul(var[s][:], ones_mean[:], sq[:, s], start=True, stop=True).then_inc(*pe.does("var"))
                    eng.wait_ge(*dve.did(g, "og"))
                    nc.tensor.matmul(out[s][:], w_out[:], og[:, s], start=True, stop=True).then_inc(*pe.does("out"))
                tiles(eng, GROUPS, 2, body)

            @block.scalar
            def _(eng):
                nc.scalar.preload_act_table_set("natural_log_exp_and_others")
                eng.wait_ge(ready, 1)
                def body(g, s, again):
                    eng.wait_ge(*dve.did(g, "xc"))
                    nc.scalar.activation(sq[:, s], xc[:, s], ACT.Square).then_inc(*act.does("sq"))
                    eng.wait_ge(*pe.did(g, "var"))
                    rsqrt_act(nc, eng, act, g, "v", var[s][:], eps[:], ln[:, s], rs[:, s], r2[:, s])
                    eng.wait_ge(*pe.did(g, "gate"))
                    nc.scalar.activation(sg[:, s], gate[s][:], ACT.Silu).then_inc(*act.does("sg"))
                tiles(eng, GROUPS, 2, body)

            @block.vector
            def _(eng):
                nc.vector.memset(eps[:], 1e-5).then_inc(ready, 1)
                def body(g, s, again):
                    eng.wait_ge(*pe.did(g, "mean"))
                    nc.vector.tensor_tensor(xc[:, s], at_group(OT, g), mean[s][:], ALU.subtract).then_inc(*dve.does("xc"))
                    rsqrt_dve(nc, eng, act, dve, g, "v", var[s][:], 1e-5, rs[:, s], r2[:, s])
                    nc.vector.tensor_tensor(on[:, s], xc[:, s], rs[:, s], ALU.mult).then_inc(*dve.does("on"))
                    eng.wait_ge(*dve.did(g, "on"))
                    nc.vector.tensor_scalar(on[:, s], on[:, s], gammaT[:, 0:1], betaT[:, 0:1], ALU.mult, ALU.add).then_inc(*dve.does("af"))
                    eng.wait_ge(*dve.did(g, "af"))
                    eng.wait_ge(*act.did(g, "sg"))
                    nc.vector.tensor_tensor(og[:, s], on[:, s], sg[:, s], ALU.mult).then_inc(*dve.does("og"))
                    eng.wait_ge(*pe.did(g, "out"))
                    nc.vector.tensor_tensor(at_group(XT, g), out[s][:], at_group(XT, g), ALU.add).then_inc(*dve.does("xt"))
                tiles(eng, GROUPS, 2, body)

LH, LD = 16, 8

def linear_attn_stage(nc, name, XN, XT, wqkv, w1, w2, g1T, g2row, g3row, coef, eye, ones_mean):
    F3 = 3 * P
    HALF = LD // 2
    with ExitStack() as stack:
        m = Space(nc, name, stack)
        sq, ln, rs, r2 = (m.sb(n, [P, GRP]) for n in "sq ln rs r2".split())
        xm = m.sb("xm", [P, GRP])
        qk = m.sb("qk", [P, 4, 2 * P])
        mn = m.sb("mn", [P, 4, 2 * P])
        v = m.sb("v", [P, 4, P])
        pr = m.sb("pr", [P, 2, LH * LD * LD])
        kv = m.sb("kv", [P, 4, LD * LD])
        at = m.sb("at", [P, 4, P])
        t1 = m.sb("t1", [P, 4, P])
        hr = m.sb("hr", [P, 4 * LH])
        gr = m.sb("gr", [P, 4])
        aT = m.sb("aT", [P, GRP])
        hT = m.sb("hT", [P, GRP])
        half = m.sb("half", [P, 4 * LH])
        eps = m.sb("eps", [P, 1])
        ms = m.ps("ms")
        pj = [m.ps(f"pj{t}") for t in range(4)]
        turned, hid, out = m.ps("turned"), m.ps("hid"), m.ps("out")
        EPS = float(np.finfo(np.float32).eps)
        an, dn = rsqrt_names("m")
        pe = Steps(m.sem("pe"), "ms p0 p1 p2 p3 aT hid out")
        act = Steps(m.sem("act"), "sq " + an + " v0 v1 v2 v3 e aT gelu")
        dve = Steps(m.sem("dve"), dn + " xm mn0 r0 mn1 r1 mn2 r2 mn3 r3 " + " ".join(f"kv{t} kc{t}" for t in range(4)) + " " +
                    " ".join(f"at{t}" for t in range(4)) + " hs he n1 n2 gs ge a1 a2 a3 ha out")
        pool = Steps(m.sem("pool"), "elu " + " ".join(f"p{t}" for t in range(4)) + " " + " ".join(f"w{t}" for t in range(4)) + " sq hr sq2 gr")
        half_set, ready = m.sem("half_set"), m.sem("ready")

        def flat(t):
            return t[:].rearrange("p a b -> p (a b)")
        with nc.Block() as block:
            @block.tensor
            def _(eng):
                def body(g, _, again):
                    def prev(who, step):
                        if again:
                            eng.wait_ge(*who.did(g - 1, step))
                    eng.wait_ge(*act.did(g, "sq"))
                    prev(dve, "xm")
                    nc.tensor.matmul(ms[:], ones_mean[:], sq[:], start=True, stop=True).then_inc(*pe.does("ms"))
                    eng.wait_ge(*dve.did(g, "xm"))
                    for t in range(4):
                        prev(dve, f"r{t}")
                        prev(act, f"v{t}")
                        nc.tensor.matmul(pj[t][:, 0:F3], xm[:, t * P:(t + 1) * P], wqkv[:], start=True, stop=True).then_inc(*pe.does(f"p{t}"))
                    eng.wait_ge(*dve.did(g, "a3"))
                    prev(act, "aT")
                    for t in range(4):
                        last = nc.tensor.transpose(turned[:, t * P:(t + 1) * P], at[:, t], eye[:])
                    last.then_inc(*pe.does("aT"))
                    eng.wait_ge(*act.did(g, "aT"))
                    prev(act, "gelu")
                    nc.tensor.matmul(hid[:], w1[:], aT[:], start=True, stop=True).then_inc(*pe.does("hid"))
                    eng.wait_ge(*act.did(g, "gelu"))
                    prev(dve, "out")
                    nc.tensor.matmul(out[:], w2[:], hT[:], start=True, stop=True).then_inc(*pe.does("out"))
                tiles(eng, GROUPS, 1, body)

            @block.scalar
            def _(eng):
                eng.wait_ge(ready, 1)
                def body(g, _, again):
                    def prev(who, step):
                        if again:
                            eng.wait_ge(*who.did(g - 1, step))
                    nc.scalar.preload_act_table_set("natural_log_exp_and_others")
                    nc.scalar.activation(sq[:], at_group(XN, g), ACT.Square).then_inc(*act.does("sq"))
                    eng.wait_ge(*pe.did(g, "ms"))
                    rsqrt_act(nc, eng, act, g, "m", ms[:], eps[:], ln[:], rs[:], r2[:])
                    for t in range(4):
                        eng.wait_ge(*dve.did(g, f"r{t}"))
                        prev(pool, f"p{t}")
                        nc.scalar.activation(v[:, t], pj[t][:, 2 * P:F3], ACT.Copy).then_inc(*act.does(f"v{t}"))
                    eng.wait_ge(*dve.did(g, "mn3"))
                    nc.scalar.activation(mn[:], mn[:], ACT.Exp).then_inc(*act.does("e"))
                    eng.wait_ge(*pe.did(g, "aT"))
                    prev(dve, "ha")
                    nc.scalar.activation(aT[:], turned[:], ACT.Copy).then_inc(*act.does("aT"))
                    eng.wait_ge(*pe.did(g, "hid"))
                    prev(pe, "out")
                    nc.scalar.activation(hT[:], hid[:], ACT.Gelu).then_inc(*act.does("gelu"))
                tiles(eng, GROUPS, 1, body)

            @block.vector
            def _(eng):
                nc.vector.memset(eps[:], EPS).then_inc(ready, 1)
                def body(g, _, again):
                    def prev(who, step):
                        if again:
                            eng.wait_ge(*who.did(g - 1, step))

                    def chain(name_):
                        eng.wait_ge(*dve.did(g, name_))
                    rsqrt_dve(nc, eng, act, dve, g, "m", ms[:], EPS, rs[:], r2[:])
                    nc.vector.scalar_tensor_tensor(xm[:], at_group(XN, g), g1T[:, 0:1], rs[:], ALU.mult, ALU.mult).then_inc(*dve.does("xm"))
                    for t in range(4):
                        eng.wait_ge(*pe.did(g, f"p{t}"))
                        prev(pool, "elu")
                        nc.vector.tensor_scalar(mn[:, t], pj[t][:, 0:2 * P], 0.0, None, ALU.min).then_inc(*dve.does(f"mn{t}"))
                        prev(pool, f"w{t}")
                        nc.vector.tensor_scalar(qk[:, t], pj[t][:, 0:2 * P], 0.0, -1.0, ALU.max, ALU.add).then_inc(*dve.does(f"r{t}"))
                    for t in range(4):
                        eng.wait_ge(*pool.did(g, f"p{t}"))
                        nc.vector.tensor_reduce(kv[:, t], pr[:, t % 2].rearrange("p (h f) -> p f h", h=LH), AX, ALU.add).then_inc(*dve.does(f"kv{t}"))
                        chain(f"kv{t}")
                        nc.vector.tensor_tensor(kv[:, t], kv[:, t], coef[:], ALU.mult).then_inc(*dve.does(f"kc{t}"))
                    for t in range(4):
                        eng.wait_ge(*pool.did(g, f"w{t}"))
                        nc.vector.tensor_reduce(at[:, t], pr[:, t % 2].rearrange("p (f e) -> p f e", e=LD), AX, ALU.add).then_inc(*dve.does(f"at{t}"))
                    eng.wait_ge(*pool.did(g, "sq"))
                    nc.vector.tensor_reduce(hr[:], flat(t1).rearrange("p (h e) -> p h e", e=LD), AX, ALU.add).then_inc(*dve.does("hs"))
                    chain("hs")
                    nc.vector.tensor_scalar(hr[:], hr[:], 1.0 / LD, EPS, ALU.mult, ALU.add).then_inc(*dve.does("he"))
                    eng.wait_ge(*pool.did(g, "hr"))
                    at3 = flat(at).rearrange("p (h e) -> p h e", e=LD)
                    nc.vector.tensor_tensor(at3, at3, along(hr[:], LD), ALU.mult).then_inc(*dve.does("n1"))
                    chain("n1")
                    nc.vector.tensor_tensor(at[:], at[:], over_heads(g2row[:], 4), ALU.mult).then_inc(*dve.does("n2"))
                    eng.wait_ge(*pool.did(g, "sq2"))
                    nc.vector.tensor_reduce(gr[:], t1[:], AX, ALU.add).then_inc(*dve.does("gs"))
                    chain("gs")
                    nc.vector.tensor_scalar(gr[:], gr[:], 1.0 / P, EPS, ALU.mult, ALU.add).then_inc(*dve.does("ge"))
                    eng.wait_ge(*pool.did(g, "gr"))
                    nc.vector.tensor_tensor(t1[:], at[:], along(gr[:], P), ALU.mult).then_inc(*dve.does("a1"))
                    chain("a1")
                    nc.vector.tensor_tensor(t1[:], t1[:], over_heads(g3row[:], 4), ALU.mult).then_inc(*dve.does("a2"))
                    chain("a2")
                    nc.vector.tensor_tensor(at[:], at[:], t1[:], ALU.add).then_inc(*dve.does("a3"))
                    eng.wait_ge(*act.did(g, "aT"))
                    nc.vector.tensor_tensor(at_group(XT, g), at_group(XT, g), aT[:], ALU.add).then_inc(*dve.does("ha"))
                    eng.wait_ge(*pe.did(g, "out"))
                    chain("ha")
                    nc.vector.tensor_tensor(at_group(XT, g), at_group(XT, g), out[:], ALU.add).then_inc(*dve.does("out"))
                tiles(eng, GROUPS, 1, body)

            @block.gpsimd
            def _(eng):
                nc.gpsimd.memset(half[:], -0.5).then_inc(half_set, 1)
                eng.wait_ge(half_set, 1)
                def body(g, _, again):
                    def prev(who, step):
                        if again:
                            eng.wait_ge(*who.did(g - 1, step))
                    eng.wait_ge(*dve.did(g, "r3"))
                    eng.wait_ge(*act.did(g, "e"))
                    nc.gpsimd.tensor_tensor(qk[:], qk[:], mn[:], ALU.add).then_inc(*pool.does("elu"))
                    eng.wait_ge(*pool.did(g, "elu"))
                    for t in range(4):
                        eng.wait_ge(*act.did(g, f"v{t}"))
                        if t >= 2:
                            eng.wait_ge(*dve.did(g, f"kv{t - 2}"))
                        k3 = qk[:, t, P:2 * P].rearrange("p (h e) -> p h e", e=LD).unsqueeze(3).to_broadcast([P, LH, LD, LD])
                        v3 = v[:, t].rearrange("p (h d) -> p h d", d=LD).unsqueeze(2).to_broadcast([P, LH, LD, LD])
                        nc.gpsimd.tensor_tensor(pr[:, t % 2].rearrange("p (h e d) -> p h e d", h=LH, e=LD), k3, v3, ALU.mult).then_inc(*pool.does(f"p{t}"))
                    for t in range(4):
                        eng.wait_ge(*dve.did(g, f"kc{t}"))
                        if t >= 2:
                            eng.wait_ge(*dve.did(g, f"at{t - 2}"))
                        else:
                            eng.wait_ge(*dve.did(g, f"kv{t + 2}"))
                        q3 = qk[:, t, 0:P].rearrange("p (h e) -> p h e", e=LD).unsqueeze(2).to_broadcast([P, LH, LD, LD])
                        kv3 = kv[:, t].rearrange("p (e d) -> p d e", d=LD).unsqueeze(1).to_broadcast([P, LH, LD, LD])
                        nc.gpsimd.tensor_tensor(pr[:, t % 2].rearrange("p (h d e) -> p h d e", h=LH, e=LD), q3, kv3, ALU.mult).then_inc(*pool.does(f"w{t}"))
                    eng.wait_ge(*dve.did(g, "at3"))
                    nc.gpsimd.tensor_tensor(t1[:], at[:], at[:], ALU.mult).then_inc(*pool.does("sq"))
                    eng.wait_ge(*dve.did(g, "he"))
                    nc.gpsimd.tensor_tensor(hr[:], hr[:], half[:], ALU.pow).then_inc(*pool.does("hr"))
                    eng.wait_ge(*dve.did(g, "n2"))
                    nc.gpsimd.tensor_tensor(t1[:], at[:], at[:], ALU.mult).then_inc(*pool.does("sq2"))
                    eng.wait_ge(*dve.did(g, "ge"))
                    nc.gpsimd.tensor_tensor(gr[:], gr[:], half[:, 0:4], ALU.pow).then_inc(*pool.does("gr"))
                tiles(eng, GROUPS, 1, body)

EX, MLP = 64, 256
BLOCKS = 2 * TOK // P + EX
SLOTS = BLOCKS * P

def sparse_route(nc, name, XN, HOT, WT, SLOT, BE, IDS, x_dram, ids_dram, w_gate, iota, eye, masks):
    C, E_ = CHUNKS, EX
    with ExitStack() as stack:
        m = Space(nc, name, stack)
        xs = m.sb("xs", [P, 2, GRP])
        xr = m.sb("xr", [P, 2, 4, P])
        lg = m.sb("lg", [P, 2, 4, E_])
        top4 = m.sb("top4", [P, 2, 4, 8])
        idx4 = m.sb("idx4", [P, 2, 4, 8], U32)
        top = m.sb("top", [P, C, 8])
        fi8 = m.sb("fi8", [P, C, 8])
        carrier = m.sb("carrier", [P, 2])
        fi = m.sb("fi", [P, 2, C])
        ex = m.sb("ex", [P, C])
        den = m.sb("den", [P, C])
        M = m.sb("M", [P, C * E_])
        rank = m.sb("rank", [P, C * E_])
        cnt = [m.sb(f"cnt{k}", [P, C * E_]) for k in range(2)]
        tot, incl, base, on1 = (m.sb(n, [P, E_]) for n in "tot incl base on1".split())
        ti = m.sb("ti", [P, E_], I32)
        sf = m.sb("sf", [P, 2, C])
        col = m.sb("col", [P, 1])
        ecol = m.sb("ecol", [P, 1])
        tokid = m.sb("tokid", [P, C], I32)
        zero = m.sb("zero", [P, BLOCKS], I32)
        si = m.sb("si", [P, 2, 2], U32)
        tk = m.sb("tk", [P, 2, 1], I32)
        back_i = m.sb("back_i", [BLOCKS, P], I32)
        back_f = m.sb("back_f", [BLOCKS, P])
        mark = m.sb("mark", [P, 3])
        zeroed, returned = m.sem("zeroed"), m.sem("returned")
        stored = [m.sem(f"stored{s}") for s in range(2)]
        scattered = [m.sem(f"scattered{s}") for s in range(2)]
        pe, act = Steps(m.sem("pe"), "lg xr"), Steps(m.sem("act"), "xs xr")
        dve = Steps(m.sem("dve"), "lg cr0 max cr1 at top idx")
        pe2 = Steps(m.sem("pe2"), "ranks be ids")
        end = Steps(m.sem("end"), "f0 f1 d den rec w1 h0 h1 M " + " ".join(f"rk{k} cn{k}" for k in range(4)) + " " + " ".join(f"px{k}" for k in range(5)) +
                    " ex rk tot t127 ti sh nb on1 incl excl base slot s0 r0 s1 r1 u le ej mn be bf ids")
        exped, consts = m.sem("exped"), m.sem("consts")
        pool = Steps(m.sem("pool"), "si tk carry")
        hot = HOT[:].rearrange("p (k c e) -> p k c e", k=2, e=E_)

        def ce(t):
            return t[:].rearrange("p (c e) -> p c e", e=E_)

        def pairs(eng, n, body):
            for s in range(2):
                body(s, s, 0)
            with eng.Fori(1, n // 2) as k:
                for s in range(2):
                    body(k * 2 + s, s, k)

        banks = [m.ps(f"bank{k}") for k in range(8)]
        with nc.Block() as block:
            @block.scalar
            def _(eng):
                def body(g, s, before):
                    again = not isinstance(g, int)
                    if again:
                        eng.wait_ge(*pe.did(g - 2, "xr"))
                    nc.scalar.activation(xs[:, s], at_group(XN, g), ACT.Copy).then_inc(*act.does("xs"))
                    eng.wait_ge(*pe.did(g, "xr"))
                    if again:
                        eng.wait_ge(stored[s], before * 16)
                    nc.scalar.activation(xr[:, s].rearrange("p t n -> p (t n)"), banks[2 + s][:], ACT.Copy).then_inc(*act.does("xr"))
                pairs(eng, GROUPS, body)
                eng.wait_ge(*end.did(0, "d"))
                nc.scalar.activation(ex[:], ex[:], ACT.Exp).then_inc(exped, 1)

            @block.sync
            def _(eng):
                def body(g, s, again):
                    eng.wait_ge(*act.did(g, "xr"))
                    eng.dma_start(x_dram.rearrange("(g t p) d -> g p t d", p=P, t=4)[bass.ds(g, 1)].rearrange("o p t d -> (o p) t d"), xr[:, s]).then_inc(stored[s], 16)
                tiles(eng, GROUPS, 2, body)
                eng.wait_ge(consts, 4)
                eng.dma_start(ids_dram.rearrange("(p n) o -> p (n o)", p=P), zero[:]).then_inc(zeroed, 16)
                for s in range(2):
                    eng.wait_ge(scattered[s], C * 16)
                eng.dma_start(back_i[:], ids_dram.rearrange("(b s) o -> b (s o)", s=P)).then_inc(returned, 16)
                eng.wait_ge(returned, 16)
                for s in range(2):
                    eng.wait_ge(stored[s], GROUPS // 2 * 16)

            @block.tensor
            def _(eng):
                def body(g, s, again):
                    eng.wait_ge(*act.did(g, "xs"))
                    if again:
                        eng.wait_ge(*dve.did(g - 2, "lg"))
                    for t in range(4):
                        last = nc.tensor.matmul(banks[s][:, t * E_:(t + 1) * E_], xs[:, s, t * P:(t + 1) * P], w_gate[:], start=True, stop=True)
                    last.then_inc(*pe.does("lg"))
                    if again:
                        eng.wait_ge(*act.did(g - 2, "xr"))
                    for t in range(4):
                        last = nc.tensor.transpose(banks[2 + s][:, t * P:(t + 1) * P], xs[:, s, t * P:(t + 1) * P], eye[:])
                    last.then_inc(*pe.does("xr"))
                tiles(eng, GROUPS, 2, body)
                eng.wait_ge(*end.did(0, "M"))
                eng.wait_ge(*act.did(GROUPS - 1, "xr"))
                for k in range(4):
                    nc.tensor.matmul(banks[k][:], masks["row_lt_col"][:], M[:, k * GRP:(k + 1) * GRP], start=True, stop=True)
                    last = nc.tensor.matmul(banks[4 + k][:], masks["ones"][:], M[:, k * GRP:(k + 1) * GRP], start=True, stop=True)
                last.then_inc(*pe2.does("ranks"))
                eng.wait_ge(*end.did(0, "mn"))
                nc.tensor.matmul(banks[0][0:1, 0:P], ecol[:], eye[:], start=True, stop=True).then_inc(*pe2.does("be"))
                eng.wait_ge(*end.did(0, "bf"))
                nc.tensor.transpose(banks[1][:, 0:BLOCKS], back_f[:], eye[:]).then_inc(*pe2.does("ids"))

            @block.vector
            def _(eng):
                def body(g, s, again):
                    eng.wait_ge(*pe.did(g, "lg"))
                    nc.vector.tensor_copy(lg[:, s].rearrange("p t e -> p (t e)"), banks[s][:, 0:4 * E_]).then_inc(*dve.does("lg"))
                    eng.wait_ge(*dve.did(g, "lg"))
                    nc.vector.memset(carrier[:, 0:1], 0.0).then_inc(*dve.does("cr0"))
                    for t in range(4):
                        last = nc.vector.max(top4[:, s, t], lg[:, s, t])
                    last.then_inc(*dve.does("max"))
                    eng.wait_ge(*dve.did(g, "max"))
                    nc.vector.memset(carrier[:, 1:2], 0.0).then_inc(*dve.does("cr1"))
                    for t in range(4):
                        last = nc.vector.max_index(idx4[:, s, t], top4[:, s, t], lg[:, s, t])
                    last.then_inc(*dve.does("at"))
                    nc.vector.tensor_copy(top[:, bass.ds(g * 4, 4), :], top4[:, s]).then_inc(*dve.does("top"))
                    eng.wait_ge(*dve.did(g, "at"))
                    nc.vector.tensor_copy(fi8[:, bass.ds(g * 4, 4), :], idx4[:, s]).then_inc(*dve.does("idx"))
                tiles(eng, GROUPS, 2, body)

                def step(ins, name_):
                    ins.then_inc(*end.does(name_))
                    eng.wait_ge(*end.did(0, name_))
                eng.wait_ge(*dve.did(GROUPS - 1, "idx"))
                for k in range(2):
                    step(nc.vector.tensor_copy(fi[:, k], fi8[:, :, k]), f"f{k}")
                step(nc.vector.tensor_tensor(ex[:], top[:, :, 1], top[:, :, 0], ALU.subtract), "d")
                eng.wait_ge(exped, 1)
                step(nc.vector.tensor_scalar(den[:], ex[:], 1.0, None, ALU.add), "den")
                step(nc.vector.reciprocal(WT[:, 0], den[:]), "rec")
                step(nc.vector.tensor_tensor(WT[:, 1], WT[:, 0], ex[:], ALU.mult), "w1")
                for k in range(2):
                    step(nc.vector.tensor_tensor(hot[:, k], iota[:, 0:E_].unsqueeze(1).to_broadcast([P, C, E_]), along(fi[:, k], E_), ALU.is_equal), f"h{k}")
                step(nc.vector.tensor_tensor(ce(M), hot[:, 0], hot[:, 1], ALU.add), "M")
                eng.wait_ge(*pe2.did(0, "ranks"))
                for k in range(4):
                    step(nc.vector.tensor_copy(rank[:, k * GRP:(k + 1) * GRP], banks[k][:]), f"rk{k}")
                    step(nc.vector.tensor_copy(cnt[0][:, k * GRP:(k + 1) * GRP], banks[4 + k][:]), f"cn{k}")
                for k in range(5):
                    a, b, n = cnt[k % 2], cnt[1 - k % 2], (1 << k) * E_
                    nc.vector.tensor_copy(b[:, 0:n], a[:, 0:n])
                    step(nc.vector.tensor_tensor(b[:, n:], a[:, n:], a[:, 0:C * E_ - n], ALU.add), f"px{k}")
                summed = cnt[1]
                step(nc.vector.tensor_copy(tot[:], summed[:, (C - 1) * E_:C * E_]), "ex")
                step(nc.vector.tensor_tensor(rank[:, E_:], rank[:, E_:], summed[:, 0:(C - 1) * E_], ALU.add), "rk")
                step(nc.vector.tensor_scalar(base[:], tot[:], float(P - 1), None, ALU.add), "tot")
                step(nc.vector.tensor_copy(ti[:], base[:]), "t127")
                step(nc.vector.tensor_scalar(ti[:], ti[:], 7, None, ALU.logical_shift_right), "ti")
                step(nc.vector.tensor_copy(tot[:], ti[:]), "sh")
                step(nc.vector.memset(on1[:], 1.0), "nb")
                step(nc.vector.tensor_tensor_scan(incl[:], on1[:], tot[:], 0.0, ALU.mult, ALU.add), "on1")
                step(nc.vector.tensor_tensor(base[:], incl[:], tot[:], ALU.subtract), "incl")
                step(nc.vector.tensor_scalar(base[:], base[:], float(P), None, ALU.mult), "excl")
                step(nc.vector.tensor_tensor(ce(rank), ce(rank), base[:].unsqueeze(1).to_broadcast([P, C, E_]), ALU.add), "base")
                eng.wait_ge(consts, 4)
                step(nc.vector.tensor_scalar(on1[:], incl[:], col[:, 0:1], None, ALU.is_le), "slot")
                for k in range(2):
                    step(nc.vector.tensor_tensor(hot[:, k], hot[:, k], ce(rank), ALU.mult), f"s{k}")
                    step(nc.vector.tensor_reduce(sf[:, k], hot[:, k], AX, ALU.add), f"r{k}")
                step(nc.vector.tensor_copy(SLOT[:], sf[:]), "u")
                step(nc.vector.tensor_reduce(ecol[:], on1[:], AX, ALU.add), "le")
                step(nc.vector.tensor_scalar(ecol[:], ecol[:], float(E_ - 1), None, ALU.min), "ej")
                step(nc.vector.tensor_copy(col[:], ecol[:]), "mn")
                eng.wait_ge(*pe2.did(0, "be"))
                step(nc.vector.tensor_copy(BE[:], banks[0][0:1, 0:BLOCKS]), "be")
                eng.wait_ge(returned, 16)
                step(nc.vector.tensor_copy(back_f[:], back_i[:]), "bf")
                eng.wait_ge(*pe2.did(0, "ids"))
                step(nc.vector.tensor_copy(IDS[:], banks[1][:, 0:BLOCKS]), "ids")

            @block.gpsimd
            def _(eng):
                nc.gpsimd.iota(tokid[:], pattern=[[P, C]], base=0, channel_multiplier=1).then_inc(consts, 1)
                nc.gpsimd.memset(zero[:], 0).then_inc(consts, 1)
                nc.gpsimd.memset(mark[:, 0:1], 0.0).then_inc(consts, 1)
                nc.gpsimd.iota(col[:], pattern=[[0, 1]], base=0, channel_multiplier=1, allow_small_or_imprecise_dtypes=True).then_inc(consts, 1)
                eng.wait_ge(*end.did(0, "u"))
                eng.wait_ge(consts, 4)
                eng.wait_ge(zeroed, 16)

                def carry(s):
                    nc.gpsimd.tensor_tensor(mark[:, 1 + s:2 + s], mark[:, 0:1], mark[:, 0:1], ALU.add).then_inc(*pool.does("carry"))

                def body(c, s, before):
                    if not isinstance(c, int):
                        eng.wait_ge(scattered[s], before * 32)
                    nc.gpsimd.tensor_copy(si[:, s], SLOT[:, :, bass.ds(c, 1)].rearrange("p k o -> p (k o)")).then_inc(*pool.does("si"))
                    nc.gpsimd.tensor_copy(tk[:, s], tokid[:, bass.ds(c, 1)]).then_inc(*pool.does("tk"))
                    eng.wait_ge(*pool.did(c, "tk"))
                    carry(s)
                    for k in range(2):
                        eng.indirect_dma_start(ids_dram, bass.IndirectOffsetOnAxis(ap=si[:, s, k:k + 1], axis=0), tk[:, s], None).then_inc(scattered[s], 16)
                pairs(eng, C, body)

def sparse_experts(nc, name, BE, IDS, x_dram, y_dram, w0_dram, w1_dram, wo_dram, eye):
    F = MLP // P
    with ExitStack() as stack:
        m = Space(nc, name, stack)
        W = 4
        w0 = m.sb("w0", [P, W, MLP])
        w1 = m.sb("w1", [P, W, MLP])
        wo = m.sb("wo", [P, W, F, P])
        ix = m.sb("ix", [P, W, 1], U32)
        xg = m.sb("xg", [P, W, P])
        xT = m.sb("xT", [P, 2, P])
        s0 = m.sb("s0", [P, 2, MLP])
        hid = m.sb("hid", [P, 2, MLP])
        y = m.sb("y", [P, W, P])
        mark, started = m.sb("mark", [P, 1 + W]), m.sem("started")
        xp = [m.ps(f"xp{k}") for k in range(2)]
        a = [m.ps(f"a{k}") for k in range(2)]
        b = [m.ps(f"b{k}") for k in range(2)]
        yp = [m.ps(f"yp{k}") for k in range(2)]
        wl = [m.sem(f"wl{k}") for k in range(W)]
        xl = [m.sem(f"xl{k}") for k in range(W)]
        ys = [m.sem(f"ys{k}") for k in range(W)]
        pe, act, dve, pool = Steps(m.sem("pe"), "xT h y"), Steps(m.sem("act"), "xT s0"), Steps(m.sem("dve"), "hid y"), Steps(m.sem("pool"), "ix carry")

        def slots(eng, body):
            for j in range(W):
                body(j, j, 1, False)
            with eng.Fori(1, BLOCKS // W) as k:
                for s in range(W):
                    body(k * W + s, s, k + 1, True)

        with nc.Block() as block:
            @block.sync
            def _(eng):
                def body(j, s, times, again):
                    e = eng.value_load(BE[0:1, bass.ds(j, 1)], min_val=0, max_val=EX - 1)
                    if again:
                        store(j - W, s)
                    eng.dma_start(w0[:, s], w0_dram[bass.ds(e, 1)].rearrange("o d f -> (o d) f")).then_inc(wl[s], 16)
                    eng.dma_start(w1[:, s], w1_dram[bass.ds(e, 1)].rearrange("o d f -> (o d) f")).then_inc(wl[s], 16)
                    eng.dma_start(wo[:, s], wo_dram[bass.ds(e, 1)].rearrange("o (c p) d -> (o p) c d", p=P)).then_inc(wl[s], 16)

                def store(j, s):
                    eng.wait_ge(*dve.did(j, "y"))
                    eng.dma_start(y_dram.rearrange("(b s) d -> b s d", s=P)[bass.ds(j, 1)].rearrange("o s d -> (o s) d"), y[:, s]).then_inc(ys[s], 16)
                slots(eng, body)
                for s in range(W):
                    store(BLOCKS - W + s, s)
                for s in range(W):
                    eng.wait_ge(ys[s], BLOCKS // W * 16)

            @block.gpsimd
            def _(eng):
                nc.gpsimd.memset(mark[:, 0:1], 0.0).then_inc(started, 1)
                eng.wait_ge(started, 1)

                def carry(s):
                    nc.gpsimd.tensor_tensor(mark[:, 1 + s:2 + s], mark[:, 0:1], mark[:, 0:1], ALU.add).then_inc(*pool.does("carry"))

                def body(j, s, times, again):
                    if again:
                        eng.wait_ge(*pe.did(j - W, "xT"))
                    nc.gpsimd.tensor_copy(ix[:, s], IDS[:, bass.ds(j, 1)]).then_inc(*pool.does("ix"))
                    eng.wait_ge(*pool.did(j, "ix"))
                    carry(s)
                    eng.indirect_dma_start(xg[:, s], None, x_dram, bass.IndirectOffsetOnAxis(ap=ix[:, s], axis=0)).then_inc(xl[s], 16)
                slots(eng, body)

            @block.tensor
            def _(eng):
                def body(j, s, times, again):
                    k = s % 2
                    eng.wait_ge(xl[s], times * 16)
                    if again or s >= 2:
                        eng.wait_ge(*act.did(j - 2, "xT"))
                    nc.tensor.transpose(xp[k][:, 0:P], xg[:, s], eye[:]).then_inc(*pe.does("xT"))
                    eng.wait_ge(wl[s], times * 48)
                    eng.wait_ge(*act.did(j, "xT"))
                    if again or s >= 2:
                        eng.wait_ge(*dve.did(j - 2, "hid"))
                    for bank, w in ((a, w0), (b, w1)):
                        for c in range(F):
                            last = nc.tensor.matmul(bank[k][:, c * P:(c + 1) * P], w[:, s, c * P:(c + 1) * P], xT[:, k], start=True, stop=True)
                    last.then_inc(*pe.does("h"))
                    eng.wait_ge(*dve.did(j, "hid"))
                    for c in range(F):
                        last = nc.tensor.matmul(yp[k][:, 0:P], hid[:, k, c * P:(c + 1) * P], wo[:, s, c], start=(c == 0), stop=(c == F - 1))
                    last.then_inc(*pe.does("y"))
                slots(eng, body)

            @block.scalar
            def _(eng):
                def body(j, s, times, again):
                    k = s % 2
                    eng.wait_ge(*pe.did(j, "xT"))
                    if again or s >= 2:
                        eng.wait_ge(*pe.did(j - 2, "h"))
                    nc.scalar.activation(xT[:, k], xp[k][:, 0:P], ACT.Copy).then_inc(*act.does("xT"))
                    eng.wait_ge(*pe.did(j, "h"))
                    if again or s >= 2:
                        eng.wait_ge(*dve.did(j - 2, "hid"))
                    nc.scalar.activation(s0[:, k], a[k][:, 0:MLP], ACT.Silu).then_inc(*act.does("s0"))
                slots(eng, body)

            @block.vector
            def _(eng):
                def body(j, s, times, again):
                    k = s % 2
                    eng.wait_ge(*act.did(j, "s0"))
                    if again or s >= 2:
                        eng.wait_ge(*pe.did(j - 2, "y"))
                    nc.vector.tensor_tensor(hid[:, k], s0[:, k], b[k][:, 0:MLP], ALU.mult).then_inc(*dve.does("hid"))
                    eng.wait_ge(*pe.did(j, "y"))
                    if again:
                        eng.wait_ge(ys[s], (times - 1) * 16)
                    nc.vector.tensor_copy(y[:, s], yp[k][:, 0:P]).then_inc(*dve.does("y"))
                slots(eng, body)

def sparse_combine(nc, name, SLOT, WT, XT, y_dram, eye):
    with ExitStack() as stack:
        m = Space(nc, name, stack)
        W = 4
        ix = m.sb("ix", [P, W, 2], U32)
        yg = m.sb("yg", [P, W, 2, P])
        wt = m.sb("wt", [P, W, 2])
        o = m.sb("o", [P, 2, P])
        mark, started = m.sb("mark", [P, 1 + W]), m.sem("started")
        turned = [m.ps(f"turned{k}") for k in range(2)]
        got = [m.sem(f"got{k}") for k in range(W)]
        pe, act, dve, pool = Steps(m.sem("pe"), "t"), Steps(m.sem("act"), "wt"), Steps(m.sem("dve"), "o0 o1 x"), Steps(m.sem("pool"), "ix carry")

        def slots(eng, body):
            for j in range(W):
                body(j, j, 1, False)
            with eng.Fori(1, CHUNKS // W) as k:
                for s in range(W):
                    body(k * W + s, s, k + 1, True)
        with nc.Block() as block:
            @block.gpsimd
            def _(eng):
                nc.gpsimd.memset(mark[:, 0:1], 0.0).then_inc(started, 1)
                eng.wait_ge(started, 1)

                def carry(s):
                    nc.gpsimd.tensor_tensor(mark[:, 1 + s:2 + s], mark[:, 0:1], mark[:, 0:1], ALU.add).then_inc(*pool.does("carry"))

                def body(c, s, times, again):
                    if again:
                        eng.wait_ge(*dve.did(c - W, "o1"))
                    nc.gpsimd.tensor_copy(ix[:, s], SLOT[:, :, bass.ds(c, 1)].rearrange("p k o -> p (k o)")).then_inc(*pool.does("ix"))
                    eng.wait_ge(*pool.did(c, "ix"))
                    carry(s)
                    for k in range(2):
                        eng.indirect_dma_start(yg[:, s, k], None, y_dram, bass.IndirectOffsetOnAxis(ap=ix[:, s, k:k + 1], axis=0)).then_inc(got[s], 16)
                slots(eng, body)

            @block.scalar
            def _(eng):
                def body(c, s, times, again):
                    if again:
                        eng.wait_ge(*dve.did(c - W, "o1"))
                    nc.scalar.activation(wt[:, s], WT[:, :, bass.ds(c, 1)].rearrange("p k o -> p (k o)"), ACT.Copy).then_inc(*act.does("wt"))
                slots(eng, body)

            @block.vector
            def _(eng):
                def body(c, s, times, again):
                    k = s % 2
                    eng.wait_ge(got[s], times * 32)
                    eng.wait_ge(*act.did(c, "wt"))
                    if again or s >= 2:
                        eng.wait_ge(*pe.did(c - 2, "t"))
                    nc.vector.tensor_scalar(o[:, k], yg[:, s, 0], wt[:, s, 0:1], None, ALU.mult).then_inc(*dve.does("o0"))
                    eng.wait_ge(*dve.did(c, "o0"))
                    nc.vector.scalar_tensor_tensor(o[:, k], yg[:, s, 1], wt[:, s, 1:2], o[:, k], ALU.mult, ALU.add).then_inc(*dve.does("o1"))
                    eng.wait_ge(*pe.did(c, "t"))
                    nc.vector.tensor_tensor(XT[:, bass.ds(c * P, P)], XT[:, bass.ds(c * P, P)], turned[k][:, 0:P], ALU.add).then_inc(*dve.does("x"))
                slots(eng, body)

            @block.tensor
            def _(eng):
                def body(c, s, times, again):
                    k = s % 2
                    eng.wait_ge(*dve.did(c, "o1"))
                    if again or s >= 2:
                        eng.wait_ge(*dve.did(c - 2, "x"))
                    nc.tensor.transpose(turned[k][:, 0:P], o[:, k], eye[:]).then_inc(*pe.does("t"))
                slots(eng, body)

LAMBDA_INIT = 0.8 - 0.6 * float(np.exp(-0.3 * 0))
LIN_SCALE = 1.0 / float(np.sqrt(D // 2))

def load_stage(nc, name, pairs):
    with nc.semaphore(name + "_a") as sem_a, nc.semaphore(name + "_b") as sem_b:
        first, second = Loads(sem_a), Loads(sem_b)
        with nc.Block() as block:
            @block.sync
            def _(eng):
                for tile, source in pairs[0::2]:
                    eng.dma_start(tile, source).then_inc(*first.one())
                eng.wait_ge(*first.all())

            @block.scalar
            def _(eng):
                for tile, source in pairs[1::2]:
                    eng.dma_start(tile, source).then_inc(*second.one())
                if second.count:
                    eng.wait_ge(*second.all())

def clear_semaphores(nc):
    with nc.Block() as block:
        @block.gpsimd
        def _(eng):
            eng.sem_clear(range(FIRST_SEM, 256))

FIRST_SEM = 99

def layer0(nc, a, XT, XN, c):
    with ExitStack() as stack:
        m = Space(nc, "l0_", stack)
        biasT, gammaT, betaT = (m.sb(n, [P, 3]) for n in "biasT gammaT betaT".split())
        bias_rows, WQ = m.sb("bias_rows", [P, 3, P]), m.sb("WQ", [P, 6, P])
        with ExitStack() as inner:
            m = Space(nc, "l0d_", inner)
            X1 = m.sb("X1", [P, TOK])
            w_up, w_down = m.sb("w_up", [P, 4 * P]), m.sb("w_down", [P, 4 * P])
            with ExitStack() as delta:
                m = Space(nc, "l0e_", delta)
                HT = m.sb("HT", [P, TOK])
                GL, SCAL, Wba = m.sb("GL", [P, CHUNKS * 16]), m.sb("SCAL", [P, CHUNKS * SC]), m.sb("Wba", [P, 16])
                w = {k: m.sb("w_" + k, [P, 8 * P]) for k in "qkvgo"}
                o_norm = m.sb("o_norm", [P, 1])
                masks = dict(c)
                masks["level"] = m.sb("level", [P, 7 * P])
                load_stage(nc, "l0_load", [(Wba[:], a["Wba"]), (masks["level"][:], a["level"]), (o_norm[:], a["o_norm_w"])] + [(w[k][:], a["W" + k]) for k in "qkvgo"] +
                           [(w_up[:], a["w_up"]), (w_down[:], a["w_down"]), (biasT[:], a["q_biasT"]), (gammaT[:], a["q_gammaT"]), (betaT[:], a["q_betaT"])] +
                           [(bias_rows[:, b], on_all_partitions(a["q_bias"][b])) for b in range(3)])
                with nc.semaphore("l0_scaled") as scaled, nc.Block() as block:
                    @block.vector
                    def _(eng):
                        nc.vector.tensor_scalar(w["o"][:], w["o"][:], o_norm[:, 0:1], None, ALU.mult).then_inc(scaled, 1)
                norm_stage(nc, "l0n_", XT, XN, c["ones_mean"], (HT, Wba, GL))
                delta_gates(nc, "l0g_", GL, SCAL, a["A_log"], a["dt_bias"], masks)
                delta_stage(nc, "l0s_", HT, XN, X1, SCAL, w, masks)
            relu_mlp_stage(nc, "l0m_", XT, X1, w_up, w_down, c["ones_mean"])
        qlora_weights(nc, "l0w_", a["q_weights"], a["q_scales"], a["q_lora_a"], a["q_lora_bT"], WQ, c["eye"])
        qlora_stage(nc, "l0q_", XT, XN, WQ, biasT, bias_rows, gammaT, betaT, c["eye"])

def layer1(nc, a, XT, XN, c):
    with ExitStack() as stack:
        m = Space(nc, "l1_", stack)
        Vh, CTX = m.sb("Vh", [P, AN * QT * VW]), m.sb("CTX", [P, AN * QT * AD])
        w, wv, w_out = [m.sb(f"w{k}", [P, P]) for k in range(4)], m.sb("wv", [P, P]), m.sb("w_out", [P, P])
        cos, sin = m.sb("cos", [P, SEQ]), m.sb("sin", [P, SEQ])
        q_dram = nc.dram_tensor("attn_q", [AN, 3, AD, SEQ], BF16).ap()
        k_dram = nc.dram_tensor("attn_k", [AN, 5, AD, SEQ], BF16).ap()
        load_stage(nc, "l1_load", [(w[k][:], a[f"rope_w{k}"]) for k in range(4)] + [(wv[:], a["attn_wv"]), (w_out[:], a["attn_wo"]), (cos[:], a["cos"]), (sin[:], a["sin"])])
        norm_stage(nc, "l1n_", XT, XN, c["ones_mean"])
        attn_project(nc, "l1p_", XN, Vh, q_dram, k_dram, w, wv, cos, sin)
        attn_heads(nc, "l1h_", Vh, CTX, q_dram, k_dram, c["eye16"])
        attn_output(nc, "l1o_", CTX, XT, w_out, c["eye"])
    clear_semaphores(nc)
    with ExitStack() as stack:
        m = Space(nc, "l1m_", stack)
        W1, W2 = m.sb("W1", [P, 8, 4 * P]), m.sb("W2", [P, 8, 4, P])
        B1, b2 = m.sb("B1", [P, 8, 4]), m.sb("b2", [8, P])
        RW, wr, br = m.sb("RW", [P, CHUNKS * 8]), m.sb("wr", [P, 8]), m.sb("br", [P, 8])
        gammaT, betaT = m.sb("gammaT", [P, 1]), m.sb("betaT", [P, 1])
        load_stage(nc, "l1m_load", [(W1[:], a["moe_W1"]), (W2[:], a["moe_W2"]), (B1[:], a["moe_B1"]), (b2[:], a["moe_b2"]), (wr[:], a["moe_wr"]),
                                    (br[:], on_all_partitions(a["moe_br"])), (gammaT[:], a["moe_gamma"]), (betaT[:], a["moe_beta"])])
        router_small(nc, "l1r_", XN, RW, wr, br, c["iota"], 8)
        dense_moe(nc, "l1e_", XN, XT, RW, W1, B1, W2, b2, gammaT, betaT, c["eye"], 8)

def layer2(nc, a, XT, XN, c):
    with ExitStack() as stack:
        m = Space(nc, "l2_", stack)
        wqkv, w1, w2 = m.sb("wqkv", [P, 3 * P]), m.sb("w1", [P, P]), m.sb("w2", [P, P])
        g1T, g2, g2row, g3row = m.sb("g1T", [P, 1]), m.sb("g2", [P, 8]), m.sb("g2row", [P, P]), m.sb("g3row", [P, P])
        coef, lam, prod, exps, lmb = m.sb("coef", [P, 64]), m.sb("lam", [P, 4]), m.sb("prod", [P, 2]), m.sb("exps", [P, 2]), m.sb("lmb", [P, 1])
        load_stage(nc, "l2_load", [(wqkv[:], a["lin_wqkv"]), (w1[:], a["lin_w1"]), (w2[:], a["lin_w2"]), (g1T[:], a["lin_g1"]), (g2[:], on_all_partitions(a["lin_g2"])),
                                   (g3row[:], on_all_partitions(a["lin_g3"])), (lam[:], on_all_partitions(a["lin_lambda"]))])
        with nc.semaphore("l2_dve") as dve_sem, nc.semaphore("l2_exp") as exp_done, nc.Block() as block:
            dve = Steps(dve_sem, "prod diff lmb fill coef")

            @block.scalar
            def _(eng):
                eng.wait_ge(*dve.did(0, "prod"))
                nc.scalar.activation(exps[:], prod[:], ACT.Exp).then_inc(exp_done, 1)

            @block.vector
            def _(eng):
                pairs = lam[:].rearrange("p (a b) -> p a b", b=2)
                nc.vector.tensor_tensor(prod[:], pairs[:, :, 0], pairs[:, :, 1], ALU.mult).then_inc(*dve.does("prod"))
                eng.wait_ge(exp_done, 1)
                nc.vector.tensor_tensor(lmb[:], exps[:, 0:1], exps[:, 1:2], ALU.subtract).then_inc(*dve.does("diff"))
                eng.wait_ge(*dve.did(0, "diff"))
                nc.vector.tensor_scalar(lmb[:], lmb[:], LAMBDA_INIT, None, ALU.add).then_inc(*dve.does("lmb"))
                nc.vector.memset(coef[:, 0:32], LIN_SCALE)
                nc.vector.memset(coef[:, 32:64], -LIN_SCALE).then_inc(*dve.does("fill"))
                nc.vector.tensor_scalar(g2row[:].rearrange("p (h d) -> p h d", d=8), over_heads(g2[:], 16), 1.0 - LAMBDA_INIT, None, ALU.mult)
                eng.wait_ge(*dve.did(0, "fill"))
                nc.vector.tensor_scalar(coef[:, 32:64], coef[:, 32:64], lmb[:, 0:1], None, ALU.mult).then_inc(*dve.does("coef"))
        norm_stage(nc, "l2n_", XT, XN, c["ones_mean"])
        linear_attn_stage(nc, "l2a_", XN, XT, wqkv, w1, w2, g1T, g2row, g3row, coef, c["eye"], c["ones_mean"])
    clear_semaphores(nc)
    with ExitStack() as stack:
        m = Space(nc, "l2s_", stack)
        w_gate, WT, SLOT = m.sb("w_gate", [P, EX]), m.sb("WT", [P, 2, CHUNKS]), m.sb("SLOT", [P, 2, CHUNKS], U32)
        BE, IDS = m.sb("BE", [1, BLOCKS], I32), m.sb("IDS", [P, BLOCKS], U32)
        x_dram = nc.dram_tensor("sparse_x", [TOK, D], F32).ap()
        y_dram = nc.dram_tensor("sparse_y", [SLOTS, D], F32).ap()
        ids_dram = nc.dram_tensor("sparse_ids", [SLOTS, 1], I32).ap()
        load_stage(nc, "l2s_load", [(w_gate[:], a["sparse_gate"])])
        with ExitStack() as scratch:
            HOT = Space(nc, "l2h_", scratch).sb("HOT", [P, 2 * CHUNKS * EX])
            sparse_route(nc, "l2r_", XN, HOT, WT, SLOT, BE, IDS, x_dram, ids_dram, w_gate, c["iota"], c["eye"], c)
        sparse_experts(nc, "l2e_", BE, IDS, x_dram, y_dram, a["sparse_w0"], a["sparse_w1"], a["sparse_wo"], c["eye"])
        sparse_combine(nc, "l2c_", SLOT, WT, XT, y_dram, c["eye"])

def layer3(nc, a, XT, XN, c):
    with ExitStack() as stack:
        m = Space(nc, "l3_", stack)
        GT, OT = m.sb("GT", [P, TOK]), m.sb("OT", [P, TOK])
        shapes = {"gk1": 16, "gb": 1, "wq": 1024, "wk": 1024, "wv": 1024, "pick": 1024, "fold": 1024, "wg": P, "wo": P, "gamma": 1, "beta": 1}
        t = {k: m.sb(k, [P, n]) for k, n in shapes.items()}
        t["gk2"] = m.sb("gk2", [16, P])
        load_stage(nc, "l3_load", [(tile[:], a["gla_" + k]) for k, tile in t.items()])
        norm_stage(nc, "l3n_", XT, XN, c["ones_mean"])
        gla_gates(nc, "l3g_", XN, GT, t["gk1"], t["gk2"], t["gb"])
        gla_states(nc, "l3s_", XN, GT, OT, t["wq"], t["wk"], t["wv"], t["pick"], t["fold"])
        gla_output(nc, "l3o_", XN, OT, XT, t["wg"], t["wo"], t["gamma"], t["beta"], c["ones_mean"])
    with ExitStack() as stack:
        m = Space(nc, "l3m_", stack)
        w1, w2, b1, b2 = m.sb("w1", [P, 4 * P]), m.sb("w2", [P, 4 * P]), m.sb("b1", [P, 4]), m.sb("b2", [P, 1])
        load_stage(nc, "l3m_load", [(b1[:], a["bin_b1"]), (b2[:], a["bin_b2"])])
        binary_weights(nc, "l3b_", a["bin_w1"], a["bin_w2"], w1, w2, c["eye"])
        gelu_mlp_stage(nc, "l3f_", XT, XN, w1, w2, b1, b2)

MASKS = "row_le_col row_gt_col row_ge_col row_lt_col ones eye".split()

def network(nc, a, out):
    with ExitStack() as stack:
        m = Space(nc, "net_", stack)
        XT, XN = m.sb("XT", [P, TOK]), m.sb("XN", [P, TOK])
        c = {k: m.sb(k, [P, P]) for k in MASKS}
        c["eye16"], c["iota"], c["ones_mean"] = m.sb("eye16", [P, P], BF16), m.sb("iota", [P, EX]), m.sb("ones_mean", [P, P])
        load_stage(nc, "net_load", [(XT[:], a["xT"])] + [(c[k][:], a[k]) for k in MASKS + ["iota", "ones_mean"]])
        with nc.semaphore("net_cast") as cast, nc.Block() as block:
            @block.vector
            def _(eng):
                nc.vector.tensor_copy(c["eye16"][:], c["eye"][:]).then_inc(cast, 1)
        for layer in (layer0, layer1, layer2, layer3):
            layer(nc, a, XT, XN, c)
            clear_semaphores(nc)
        with nc.semaphore("out_stored") as stored, nc.Block() as block:
            @block.sync
            def _(eng):
                eng.dma_start(out, XT[:]).then_inc(stored, 16)
                eng.wait_ge(stored, 16)

def shape_constants():
    i = np.arange(P)
    row, col = i[:, None], i[None]
    eye = np.eye(P, dtype=np.float32)
    levels = []
    for n in (1 << l for l in range(7)):
        levels.append(((row // (2 * n) == col // (2 * n)) & (row // n % 2 == 0) & (col // n % 2 == 1)).astype(np.float32) + eye)
    rates = (1.0 / 10000.0 ** (np.arange(0, 8, 2, dtype=np.float32) / np.float32(8))).astype(np.float32)
    angles = np.outer(np.arange(SEQ, dtype=np.float32), rates)
    cos, sin = np.repeat(np.cos(angles), 2, -1), np.repeat(np.sin(angles), 2, -1)
    sin[:, ::2] *= -1
    rows = np.arange(1024)
    head, value = rows // 64, rows // 8 % 8
    pick = np.zeros((P, 1024), np.float32)
    pick[head * 8 + value, rows] = 1
    return {
        "row_le_col": (row <= col), "row_gt_col": (row > col), "row_ge_col": (row >= col), "row_lt_col": (row < col), "ones": np.ones((P, P)), "eye": eye,
        "iota": np.tile(np.arange(EX), (P, 1)), "ones_mean": np.full((P, P), 1 / D), "level": np.concatenate(levels, 1),
        "cos": np.tile(cos.T, (16, 1)), "sin": np.tile(sin.T, (16, 1)), "gla_pick": pick, "gla_fold": pick.T.reshape(8, P, P).transpose(1, 0, 2).reshape(P, 1024),
    }

def layouts(x):
    rows = np.arange(1024)
    head, value, key = rows // 64, rows // 8 % 8, rows % 8
    swapped = np.arange(P) ^ 1
    l0 = lambda k: x["L0_attn_" + k]
    q = lambda k: x["L0_ffn_" + k]
    l1 = lambda k: x["L1_attn_" + k]
    moe = lambda k: x["L1_ffn_" + k]
    l2 = lambda k: x["L2_attn_" + k]
    l3 = lambda k: x["L3_attn_" + k]
    f3 = lambda k: x["L3_ffn_" + k]
    return {
        "xT": l0("x").reshape(TOK, D).T, "Wba": np.concatenate([l0("Wb"), l0("Wa")], 1), "Wq": l0("Wq"), "Wk": l0("Wk"), "Wv": l0("Wv"), "Wg": l0("Wg"),
        "Wo": l0("Wo").reshape(8, P, P).transpose(1, 0, 2).reshape(P, 1024), "o_norm_w": l0("o_norm_w")[:, None], "A_log": l0("A_log"), "dt_bias": l0("dt_bias"),
        "w_up": l0("W_fc"), "w_down": l0("W_proj").reshape(4, P, P).transpose(1, 0, 2).reshape(P, 4 * P),
        "q_weights": q("qweights"), "q_scales": q("scales"), "q_lora_a": q("lora_a"), "q_lora_bT": q("lora_b").transpose(0, 2, 1),
        "q_biasT": q("biases")[1::2].T, "q_bias": q("biases")[0::2], "q_gammaT": q("ln_gamma").T, "q_betaT": q("ln_beta").T,
        "rope_w0": l1("W_Q").T, "rope_w1": l1("W_Q")[swapped].T, "rope_w2": l1("W_K").T, "rope_w3": l1("W_K")[swapped].T, "attn_wv": l1("W_V").T, "attn_wo": l1("W_O").T,
        "moe_wr": moe("Wr").T, "moe_br": moe("br"), "moe_W1": moe("W1").transpose(2, 0, 1), "moe_B1": moe("b1").reshape(8, 4, P).transpose(2, 0, 1),
        "moe_W2": moe("W2").transpose(2, 0, 1).reshape(4, P, 8, P).transpose(1, 2, 0, 3), "moe_b2": moe("b2"), "moe_gamma": moe("gamma")[:, None], "moe_beta": moe("beta")[:, None],
        "lin_wqkv": np.concatenate([l2("Wq").T, l2("Wk").T, l2("Wv").T], 1), "lin_w1": l2("W1").T, "lin_w2": l2("W2").T,
        "lin_g1": l2("g1")[:, None], "lin_g2": l2("g2"), "lin_g3": l2("g3"), "lin_lambda": l2("lambda_params"),
        "sparse_gate": x["L2_ffn_gate_kernel"], "sparse_w0": x["L2_ffn_w0"], "sparse_w1": x["L2_ffn_w1"], "sparse_wo": x["L2_ffn_wo"],
        "gla_gk1": l3("Wgk1"), "gla_gk2": l3("Wgk2"), "gla_gb": l3("bgk2")[:, None], "gla_wq": l3("Wq")[:, head * 8 + key], "gla_wk": l3("Wk")[:, head * 8 + key],
        "gla_wv": l3("Wv")[:, head * 8 + value], "gla_wg": l3("Wg"), "gla_wo": l3("Wout"), "gla_gamma": l3("gamma")[:, None], "gla_beta": l3("beta")[:, None],
        "bin_w1": f3("w1"), "bin_b1": f3("b1").reshape(4, P).T, "bin_w2": f3("w2"), "bin_b2": f3("b2")[:, None],
    }

def kernel(**inputs):
    import concourse.bacc as bacc
    from concourse.bass_utils import run_bass_kernel_spmd

    arrays = {k: np.ascontiguousarray(v) for k, v in layouts({k: np.asarray(v) for k, v in inputs.items()}).items()}
    arrays.update({k: np.ascontiguousarray(v, dtype=np.float32) for k, v in shape_constants().items()})
    nc = bacc.Bacc("TRN2", target_bir_lowering=False, num_devices=1)
    a = {k: nc.dram_tensor("in_" + k, v.shape, mybir.dt.from_np(v.dtype), kind="ExternalInput").ap() for k, v in arrays.items()}
    out = nc.dram_tensor("out_T", [D, TOK], F32, kind="ExternalOutput").ap()
    network(nc, a, out)
    result = run_bass_kernel_spmd(nc, [{"in_" + k: v for k, v in arrays.items()}], core_ids=[0])
    return np.ascontiguousarray(result.results[0]["out_T"].T).reshape(BATCH, SEQ, D)
```

```python
from contextlib import ExitStack

import numpy as np

import concourse.bass as bass
from concourse import mybir

F32 = mybir.dt.float32
BF16 = mybir.dt.bfloat16
I32 = mybir.dt.int32
U32 = mybir.dt.uint32
ALU = mybir.AluOpType
ACT = mybir.ActivationFunctionType
AX = mybir.AxisListType.X

P = 128
BATCH, SEQ, D = 4, 1024, 128
TOK = BATCH * SEQ
GRP = 512
GROUPS = TOK // GRP
CHUNK = 128
CHUNKS = TOK // CHUNK

class Steps:

    def __init__(self, sem, names):
        self.sem, self.names, self.next = sem, names.split(), 0

    def does(self, name):
        assert self.names[self.next] == name, (self.names[self.next], name)
        self.next = (self.next + 1) % len(self.names)
        return self.sem, 1

    def did(self, tile, name):
        return self.sem, tile * len(self.names) + (self.names.index(name) + 1)

class Loads:

    def __init__(self, sem):
        self.sem, self.count = sem, 0

    def one(self):
        self.count += 16
        return self.sem, 16

    def all(self):
        return self.sem, self.count

def tiles(eng, n, depth, body):
    for i in range(depth):
        body(i, i, False)
    with eng.Fori(1, n // depth) as turn:
        for s in range(depth):
            body(turn * depth + s, s, True)

class Space:

    def __init__(self, nc, prefix, stack):
        self.nc, self.prefix, self.stack = nc, prefix, stack

    def sb(self, name, shape, dt=F32):
        return self.stack.enter_context(self.nc.sbuf_tensor(self.prefix + name, shape, dt))

    def ps(self, name, shape=(P, 512), dt=F32):
        return self.stack.enter_context(self.nc.psum_tensor(self.prefix + name, list(shape), dt))

    def sem(self, name):
        return self.stack.enter_context(self.nc.semaphore(self.prefix + name))

def over_heads(ap, n):
    return ap.unsqueeze(1).to_broadcast([P, n, ap.shape[1]])

def along(ap, n):
    return ap.unsqueeze(2).to_broadcast([P, ap.shape[1], n])

def on_all_partitions(ap):
    flat = ap.rearrange("(a n) -> a n", a=1)
    return flat.to_broadcast([P, flat.shape[1]])

def rsqrt_names(k):
    return f"ln{k} rs{k} r2{k}", f"vr{k} nt{k} rn{k}"

def rsqrt_act(nc, eng, act, g, k, v, eps, ln, rs, r2):
    nc.scalar.activation(ln, v, ACT.Ln, bias=eps).then_inc(*act.does(f"ln{k}"))
    eng.wait_ge(*act.did(g, f"ln{k}"))
    nc.scalar.activation(rs, ln, ACT.Exp, scale=-0.5).then_inc(*act.does(f"rs{k}"))
    eng.wait_ge(*act.did(g, f"rs{k}"))
    nc.scalar.activation(r2, rs, ACT.Square).then_inc(*act.does(f"r2{k}"))

def rsqrt_dve(nc, eng, act, dve, g, k, v, eps, rs, r2):
    eng.wait_ge(*act.did(g, f"r2{k}"))
    nc.vector.scalar_tensor_tensor(r2, v, eps, r2, ALU.add, ALU.mult).then_inc(*dve.does(f"vr{k}"))
    eng.wait_ge(*dve.did(g, f"vr{k}"))
    nc.vector.tensor_scalar(r2, r2, -0.5, 1.5, ALU.mult, ALU.add).then_inc(*dve.does(f"nt{k}"))
    eng.wait_ge(*dve.did(g, f"nt{k}"))
    nc.vector.tensor_tensor(rs, rs, r2, ALU.mult).then_inc(*dve.does(f"rn{k}"))
    eng.wait_ge(*dve.did(g, f"rn{k}"))

def norm_stage(nc, name, XT, XN, ones_mean, rms=None):
    with ExitStack() as stack:
        m = Space(nc, name, stack)
        xc = m.sb("xc", [P, 2, GRP])
        sq = m.sb("sq", [P, 2, GRP])
        ln = m.sb("ln", [P, 2, GRP])
        rs = m.sb("rs", [P, 2, GRP])
        r2 = m.sb("r2", [P, 2, GRP])
        eps = m.sb("eps", [P, 2])
        mean = [m.ps(f"mean{s}") for s in range(2)]
        var = [m.ps(f"var{s}") for s in range(2)]
        pe_names, act_names, dve_names = "mean var", "sq " + rsqrt_names("v")[0], "xc " + rsqrt_names("v")[1] + " xn"
        if rms:
            HT, Wba, GL = rms
            hs = m.sb("hs", [P, 2, GRP])
            ms = [m.ps(f"ms{s}") for s in range(2)]
            gl = [m.ps(f"gl{s}") for s in range(2)]
            pe_names, act_names, dve_names = pe_names + " ms gl", act_names + " sq2 " + rsqrt_names("m")[0] + " ht", dve_names + " " + rsqrt_names("m")[1] + " hs gl"
        pe, act, dve = Steps(m.sem("pe"), pe_names), Steps(m.sem("act"), act_names), Steps(m.sem("dve"), dve_names)
        ready = m.sem("ready")

        def at(t, g):
            return t[:, bass.ds(g * GRP, GRP)]

        with nc.Block() as block:
            @block.tensor
            def _(eng):
                def body(g, s, again):
                    if again:
                        eng.wait_ge(*dve.did(g - 2, "xn"))
                    nc.tensor.matmul(mean[s][:], ones_mean[:], at(XT, g), start=True, stop=True).then_inc(*pe.does("mean"))
                    eng.wait_ge(*act.did(g, "sq"))
                    nc.tensor.matmul(var[s][:], ones_mean[:], sq[:, s], start=True, stop=True).then_inc(*pe.does("var"))
                    if rms:
                        eng.wait_ge(*act.did(g, "sq2"))
                        nc.tensor.matmul(ms[s][:], ones_mean[:], sq[:, s], start=True, stop=True).then_inc(*pe.does("ms"))
                        eng.wait_ge(*dve.did(g, "hs"))
                        if again:
                            eng.wait_ge(*dve.did(g - 2, "gl"))
                        for t in range(4):
                            last = nc.tensor.matmul(gl[s][:, t * 16:t * 16 + 16], hs[:, s, t * P:t * P + P], Wba[:], start=True, stop=True)
                        last.then_inc(*pe.does("gl"))
                tiles(eng, GROUPS, 2, body)

            @block.scalar
            def _(eng):
                nc.scalar.preload_act_table_set("natural_log_exp_and_others")
                eng.wait_ge(ready, 2)
                def body(g, s, again):
                    eng.wait_ge(*dve.did(g, "xc"))
                    nc.scalar.activation(sq[:, s], xc[:, s], ACT.Square).then_inc(*act.does("sq"))
                    eng.wait_ge(*pe.did(g, "var"))
                    rsqrt_act(nc, eng, act, g, "v", var[s][:], eps[:, 0:1], ln[:, s], rs[:, s], r2[:, s])
                    if rms:
                        eng.wait_ge(*dve.did(g, "xn"))
                        nc.scalar.activation(sq[:, s], at(XN, g), ACT.Square).then_inc(*act.does("sq2"))
                        eng.wait_ge(*pe.did(g, "ms"))
                        rsqrt_act(nc, eng, act, g, "m", ms[s][:], eps[:, 1:2], ln[:, s], rs[:, s], r2[:, s])
                        eng.wait_ge(*dve.did(g, "hs"))
                        nc.scalar.activation(at(HT, g), hs[:, s], ACT.Copy).then_inc(*act.does("ht"))
                tiles(eng, GROUPS, 2, body)

            @block.vector
            def _(eng):
                nc.vector.memset(eps[:, 0:1], 1e-5).then_inc(ready, 1)
                nc.vector.memset(eps[:, 1:2], 1e-6).then_inc(ready, 1)
                def body(g, s, again):
                    eng.wait_ge(*pe.did(g, "mean"))
                    nc.vector.tensor_tensor(xc[:, s], at(XT, g), mean[s][:], ALU.subtract).then_inc(*dve.does("xc"))
                    rsqrt_dve(nc, eng, act, dve, g, "v", var[s][:], 1e-5, rs[:, s], r2[:, s])
                    nc.vector.tensor_tensor(at(XN, g), xc[:, s], rs[:, s], ALU.mult).then_inc(*dve.does("xn"))
                    if rms:
                        rsqrt_dve(nc, eng, act, dve, g, "m", ms[s][:], 1e-6, rs[:, s], r2[:, s])
                        if again:
                            eng.wait_ge(*act.did(g - 2, "ht"))
                        nc.vector.tensor_tensor(hs[:, s], at(XN, g), rs[:, s], ALU.mult).then_inc(*dve.does("hs"))
                        eng.wait_ge(*pe.did(g, "gl"))
                        nc.vector.tensor_copy(GL[:, bass.ds(g * 64, 64)], gl[s][:, 0:64]).then_inc(*dve.does("gl"))
                tiles(eng, GROUPS, 2, body)

HEADS, DK = 8, 128
PAIR = 4 * P
SC = 48

def delta_gates(nc, name, GL, SCAL, A_log, dt_bias, masks):
    N = CHUNKS * HEADS
    with ExitStack() as stack:
        m = Space(nc, name, stack)
        la = m.sb("la", [P, HEADS])
        db = m.sb("db", [P, HEADS])
        ea = m.sb("ea", [P, HEADS])
        a, y, u, d, lu, g, eb = (m.sb(n, [P, N]) for n in "a y u d lu g eb".split())
        psum = [m.ps(f"sum{k}") for k in range(3)]
        loaded, act, dve, pe = Loads(m.sem("loaded")), Steps(m.sem("act"), "ea y lu eb e0 e1 e2"), \
            Steps(m.sem("dve"), "a na u d dm rd w1 is0 w2 w sp g ps b1 b2 b zero zc neg"), Steps(m.sem("pe"), "sums")
        before_incl, everyone, after = masks["row_le_col"], masks["ones"], masks["row_gt_col"]
        gl = GL[:].rearrange("p (c k) -> p c k", k=16)
        sc = SCAL[:].rearrange("p (c k) -> p c k", k=SC)

        def v3(t):
            return t[:].rearrange("p (c h) -> p c h", h=HEADS)

        def chunks(t):
            return t[:].unsqueeze(1).to_broadcast([P, CHUNKS, HEADS])

        with nc.Block() as block:
            @block.sync
            def _(eng):
                eng.dma_start(la[:], on_all_partitions(A_log)).then_inc(*loaded.one())
                eng.dma_start(db[:], on_all_partitions(dt_bias)).then_inc(*loaded.one())
                eng.wait_ge(*loaded.all())

            @block.scalar
            def _(eng):
                nc.scalar.preload_act_table_set("natural_log_exp_and_others")
                eng.wait_ge(*loaded.all())
                nc.scalar.activation(ea[:], la[:], ACT.Exp).then_inc(*act.does("ea"))
                eng.wait_ge(*dve.did(0, "na"))
                nc.scalar.activation(y[:], y[:], ACT.Exp).then_inc(*act.does("y"))
                eng.wait_ge(*dve.did(0, "u"))
                nc.scalar.activation(lu[:], u[:], ACT.Ln).then_inc(*act.does("lu"))
                nc.scalar.activation(v3(eb), gl[:, :, 0:HEADS], ACT.Exp, scale=-1.0).then_inc(*act.does("eb"))
                eng.wait_ge(*pe.did(0, "sums"))
                for k in range(3):
                    lo = (16, 32, 40)[k]
                    nc.scalar.activation(sc[:, :, lo:lo + HEADS], psum[k][:, 0:N].rearrange("p (c h) -> p c h", h=HEADS), ACT.Exp).then_inc(*act.does(f"e{k}"))

            @block.vector
            def _(eng):
                def step(ins, name_):
                    ins.then_inc(*dve.does(name_))
                    eng.wait_ge(*dve.did(0, name_))
                eng.wait_ge(*loaded.all())
                step(nc.vector.tensor_tensor(v3(a), gl[:, :, HEADS:16], chunks(db), ALU.add), "a")
                step(nc.vector.scalar_tensor_tensor(y[:], a[:], -1.0, a[:], ALU.mult, ALU.min), "na")
                eng.wait_ge(*act.did(0, "y"))
                step(nc.vector.tensor_scalar(u[:], y[:], 1.0, None, ALU.add), "u")
                step(nc.vector.tensor_scalar(d[:], u[:], -1.0, None, ALU.add), "d")
                step(nc.vector.tensor_scalar(g[:], d[:], 1e-30, None, ALU.max), "dm")
                step(nc.vector.reciprocal(g[:], g[:]), "rd")
                step(nc.vector.tensor_tensor(g[:], g[:], y[:], ALU.mult), "w1")
                step(nc.vector.tensor_scalar(d[:], d[:], 0.0, None, ALU.is_equal), "is0")
                eng.wait_ge(*act.did(0, "lu"))
                step(nc.vector.tensor_tensor(g[:], g[:], lu[:], ALU.mult), "w2")
                step(nc.vector.tensor_tensor(d[:], d[:], y[:], ALU.mult), "w")
                step(nc.vector.scalar_tensor_tensor(d[:], a[:], 0.0, d[:], ALU.max, ALU.add), "sp")
                step(nc.vector.tensor_tensor(g[:], g[:], d[:], ALU.add), "g")
                eng.wait_ge(*act.did(0, "ea"))
                step(nc.vector.scalar_tensor_tensor(sc[:, :, 0:HEADS], v3(g), -1.0, chunks(ea), ALU.mult, ALU.mult), "ps")
                eng.wait_ge(*act.did(0, "eb"))
                step(nc.vector.tensor_scalar(eb[:], eb[:], 1.0, None, ALU.add), "b1")
                step(nc.vector.reciprocal(eb[:], eb[:]), "b2")
                step(nc.vector.tensor_copy(sc[:, :, 8:16], v3(eb)), "b")
                eng.wait_ge(*act.did(0, "e2"))
                first = SCAL[:].rearrange("p (b c k) -> p b c k", b=BATCH, k=SC)[:, :, 0, :]
                step(nc.vector.memset(first[:, :, 16:24], 0.0), "zero")
                step(nc.vector.memset(first[:, :, 32:40], 0.0), "zc")
                step(nc.vector.scalar_tensor_tensor(sc[:, :, 24:32], sc[:, :, 16:24], -1.0, sc[:, :, 8:16], ALU.mult, ALU.mult), "neg")

            @block.tensor
            def _(eng):
                eng.wait_ge(*dve.did(0, "ps"))
                for k, who in enumerate((before_incl, everyone, after)):
                    last = nc.tensor.matmul(psum[k][:, 0:N].rearrange("p (c h) -> p c h", h=HEADS), who[:], sc[:, :, 0:HEADS], start=True, stop=True)
                last.then_inc(*pe.does("sums"))

def delta_stage(nc, name, HT, XN, SCAL, w, masks):
    with ExitStack() as stack:
        m = Space(nc, name, stack)

        def heads(n):
            return m.sb(n, [P, HEADS, P])

        def heads2(n):
            return [heads(f"{n}{s}") for s in range(2)]

        hc = m.sb("hc", [P, P])
        q, k, E, Em, Gm = map(heads, "q k E Em Gm".split())
        v, sg, kd, kT, qT, An, PT = map(heads2, "v sg kd kT qT An PT".split())
        U, T, W, r, dl, oP, o, S = map(heads, "U T W r dl oP o S".split())
        osq, oT = r, oP
        ss = m.sb("ss", [P, 16])
        rr = m.sb("rr", [P, 16])
        os_ = m.sb("os", [P, 8])
        ro = m.sb("ro", [P, 8])
        half = m.sb("half", [P, 16])
        sc = m.sb("sc", [P, 2, SC])
        nb = m.sb("nb", [P, 2, HEADS])
        A = [m.ps(f"A{j}") for j in range(2)]
        B = [m.ps(f"B{j}") for j in range(2)]
        C = [m.ps(f"C{j}") for j in range(2)]
        X = [m.ps(f"X{j}") for j in range(2)]
        LEVELS = 7

        SIDES = "T A T A T A T A T A A A A A A - -".split()

        inv_pe = "z00 z01 t00 t01 " + " ".join(f"z{l}0 z{l}1 u{l}0 t{l}0 u{l}1 t{l}1" for l in range(1, LEVELS - 1)) + " z60 z61 u60 u61"
        inv_act = "t00 t01 " + " ".join(f"u{l}0 t{l}0 u{l}1 t{l}1" for l in range(1, LEVELS - 1)) + " u60 u61"
        pe_main = Steps(m.sem("pe_main"), inv_pe + " KS0 KS1 QS0 QS1 dl0 dl1 KD0 KD1 PD0 PD1")
        pe_ahead = Steps(m.sem("pe_ahead"), "q0 q1 k0 k1 v0 v1 g0 g1 D0 D1 kT0 kT1 qT0 qT1 KK0 KK1 QK0 QK1 PT0 PT1")
        pe_tail = Steps(m.sem("pe_tail"), "oT0 oT1 Y")
        act_main = Steps(m.sem("act_main"), inv_act + " dl0 dl1 oP0 oP1")
        act_ahead = Steps(m.sem("act_ahead"), "h sc q0 q1 k0 k1 v0 v1 g0 g1 E0 E1 kT0 kT1 qT0 qT1 PT0 PT1")
        act_tail = Steps(m.sem("act_tail"), "oT0 oT1")
        dve_main = Steps(m.sem("dve_main"), " ".join(f"w{l}0 w{l}1" for l in range(LEVELS)) + " r0 r1 S0 S1 o0 o1")
        dve_ahead = Steps(m.sem("dve_ahead"), "nb ssq ssk se sq kn0 kn1 qn0 qn1 A0 A1 P0 P1")
        dve_tail = Steps(m.sem("dve_tail"), "os0 os1 oe on0 on1 og0 og1 x1")
        pool_ahead = Steps(m.sem("pool_ahead"), "qq kk Gm rr bv kd Em0 Es0 Em1 Es1")
        pool_tail = Steps(m.sem("pool_tail"), "osq0 osq1 ro")
        cleared, half_set = m.sem("cleared"), m.sem("half_set")
        hs = [slice(4 * j, 4 * j + 4) for j in range(2)]

        def bank(t):
            return t[:].rearrange("p (h n) -> p h n", h=4)

        def tok(t, i):
            return t[:, bass.ds(i * CHUNK, CHUNK)]

        def run(eng, main, ahead, tail):
            def turn(i, s, has_ahead, has_tail, again):
                parts = {"A": ahead(i + 1, 1 - s, True, again) if has_ahead else iter(()), "T": tail(i - 1, 1 - s) if has_tail else iter(()), "-": iter(())}
                order = iter(SIDES)
                main(i, s, again, lambda: next(parts[next(order)], None))
                for which in "TA":
                    for _ in parts[which]:
                        pass
            for _ in ahead(0, 0, False, False):
                pass
            turn(0, 0, True, False, False)
            with eng.Fori(0, CHUNKS // 2 - 1) as kk:
                turn(kk * 2 + 1, 1, True, True, True)
                turn(kk * 2 + 2, 0, True, True, True)
            turn(CHUNKS - 1, 1, False, True, True)
            for _ in tail(CHUNKS - 1, 1):
                pass

        with nc.Block() as block:
            @block.tensor
            def _(eng):
                def mm(out, lhsT, rhs):
                    return nc.tensor.matmul(out, lhsT, rhs, start=True, stop=True)

                def ahead(i, s, again, again2):
                    eng.wait_ge(*act_ahead.did(i, "h"))
                    for n, before in (("q", "PT"), ("k", "q"), ("v", "k"), ("g", "v")):
                        for j in range(2):
                            if n != "q":
                                eng.wait_ge(*act_ahead.did(i, f"{before}{j}"))
                            elif again:
                                eng.wait_ge(*act_ahead.did(i - 1, f"{before}{j}"))
                            if n == "g" and again2:
                                eng.wait_ge(*act_tail.did(i - 2, f"oT{j}"))
                            mm(X[j][:], hc[:], w[n][:, j * PAIR:(j + 1) * PAIR]).then_inc(*pe_ahead.does(f"{n}{j}"))
                        yield
                    eng.wait_ge(*pool_ahead.did(i, "Gm"))
                    if again2:
                        eng.wait_ge(*dve_tail.did(i - 2, "x1"))
                    for j in range(2):
                        eng.wait_ge(*act_ahead.did(i, f"g{j}"))
                        mm(X[j][:], masks["row_le_col"][:], Gm[:, hs[j], :].rearrange("p h n -> p (h n)")).then_inc(*pe_ahead.does(f"D{j}"))
                    yield
                    for n, src, before in (("kT", k, "E"), ("qT", q, "kT")):
                        for j in range(2):
                            eng.wait_ge(*act_ahead.did(i, f"{before}{j}"))
                            eng.wait_ge(*dve_ahead.did(i, f"{n[0]}n{j}"))
                            for h in range(4):
                                last = nc.tensor.transpose(bank(X[j])[:, h, :], src[:, 4 * j + h, :], masks["eye"][:])
                            last.then_inc(*pe_ahead.does(f"{n}{j}"))
                        yield
                    for j in range(2):
                        eng.wait_ge(*act_ahead.did(i, f"qT{j}"))
                        for h in range(4 * j, 4 * j + 4):
                            last = mm(bank(X[j])[:, h % 4, :], kT[s][:, h, :], kT[s][:, h, :])
                        last.then_inc(*pe_ahead.does(f"KK{j}"))
                    yield
                    for j in range(2):
                        eng.wait_ge(*dve_ahead.did(i, f"A{j}"))
                        for h in range(4 * j, 4 * j + 4):
                            last = mm(bank(X[j])[:, h % 4, :], qT[s][:, h, :], kT[s][:, h, :])
                        last.then_inc(*pe_ahead.does(f"QK{j}"))
                    yield
                    for j in range(2):
                        eng.wait_ge(*dve_ahead.did(i, f"P{j}"))
                        for h in range(4 * j, 4 * j + 4):
                            last = nc.tensor.transpose(bank(X[j])[:, h % 4, :], Em[:, h, :], masks["eye"][:])
                        last.then_inc(*pe_ahead.does(f"PT{j}"))
                    yield

                def main(i, s, again, place):
                    def prev(who, step):
                        if again:
                            eng.wait_ge(*who.did(i - 1, step))
                    for l in range(LEVELS):
                        for j in range(2):
                            if l:
                                eng.wait_ge(*dve_main.did(i, f"w{l - 1}{j}"))
                                if l > 1:
                                    eng.wait_ge(*act_main.did(i, f"u{l - 1}{j}"))
                            else:
                                eng.wait_ge(*dve_ahead.did(i, f"A{j}"))
                                prev(act_main, f"oP{j}")
                            for h in range(4 * j, 4 * j + 4):
                                nc.tensor.matmul(bank(B[j])[:, h % 4, :], masks["eye16"][:], masks["eye16"][:], start=True, stop=False)
                                last = nc.tensor.matmul(bank(B[j])[:, h % 4, :], An[s][:, h, :], U[:, h, :] if l else masks["eye"][:], start=False, stop=True)
                            last.then_inc(*pe_main.does(f"z{l}{j}"))
                        place()
                        for j in range(2):
                            eng.wait_ge(*dve_main.did(i, f"w{l}{j}"))
                            if l:
                                eng.wait_ge(*(act_main.did(i, f"t{l - 1}{j}")))
                                if l == 1:
                                    prev(dve_main, f"S{j}")
                                for h in range(4 * j, 4 * j + 4):
                                    last = mm(bank(C[j])[:, h % 4, :], T[:, h, :], W[:, h, :])
                                last.then_inc(*pe_main.does(f"u{l}{j}"))
                            if l < LEVELS - 1:
                                if l == 0:
                                    prev(dve_main, f"o{j}")
                                for h in range(4 * j, 4 * j + 4):
                                    if l:
                                        last = mm(bank(A[j])[:, h % 4, :], W[:, h, :], T[:, h, :])
                                    else:
                                        last = mm(bank(A[j])[:, h % 4, :], U[:, h, :], masks["eye"][:])
                                last.then_inc(*pe_main.does(f"t{l}{j}"))
                        place()
                    if not again:
                        eng.wait_ge(cleared, 1)
                    for n, src, bk in (("KS", kT[s], B), ("QS", qT[s], A)):
                        for j in range(2):
                            prev(dve_main, f"S{j}")
                            for h in range(4 * j, 4 * j + 4):
                                last = mm(bank(bk[j])[:, h % 4, :], src[:, h, :], S[:, h, :])
                            last.then_inc(*pe_main.does(f"{n}{j}"))
                    place()
                    for j in range(2):
                        eng.wait_ge(*dve_main.did(i, f"r{j}"))
                        eng.wait_ge(*act_main.did(i, f"u6{j}"))
                        for h in range(4 * j, 4 * j + 4):
                            last = mm(bank(C[j])[:, h % 4, :], U[:, h, :], r[:, h, :])
                        last.then_inc(*pe_main.does(f"dl{j}"))
                    place()
                    for n, src, bk in (("KD", kd[s], C), ("PD", PT[s], B)):
                        for j in range(2):
                            eng.wait_ge(*act_main.did(i, f"dl{j}"))
                            if n == "KD":
                                eng.wait_ge(*pool_ahead.did(i, "kd"))
                            else:
                                eng.wait_ge(*act_ahead.did(i, f"PT{j}"))
                            for h in range(4 * j, 4 * j + 4):
                                last = mm(bank(bk[j])[:, h % 4, :], src[:, h, :], dl[:, h, :])
                            last.then_inc(*pe_main.does(f"{n}{j}"))
                    place()

                def tail(i, s):
                    yield
                    yield
                    yield
                    for j in range(2):
                        eng.wait_ge(*dve_tail.did(i, f"og{j}"))
                        if not (isinstance(i, int) and i >= CHUNKS - 2):
                            eng.wait_ge(*act_ahead.did(i + 2, f"v{j}"))
                        for h in range(4 * j, 4 * j + 4):
                            last = nc.tensor.transpose(bank(X[j])[:, h % 4, :], o[:, h, :], masks["eye"][:])
                        last.then_inc(*pe_tail.does(f"oT{j}"))
                    yield
                    eng.wait_ge(*act_tail.did(i, "oT1"))
                    if not (isinstance(i, int) and i >= CHUNKS - 2):
                        eng.wait_ge(*act_ahead.did(i + 2, "g0"))
                    for h in range(HEADS):
                        last = nc.tensor.matmul(X[0][:, 0:P], w["o"][:, h * P:(h + 1) * P], oT[:, h, :], start=(h == 0), stop=(h == HEADS - 1))
                    last.then_inc(*pe_tail.does("Y"))
                    yield
                run(eng, main, ahead, tail)

            @block.scalar
            def _(eng):
                def ahead(i, s, again, again2):
                    def prev(who, step):
                        if again:
                            eng.wait_ge(*who.did(i - 1, step))

                    def prev2(who, step):
                        if again2:
                            eng.wait_ge(*who.did(i - 2, step))
                    prev(pe_ahead, "g1")
                    nc.scalar.activation(hc[:], tok(HT, i), ACT.Copy).then_inc(*act_ahead.does("h"))
                    prev2(dve_main, "o1")
                    prev2(pool_ahead, "kd")
                    nc.scalar.activation(sc[:, s], SCAL[:, bass.ds(i * SC, SC)], ACT.Copy).then_inc(*act_ahead.does("sc"))
                    for n, dst in (("q", q), ("k", k), ("v", v[s]), ("g", sg[s])):
                        for j in range(2):
                            eng.wait_ge(*pe_ahead.did(i, f"{n}{j}"))
                            if n == "q":
                                prev(pe_ahead, "qT1")
                            elif n == "k":
                                prev(pool_ahead, "kd")
                            elif n == "v":
                                prev2(dve_main, f"r{j}")
                            else:
                                prev2(dve_tail, f"og{j}")
                            nc.scalar.activation(dst[:, hs[j], :], bank(X[j]), ACT.Silu).then_inc(*act_ahead.does(f"{n}{j}"))
                        yield
                    for j in range(2):
                        eng.wait_ge(*pe_ahead.did(i, f"D{j}"))
                        prev(dve_ahead, f"A{j}")
                        nc.scalar.activation(E[:, hs[j], :], bank(X[j]), ACT.Exp).then_inc(*act_ahead.does(f"E{j}"))
                    yield
                    for n, dst, used in (("kT", kT[s], "KS"), ("qT", qT[s], "QS")):
                        for j in range(2):
                            eng.wait_ge(*pe_ahead.did(i, f"{n}{j}"))
                            prev2(pe_main, f"{used}{j}")
                            nc.scalar.activation(dst[:, hs[j], :], bank(X[j]), ACT.Copy).then_inc(*act_ahead.does(f"{n}{j}"))
                        yield
                    yield
                    yield
                    for j in range(2):
                        eng.wait_ge(*pe_ahead.did(i, f"PT{j}"))
                        prev2(pe_main, f"PD{j}")
                        nc.scalar.activation(PT[s][:, hs[j], :], bank(X[j]), ACT.Copy).then_inc(*act_ahead.does(f"PT{j}"))
                    yield

                def main(i, s, again, place):
                    for l in range(LEVELS):
                        place()
                        for j in range(2):
                            if l:
                                eng.wait_ge(*pe_main.did(i, f"u{l}{j}"))
                                nc.scalar.activation(U[:, hs[j], :], bank(C[j]), ACT.Copy).then_inc(*act_main.does(f"u{l}{j}"))
                            if l < LEVELS - 1:
                                eng.wait_ge(*pe_main.did(i, f"t{l}{j}"))
                                nc.scalar.activation(T[:, hs[j], :], bank(A[j]), ACT.Copy).then_inc(*act_main.does(f"t{l}{j}"))
                        place()
                    place()
                    for j in range(2):
                        eng.wait_ge(*pe_main.did(i, f"dl{j}"))
                        nc.scalar.activation(dl[:, hs[j], :], bank(C[j]), ACT.Copy).then_inc(*act_main.does(f"dl{j}"))
                    place()
                    for j in range(2):
                        eng.wait_ge(*pe_main.did(i, f"PD{j}"))
                        if again:
                            eng.wait_ge(*pe_tail.did(i - 1, "Y"))
                        nc.scalar.activation(oP[:, hs[j], :], bank(B[j]), ACT.Copy).then_inc(*act_main.does(f"oP{j}"))
                    place()

                def tail(i, s):
                    yield
                    yield
                    yield
                    for j in range(2):
                        eng.wait_ge(*pe_tail.did(i, f"oT{j}"))
                        if j == 0:
                            eng.wait_ge(*dve_main.did(i, "o1"))
                        nc.scalar.activation(oT[:, hs[j], :], bank(X[j]), ACT.Copy).then_inc(*act_tail.does(f"oT{j}"))
                    yield
                    yield
                run(eng, main, ahead, tail)

            @block.vector
            def _(eng):
                nc.vector.memset(S[:], 0.0).then_inc(cleared, 1)

                def ahead(i, s, again, again2):
                    yield
                    yield
                    eng.wait_ge(*act_ahead.did(i, "sc"))
                    nc.vector.tensor_scalar(nb[:, s], sc[:, s, 8:16], -1.0, None, ALU.mult).then_inc(*dve_ahead.does("nb"))
                    eng.wait_ge(*pool_ahead.did(i, "qq"))
                    if again:
                        eng.wait_ge(*pool_ahead.did(i - 1, "rr"))
                    nc.vector.tensor_reduce(ss[:, 0:8], Gm[:], AX, ALU.add).then_inc(*dve_ahead.does("ssq"))
                    yield
                    eng.wait_ge(*pool_ahead.did(i, "kk"))
                    nc.vector.tensor_reduce(ss[:, 8:16], Em[:], AX, ALU.add).then_inc(*dve_ahead.does("ssk"))
                    eng.wait_ge(*dve_ahead.did(i, "ssk"))
                    nc.vector.tensor_scalar(ss[:], ss[:], 1e-6, None, ALU.add).then_inc(*dve_ahead.does("se"))
                    yield
                    eng.wait_ge(*pool_ahead.did(i, "rr"))
                    nc.vector.tensor_scalar(rr[:, 0:8], rr[:, 0:8], float(DK) ** -0.5, None, ALU.mult).then_inc(*dve_ahead.does("sq"))
                    eng.wait_ge(*dve_ahead.did(i, "sq"))
                    for n, t, lo in (("k", k, 8), ("q", q, 0)):
                        for j in range(2):
                            nc.vector.tensor_tensor(t[:, hs[j], :], t[:, hs[j], :], along(rr[:, lo + 4 * j:lo + 4 * j + 4], P), ALU.mult).then_inc(*dve_ahead.does(f"{n}n{j}"))
                        yield
                    yield
                    for j in range(2):
                        eng.wait_ge(*pe_ahead.did(i, f"KK{j}"))
                        eng.wait_ge(*pool_ahead.did(i, f"Es{j}"))
                        if again2:
                            eng.wait_ge(*pe_main.did(i - 2, f"z{LEVELS - 1}{j}"))
                        for h in range(4 * j, 4 * j + 4):
                            last = nc.vector.scalar_tensor_tensor(An[s][:, h, :], bank(X[j])[:, h % 4, :], nb[:, s, h:h + 1], E[:, h, :], ALU.mult, ALU.mult)
                        last.then_inc(*dve_ahead.does(f"A{j}"))
                    yield
                    for j in range(2):
                        eng.wait_ge(*pe_ahead.did(i, f"QK{j}"))
                        nc.vector.tensor_tensor(Em[:, hs[j], :], bank(X[j]), Em[:, hs[j], :], ALU.mult).then_inc(*dve_ahead.does(f"P{j}"))
                    yield
                    yield

                def main(i, s, again, place):
                    for l in range(LEVELS):
                        dst = W if l else U
                        for j in range(2):
                            eng.wait_ge(*pe_main.did(i, f"z{l}{j}"))
                            if l == 0 and again:
                                eng.wait_ge(*pe_main.did(i - 1, f"dl{j}"))
                            nc.vector.tensor_tensor(dst[:, hs[j], :], bank(B[j]), over_heads(masks["level"][:, l * P:(l + 1) * P], 4), ALU.mult).then_inc(*dve_main.does(f"w{l}{j}"))
                        place()
                        place()
                    for j in range(2):
                        eng.wait_ge(*pe_main.did(i, f"KS{j}"))
                        eng.wait_ge(*pool_ahead.did(i, "bv"))
                        for h in range(4 * j, 4 * j + 4):
                            last = nc.vector.scalar_tensor_tensor(r[:, h, :], bank(B[j])[:, h % 4, :], sc[:, s, 24 + h:25 + h], v[s][:, h, :], ALU.mult, ALU.add)
                        last.then_inc(*dve_main.does(f"r{j}"))
                    place()
                    place()
                    for j in range(2):
                        eng.wait_ge(*pe_main.did(i, f"KD{j}"))
                        for h in range(4 * j, 4 * j + 4):
                            last = nc.vector.scalar_tensor_tensor(S[:, h, :], S[:, h, :], sc[:, s, 32 + h:33 + h], bank(C[j])[:, h % 4, :], ALU.mult, ALU.add)
                        last.then_inc(*dve_main.does(f"S{j}"))
                    for j in range(2):
                        eng.wait_ge(*pe_main.did(i, f"QS{j}"))
                        eng.wait_ge(*act_main.did(i, f"oP{j}"))
                        if again:
                            eng.wait_ge(*pe_tail.did(i - 1, f"oT{j}"))
                        for h in range(4 * j, 4 * j + 4):
                            last = nc.vector.scalar_tensor_tensor(o[:, h, :], bank(A[j])[:, h % 4, :], sc[:, s, 16 + h:17 + h], oP[:, h, :], ALU.mult, ALU.add)
                        last.then_inc(*dve_main.does(f"o{j}"))
                    place()

                def tail(i, s):
                    yield
                    for j in range(2):
                        eng.wait_ge(*pool_tail.did(i, f"osq{j}"))
                        nc.vector.tensor_reduce(os_[:, 4 * j:4 * j + 4], osq[:, hs[j], :], AX, ALU.add).then_inc(*dve_tail.does(f"os{j}"))
                    eng.wait_ge(*dve_tail.did(i, "os1"))
                    nc.vector.tensor_scalar(os_[:], os_[:], 1.0 / DK, 1e-6, ALU.mult, ALU.add).then_inc(*dve_tail.does("oe"))
                    yield
                    eng.wait_ge(*pool_tail.did(i, "ro"))
                    for j in range(2):
                        nc.vector.tensor_tensor(o[:, hs[j], :], o[:, hs[j], :], along(ro[:, 4 * j:4 * j + 4], P), ALU.mult).then_inc(*dve_tail.does(f"on{j}"))
                    for j in range(2):
                        eng.wait_ge(*dve_tail.did(i, f"on{j}"))
                        nc.vector.tensor_tensor(o[:, hs[j], :], o[:, hs[j], :], sg[s][:, hs[j], :], ALU.mult).then_inc(*dve_tail.does(f"og{j}"))
                    yield
                    yield
                    eng.wait_ge(*pe_tail.did(i, "Y"))
                    nc.vector.tensor_tensor(tok(HT, i), X[0][:, 0:P], tok(XN, i), ALU.add).then_inc(*dve_tail.does("x1"))
                    yield
                run(eng, main, ahead, tail)

            @block.gpsimd
            def _(eng):
                nc.gpsimd.memset(half[:], -0.5).then_inc(half_set, 1)
                eng.wait_ge(half_set, 1)

                def ahead(i, s, again, again2):
                    def prev(who, step):
                        if again:
                            eng.wait_ge(*who.did(i - 1, step))
                    yield
                    eng.wait_ge(*act_ahead.did(i, "q1"))
                    prev(pe_ahead, "D1")
                    nc.gpsimd.tensor_tensor(Gm[:], q[:], q[:], ALU.mult).then_inc(*pool_ahead.does("qq"))
                    yield
                    eng.wait_ge(*act_ahead.did(i, "k1"))
                    prev(pe_ahead, "PT1")
                    nc.gpsimd.tensor_tensor(Em[:], k[:], k[:], ALU.mult).then_inc(*pool_ahead.does("kk"))
                    eng.wait_ge(*dve_ahead.did(i, "ssq"))
                    nc.gpsimd.tensor_tensor(Gm[:], over_heads(masks["row_gt_col"][:], HEADS), along(sc[:, s, 0:8], P), ALU.mult).then_inc(*pool_ahead.does("Gm"))
                    yield
                    eng.wait_ge(*dve_ahead.did(i, "se"))
                    prev(dve_ahead, "qn1")
                    nc.gpsimd.tensor_tensor(rr[:], ss[:], half[:], ALU.pow).then_inc(*pool_ahead.does("rr"))
                    yield
                    eng.wait_ge(*act_ahead.did(i, "v1"))
                    nc.gpsimd.tensor_tensor(v[s][:], v[s][:], along(sc[:, s, 8:16], P), ALU.mult).then_inc(*pool_ahead.does("bv"))
                    eng.wait_ge(*dve_ahead.did(i, "kn1"))
                    if again2:
                        eng.wait_ge(*pe_main.did(i - 2, "KD1"))
                    nc.gpsimd.tensor_tensor(kd[s][:], k[:], along(sc[:, s, 40:48], P), ALU.mult).then_inc(*pool_ahead.does("kd"))
                    yield
                    for j in range(2):
                        eng.wait_ge(*act_ahead.did(i, f"E{j}"))
                        nc.gpsimd.tensor_tensor(Em[:, hs[j], :], E[:, hs[j], :], over_heads(masks["row_ge_col"][:], 4), ALU.mult).then_inc(*pool_ahead.does(f"Em{j}"))
                        eng.wait_ge(*pool_ahead.did(i, f"Em{j}"))
                        nc.gpsimd.tensor_tensor(E[:, hs[j], :], E[:, hs[j], :], over_heads(masks["row_gt_col"][:], 4), ALU.mult).then_inc(*pool_ahead.does(f"Es{j}"))
                    yield

                def main(i, s, again, place):
                    for _ in SIDES:
                        place()

                def tail(i, s):
                    for j in range(2):
                        eng.wait_ge(*dve_main.did(i, f"o{j}"))
                        eng.wait_ge(*pe_main.did(i, f"dl{j}"))
                        nc.gpsimd.tensor_tensor(osq[:, hs[j], :], o[:, hs[j], :], o[:, hs[j], :], ALU.mult).then_inc(*pool_tail.does(f"osq{j}"))
                    yield
                    eng.wait_ge(*dve_tail.did(i, "oe"))
                    nc.gpsimd.tensor_tensor(ro[:], os_[:], half[:, 0:8], ALU.pow).then_inc(*pool_tail.does("ro"))
                    yield
                run(eng, main, ahead, tail)

def at_group(t, g):
    return t[:, bass.ds(g * GRP, GRP)]

def relu_mlp_stage(nc, name, XT, X1, w_up, w_down, ones_mean):
    F = w_up.shape[1] // P
    with ExitStack() as stack:
        m = Space(nc, name, stack)
        sq, ln, rs, r2, xm = (m.sb(n, [P, 2, GRP]) for n in "sq ln rs r2 xm".split())
        r = m.sb("r", [P, F, GRP])
        hid = m.sb("hid", [P, F, GRP])
        xs = m.sb("xs", [P, 2, GRP])
        eps = m.sb("eps", [P, 1])
        ms = m.ps("ms")
        up = [m.ps(f"up{c}") for c in range(F)]
        down = m.ps("down")
        pe = Steps(m.sem("pe"), "ms " + " ".join(f"up{c}" for c in range(F)) + " down")
        act = Steps(m.sem("act"), "sq " + rsqrt_names("m")[0] + " " + " ".join(f"r{c}" for c in range(F)))
        dve = Steps(m.sem("dve"), rsqrt_names("m")[1] + " xm xs " + " ".join(f"hid{c}" for c in range(F)) + " out")
        ready = m.sem("ready")
        with nc.Block() as block:
            @block.tensor
            def _(eng):
                def body(g, s, again):
                    eng.wait_ge(*act.did(g, "sq"))
                    if s or again:
                        eng.wait_ge(*dve.did(g - 1, "xm"))
                    nc.tensor.matmul(ms[:], ones_mean[:], sq[:, s], start=True, stop=True).then_inc(*pe.does("ms"))
                    eng.wait_ge(*dve.did(g, "xm"))
                    for c in range(F):
                        if s or again:
                            eng.wait_ge(*dve.did(g - 1, f"hid{c}"))
                        nc.tensor.matmul(up[c][:], w_up[:, c * P:(c + 1) * P], xm[:, s], start=True, stop=True).then_inc(*pe.does(f"up{c}"))
                    if s or again:
                        eng.wait_ge(*dve.did(g - 1, "out"))
                    for c in range(F):
                        eng.wait_ge(*dve.did(g, f"hid{c}"))
                        last = nc.tensor.matmul(down[:], w_down[:, c * P:(c + 1) * P], hid[:, c], start=(c == 0), stop=(c == F - 1))
                    last.then_inc(*pe.does("down"))
                tiles(eng, GROUPS, 2, body)

            @block.scalar
            def _(eng):
                nc.scalar.preload_act_table_set("natural_log_exp_and_others")
                eng.wait_ge(ready, 1)
                def body(g, s, again):
                    nc.scalar.activation(sq[:, s], at_group(X1, g), ACT.Square).then_inc(*act.does("sq"))
                    eng.wait_ge(*pe.did(g, "ms"))
                    rsqrt_act(nc, eng, act, g, "m", ms[:], eps[:], ln[:, s], rs[:, s], r2[:, s])
                    for c in range(F):
                        eng.wait_ge(*pe.did(g, f"up{c}"))
                        if s or again:
                            eng.wait_ge(*dve.did(g - 1, f"hid{c}"))
                        nc.scalar.activation(r[:, c], up[c][:], ACT.Relu).then_inc(*act.does(f"r{c}"))
                tiles(eng, GROUPS, 2, body)

            @block.vector
            def _(eng):
                nc.vector.memset(eps[:], 1e-6).then_inc(ready, 1)
                def body(g, s, again):
                    rsqrt_dve(nc, eng, act, dve, g, "m", ms[:], 1e-6, rs[:, s], r2[:, s])
                    nc.vector.tensor_tensor(xm[:, s], at_group(X1, g), rs[:, s], ALU.mult).then_inc(*dve.does("xm"))
                    nc.vector.tensor_tensor(xs[:, s], at_group(XT, g), at_group(X1, g), ALU.add).then_inc(*dve.does("xs"))
                    for c in range(F):
                        eng.wait_ge(*act.did(g, f"r{c}"))
                        if s or again:
                            eng.wait_ge(*pe.did(g - 1, "down"))
                        nc.vector.scalar_tensor_tensor(hid[:, c], up[c][:], 0.0, r[:, c], ALU.max, ALU.mult).then_inc(*dve.does(f"hid{c}"))
                    eng.wait_ge(*pe.did(g, "down"))
                    eng.wait_ge(*dve.did(g, "xs"))
                    nc.vector.tensor_tensor(at_group(XT, g), down[:], xs[:, s], ALU.add).then_inc(*dve.does("out"))
                tiles(eng, GROUPS, 2, body)

def gelu_mlp_stage(nc, name, XT, XN, w1, w2, bias1, bias2):
    F = w1.shape[1] // P
    with ExitStack() as stack:
        m = Space(nc, name, stack)
        hid = m.sb("hid", [P, 2, F, GRP])
        up = [m.ps(f"up{c}") for c in range(F)]
        down = [m.ps(f"down{s}") for s in range(2)]
        pe = Steps(m.sem("pe"), " ".join(f"up{c}" for c in range(F)) + " down")
        act = Steps(m.sem("act"), " ".join(f"hid{c}" for c in range(F)))
        dve = Steps(m.sem("dve"), "out")
        with nc.Block() as block:
            @block.tensor
            def _(eng):
                def body(g, s, again):
                    for c in range(F):
                        if s or again:
                            eng.wait_ge(*act.did(g - 1, f"hid{c}"))
                        nc.tensor.matmul(up[c][:], w1[:, c * P:(c + 1) * P], at_group(XN, g), start=True, stop=True).then_inc(*pe.does(f"up{c}"))
                    if again:
                        eng.wait_ge(*dve.did(g - 2, "out"))
                    for c in range(F):
                        eng.wait_ge(*act.did(g, f"hid{c}"))
                        last = nc.tensor.matmul(down[s][:], w2[:, c * P:(c + 1) * P], hid[:, s, c], start=(c == 0), stop=(c == F - 1))
                    last.then_inc(*pe.does("down"))
                tiles(eng, GROUPS, 2, body)

            @block.scalar
            def _(eng):
                def body(g, s, again):
                    if again:
                        eng.wait_ge(*pe.did(g - 2, "down"))
                    for c in range(F):
                        eng.wait_ge(*pe.did(g, f"up{c}"))
                        nc.scalar.activation(hid[:, s, c], up[c][:], ACT.Gelu, bias=bias1[:, c:c + 1]).then_inc(*act.does(f"hid{c}"))
                tiles(eng, GROUPS, 2, body)

            @block.vector
            def _(eng):
                def body(g, s, again):
                    eng.wait_ge(*pe.did(g, "down"))
                    nc.vector.scalar_tensor_tensor(at_group(XT, g), down[s][:], bias2[:, 0:1], at_group(XT, g), ALU.add, ALU.add).then_inc(*dve.does("out"))
                tiles(eng, GROUPS, 2, body)

def binary_weights(nc, name, w1_in, w2_in, w1, w2, eye):
    H = w1_in.shape[0]
    F = H // P
    with ExitStack() as stack:
        m = Space(nc, name, stack)
        raw = m.sb("raw", [P, 2, F, P])
        mag = m.sb("mag", [P, 2, F, P])
        sign = m.sb("sign", [P, 2, F, P])
        al = m.sb("al", [P, 2, F])
        turned = [m.ps(f"turned{k}") for k in range(2)]
        loaded = Loads(m.sem("loaded"))
        act, dve, pe = Steps(m.sem("act"), "mag sign w0 w1"), Steps(m.sem("dve"), "sum1 sum2 mean1 mean2 a1 a2 diff w"), Steps(m.sem("pe"), "t0 t1")
        with nc.Block() as block:
            @block.sync
            def _(eng):
                eng.dma_start(raw[:, 0], w1_in.rearrange("(c p) d -> p c d", p=P)).then_inc(*loaded.one())
                eng.dma_start(raw[:, 1], w2_in.rearrange("d (c p) -> d c p", p=P)).then_inc(*loaded.one())

            @block.scalar
            def _(eng):
                eng.wait_ge(*loaded.all())
                nc.scalar.activation(mag[:], raw[:], ACT.Abs).then_inc(*act.does("mag"))
                nc.scalar.activation(sign[:], raw[:], ACT.Sign).then_inc(*act.does("sign"))
                for k, dst in enumerate((w1, w2)):
                    eng.wait_ge(*pe.did(0, f"t{k}"))
                    nc.scalar.activation(dst[:], turned[k][:], ACT.Copy).then_inc(*act.does(f"w{k}"))

            @block.vector
            def _(eng):
                def step(ins, name_):
                    ins.then_inc(*dve.does(name_))
                    eng.wait_ge(*dve.did(0, name_))
                eng.wait_ge(*act.did(0, "mag"))
                step(nc.vector.tensor_reduce(al[:, 0], mag[:, 0], AX, ALU.add), "sum1")
                step(nc.vector.tensor_reduce(al[:, 1, 0:1], mag[:, 1].rearrange("p c n -> p (c n)"), AX, ALU.add), "sum2")
                step(nc.vector.tensor_scalar(al[:, 0], al[:, 0], 1.0 / P, None, ALU.mult), "mean1")
                step(nc.vector.tensor_scalar(al[:, 1, 0:1], al[:, 1, 0:1], 1.0 / H, None, ALU.mult), "mean2")
                eng.wait_ge(*act.did(0, "sign"))
                step(nc.vector.tensor_tensor(mag[:, 0], sign[:, 0], along(al[:, 0], P), ALU.mult), "a1")
                step(nc.vector.tensor_scalar(mag[:, 1], sign[:, 1], al[:, 1, 0:1], None, ALU.mult), "a2")
                step(nc.vector.tensor_tensor(mag[:], mag[:], raw[:], ALU.subtract), "diff")
                step(nc.vector.tensor_tensor(mag[:], mag[:], raw[:], ALU.add), "w")

            @block.tensor
            def _(eng):
                eng.wait_ge(*dve.did(0, "w"))
                for k in range(2):
                    for c in range(F):
                        last = nc.tensor.transpose(turned[k][:, c * P:(c + 1) * P], mag[:, k, c], eye[:])
                    last.then_inc(*pe.does(f"t{k}"))

def qlora_weights(nc, name, q_in, scales, lora_a, lora_bT, WQ, eye):
    L, GROUP = q_in.shape[0], 16
    R = lora_a.shape[1]
    with ExitStack() as stack:
        m = Space(nc, name, stack)
        qi = m.sb("qi", [P, L, P], q_in.dtype)
        wf = m.sb("wf", [P, L, P])
        sc = m.sb("sc", [P, L, P // GROUP])
        la = m.sb("la", [R, L, P])
        lb = m.sb("lb", [R, L, P])
        low = [m.ps(f"low{k}") for k in range(2)]
        turned = [m.ps(f"turned{k}") for k in range(2)]
        loaded = Loads(m.sem("loaded"))
        pe, dve = Steps(m.sem("pe"), "low turned"), Steps(m.sem("dve"), "float affine scaled sum0 sum1 w0 w1")
        parts = [slice(0, 4), slice(4, L)]

        def bank(t, n):
            return t[:, 0:n * P].rearrange("p (l n) -> p l n", n=P)
        with nc.Block() as block:
            @block.sync
            def _(eng):
                eng.dma_start(qi[:], q_in.rearrange("l o i -> o l i")).then_inc(*loaded.one())
                eng.dma_start(sc[:], scales.rearrange("l o g -> o l g")).then_inc(*loaded.one())
                eng.dma_start(la[:], lora_a.rearrange("l r i -> r l i")).then_inc(*loaded.one())
                eng.dma_start(lb[:], lora_bT.rearrange("l r o -> r l o")).then_inc(*loaded.one())

            @block.tensor
            def _(eng):
                eng.wait_ge(*loaded.all())
                for l in range(L):
                    last = nc.tensor.matmul(bank(low[l // 4], 4)[:, l % 4, :], lb[:, l], la[:, l], start=True, stop=True)
                last.then_inc(*pe.does("low"))
                eng.wait_ge(*dve.did(0, "sum1"))
                for l in range(L):
                    last = nc.tensor.transpose(bank(turned[l // 4], 4)[:, l % 4, :], wf[:, l], eye[:])
                last.then_inc(*pe.does("turned"))

            @block.vector
            def _(eng):
                def step(ins, name_):
                    ins.then_inc(*dve.does(name_))
                    eng.wait_ge(*dve.did(0, name_))
                eng.wait_ge(*loaded.all())
                step(nc.vector.tensor_copy(wf[:], qi[:]), "float")
                step(nc.vector.tensor_scalar(wf[:], wf[:], 1.0 / 7.5, -1.0, ALU.mult, ALU.add), "affine")
                w4 = wf[:].rearrange("p l (g k) -> p (l g) k", k=GROUP)
                step(nc.vector.tensor_tensor(w4, w4, along(sc[:].rearrange("p l g -> p (l g)"), GROUP), ALU.mult), "scaled")
                eng.wait_ge(*pe.did(0, "low"))
                for k, part in enumerate(parts):
                    step(nc.vector.tensor_tensor(wf[:, part], wf[:, part], bank(low[k], part.stop - part.start), ALU.add), f"sum{k}")
                eng.wait_ge(*pe.did(0, "turned"))
                for k, part in enumerate(parts):
                    nc.vector.tensor_copy(WQ[:, part], bank(turned[k], part.stop - part.start)).then_inc(*dve.does(f"w{k}"))

def qlora_stage(nc, name, XT, XN, WQ, biasT, bias_rows, gammaT, betaT, eye):
    with ExitStack() as stack:
        m = Space(nc, name, stack)
        h = m.sb("h", [P, 2, GRP])
        y = m.sb("y", [P, 2, 4, P])
        z = m.sb("z", [P, 2, 4, P])
        yT = m.sb("yT", [P, 2, GRP])
        st = m.sb("st", [P, 2, 4, 6])
        ag = m.sb("ag", [P, 2, 4, 2])
        rs = m.sb("rs", [P, 2, 4])
        ve = m.sb("ve", [P, 2, 4])
        half = m.sb("half", [P, 4])
        carrier = m.sb("carrier", [P, 2])
        lin = [m.ps(f"lin{s}") for s in range(2)]
        turned = [m.ps(f"turned{s}") for s in range(2)]
        back = [m.ps(f"back{s}") for s in range(2)]
        N = 3
        per = lambda names: " ".join(f"{n}{b}" for b in range(N) for n in names.split())
        def pairs(names):
            return " ".join(f"{n}{b}{s}" for b in range(N) for n in names.split() for s in range(2))
        pe = Steps(m.sem("pe"), pairs("lin turned back"))
        act = Steps(m.sem("act"), "h0 h1 " + pairs("gelu"))
        dve = Steps(m.sem("dve"), " ".join(f"y{b}0 y{b}1 st{b}0 st{b}1 cr{b}0 ag{b}0 cr{b}1 ag{b}1 ve{b}0 ve{b}1 z{b}0 z{b}1 h{b}0 h{b}1" for b in range(N)) + " out0 out1")
        pool = Steps(m.sem("pool"), pairs("rs"))
        half_set = m.sem("half_set")

        with nc.Block() as block:
            @block.tensor
            def _(eng):
                def body(i, _, again):
                    for b in range(N):
                        for s in range(2):
                            if b == 0:
                                eng.wait_ge(*act.did(i, f"h{s}"))
                                if again:
                                    eng.wait_ge(*dve.did(i - 1, f"y{N - 1}{s}"))
                            else:
                                eng.wait_ge(*dve.did(i, f"h{b - 1}{s}"))
                            for t in range(4):
                                last = nc.tensor.matmul(lin[s][:, t * P:(t + 1) * P], h[:, s, t * P:(t + 1) * P], WQ[:, 2 * b], start=True, stop=True)
                            last.then_inc(*pe.does(f"lin{b}{s}"))
                        for s in range(2):
                            eng.wait_ge(*dve.did(i, f"z{b}{s}"))
                            for t in range(4):
                                last = nc.tensor.transpose(turned[s][:, t * P:(t + 1) * P], z[:, s, t], eye[:])
                            last.then_inc(*pe.does(f"turned{b}{s}"))
                        for s in range(2):
                            eng.wait_ge(*act.did(i, f"gelu{b}{s}"))
                            nc.tensor.matmul(back[s][:], WQ[:, 2 * b + 1], yT[:, s], start=True, stop=True).then_inc(*pe.does(f"back{b}{s}"))
                tiles(eng, GROUPS // 2, 1, body)

            @block.scalar
            def _(eng):
                def body(i, _, again):
                    for s in range(2):
                        if again:
                            eng.wait_ge(*dve.did(i - 1, f"out{s}"))
                        nc.scalar.activation(h[:, s], at_group(XN, i * 2 + s), ACT.Copy).then_inc(*act.does(f"h{s}"))
                    for b in range(N):
                        for s in range(2):
                            eng.wait_ge(*pe.did(i, f"turned{b}{s}"))
                            nc.scalar.activation(yT[:, s], turned[s][:], ACT.Gelu, scale=gammaT[:, b:b + 1], bias=betaT[:, b:b + 1]).then_inc(*act.does(f"gelu{b}{s}"))
                tiles(eng, GROUPS // 2, 1, body)

            @block.vector
            def _(eng):
                def body(i, _, again):
                    for b in range(N):
                        for s in range(2):
                            eng.wait_ge(*pe.did(i, f"lin{b}{s}"))
                            nc.vector.tensor_tensor(y[:, s], lin[s][:].rearrange("p (t n) -> p t n", n=P), over_heads(bias_rows[:, b], 4), ALU.add).then_inc(*dve.does(f"y{b}{s}"))
                        for s in range(2):
                            eng.wait_ge(*dve.did(i, f"y{b}{s}"))
                            for t in range(4):
                                last = nc.vector.bn_stats(st[:, s, t], y[:, s, t])
                            last.then_inc(*dve.does(f"st{b}{s}"))
                        for s in range(2):
                            eng.wait_ge(*dve.did(i, f"st{b}{s}"))
                            nc.vector.memset(carrier[:, s:s + 1], 0.0).then_inc(*dve.does(f"cr{b}{s}"))
                            for t in range(4):
                                last = nc.vector.bn_aggr(ag[:, s, t], st[:, s, t])
                            last.then_inc(*dve.does(f"ag{b}{s}"))
                        for s in range(2):
                            eng.wait_ge(*dve.did(i, f"ag{b}{s}"))
                            nc.vector.tensor_scalar(ve[:, s], ag[:, s, :, 1], 1e-5, None, ALU.add).then_inc(*dve.does(f"ve{b}{s}"))
                        for s in range(2):
                            eng.wait_ge(*pool.did(i, f"rs{b}{s}"))
                            for t in range(4):
                                last = nc.vector.tensor_scalar(z[:, s, t], y[:, s, t], ag[:, s, t, 0:1], rs[:, s, t:t + 1], ALU.subtract, ALU.mult)
                            last.then_inc(*dve.does(f"z{b}{s}"))
                        for s in range(2):
                            eng.wait_ge(*pe.did(i, f"back{b}{s}"))
                            nc.vector.scalar_tensor_tensor(h[:, s], back[s][:], biasT[:, b:b + 1], h[:, s], ALU.add, ALU.add).then_inc(*dve.does(f"h{b}{s}"))
                    for s in range(2):
                        eng.wait_ge(*dve.did(i, f"h{N - 1}{s}"))
                        nc.vector.tensor_tensor(at_group(XT, i * 2 + s), at_group(XT, i * 2 + s), h[:, s], ALU.add).then_inc(*dve.does(f"out{s}"))
                tiles(eng, GROUPS // 2, 1, body)

            @block.gpsimd
            def _(eng):
                nc.gpsimd.memset(half[:], -0.5).then_inc(half_set, 1)
                eng.wait_ge(half_set, 1)
                def body(i, _, again):
                    for b in range(N):
                        for s in range(2):
                            eng.wait_ge(*dve.did(i, f"ve{b}{s}"))
                            nc.gpsimd.tensor_tensor(rs[:, s], ve[:, s], half[:], ALU.pow).then_inc(*pool.does(f"rs{b}{s}"))
                tiles(eng, GROUPS // 2, 1, body)

AH, AD = 16, 8
AN = BATCH * AH
PARTS = 3
STACK = PARTS * PARTS * AD
QT = SEQ // P
SHIFT = 96
VW = AD + 1

def attn_project(nc, name, XN, Vh, q_dram, k_dram, w, wv, cos, sin):
    with ExitStack() as stack:
        m = Space(nc, name, stack)
        xs = m.sb("xs", [P, GRP])
        a = m.sb("a", [P, 2, GRP])
        b = m.sb("b", [P, 2, GRP])
        part = m.sb("part", [P, 2, PARTS, GRP], BF16)
        banks = [m.ps(f"w{k}") for k in range(4)]
        vb = m.ps("vb")
        pe = Steps(m.sem("pe"), "w0 w1 w2 w3 v")
        act = Steps(m.sem("act"), "xs v " + " ".join(f"c{p}{k}" for p in range(PARTS) for k in range(2)))
        dve = Steps(m.sem("dve"), "c0 s0 c1 s1")
        pool = Steps(m.sem("pool"), "r0 r1 d10 d11 d20 d21")
        ones_set, stored = m.sem("ones"), m.sem("stored")
        vh = Vh[:].rearrange("p (b h t e) -> p b h t e", b=BATCH, h=AH, e=VW)

        def both(eng, body):
            body(0, 0, False)
            body(0, 1, True)
            with eng.Fori(1, BATCH) as seq:
                body(seq, 0, True)
                body(seq, 1, True)

        with nc.Block() as block:
            @block.tensor
            def _(eng):
                def body(seq, s, again):
                    g = seq * 2 + s
                    for k in range(4):
                        if again:
                            eng.wait_ge(*dve.did(g - 1, f"{'cs'[k % 2]}{k // 2}"))
                        nc.tensor.matmul(banks[k][:], w[k][:], at_group(XN, g), start=True, stop=True).then_inc(*pe.does(f"w{k}"))
                    eng.wait_ge(*act.did(g, "xs"))
                    if again:
                        eng.wait_ge(*act.did(g - 1, "v"))
                    for t in range(4):
                        last = nc.tensor.matmul(vb[:, t * P:(t + 1) * P], xs[:, t * P:(t + 1) * P], wv[:], start=True, stop=True)
                    last.then_inc(*pe.does("v"))
                both(eng, body)

            @block.scalar
            def _(eng):
                eng.wait_ge(ones_set, 1)
                def body(seq, s, again):
                    g = seq * 2 + s
                    if again:
                        eng.wait_ge(*pe.did(g - 1, "v"))
                    nc.scalar.activation(xs[:], at_group(XN, g), ACT.Copy).then_inc(*act.does("xs"))
                    eng.wait_ge(*pe.did(g, "v"))
                    for t in range(4):
                        last = nc.scalar.activation(vh[:, bass.ds(seq, 1), :, 4 * s + t, 0:AD].rearrange("p o h e -> p (o h) e"),
                                                    vb[:, t * P:(t + 1) * P].rearrange("p (h e) -> p h e", e=AD), ACT.Copy)
                    last.then_inc(*act.does("v"))
                    for p in range(PARTS):
                        for k in range(2):
                            eng.wait_ge(*pool.did(g, f"d{p}{k}" if p else f"r{k}"))
                            if again:
                                eng.wait_ge(stored, g * (5 + 3) * 16)
                            nc.scalar.activation(part[:, k, p], a[:, k], ACT.Copy).then_inc(*act.does(f"c{p}{k}"))
                both(eng, body)

            @block.vector
            def _(eng):
                def body(seq, s, again):
                    g = seq * 2 + s
                    for k in range(2):
                        if again:
                            eng.wait_ge(*act.did(g - 1, f"c{PARTS - 1}{k}"))
                        for n, dst, table in ((0, a, cos), (1, b, sin)):
                            eng.wait_ge(*pe.did(g, f"w{2 * k + n}"))
                            nc.vector.tensor_tensor(dst[:, k], banks[2 * k + n][:], table[:, s * GRP:(s + 1) * GRP], ALU.mult).then_inc(*dve.does(f"{'cs'[n]}{k}"))
                both(eng, body)

            @block.gpsimd
            def _(eng):
                nc.gpsimd.memset(Vh[:], 1.0).then_inc(ones_set, 1)
                def body(seq, s, again):
                    g = seq * 2 + s
                    for k in range(2):
                        eng.wait_ge(*dve.did(g, f"s{k}"))
                        nc.gpsimd.tensor_tensor(a[:, k], a[:, k], b[:, k], ALU.add).then_inc(*pool.does(f"r{k}"))
                    for p in range(1, PARTS):
                        for k in range(2):
                            eng.wait_ge(*act.did(g, f"c{p - 1}{k}"))
                            nc.gpsimd.tensor_tensor(a[:, k], a[:, k], part[:, k, p - 1], ALU.subtract).then_inc(*pool.does(f"d{p}{k}"))
                both(eng, body)

            @block.sync
            def _(eng):
                def body(seq, s, again):
                    g = seq * 2 + s
                    for p in range(PARTS):
                        for k, dram in enumerate((q_dram, k_dram)):
                            eng.wait_ge(*act.did(g, f"c{p}{k}"))
                            for row in [p] + ([p + PARTS] if k and p < 2 else []):
                                dst = dram.rearrange("(b h) r d t -> b h r d t", h=AH)[bass.ds(seq, 1), :, row, :, s * GRP:(s + 1) * GRP]
                                eng.dma_start(dst.rearrange("o h d t -> (o h) d t"), part[:, k, p]).then_inc(stored, 16)
                both(eng, body)
                eng.wait_ge(stored, GROUPS * 8 * 16)

def attn_heads(nc, name, Vh, ctx_dram, sum_dram, q_dram, k_dram, eye16):
    BANKS = 2
    UNITS = 2 * QT
    STEPS = 3
    PLAN = [1] * UNITS + [0] * 6 + [1, 0]
    with ExitStack() as stack:
        m = Space(nc, name, stack)
        qs = [m.sb(f"qs{s}", [P, SEQ], BF16) for s in range(2)]
        ks = [m.sb(f"ks{s}", [P, SEQ], BF16) for s in range(2)]
        vs = [m.sb(f"vs{s}", [P, QT * VW]) for s in range(2)]
        pt = m.sb("pt", [P, 2, SEQ])
        mx = m.sb("mx", [P, QT, 2])
        nm = m.sb("nm", [P, QT])
        d1 = m.sb("d1", [P, QT])
        d2 = m.sb("d2", [P, QT])
        mp = m.sb("mp", [P, QT, PARTS], BF16)
        out = m.sb("out", [VW, 2, 2, GRP])
        first = [m.ps(f"first{k}") for k in range(BANKS)]
        second = [m.ps(f"second{k}", [P, 2, GRP]) for k in range(2)]
        O = m.ps("O", [P, 2, GRP])
        loaded = [m.sem(f"loaded{s}") for s in range(2)]
        stored = [m.sem(f"stored{s}") for s in range(2)]
        ready = m.sem("ready")
        a_pe = Steps(m.sem("ape"), " ".join(f"n{u}" for u in range(UNITS)) + " row0 row1")
        b_pe = Steps(m.sem("bpe"), "s0 " + " ".join(f"s{t} v{t - 1}" for t in range(1, QT)) + f" v{QT - 1}")
        a_dve = Steps(m.sem("adve"), " ".join(f"m{u}" for u in range(UNITS)) + " nm p1 d1 p2 d2 p3")
        b_dve = Steps(m.sem("bdve"), "out")
        a_act = Steps(m.sem("aact"), "row0 row1")
        b_act = Steps(m.sem("bact"), " ".join(f"e{t}" for t in range(QT)))
        pool = Steps(m.sem("pool"), "v")
        LOADS = 6

        def run(eng, maxima, weights):
            def turn(n, s, wt, mx_, again2, again3, again4=False):
                units = maxima(n, s, again2) if mx_ else iter(())

                def step(i):
                    todo = PLAN[i] if i is not None else UNITS + 2
                    for _ in range(todo):
                        if next(units, None) is None:
                            return
                if wt:
                    weights(n - 1, 1 - s, again3, again4, step)
                else:
                    step(None)
            turn(0, 0, False, True, False, False)
            turn(1, 1, True, True, False, False)
            turn(2, 0, True, True, True, True)
            with eng.Fori(0, (AN - 4) // 2) as k:
                turn(k * 2 + 3, 1, True, True, True, True, True)
                turn(k * 2 + 4, 0, True, True, True, True, True)
            turn(AN - 1, 1, True, True, True, True, True)
            turn(AN, 0, True, False, True, True, True)

        with nc.Block() as block:
            @block.sync
            def _(eng):
                eng.wait_ge(ready, 6)

                def load(n, s):
                    for r in range(PARTS):
                        rows = slice(r * 24, r * 24 + 24)
                        eng.dma_start(qs[s][rows, :], q_dram[bass.ds(n, 1)].rearrange("o r d t -> (o r d) t")).then_inc(loaded[s], 16)
                        eng.dma_start(ks[s][rows, :], k_dram[bass.ds(n, 1), r:r + 3].rearrange("o r d t -> (o r d) t")).then_inc(loaded[s], 16)

                def store(n, s):
                    eng.wait_ge(*b_dve.did(n, "out"))
                    eng.dma_start(ctx_dram[bass.ds(n, 1)].rearrange("o d t -> (o d) t"), out[0:AD, s].rearrange("p a t -> p (a t)")).then_inc(stored[s], 16)
                    eng.dma_start(sum_dram[bass.ds(n, 1)], out[AD:VW, s].rearrange("p a t -> p (a t)")).then_inc(stored[s], 16)
                for s in range(2):
                    load(s, s)

                def body(n, s):
                    eng.wait_ge(*b_pe.did(n, f"s{QT - 1}"))
                    load(n + 2, s)
                    store(n, s)
                with eng.Fori(0, AN // 2 - 1) as k:
                    for s in range(2):
                        body(k * 2 + s, s)
                for s in range(2):
                    store(AN - 2 + s, s)
                for s in range(2):
                    eng.wait_ge(stored[s], AN // 2 * 32)

            @block.gpsimd
            def _(eng):
                fills = [(t[lo:hi, :], x) for s in range(2) for t, lo, hi, x in ((qs[s], 64, P, 0.0), (ks[s], 64, SHIFT, 0.0), (ks[s], SHIFT, P, 1.0))]
                for n, (rows, x) in enumerate(fills):
                    nc.gpsimd.memset(rows, x).then_inc(ready, 1)
                    eng.wait_ge(ready, n + 1)

                def values(n, s, again):
                    if again:
                        eng.wait_ge(*b_pe.did(n - 2, f"v{QT - 1}"))
                    nc.gpsimd.tensor_copy(vs[s][:], Vh[:, bass.ds(n * (QT * VW), QT * VW)]).then_inc(*pool.does("v"))
                tiles(eng, AN, 2, values)

            @block.tensor
            def _(eng):
                def maxima(n, s, again):
                    eng.wait_ge(loaded[s], (n // 2 + 1) * LOADS * 16 if isinstance(n, int) else (n - s) * (LOADS * 8) + LOADS * 16)
                    for u in range(UNITS):
                        k = u % BANKS
                        if u >= BANKS:
                            eng.wait_ge(*a_dve.did(n, f"m{u - BANKS}"))
                        elif again or (isinstance(n, int) and n):
                            eng.wait_ge(*a_act.did(n - 1, f"row{k}"))
                        qt, half = divmod(u, 2)
                        nc.tensor.matmul(first[k][:], qs[s][0:STACK, qt * P:(qt + 1) * P], ks[s][0:STACK, half * GRP:(half + 1) * GRP],
                                         start=True, stop=True).then_inc(*a_pe.does(f"n{u}"))
                        yield True
                    eng.wait_ge(*a_dve.did(n, "p3"))
                    for half in range(2):
                        for t in range(4):
                            last = nc.tensor.matmul(first[half][SHIFT:SHIFT + PARTS, t * P:(t + 1) * P], mp[:, 4 * half + t, :], eye16[:],
                                                    start=True, stop=True)
                        last.then_inc(*a_pe.does(f"row{half}"))
                    yield True

                def weights(n, s, again, again2, step):
                    eng.wait_ge(*a_act.did(n, "row1"))

                    def values(t):
                        eng.wait_ge(*b_act.did(n, f"e{t}"))
                        if t == 0:
                            eng.wait_ge(*pool.did(n, "v"))
                            if again:
                                eng.wait_ge(*b_dve.did(n - 1, "out"))
                        for half in range(2):
                            if half:
                                step(t * STEPS + 2)
                            last = nc.tensor.matmul(O[0:VW, half], vs[s][:, t * VW:(t + 1) * VW], pt[:, t % 2, half * GRP:(half + 1) * GRP],
                                                    start=(t == 0), stop=(t == QT - 1))
                        last.then_inc(*b_pe.does(f"v{t}"))
                    for t in range(QT):
                        step(t * STEPS)
                        if t >= 2:
                            eng.wait_ge(*b_act.did(n, f"e{t - 2}"))
                        elif again:
                            eng.wait_ge(*b_act.did(n - 1, f"e{QT - 2 + t}"))
                        for half in range(2):
                            last = nc.tensor.matmul(second[t % 2][:, half], ks[s][0:SHIFT + PARTS, t * P:(t + 1) * P], qs[s][0:SHIFT + PARTS, half * GRP:(half + 1) * GRP],
                                                    start=True, stop=True)
                        last.then_inc(*b_pe.does(f"s{t}"))
                        step(t * STEPS + 1)
                        if t:
                            values(t - 1)
                    values(QT - 1)
                    step(None)
                run(eng, maxima, weights)

            def other_steps(step, at):
                for t in range(QT):
                    step(t * STEPS)
                    at(t)
                    step(t * STEPS + 1)
                    if t:
                        step(t * STEPS - 1)
                step(QT * STEPS - 1)

            @block.scalar
            def _(eng):
                nc.scalar.preload_act_table_set("exp_and_others")
                eng.wait_ge(ready, 6)
                def maxima(n, s, again):
                    for u in range(UNITS):
                        yield True
                    for half in range(2):
                        eng.wait_ge(*a_pe.did(n, f"row{half}"))
                        if again:
                            eng.wait_ge(*b_pe.did(n - 2, f"s{QT - 1}"))
                        nc.scalar.activation(qs[s][SHIFT:SHIFT + PARTS, half * GRP:(half + 1) * GRP], first[half][SHIFT:SHIFT + PARTS, :],
                                             ACT.Copy).then_inc(*a_act.does(f"row{half}"))
                    yield True

                def weights(n, s, again, again2, step):
                    def exps(t):
                        eng.wait_ge(*b_pe.did(n, f"s{t}"))
                        if t >= 2:
                            eng.wait_ge(*b_pe.did(n, f"v{t - 2}"))
                        elif again:
                            eng.wait_ge(*b_pe.did(n - 1, f"v{QT - 2 + t}"))
                        nc.scalar.activation(pt[:, t % 2].rearrange("p (a b) -> p a b", a=2), second[t % 2][:], ACT.Exp, scale=float(AD) ** -0.5).then_inc(*b_act.does(f"e{t}"))
                    other_steps(step, exps)
                    step(None)
                run(eng, maxima, weights)

            @block.vector
            def _(eng):
                def maxima(n, s, again):
                    for u in range(UNITS):
                        eng.wait_ge(*a_pe.did(n, f"n{u}"))
                        nc.vector.tensor_reduce(mx[:, u // 2, u % 2:u % 2 + 1], first[u % BANKS][:], AX, ALU.max).then_inc(*a_dve.does(f"m{u}"))
                        yield True

                    def small(ins, name_):
                        ins.then_inc(*a_dve.does(name_))
                        eng.wait_ge(*a_dve.did(n, name_))
                    eng.wait_ge(*a_dve.did(n, f"m{UNITS - 1}"))
                    small(nc.vector.tensor_reduce(nm[:], mx[:], AX, ALU.max), "nm")
                    if again or (isinstance(n, int) and n):
                        eng.wait_ge(*a_pe.did(n - 1, "row1"))
                    small(nc.vector.tensor_scalar(mp[:, :, 0], nm[:], -1.0, None, ALU.mult), "p1")
                    small(nc.vector.scalar_tensor_tensor(d1[:], nm[:], -1.0, mp[:, :, 0], ALU.mult, ALU.subtract), "d1")
                    small(nc.vector.tensor_copy(mp[:, :, 1], d1[:]), "p2")
                    small(nc.vector.tensor_tensor(d2[:], d1[:], mp[:, :, 1], ALU.subtract), "d2")
                    small(nc.vector.tensor_copy(mp[:, :, 2], d2[:]), "p3")
                    yield True

                def weights(n, s, again, again2, step):
                    step(None)
                    eng.wait_ge(*b_pe.did(n, f"v{QT - 1}"))
                    if again2:
                        eng.wait_ge(stored[s], (n - s) * 16)
                    nc.vector.tensor_copy(out[:, s], O[0:VW]).then_inc(*b_dve.does("out"))
                run(eng, maxima, weights)

def attn_output(nc, name, ctx_dram, sum_dram, rec_dram, XT, w_out, head_rows):
    with ExitStack() as stack:
        m = Space(nc, name, stack)
        ctx = m.sb("ctx", [P, TOK])
        total, inverse = m.sb("total", [P, AN * SEQ // P]), m.sb("inverse", [P, AN * SEQ // P])
        rec = m.sb("rec", [AH, TOK])
        spread = [m.ps(f"spread{s}") for s in range(2)]
        proj = [m.ps(f"proj{s}") for s in range(2)]
        pe, dve = Steps(m.sem("pe"), "spread proj"), Steps(m.sem("dve"), "ctx x")
        sums_in, rec_out, rec_in, ctx_in, inverted = m.sem("sums_in"), m.sem("rec_out"), m.sem("rec_in"), m.sem("ctx_in"), m.sem("inverted")
        by_row = "n (a t) -> (n a) t"
        with nc.Block() as block:
            @block.sync
            def _(eng):
                eng.dma_start(total[:], sum_dram.rearrange(by_row, a=2)).then_inc(sums_in, 16)
                for b in range(BATCH):
                    eng.dma_start(ctx[:, b * SEQ:(b + 1) * SEQ], ctx_dram[b * AH:(b + 1) * AH].rearrange("h d t -> (h d) t")).then_inc(ctx_in, 16)
                eng.wait_ge(inverted, 1)
                eng.dma_start(rec_dram.rearrange(by_row, a=2), inverse[:]).then_inc(rec_out, 16)
                eng.wait_ge(rec_out, 16)
                eng.dma_start(rec[:].rearrange("h (b t) -> h b t", b=BATCH), rec_dram.rearrange("(b h) t -> h b t", b=BATCH)).then_inc(rec_in, 16)

            @block.tensor
            def _(eng):
                eng.wait_ge(rec_in, 16)

                def body(g, s, again):
                    if again:
                        eng.wait_ge(*dve.did(g - 2, "ctx"))
                    nc.tensor.matmul(spread[s][:], head_rows[0:AH, :], rec[:, bass.ds(g * GRP, GRP)], start=True, stop=True).then_inc(*pe.does("spread"))
                    eng.wait_ge(*dve.did(g, "ctx"))
                    if again:
                        eng.wait_ge(*dve.did(g - 2, "x"))
                    nc.tensor.matmul(proj[s][:], w_out[:], at_group(ctx, g), start=True, stop=True).then_inc(*pe.does("proj"))
                tiles(eng, GROUPS, 2, body)

            @block.vector
            def _(eng):
                eng.wait_ge(sums_in, 16)
                nc.vector.reciprocal(inverse[:], total[:]).then_inc(inverted, 1)
                eng.wait_ge(ctx_in, BATCH * 16)

                def body(g, s, again):
                    eng.wait_ge(*pe.did(g, "spread"))
                    nc.vector.tensor_tensor(at_group(ctx, g), at_group(ctx, g), spread[s][:], ALU.mult).then_inc(*dve.does("ctx"))
                    eng.wait_ge(*pe.did(g, "proj"))
                    nc.vector.tensor_tensor(at_group(XT, g), at_group(XT, g), proj[s][:], ALU.add).then_inc(*dve.does("x"))
                tiles(eng, GROUPS, 2, body)

def router_small(nc, name, XN, RW, w_router, bias_row, iota, E_):
    with ExitStack() as stack:
        m = Space(nc, name, stack)
        xs = m.sb("xs", [P, 2, GRP])
        lg = m.sb("lg", [P, 2, 4, E_])
        top = m.sb("top", [P, CHUNKS, 8])
        top4 = m.sb("top4", [P, 2, 4, 8])
        idx4 = m.sb("idx4", [P, 2, 4, 8], U32)
        fi8 = m.sb("fi8", [P, CHUNKS, 8])
        carrier = m.sb("carrier", [P, 2])
        fi = m.sb("fi", [P, 2, CHUNKS])
        ex = m.sb("ex", [P, CHUNKS])
        den = m.sb("den", [P, CHUNKS])
        wt = m.sb("wt", [P, 2, CHUNKS])
        hot = m.sb("hot", [P, 2, CHUNKS, E_])
        lp = [m.ps(f"lp{s}") for s in range(2)]
        pe, act = Steps(m.sem("pe"), "lg"), Steps(m.sem("act"), "xs")
        dve = Steps(m.sem("dve"), "lg cr0 max cr1 at top idx")
        end = Steps(m.sem("end"), "f0 f1 d den rec w1 h0 h1 s0 s1 rw")
        exped = m.sem("exped")
        with nc.Block() as block:
            @block.scalar
            def _(eng):
                def body(g, s, again):
                    if again:
                        eng.wait_ge(*pe.did(g - 2, "lg"))
                    nc.scalar.activation(xs[:, s], at_group(XN, g), ACT.Copy).then_inc(*act.does("xs"))
                tiles(eng, GROUPS, 2, body)
                eng.wait_ge(*end.did(0, "d"))
                nc.scalar.activation(ex[:], ex[:], ACT.Exp).then_inc(exped, 1)

            @block.tensor
            def _(eng):
                def body(g, s, again):
                    eng.wait_ge(*act.did(g, "xs"))
                    if again:
                        eng.wait_ge(*dve.did(g - 2, "lg"))
                    for t in range(4):
                        last = nc.tensor.matmul(lp[s][:, t * E_:(t + 1) * E_], xs[:, s, t * P:(t + 1) * P], w_router[:], start=True, stop=True)
                    last.then_inc(*pe.does("lg"))
                tiles(eng, GROUPS, 2, body)

            @block.vector
            def _(eng):
                def body(g, s, again):
                    eng.wait_ge(*pe.did(g, "lg"))
                    src = lp[s][:, 0:4 * E_].rearrange("p (t e) -> p t e", e=E_)
                    nc.vector.tensor_tensor(lg[:, s], src, over_heads(bias_row[:], 4), ALU.add).then_inc(*dve.does("lg"))
                    eng.wait_ge(*dve.did(g, "lg"))
                    nc.vector.memset(carrier[:, 0:1], 0.0).then_inc(*dve.does("cr0"))
                    for t in range(4):
                        last = nc.vector.max(top4[:, s, t], lg[:, s, t])
                    last.then_inc(*dve.does("max"))
                    eng.wait_ge(*dve.did(g, "max"))
                    nc.vector.memset(carrier[:, 1:2], 0.0).then_inc(*dve.does("cr1"))
                    for t in range(4):
                        last = nc.vector.max_index(idx4[:, s, t], top4[:, s, t], lg[:, s, t])
                    last.then_inc(*dve.does("at"))
                    nc.vector.tensor_copy(top[:, bass.ds(g * 4, 4), :], top4[:, s]).then_inc(*dve.does("top"))
                    eng.wait_ge(*dve.did(g, "at"))
                    nc.vector.tensor_copy(fi8[:, bass.ds(g * 4, 4), :], idx4[:, s]).then_inc(*dve.does("idx"))
                tiles(eng, GROUPS, 2, body)

                def step(ins, name_):
                    ins.then_inc(*end.does(name_))
                    eng.wait_ge(*end.did(0, name_))
                eng.wait_ge(*dve.did(GROUPS - 1, "idx"))
                for k in range(2):
                    step(nc.vector.tensor_copy(fi[:, k], fi8[:, :, k]), f"f{k}")
                step(nc.vector.tensor_tensor(ex[:], top[:, :, 1], top[:, :, 0], ALU.subtract), "d")
                eng.wait_ge(exped, 1)
                step(nc.vector.tensor_scalar(den[:], ex[:], 1.0, None, ALU.add), "den")
                step(nc.vector.reciprocal(wt[:, 0], den[:]), "rec")
                step(nc.vector.tensor_tensor(wt[:, 1], wt[:, 0], ex[:], ALU.mult), "w1")
                for k in range(2):
                    step(nc.vector.tensor_tensor(hot[:, k], iota[:, 0:E_].unsqueeze(1).to_broadcast([P, CHUNKS, E_]), along(fi[:, k], E_), ALU.is_equal), f"h{k}")
                for k in range(2):
                    step(nc.vector.tensor_tensor(hot[:, k], hot[:, k], along(wt[:, k], E_), ALU.mult), f"s{k}")
                step(nc.vector.tensor_tensor(RW[:].rearrange("p (c e) -> p c e", e=E_), hot[:, 0], hot[:, 1], ALU.add), "rw")

def dense_moe(nc, name, XN, XT, RW, W1, B1, W2, b2, gammaT, betaT, eye, E_):
    F = 4
    with ExitStack() as stack:
        m = Space(nc, name, stack)
        xs = m.sb("xs", [P, GRP])
        rw = m.sb("rw", [P, 4, E_])
        rwT = m.sb("rwT", [E_, GRP])
        hid = m.sb("hid", [P, 2, F, GRP])
        acc = m.sb("acc", [P, 4, P])
        z = m.sb("z", [P, 4, P])
        zT = m.sb("zT", [P, GRP])
        st, ag, rs, ve = m.sb("st", [P, 4, 6]), m.sb("ag", [P, 4, 2]), m.sb("rs", [P, 4]), m.sb("ve", [P, 4])
        half, carrier = m.sb("half", [P, 4]), m.sb("carrier", [P, 1])
        up = [m.ps(f"up{c}") for c in range(F)]
        down = [m.ps(f"down{k}") for k in range(2)]
        side = m.ps("side")
        small = m.ps("small")
        pe = Steps(m.sem("pe"), "rwT init " + " ".join(f"up{e}{c}" for e in range(1) for c in range(F)) + " " +
                   " ".join(" ".join(f"up{e + 1}{c}" for c in range(F) if e + 1 < E_) + f" down{e}" for e in range(E_)) + " zT")
        act = Steps(m.sem("act"), "xs rw rwT init " + " ".join(f"hid{e}{c}" for e in range(E_) for c in range(F)) + " zT")
        dve = Steps(m.sem("dve"), " ".join(f"acc{e}" for e in range(E_)) + " st cr ag ve z out")
        pool = Steps(m.sem("pool"), "rs")
        half_set = m.sem("half_set")

        def tiles4(t):
            return t[:].rearrange("p (t n) -> p t n", n=P)
        with nc.Block() as block:
            @block.tensor
            def _(eng):
                def body(g, _, again):
                    def prev(who, step):
                        if again:
                            eng.wait_ge(*who.did(g - 1, step))
                    eng.wait_ge(*act.did(g, "rw"))
                    prev(act, "zT")
                    prev(act, "rwT")
                    for t in range(4):
                        last = nc.tensor.transpose(small[0:E_, t * P:(t + 1) * P], rw[:, t], eye[:])
                    last.then_inc(*pe.does("rwT"))
                    eng.wait_ge(*act.did(g, "rwT"))
                    for t in range(4):
                        nc.tensor.matmul(side[:, t * P:(t + 1) * P], xs[:, t * P:(t + 1) * P], eye[:], start=True, stop=False)
                        last = nc.tensor.matmul(side[:, t * P:(t + 1) * P], rwT[:, t * P:(t + 1) * P], b2[:], start=False, stop=True)
                    last.then_inc(*pe.does("init"))

                    def hidden(e):
                        for c in range(F):
                            if e:
                                eng.wait_ge(*act.did(g, f"hid{e - 1}{c}"))
                            elif again:
                                eng.wait_ge(*act.did(g - 1, f"hid{E_ - 1}{c}"))
                            nc.tensor.matmul(up[c][:], W1[:, e, c * P:(c + 1) * P], xs[:], start=True, stop=True).then_inc(*pe.does(f"up{e}{c}"))
                    hidden(0)
                    for e in range(E_):
                        if e + 1 < E_:
                            hidden(e + 1)
                        if e >= 2:
                            eng.wait_ge(*dve.did(g, f"acc{e - 2}"))
                        else:
                            prev(dve, f"acc{E_ - 2 + e}")
                        for t in range(4):
                            for c in range(F):
                                eng.wait_ge(*act.did(g, f"hid{e}{c}")) if t == 0 else None
                                last = nc.tensor.matmul(down[e % 2][:, t * P:(t + 1) * P], hid[:, e % 2, c, t * P:(t + 1) * P], W2[:, e, c], start=(c == 0), stop=(c == F - 1))
                        last.then_inc(*pe.does(f"down{e}"))
                    eng.wait_ge(*dve.did(g, "z"))
                    for t in range(4):
                        last = nc.tensor.transpose(side[:, t * P:(t + 1) * P], z[:, t], eye[:])
                    last.then_inc(*pe.does("zT"))
                tiles(eng, GROUPS, 1, body)

            @block.scalar
            def _(eng):
                def body(g, _, again):
                    def prev(who, step):
                        if again:
                            eng.wait_ge(*who.did(g - 1, step))
                    prev(pe, f"up{E_ - 1}{F - 1}")
                    nc.scalar.activation(xs[:], at_group(XN, g), ACT.Copy).then_inc(*act.does("xs"))
                    prev(dve, f"acc{E_ - 1}")
                    nc.scalar.activation(rw[:].rearrange("p t e -> p (t e)"), RW[:, bass.ds(g * (4 * E_), 4 * E_)], ACT.Copy).then_inc(*act.does("rw"))
                    eng.wait_ge(*pe.did(g, "rwT"))
                    nc.scalar.activation(rwT[:], small[0:E_, :], ACT.Copy).then_inc(*act.does("rwT"))
                    eng.wait_ge(*pe.did(g, "init"))
                    prev(dve, "z")
                    nc.scalar.activation(acc[:], tiles4(side), ACT.Copy).then_inc(*act.does("init"))
                    for e in range(E_):
                        for c in range(F):
                            eng.wait_ge(*pe.did(g, f"up{e}{c}"))
                            if c == 0:
                                if e >= 2:
                                    eng.wait_ge(*pe.did(g, f"down{e - 2}"))
                                else:
                                    prev(pe, f"down{E_ - 2 + e}")
                            nc.scalar.activation(hid[:, e % 2, c], up[c][:], ACT.Relu, bias=B1[:, e, c:c + 1]).then_inc(*act.does(f"hid{e}{c}"))
                    eng.wait_ge(*pe.did(g, "zT"))
                    prev(dve, "out")
                    nc.scalar.activation(zT[:], side[:], ACT.Identity, scale=gammaT[:, 0:1], bias=betaT[:, 0:1]).then_inc(*act.does("zT"))
                tiles(eng, GROUPS, 1, body)

            @block.vector
            def _(eng):
                def body(g, _, again):
                    for e in range(E_):
                        eng.wait_ge(*pe.did(g, f"down{e}"))
                        eng.wait_ge(*act.did(g, "init")) if e == 0 else eng.wait_ge(*dve.did(g, f"acc{e - 1}"))
                        for t in range(4):
                            last = nc.vector.scalar_tensor_tensor(acc[:, t], tiles4(down[e % 2])[:, t], rw[:, t, e:e + 1], acc[:, t], ALU.mult, ALU.add)
                        last.then_inc(*dve.does(f"acc{e}"))
                    eng.wait_ge(*dve.did(g, f"acc{E_ - 1}"))
                    for t in range(4):
                        last = nc.vector.bn_stats(st[:, t], acc[:, t])
                    last.then_inc(*dve.does("st"))
                    eng.wait_ge(*dve.did(g, "st"))
                    nc.vector.memset(carrier[:], 0.0).then_inc(*dve.does("cr"))
                    for t in range(4):
                        last = nc.vector.bn_aggr(ag[:, t], st[:, t])
                    last.then_inc(*dve.does("ag"))
                    eng.wait_ge(*dve.did(g, "ag"))
                    nc.vector.tensor_scalar(ve[:], ag[:, :, 1], 1e-5, None, ALU.add).then_inc(*dve.does("ve"))
                    eng.wait_ge(*pool.did(g, "rs"))
                    for t in range(4):
                        last = nc.vector.tensor_scalar(z[:, t], acc[:, t], ag[:, t, 0:1], rs[:, t:t + 1], ALU.subtract, ALU.mult)
                    last.then_inc(*dve.does("z"))
                    eng.wait_ge(*act.did(g, "zT"))
                    nc.vector.tensor_tensor(at_group(XT, g), at_group(XT, g), zT[:], ALU.add).then_inc(*dve.does("out"))
                tiles(eng, GROUPS, 1, body)

            @block.gpsimd
            def _(eng):
                nc.gpsimd.memset(half[:], -0.5).then_inc(half_set, 1)
                eng.wait_ge(half_set, 1)
                def body(g, _, again):
                    eng.wait_ge(*dve.did(g, "ve"))
                    nc.gpsimd.tensor_tensor(rs[:], ve[:], half[:], ALU.pow).then_inc(*pool.does("rs"))
                tiles(eng, GROUPS, 1, body)

GH, GD = 16, 8
STATES = GH * GD * GD
RT = STATES // P

def gla_gates(nc, name, XN, GT, w1, w2, bias):
    with ExitStack() as stack:
        m = Space(nc, name, stack)
        R = w1.shape[1]
        lo = m.sb("lo", [R, 2, GRP])
        z, y, u, d, lu, c = (m.sb(n, [P, 2, GRP]) for n in "z y u d lu c".split())
        lp = [m.ps(f"lp{s}") for s in range(2)]
        zp = [m.ps(f"zp{s}") for s in range(2)]
        pe, act = Steps(m.sem("pe"), "lo z"), Steps(m.sem("act"), "lo y lu gate")
        dve = Steps(m.sem("dve"), "z na u d m ls")
        with nc.Block() as block:
            @block.tensor
            def _(eng):
                def body(g, s, again):
                    if again:
                        eng.wait_ge(*act.did(g - 2, "lo"))
                    nc.tensor.matmul(lp[s][0:R, :], w1[:], at_group(XN, g), start=True, stop=True).then_inc(*pe.does("lo"))
                    eng.wait_ge(*act.did(g, "lo"))
                    if again:
                        eng.wait_ge(*dve.did(g - 2, "z"))
                    nc.tensor.matmul(zp[s][:], w2[:], lo[:, s], start=True, stop=True).then_inc(*pe.does("z"))
                tiles(eng, GROUPS, 2, body)

            @block.scalar
            def _(eng):
                nc.scalar.preload_act_table_set("natural_log_exp_and_others")
                def body(g, s, again):
                    eng.wait_ge(*pe.did(g, "lo"))
                    if again:
                        eng.wait_ge(*pe.did(g - 2, "z"))
                    nc.scalar.activation(lo[:, s], lp[s][0:R, :], ACT.Copy).then_inc(*act.does("lo"))
                    eng.wait_ge(*dve.did(g, "na"))
                    nc.scalar.activation(y[:, s], y[:, s], ACT.Exp).then_inc(*act.does("y"))
                    eng.wait_ge(*dve.did(g, "u"))
                    nc.scalar.activation(lu[:, s], u[:, s], ACT.Ln).then_inc(*act.does("lu"))
                    eng.wait_ge(*dve.did(g, "ls"))
                    nc.scalar.activation(at_group(GT, g), d[:, s], ACT.Exp, scale=1.0 / 16).then_inc(*act.does("gate"))
                tiles(eng, GROUPS, 2, body)

            @block.vector
            def _(eng):
                def body(g, s, again):
                    def chain(name_):
                        eng.wait_ge(*dve.did(g, name_))
                    eng.wait_ge(*pe.did(g, "z"))
                    nc.vector.tensor_scalar(z[:, s], zp[s][:], bias[:, 0:1], None, ALU.add).then_inc(*dve.does("z"))
                    chain("z")
                    nc.vector.scalar_tensor_tensor(y[:, s], z[:, s], -1.0, z[:, s], ALU.mult, ALU.min).then_inc(*dve.does("na"))
                    eng.wait_ge(*act.did(g, "y"))
                    nc.vector.tensor_scalar(u[:, s], y[:, s], 1.0, None, ALU.add).then_inc(*dve.does("u"))
                    chain("u")
                    if again:
                        eng.wait_ge(*act.did(g - 2, "gate"))
                    nc.vector.scalar_tensor_tensor(d[:, s], u[:, s], -1.0, y[:, s], ALU.add, ALU.subtract).then_inc(*dve.does("d"))
                    chain("d")
                    nc.vector.scalar_tensor_tensor(c[:, s], z[:, s], 0.0, d[:, s], ALU.min, ALU.add).then_inc(*dve.does("m"))
                    eng.wait_ge(*act.did(g, "lu"))
                    chain("m")
                    nc.vector.tensor_tensor(d[:, s], c[:, s], lu[:, s], ALU.subtract).then_inc(*dve.does("ls"))
                tiles(eng, GROUPS, 2, body)

def gla_states(nc, name, XN, GT, OT, wq, wk, wv, pick, fold):
    with ExitStack() as stack:
        m = Space(nc, name, stack)
        k_sb = m.sb("k", [P, 2, GRP])
        kv = m.sb("kv", [P, 2, GRP])
        st = m.sb("st", [P, 2, GRP])
        y = m.sb("y", [P, 2, GRP])
        carry = m.sb("carry", [P, RT])
        K, V, G, Q = (m.ps(n) for n in "KVGQ")
        out = [m.ps(f"out{s}") for s in range(2)]
        pe = Steps(m.sem("pe"), "K0 V0 G0 Q0 " + " ".join(f"K{r} V{r} G{r} Q{r} f{r - 1}" for r in range(1, RT)) + f" f{RT - 1}")
        act = Steps(m.sem("act"), " ".join(f"k{r}" for r in range(RT)) + " o")
        dve = Steps(m.sem("dve"), " ".join(f"kv{r} st{r} ca{r} y{r}" for r in range(RT)))

        def halves(eng, body):
            body(0, 0, False)
            body(0, 1, True)
            with eng.Fori(1, BATCH) as seq:
                body(seq, 0, True)
                body(seq, 1, True)

        with nc.Block() as block:
            @block.tensor
            def _(eng):
                def body(seq, s, again):
                    g = seq * 2 + s

                    def prev(who, kind, r):
                        if r:
                            eng.wait_ge(*who.did(g, f"{kind}{r - 1}"))
                        elif again:
                            eng.wait_ge(*who.did(g - 1, f"{kind}{RT - 1}"))

                    def fold_rows(r):
                        eng.wait_ge(*dve.did(g, f"y{r}"))
                        if r == 0 and not isinstance(seq, int):
                            eng.wait_ge(*act.did(g - 2, "o"))
                        nc.tensor.matmul(out[s][:], fold[:, r * P:(r + 1) * P], y[:, r % 2], start=(r == 0), stop=(r == RT - 1)).then_inc(*pe.does(f"f{r}"))
                    for r in range(RT):
                        for n, bk, w, src, who, kind in (("K", K, wk, XN, act, "k"), ("V", V, wv, XN, dve, "kv"), ("G", G, pick, GT, dve, "st"), ("Q", Q, wq, XN, dve, "y")):
                            prev(who, kind, r)
                            nc.tensor.matmul(bk[:], w[:, r * P:(r + 1) * P], at_group(src, g), start=True, stop=True).then_inc(*pe.does(f"{n}{r}"))
                        if r:
                            fold_rows(r - 1)
                    fold_rows(RT - 1)
                halves(eng, body)

            @block.scalar
            def _(eng):
                def body(seq, s, again):
                    g = seq * 2 + s
                    for r in range(RT):
                        eng.wait_ge(*pe.did(g, f"K{r}"))
                        if r >= 2:
                            eng.wait_ge(*dve.did(g, f"kv{r - 2}"))
                        elif again:
                            eng.wait_ge(*dve.did(g - 1, f"kv{RT - 2 + r}"))
                        nc.scalar.activation(k_sb[:, r % 2], K[:], ACT.Copy).then_inc(*act.does(f"k{r}"))
                    eng.wait_ge(*pe.did(g, f"f{RT - 1}"))
                    nc.scalar.activation(at_group(OT, g), out[s][:], ACT.Copy).then_inc(*act.does("o"))
                halves(eng, body)

            @block.vector
            def _(eng):
                def body(seq, s, again):
                    g = seq * 2 + s
                    for r in range(RT):
                        eng.wait_ge(*pe.did(g, f"V{r}"))
                        eng.wait_ge(*act.did(g, f"k{r}"))
                        nc.vector.tensor_tensor(kv[:, r % 2], V[:], k_sb[:, r % 2], ALU.mult).then_inc(*dve.does(f"kv{r}"))
                        eng.wait_ge(*pe.did(g, f"G{r}"))
                        eng.wait_ge(*dve.did(g, f"kv{r}"))
                        nc.vector.tensor_tensor_scan(st[:, r % 2], G[:], kv[:, r % 2], carry[:, r:r + 1] if s else 0.0, ALU.mult, ALU.add).then_inc(*dve.does(f"st{r}"))
                        eng.wait_ge(*dve.did(g, f"st{r}"))
                        nc.vector.tensor_copy(carry[:, r:r + 1], st[:, r % 2, GRP - 1:GRP]).then_inc(*dve.does(f"ca{r}"))
                        eng.wait_ge(*pe.did(g, f"Q{r}"))
                        if r >= 2:
                            eng.wait_ge(*pe.did(g, f"f{r - 2}"))
                        elif again:
                            eng.wait_ge(*pe.did(g - 1, f"f{RT - 2 + r}"))
                        nc.vector.tensor_tensor(y[:, r % 2], Q[:], st[:, r % 2], ALU.mult).then_inc(*dve.does(f"y{r}"))
                halves(eng, body)

def gla_output(nc, name, XN, OT, XT, w_gate, w_out, gammaT, betaT, ones_mean):
    with ExitStack() as stack:
        m = Space(nc, name, stack)
        xc, sq, ln, rs, r2, on, sg, og = (m.sb(n, [P, 2, GRP]) for n in "xc sq ln rs r2 on sg og".split())
        eps = m.sb("eps", [P, 1])
        mean = [m.ps(f"mean{s}") for s in range(2)]
        var = [m.ps(f"var{s}") for s in range(2)]
        gate = [m.ps(f"gate{s}") for s in range(2)]
        out = [m.ps(f"out{s}") for s in range(2)]
        an, dn = rsqrt_names("v")
        pe, act = Steps(m.sem("pe"), "mean gate var out"), Steps(m.sem("act"), "sq " + an + " sg")
        dve, ready = Steps(m.sem("dve"), "xc " + dn + " on af og xt"), m.sem("ready")
        with nc.Block() as block:
            @block.tensor
            def _(eng):
                def body(g, s, again):
                    if again:
                        eng.wait_ge(*dve.did(g - 2, "xt"))
                    nc.tensor.matmul(mean[s][:], ones_mean[:], at_group(OT, g), start=True, stop=True).then_inc(*pe.does("mean"))
                    nc.tensor.matmul(gate[s][:], w_gate[:], at_group(XN, g), start=True, stop=True).then_inc(*pe.does("gate"))
                    eng.wait_ge(*act.did(g, "sq"))
                    nc.tensor.matmul(var[s][:], ones_mean[:], sq[:, s], start=True, stop=True).then_inc(*pe.does("var"))
                    eng.wait_ge(*dve.did(g, "og"))
                    nc.tensor.matmul(out[s][:], w_out[:], og[:, s], start=True, stop=True).then_inc(*pe.does("out"))
                tiles(eng, GROUPS, 2, body)

            @block.scalar
            def _(eng):
                nc.scalar.preload_act_table_set("natural_log_exp_and_others")
                eng.wait_ge(ready, 1)
                def body(g, s, again):
                    eng.wait_ge(*dve.did(g, "xc"))
                    nc.scalar.activation(sq[:, s], xc[:, s], ACT.Square).then_inc(*act.does("sq"))
                    eng.wait_ge(*pe.did(g, "var"))
                    rsqrt_act(nc, eng, act, g, "v", var[s][:], eps[:], ln[:, s], rs[:, s], r2[:, s])
                    eng.wait_ge(*pe.did(g, "gate"))
                    nc.scalar.activation(sg[:, s], gate[s][:], ACT.Silu).then_inc(*act.does("sg"))
                tiles(eng, GROUPS, 2, body)

            @block.vector
            def _(eng):
                nc.vector.memset(eps[:], 1e-5).then_inc(ready, 1)
                def body(g, s, again):
                    eng.wait_ge(*pe.did(g, "mean"))
                    nc.vector.tensor_tensor(xc[:, s], at_group(OT, g), mean[s][:], ALU.subtract).then_inc(*dve.does("xc"))
                    rsqrt_dve(nc, eng, act, dve, g, "v", var[s][:], 1e-5, rs[:, s], r2[:, s])
                    nc.vector.tensor_tensor(on[:, s], xc[:, s], rs[:, s], ALU.mult).then_inc(*dve.does("on"))
                    eng.wait_ge(*dve.did(g, "on"))
                    nc.vector.tensor_scalar(on[:, s], on[:, s], gammaT[:, 0:1], betaT[:, 0:1], ALU.mult, ALU.add).then_inc(*dve.does("af"))
                    eng.wait_ge(*dve.did(g, "af"))
                    eng.wait_ge(*act.did(g, "sg"))
                    nc.vector.tensor_tensor(og[:, s], on[:, s], sg[:, s], ALU.mult).then_inc(*dve.does("og"))
                    eng.wait_ge(*pe.did(g, "out"))
                    nc.vector.tensor_tensor(at_group(XT, g), out[s][:], at_group(XT, g), ALU.add).then_inc(*dve.does("xt"))
                tiles(eng, GROUPS, 2, body)

LH, LD = 16, 8

def linear_attn_stage(nc, name, XN, XT, wqkv, w1, w2, g1T, g2row, g3row, coef, eye, ones_mean):
    F3 = 3 * P
    HALF = LD // 2
    with ExitStack() as stack:
        m = Space(nc, name, stack)
        sq, ln, rs, r2 = (m.sb(n, [P, GRP]) for n in "sq ln rs r2".split())
        xm = m.sb("xm", [P, GRP])
        qk = m.sb("qk", [P, 4, 2 * P])
        mn = m.sb("mn", [P, 4, 2 * P])
        v = m.sb("v", [P, 4, P])
        pr = m.sb("pr", [P, 2, LH * LD * LD])
        kv = m.sb("kv", [P, 4, LD * LD])
        at = m.sb("at", [P, 4, P])
        t1 = m.sb("t1", [P, 4, P])
        hr = m.sb("hr", [P, 4 * LH])
        gr = m.sb("gr", [P, 4])
        aT = m.sb("aT", [P, GRP])
        hT = m.sb("hT", [P, GRP])
        half = m.sb("half", [P, 4 * LH])
        eps = m.sb("eps", [P, 1])
        ms = m.ps("ms")
        pj = [m.ps(f"pj{t}") for t in range(4)]
        turned, hid, out = m.ps("turned"), m.ps("hid"), m.ps("out")
        EPS = float(np.finfo(np.float32).eps)
        an, dn = rsqrt_names("m")
        pe = Steps(m.sem("pe"), "ms p0 p1 p2 p3 aT hid out")
        act = Steps(m.sem("act"), "sq " + an + " v0 v1 v2 v3 e aT gelu")
        dve = Steps(m.sem("dve"), dn + " xm mn0 r0 mn1 r1 mn2 r2 mn3 r3 " + " ".join(f"kv{t} kc{t}" for t in range(4)) + " " +
                    " ".join(f"at{t}" for t in range(4)) + " hs he n1 n2 gs ge a1 a2 a3 ha out")
        pool = Steps(m.sem("pool"), "elu " + " ".join(f"p{t}" for t in range(4)) + " " + " ".join(f"w{t}" for t in range(4)) + " sq hr sq2 gr")
        half_set, ready = m.sem("half_set"), m.sem("ready")

        def flat(t):
            return t[:].rearrange("p a b -> p (a b)")
        with nc.Block() as block:
            @block.tensor
            def _(eng):
                def body(g, _, again):
                    def prev(who, step):
                        if again:
                            eng.wait_ge(*who.did(g - 1, step))
                    eng.wait_ge(*act.did(g, "sq"))
                    prev(dve, "xm")
                    nc.tensor.matmul(ms[:], ones_mean[:], sq[:], start=True, stop=True).then_inc(*pe.does("ms"))
                    eng.wait_ge(*dve.did(g, "xm"))
                    for t in range(4):
                        prev(dve, f"r{t}")
                        prev(act, f"v{t}")
                        nc.tensor.matmul(pj[t][:, 0:F3], xm[:, t * P:(t + 1) * P], wqkv[:], start=True, stop=True).then_inc(*pe.does(f"p{t}"))
                    eng.wait_ge(*dve.did(g, "a3"))
                    prev(act, "aT")
                    for t in range(4):
                        last = nc.tensor.transpose(turned[:, t * P:(t + 1) * P], at[:, t], eye[:])
                    last.then_inc(*pe.does("aT"))
                    eng.wait_ge(*act.did(g, "aT"))
                    prev(act, "gelu")
                    nc.tensor.matmul(hid[:], w1[:], aT[:], start=True, stop=True).then_inc(*pe.does("hid"))
                    eng.wait_ge(*act.did(g, "gelu"))
                    prev(dve, "out")
                    nc.tensor.matmul(out[:], w2[:], hT[:], start=True, stop=True).then_inc(*pe.does("out"))
                tiles(eng, GROUPS, 1, body)

            @block.scalar
            def _(eng):
                eng.wait_ge(ready, 1)
                def body(g, _, again):
                    def prev(who, step):
                        if again:
                            eng.wait_ge(*who.did(g - 1, step))
                    nc.scalar.preload_act_table_set("natural_log_exp_and_others")
                    nc.scalar.activation(sq[:], at_group(XN, g), ACT.Square).then_inc(*act.does("sq"))
                    eng.wait_ge(*pe.did(g, "ms"))
                    rsqrt_act(nc, eng, act, g, "m", ms[:], eps[:], ln[:], rs[:], r2[:])
                    for t in range(4):
                        eng.wait_ge(*dve.did(g, f"r{t}"))
                        prev(pool, f"p{t}")
                        nc.scalar.activation(v[:, t], pj[t][:, 2 * P:F3], ACT.Copy).then_inc(*act.does(f"v{t}"))
                    eng.wait_ge(*dve.did(g, "mn3"))
                    nc.scalar.activation(mn[:], mn[:], ACT.Exp).then_inc(*act.does("e"))
                    eng.wait_ge(*pe.did(g, "aT"))
                    prev(dve, "ha")
                    nc.scalar.activation(aT[:], turned[:], ACT.Copy).then_inc(*act.does("aT"))
                    eng.wait_ge(*pe.did(g, "hid"))
                    prev(pe, "out")
                    nc.scalar.activation(hT[:], hid[:], ACT.Gelu).then_inc(*act.does("gelu"))
                tiles(eng, GROUPS, 1, body)

            @block.vector
            def _(eng):
                nc.vector.memset(eps[:], EPS).then_inc(ready, 1)
                def body(g, _, again):
                    def prev(who, step):
                        if again:
                            eng.wait_ge(*who.did(g - 1, step))

                    def chain(name_):
                        eng.wait_ge(*dve.did(g, name_))
                    rsqrt_dve(nc, eng, act, dve, g, "m", ms[:], EPS, rs[:], r2[:])
                    nc.vector.scalar_tensor_tensor(xm[:], at_group(XN, g), g1T[:, 0:1], rs[:], ALU.mult, ALU.mult).then_inc(*dve.does("xm"))
                    for t in range(4):
                        eng.wait_ge(*pe.did(g, f"p{t}"))
                        prev(pool, "elu")
                        nc.vector.tensor_scalar(mn[:, t], pj[t][:, 0:2 * P], 0.0, None, ALU.min).then_inc(*dve.does(f"mn{t}"))
                        prev(pool, f"w{t}")
                        nc.vector.tensor_scalar(qk[:, t], pj[t][:, 0:2 * P], 0.0, -1.0, ALU.max, ALU.add).then_inc(*dve.does(f"r{t}"))
                    for t in range(4):
                        eng.wait_ge(*pool.did(g, f"p{t}"))
                        nc.vector.tensor_reduce(kv[:, t], pr[:, t % 2].rearrange("p (h f) -> p f h", h=LH), AX, ALU.add).then_inc(*dve.does(f"kv{t}"))
                        chain(f"kv{t}")
                        nc.vector.tensor_tensor(kv[:, t], kv[:, t], coef[:], ALU.mult).then_inc(*dve.does(f"kc{t}"))
                    for t in range(4):
                        eng.wait_ge(*pool.did(g, f"w{t}"))
                        nc.vector.tensor_reduce(at[:, t], pr[:, t % 2].rearrange("p (f e) -> p f e", e=LD), AX, ALU.add).then_inc(*dve.does(f"at{t}"))
                    eng.wait_ge(*pool.did(g, "sq"))
                    nc.vector.tensor_reduce(hr[:], flat(t1).rearrange("p (h e) -> p h e", e=LD), AX, ALU.add).then_inc(*dve.does("hs"))
                    chain("hs")
                    nc.vector.tensor_scalar(hr[:], hr[:], 1.0 / LD, EPS, ALU.mult, ALU.add).then_inc(*dve.does("he"))
                    eng.wait_ge(*pool.did(g, "hr"))
                    at3 = flat(at).rearrange("p (h e) -> p h e", e=LD)
                    nc.vector.tensor_tensor(at3, at3, along(hr[:], LD), ALU.mult).then_inc(*dve.does("n1"))
                    chain("n1")
                    nc.vector.tensor_tensor(at[:], at[:], over_heads(g2row[:], 4), ALU.mult).then_inc(*dve.does("n2"))
                    eng.wait_ge(*pool.did(g, "sq2"))
                    nc.vector.tensor_reduce(gr[:], t1[:], AX, ALU.add).then_inc(*dve.does("gs"))
                    chain("gs")
                    nc.vector.tensor_scalar(gr[:], gr[:], 1.0 / P, EPS, ALU.mult, ALU.add).then_inc(*dve.does("ge"))
                    eng.wait_ge(*pool.did(g, "gr"))
                    nc.vector.tensor_tensor(t1[:], at[:], along(gr[:], P), ALU.mult).then_inc(*dve.does("a1"))
                    chain("a1")
                    nc.vector.tensor_tensor(t1[:], t1[:], over_heads(g3row[:], 4), ALU.mult).then_inc(*dve.does("a2"))
                    chain("a2")
                    nc.vector.tensor_tensor(at[:], at[:], t1[:], ALU.add).then_inc(*dve.does("a3"))
                    eng.wait_ge(*act.did(g, "aT"))
                    nc.vector.tensor_tensor(at_group(XT, g), at_group(XT, g), aT[:], ALU.add).then_inc(*dve.does("ha"))
                    eng.wait_ge(*pe.did(g, "out"))
                    chain("ha")
                    nc.vector.tensor_tensor(at_group(XT, g), at_group(XT, g), out[:], ALU.add).then_inc(*dve.does("out"))
                tiles(eng, GROUPS, 1, body)

            @block.gpsimd
            def _(eng):
                nc.gpsimd.memset(half[:], -0.5).then_inc(half_set, 1)
                eng.wait_ge(half_set, 1)
                def body(g, _, again):
                    def prev(who, step):
                        if again:
                            eng.wait_ge(*who.did(g - 1, step))
                    eng.wait_ge(*dve.did(g, "r3"))
                    eng.wait_ge(*act.did(g, "e"))
                    nc.gpsimd.tensor_tensor(qk[:], qk[:], mn[:], ALU.add).then_inc(*pool.does("elu"))
                    eng.wait_ge(*pool.did(g, "elu"))
                    for t in range(4):
                        eng.wait_ge(*act.did(g, f"v{t}"))
                        if t >= 2:
                            eng.wait_ge(*dve.did(g, f"kv{t - 2}"))
                        k3 = qk[:, t, P:2 * P].rearrange("p (h e) -> p h e", e=LD).unsqueeze(3).to_broadcast([P, LH, LD, LD])
                        v3 = v[:, t].rearrange("p (h d) -> p h d", d=LD).unsqueeze(2).to_broadcast([P, LH, LD, LD])
                        nc.gpsimd.tensor_tensor(pr[:, t % 2].rearrange("p (h e d) -> p h e d", h=LH, e=LD), k3, v3, ALU.mult).then_inc(*pool.does(f"p{t}"))
                    for t in range(4):
                        eng.wait_ge(*dve.did(g, f"kc{t}"))
                        if t >= 2:
                            eng.wait_ge(*dve.did(g, f"at{t - 2}"))
                        else:
                            eng.wait_ge(*dve.did(g, f"kv{t + 2}"))
                        q3 = qk[:, t, 0:P].rearrange("p (h e) -> p h e", e=LD).unsqueeze(2).to_broadcast([P, LH, LD, LD])
                        kv3 = kv[:, t].rearrange("p (e d) -> p d e", d=LD).unsqueeze(1).to_broadcast([P, LH, LD, LD])
                        nc.gpsimd.tensor_tensor(pr[:, t % 2].rearrange("p (h d e) -> p h d e", h=LH, e=LD), q3, kv3, ALU.mult).then_inc(*pool.does(f"w{t}"))
                    eng.wait_ge(*dve.did(g, "at3"))
                    nc.gpsimd.tensor_tensor(t1[:], at[:], at[:], ALU.mult).then_inc(*pool.does("sq"))
                    eng.wait_ge(*dve.did(g, "he"))
                    nc.gpsimd.tensor_tensor(hr[:], hr[:], half[:], ALU.pow).then_inc(*pool.does("hr"))
                    eng.wait_ge(*dve.did(g, "n2"))
                    nc.gpsimd.tensor_tensor(t1[:], at[:], at[:], ALU.mult).then_inc(*pool.does("sq2"))
                    eng.wait_ge(*dve.did(g, "ge"))
                    nc.gpsimd.tensor_tensor(gr[:], gr[:], half[:, 0:4], ALU.pow).then_inc(*pool.does("gr"))
                tiles(eng, GROUPS, 1, body)

EX, MLP = 64, 256
BLOCKS = 2 * TOK // P + EX
SLOTS = BLOCKS * P

def sparse_route(nc, name, XN, HOT, WT, SLOT, BE, IDS, x_dram, ids_dram, w_gate, iota, eye, masks):
    C, E_ = CHUNKS, EX
    with ExitStack() as stack:
        m = Space(nc, name, stack)
        xs = m.sb("xs", [P, 2, GRP])
        xr = m.sb("xr", [P, 2, 4, P])
        lg = m.sb("lg", [P, 2, 4, E_])
        top4 = m.sb("top4", [P, 2, 4, 8])
        idx4 = m.sb("idx4", [P, 2, 4, 8], U32)
        top = m.sb("top", [P, C, 8])
        fi8 = m.sb("fi8", [P, C, 8])
        carrier = m.sb("carrier", [P, 2])
        fi = m.sb("fi", [P, 2, C])
        ex = m.sb("ex", [P, C])
        den = m.sb("den", [P, C])
        M = m.sb("M", [P, C * E_])
        rank = m.sb("rank", [P, C * E_])
        cnt = [m.sb(f"cnt{k}", [P, C * E_]) for k in range(2)]
        tot, incl, base, on1 = (m.sb(n, [P, E_]) for n in "tot incl base on1".split())
        ti = m.sb("ti", [P, E_], I32)
        sf = m.sb("sf", [P, 2, C])
        col = m.sb("col", [P, 1])
        ecol = m.sb("ecol", [P, 1])
        tokid = m.sb("tokid", [P, C], I32)
        zero = m.sb("zero", [P, BLOCKS], I32)
        si = m.sb("si", [P, 2, 2], U32)
        tk = m.sb("tk", [P, 2, 1], I32)
        back_i = m.sb("back_i", [BLOCKS, P], I32)
        back_f = m.sb("back_f", [BLOCKS, P])
        mark = m.sb("mark", [P, 3])
        zeroed, returned = m.sem("zeroed"), m.sem("returned")
        stored = [m.sem(f"stored{s}") for s in range(2)]
        scattered = [m.sem(f"scattered{s}") for s in range(2)]
        pe, act = Steps(m.sem("pe"), "lg xr"), Steps(m.sem("act"), "xs xr")
        dve = Steps(m.sem("dve"), "lg cr0 max cr1 at top idx")
        pe2 = Steps(m.sem("pe2"), "ranks be ids")
        end = Steps(m.sem("end"), "f0 f1 d den rec w1 h0 h1 M " + " ".join(f"rk{k} cn{k}" for k in range(4)) + " " + " ".join(f"px{k}" for k in range(5)) +
                    " ex rk tot t127 ti sh nb on1 incl excl base slot s0 r0 s1 r1 u le ej mn be bf ids")
        exped, consts = m.sem("exped"), m.sem("consts")
        pool = Steps(m.sem("pool"), "si tk carry")
        hot = HOT[:].rearrange("p (k c e) -> p k c e", k=2, e=E_)

        def ce(t):
            return t[:].rearrange("p (c e) -> p c e", e=E_)

        def pairs(eng, n, body):
            for s in range(2):
                body(s, s, 0)
            with eng.Fori(1, n // 2) as k:
                for s in range(2):
                    body(k * 2 + s, s, k)

        banks = [m.ps(f"bank{k}") for k in range(8)]
        with nc.Block() as block:
            @block.scalar
            def _(eng):
                def body(g, s, before):
                    again = not isinstance(g, int)
                    if again:
                        eng.wait_ge(*pe.did(g - 2, "xr"))
                    nc.scalar.activation(xs[:, s], at_group(XN, g), ACT.Copy).then_inc(*act.does("xs"))
                    eng.wait_ge(*pe.did(g, "xr"))
                    if again:
                        eng.wait_ge(stored[s], before * 16)
                    nc.scalar.activation(xr[:, s].rearrange("p t n -> p (t n)"), banks[2 + s][:], ACT.Copy).then_inc(*act.does("xr"))
                pairs(eng, GROUPS, body)
                eng.wait_ge(*end.did(0, "d"))
                nc.scalar.activation(ex[:], ex[:], ACT.Exp).then_inc(exped, 1)

            @block.sync
            def _(eng):
                def body(g, s, again):
                    eng.wait_ge(*act.did(g, "xr"))
                    eng.dma_start(x_dram.rearrange("(g t p) d -> g p t d", p=P, t=4)[bass.ds(g, 1)].rearrange("o p t d -> (o p) t d"), xr[:, s]).then_inc(stored[s], 16)
                tiles(eng, GROUPS, 2, body)
                eng.wait_ge(consts, 4)
                eng.dma_start(ids_dram.rearrange("(p n) o -> p (n o)", p=P), zero[:]).then_inc(zeroed, 16)
                for s in range(2):
                    eng.wait_ge(scattered[s], C * 16)
                eng.dma_start(back_i[:], ids_dram.rearrange("(b s) o -> b (s o)", s=P)).then_inc(returned, 16)
                eng.wait_ge(returned, 16)
                for s in range(2):
                    eng.wait_ge(stored[s], GROUPS // 2 * 16)

            @block.tensor
            def _(eng):
                def body(g, s, again):
                    eng.wait_ge(*act.did(g, "xs"))
                    if again:
                        eng.wait_ge(*dve.did(g - 2, "lg"))
                    for t in range(4):
                        last = nc.tensor.matmul(banks[s][:, t * E_:(t + 1) * E_], xs[:, s, t * P:(t + 1) * P], w_gate[:], start=True, stop=True)
                    last.then_inc(*pe.does("lg"))
                    if again:
                        eng.wait_ge(*act.did(g - 2, "xr"))
                    for t in range(4):
                        last = nc.tensor.transpose(banks[2 + s][:, t * P:(t + 1) * P], xs[:, s, t * P:(t + 1) * P], eye[:])
                    last.then_inc(*pe.does("xr"))
                tiles(eng, GROUPS, 2, body)
                eng.wait_ge(*end.did(0, "M"))
                eng.wait_ge(*act.did(GROUPS - 1, "xr"))
                for k in range(4):
                    nc.tensor.matmul(banks[k][:], masks["row_lt_col"][:], M[:, k * GRP:(k + 1) * GRP], start=True, stop=True)
                    last = nc.tensor.matmul(banks[4 + k][:], masks["ones"][:], M[:, k * GRP:(k + 1) * GRP], start=True, stop=True)
                last.then_inc(*pe2.does("ranks"))
                eng.wait_ge(*end.did(0, "mn"))
                nc.tensor.matmul(banks[0][0:1, 0:P], ecol[:], eye[:], start=True, stop=True).then_inc(*pe2.does("be"))
                eng.wait_ge(*end.did(0, "bf"))
                nc.tensor.transpose(banks[1][:, 0:BLOCKS], back_f[:], eye[:]).then_inc(*pe2.does("ids"))

            @block.vector
            def _(eng):
                def body(g, s, again):
                    eng.wait_ge(*pe.did(g, "lg"))
                    nc.vector.tensor_copy(lg[:, s].rearrange("p t e -> p (t e)"), banks[s][:, 0:4 * E_]).then_inc(*dve.does("lg"))
                    eng.wait_ge(*dve.did(g, "lg"))
                    nc.vector.memset(carrier[:, 0:1], 0.0).then_inc(*dve.does("cr0"))
                    for t in range(4):
                        last = nc.vector.max(top4[:, s, t], lg[:, s, t])
                    last.then_inc(*dve.does("max"))
                    eng.wait_ge(*dve.did(g, "max"))
                    nc.vector.memset(carrier[:, 1:2], 0.0).then_inc(*dve.does("cr1"))
                    for t in range(4):
                        last = nc.vector.max_index(idx4[:, s, t], top4[:, s, t], lg[:, s, t])
                    last.then_inc(*dve.does("at"))
                    nc.vector.tensor_copy(top[:, bass.ds(g * 4, 4), :], top4[:, s]).then_inc(*dve.does("top"))
                    eng.wait_ge(*dve.did(g, "at"))
                    nc.vector.tensor_copy(fi8[:, bass.ds(g * 4, 4), :], idx4[:, s]).then_inc(*dve.does("idx"))
                tiles(eng, GROUPS, 2, body)

                def step(ins, name_):
                    ins.then_inc(*end.does(name_))
                    eng.wait_ge(*end.did(0, name_))
                eng.wait_ge(*dve.did(GROUPS - 1, "idx"))
                for k in range(2):
                    step(nc.vector.tensor_copy(fi[:, k], fi8[:, :, k]), f"f{k}")
                step(nc.vector.tensor_tensor(ex[:], top[:, :, 1], top[:, :, 0], ALU.subtract), "d")
                eng.wait_ge(exped, 1)
                step(nc.vector.tensor_scalar(den[:], ex[:], 1.0, None, ALU.add), "den")
                step(nc.vector.reciprocal(WT[:, 0], den[:]), "rec")
                step(nc.vector.tensor_tensor(WT[:, 1], WT[:, 0], ex[:], ALU.mult), "w1")
                for k in range(2):
                    step(nc.vector.tensor_tensor(hot[:, k], iota[:, 0:E_].unsqueeze(1).to_broadcast([P, C, E_]), along(fi[:, k], E_), ALU.is_equal), f"h{k}")
                step(nc.vector.tensor_tensor(ce(M), hot[:, 0], hot[:, 1], ALU.add), "M")
                eng.wait_ge(*pe2.did(0, "ranks"))
                for k in range(4):
                    step(nc.vector.tensor_copy(rank[:, k * GRP:(k + 1) * GRP], banks[k][:]), f"rk{k}")
                    step(nc.vector.tensor_copy(cnt[0][:, k * GRP:(k + 1) * GRP], banks[4 + k][:]), f"cn{k}")
                for k in range(5):
                    a, b, n = cnt[k % 2], cnt[1 - k % 2], (1 << k) * E_
                    nc.vector.tensor_copy(b[:, 0:n], a[:, 0:n])
                    step(nc.vector.tensor_tensor(b[:, n:], a[:, n:], a[:, 0:C * E_ - n], ALU.add), f"px{k}")
                summed = cnt[1]
                step(nc.vector.tensor_copy(tot[:], summed[:, (C - 1) * E_:C * E_]), "ex")
                step(nc.vector.tensor_tensor(rank[:, E_:], rank[:, E_:], summed[:, 0:(C - 1) * E_], ALU.add), "rk")
                step(nc.vector.tensor_scalar(base[:], tot[:], float(P - 1), None, ALU.add), "tot")
                step(nc.vector.tensor_copy(ti[:], base[:]), "t127")
                step(nc.vector.tensor_scalar(ti[:], ti[:], 7, None, ALU.logical_shift_right), "ti")
                step(nc.vector.tensor_copy(tot[:], ti[:]), "sh")
                step(nc.vector.memset(on1[:], 1.0), "nb")
                step(nc.vector.tensor_tensor_scan(incl[:], on1[:], tot[:], 0.0, ALU.mult, ALU.add), "on1")
                step(nc.vector.tensor_tensor(base[:], incl[:], tot[:], ALU.subtract), "incl")
                step(nc.vector.tensor_scalar(base[:], base[:], float(P), None, ALU.mult), "excl")
                step(nc.vector.tensor_tensor(ce(rank), ce(rank), base[:].unsqueeze(1).to_broadcast([P, C, E_]), ALU.add), "base")
                eng.wait_ge(consts, 4)
                step(nc.vector.tensor_scalar(on1[:], incl[:], col[:, 0:1], None, ALU.is_le), "slot")
                for k in range(2):
                    step(nc.vector.tensor_tensor(hot[:, k], hot[:, k], ce(rank), ALU.mult), f"s{k}")
                    step(nc.vector.tensor_reduce(sf[:, k], hot[:, k], AX, ALU.add), f"r{k}")
                step(nc.vector.tensor_copy(SLOT[:], sf[:]), "u")
                step(nc.vector.tensor_reduce(ecol[:], on1[:], AX, ALU.add), "le")
                step(nc.vector.tensor_scalar(ecol[:], ecol[:], float(E_ - 1), None, ALU.min), "ej")
                step(nc.vector.tensor_copy(col[:], ecol[:]), "mn")
                eng.wait_ge(*pe2.did(0, "be"))
                step(nc.vector.tensor_copy(BE[:], banks[0][0:1, 0:BLOCKS]), "be")
                eng.wait_ge(returned, 16)
                step(nc.vector.tensor_copy(back_f[:], back_i[:]), "bf")
                eng.wait_ge(*pe2.did(0, "ids"))
                step(nc.vector.tensor_copy(IDS[:], banks[1][:, 0:BLOCKS]), "ids")

            @block.gpsimd
            def _(eng):
                nc.gpsimd.iota(tokid[:], pattern=[[P, C]], base=0, channel_multiplier=1).then_inc(consts, 1)
                nc.gpsimd.memset(zero[:], 0).then_inc(consts, 1)
                nc.gpsimd.memset(mark[:, 0:1], 0.0).then_inc(consts, 1)
                nc.gpsimd.iota(col[:], pattern=[[0, 1]], base=0, channel_multiplier=1, allow_small_or_imprecise_dtypes=True).then_inc(consts, 1)
                eng.wait_ge(*end.did(0, "u"))
                eng.wait_ge(consts, 4)
                eng.wait_ge(zeroed, 16)

                def carry(s):
                    nc.gpsimd.tensor_tensor(mark[:, 1 + s:2 + s], mark[:, 0:1], mark[:, 0:1], ALU.add).then_inc(*pool.does("carry"))

                def body(c, s, before):
                    if not isinstance(c, int):
                        eng.wait_ge(scattered[s], before * 32)
                    nc.gpsimd.tensor_copy(si[:, s], SLOT[:, :, bass.ds(c, 1)].rearrange("p k o -> p (k o)")).then_inc(*pool.does("si"))
                    nc.gpsimd.tensor_copy(tk[:, s], tokid[:, bass.ds(c, 1)]).then_inc(*pool.does("tk"))
                    eng.wait_ge(*pool.did(c, "tk"))
                    carry(s)
                    for k in range(2):
                        eng.indirect_dma_start(ids_dram, bass.IndirectOffsetOnAxis(ap=si[:, s, k:k + 1], axis=0), tk[:, s], None).then_inc(scattered[s], 16)
                pairs(eng, C, body)

def sparse_experts(nc, name, BE, IDS, x_dram, y_dram, w0_dram, w1_dram, wo_dram, eye):
    F = MLP // P
    with ExitStack() as stack:
        m = Space(nc, name, stack)
        W = 4
        w0 = m.sb("w0", [P, W, MLP])
        w1 = m.sb("w1", [P, W, MLP])
        wo = m.sb("wo", [P, W, F, P])
        ix = m.sb("ix", [P, W, 1], U32)
        xg = m.sb("xg", [P, W, P])
        xT = m.sb("xT", [P, 2, P])
        s0 = m.sb("s0", [P, 2, MLP])
        hid = m.sb("hid", [P, 2, MLP])
        y = m.sb("y", [P, W, P])
        mark, started = m.sb("mark", [P, 1 + W]), m.sem("started")
        xp = [m.ps(f"xp{k}") for k in range(2)]
        a = [m.ps(f"a{k}") for k in range(2)]
        b = [m.ps(f"b{k}") for k in range(2)]
        yp = [m.ps(f"yp{k}") for k in range(2)]
        wl = [m.sem(f"wl{k}") for k in range(W)]
        xl = [m.sem(f"xl{k}") for k in range(W)]
        ys = [m.sem(f"ys{k}") for k in range(W)]
        pe, act, dve, pool = Steps(m.sem("pe"), "xT h y"), Steps(m.sem("act"), "xT s0"), Steps(m.sem("dve"), "hid y"), Steps(m.sem("pool"), "ix carry")

        def slots(eng, body):
            for j in range(W):
                body(j, j, 1, False)
            with eng.Fori(1, BLOCKS // W) as k:
                for s in range(W):
                    body(k * W + s, s, k + 1, True)

        with nc.Block() as block:
            @block.sync
            def _(eng):
                def body(j, s, times, again):
                    e = eng.value_load(BE[0:1, bass.ds(j, 1)], min_val=0, max_val=EX - 1)
                    if again:
                        store(j - W, s)
                    eng.dma_start(w0[:, s], w0_dram[bass.ds(e, 1)].rearrange("o d f -> (o d) f")).then_inc(wl[s], 16)
                    eng.dma_start(w1[:, s], w1_dram[bass.ds(e, 1)].rearrange("o d f -> (o d) f")).then_inc(wl[s], 16)
                    eng.dma_start(wo[:, s], wo_dram[bass.ds(e, 1)].rearrange("o (c p) d -> (o p) c d", p=P)).then_inc(wl[s], 16)

                def store(j, s):
                    eng.wait_ge(*dve.did(j, "y"))
                    eng.dma_start(y_dram.rearrange("(b s) d -> b s d", s=P)[bass.ds(j, 1)].rearrange("o s d -> (o s) d"), y[:, s]).then_inc(ys[s], 16)
                slots(eng, body)
                for s in range(W):
                    store(BLOCKS - W + s, s)
                for s in range(W):
                    eng.wait_ge(ys[s], BLOCKS // W * 16)

            @block.gpsimd
            def _(eng):
                nc.gpsimd.memset(mark[:, 0:1], 0.0).then_inc(started, 1)
                eng.wait_ge(started, 1)

                def carry(s):
                    nc.gpsimd.tensor_tensor(mark[:, 1 + s:2 + s], mark[:, 0:1], mark[:, 0:1], ALU.add).then_inc(*pool.does("carry"))

                def body(j, s, times, again):
                    if again:
                        eng.wait_ge(*pe.did(j - W, "xT"))
                    nc.gpsimd.tensor_copy(ix[:, s], IDS[:, bass.ds(j, 1)]).then_inc(*pool.does("ix"))
                    eng.wait_ge(*pool.did(j, "ix"))
                    carry(s)
                    eng.indirect_dma_start(xg[:, s], None, x_dram, bass.IndirectOffsetOnAxis(ap=ix[:, s], axis=0)).then_inc(xl[s], 16)
                slots(eng, body)

            @block.tensor
            def _(eng):
                def body(j, s, times, again):
                    k = s % 2
                    eng.wait_ge(xl[s], times * 16)
                    if again or s >= 2:
                        eng.wait_ge(*act.did(j - 2, "xT"))
                    nc.tensor.transpose(xp[k][:, 0:P], xg[:, s], eye[:]).then_inc(*pe.does("xT"))
                    eng.wait_ge(wl[s], times * 48)
                    eng.wait_ge(*act.did(j, "xT"))
                    if again or s >= 2:
                        eng.wait_ge(*dve.did(j - 2, "hid"))
                    for bank, w in ((a, w0), (b, w1)):
                        for c in range(F):
                            last = nc.tensor.matmul(bank[k][:, c * P:(c + 1) * P], w[:, s, c * P:(c + 1) * P], xT[:, k], start=True, stop=True)
                    last.then_inc(*pe.does("h"))
                    eng.wait_ge(*dve.did(j, "hid"))
                    for c in range(F):
                        last = nc.tensor.matmul(yp[k][:, 0:P], hid[:, k, c * P:(c + 1) * P], wo[:, s, c], start=(c == 0), stop=(c == F - 1))
                    last.then_inc(*pe.does("y"))
                slots(eng, body)

            @block.scalar
            def _(eng):
                def body(j, s, times, again):
                    k = s % 2
                    eng.wait_ge(*pe.did(j, "xT"))
                    if again or s >= 2:
                        eng.wait_ge(*pe.did(j - 2, "h"))
                    nc.scalar.activation(xT[:, k], xp[k][:, 0:P], ACT.Copy).then_inc(*act.does("xT"))
                    eng.wait_ge(*pe.did(j, "h"))
                    if again or s >= 2:
                        eng.wait_ge(*dve.did(j - 2, "hid"))
                    nc.scalar.activation(s0[:, k], a[k][:, 0:MLP], ACT.Silu).then_inc(*act.does("s0"))
                slots(eng, body)

            @block.vector
            def _(eng):
                def body(j, s, times, again):
                    k = s % 2
                    eng.wait_ge(*act.did(j, "s0"))
                    if again or s >= 2:
                        eng.wait_ge(*pe.did(j - 2, "y"))
                    nc.vector.tensor_tensor(hid[:, k], s0[:, k], b[k][:, 0:MLP], ALU.mult).then_inc(*dve.does("hid"))
                    eng.wait_ge(*pe.did(j, "y"))
                    if again:
                        eng.wait_ge(ys[s], (times - 1) * 16)
                    nc.vector.tensor_copy(y[:, s], yp[k][:, 0:P]).then_inc(*dve.does("y"))
                slots(eng, body)

def sparse_combine(nc, name, SLOT, WT, XT, y_dram, eye):
    with ExitStack() as stack:
        m = Space(nc, name, stack)
        W = 4
        ix = m.sb("ix", [P, W, 2], U32)
        yg = m.sb("yg", [P, W, 2, P])
        wt = m.sb("wt", [P, W, 2])
        o = m.sb("o", [P, 2, P])
        mark, started = m.sb("mark", [P, 1 + W]), m.sem("started")
        turned = [m.ps(f"turned{k}") for k in range(2)]
        got = [m.sem(f"got{k}") for k in range(W)]
        pe, act, dve, pool = Steps(m.sem("pe"), "t"), Steps(m.sem("act"), "wt"), Steps(m.sem("dve"), "o0 o1 x"), Steps(m.sem("pool"), "ix carry")

        def slots(eng, body):
            for j in range(W):
                body(j, j, 1, False)
            with eng.Fori(1, CHUNKS // W) as k:
                for s in range(W):
                    body(k * W + s, s, k + 1, True)
        with nc.Block() as block:
            @block.gpsimd
            def _(eng):
                nc.gpsimd.memset(mark[:, 0:1], 0.0).then_inc(started, 1)
                eng.wait_ge(started, 1)

                def carry(s):
                    nc.gpsimd.tensor_tensor(mark[:, 1 + s:2 + s], mark[:, 0:1], mark[:, 0:1], ALU.add).then_inc(*pool.does("carry"))

                def body(c, s, times, again):
                    if again:
                        eng.wait_ge(*dve.did(c - W, "o1"))
                    nc.gpsimd.tensor_copy(ix[:, s], SLOT[:, :, bass.ds(c, 1)].rearrange("p k o -> p (k o)")).then_inc(*pool.does("ix"))
                    eng.wait_ge(*pool.did(c, "ix"))
                    carry(s)
                    for k in range(2):
                        eng.indirect_dma_start(yg[:, s, k], None, y_dram, bass.IndirectOffsetOnAxis(ap=ix[:, s, k:k + 1], axis=0)).then_inc(got[s], 16)
                slots(eng, body)

            @block.scalar
            def _(eng):
                def body(c, s, times, again):
                    if again:
                        eng.wait_ge(*dve.did(c - W, "o1"))
                    nc.scalar.activation(wt[:, s], WT[:, :, bass.ds(c, 1)].rearrange("p k o -> p (k o)"), ACT.Copy).then_inc(*act.does("wt"))
                slots(eng, body)

            @block.vector
            def _(eng):
                def body(c, s, times, again):
                    k = s % 2
                    eng.wait_ge(got[s], times * 32)
                    eng.wait_ge(*act.did(c, "wt"))
                    if again or s >= 2:
                        eng.wait_ge(*pe.did(c - 2, "t"))
                    nc.vector.tensor_scalar(o[:, k], yg[:, s, 0], wt[:, s, 0:1], None, ALU.mult).then_inc(*dve.does("o0"))
                    eng.wait_ge(*dve.did(c, "o0"))
                    nc.vector.scalar_tensor_tensor(o[:, k], yg[:, s, 1], wt[:, s, 1:2], o[:, k], ALU.mult, ALU.add).then_inc(*dve.does("o1"))
                    eng.wait_ge(*pe.did(c, "t"))
                    nc.vector.tensor_tensor(XT[:, bass.ds(c * P, P)], XT[:, bass.ds(c * P, P)], turned[k][:, 0:P], ALU.add).then_inc(*dve.does("x"))
                slots(eng, body)

            @block.tensor
            def _(eng):
                def body(c, s, times, again):
                    k = s % 2
                    eng.wait_ge(*dve.did(c, "o1"))
                    if again or s >= 2:
                        eng.wait_ge(*dve.did(c - 2, "x"))
                    nc.tensor.transpose(turned[k][:, 0:P], o[:, k], eye[:]).then_inc(*pe.does("t"))
                slots(eng, body)

LAMBDA_INIT = 0.8 - 0.6 * float(np.exp(-0.3 * 0))
LIN_SCALE = 1.0 / float(np.sqrt(D // 2))

def load_stage(nc, name, pairs):
    with nc.semaphore(name + "_a") as sem_a, nc.semaphore(name + "_b") as sem_b:
        first, second = Loads(sem_a), Loads(sem_b)
        with nc.Block() as block:
            @block.sync
            def _(eng):
                for tile, source in pairs[0::2]:
                    eng.dma_start(tile, source).then_inc(*first.one())
                eng.wait_ge(*first.all())

            @block.scalar
            def _(eng):
                for tile, source in pairs[1::2]:
                    eng.dma_start(tile, source).then_inc(*second.one())
                if second.count:
                    eng.wait_ge(*second.all())

def clear_semaphores(nc):
    with nc.Block() as block:
        @block.gpsimd
        def _(eng):
            eng.sem_clear(range(FIRST_SEM, 256))

FIRST_SEM = 99

def layer0(nc, a, XT, XN, c):
    with ExitStack() as stack:
        m = Space(nc, "l0_", stack)
        biasT, gammaT, betaT = (m.sb(n, [P, 3]) for n in "biasT gammaT betaT".split())
        bias_rows, WQ = m.sb("bias_rows", [P, 3, P]), m.sb("WQ", [P, 6, P])
        with ExitStack() as inner:
            m = Space(nc, "l0d_", inner)
            HT = m.sb("HT", [P, TOK])
            w_up, w_down = m.sb("w_up", [P, 4 * P]), m.sb("w_down", [P, 4 * P])
            with ExitStack() as delta:
                m = Space(nc, "l0e_", delta)
                GL, SCAL, Wba = m.sb("GL", [P, CHUNKS * 16]), m.sb("SCAL", [P, CHUNKS * SC]), m.sb("Wba", [P, 16])
                w = {k: m.sb("w_" + k, [P, 8 * P]) for k in "qkvgo"}
                o_norm = m.sb("o_norm", [P, 1])
                masks = dict(c)
                masks["level"] = m.sb("level", [P, 7 * P])
                load_stage(nc, "l0_load", [(Wba[:], a["Wba"]), (masks["level"][:], a["level"]), (o_norm[:], a["o_norm_w"])] + [(w[k][:], a["W" + k]) for k in "qkvgo"] +
                           [(w_up[:], a["w_up"]), (w_down[:], a["w_down"]), (biasT[:], a["q_biasT"]), (gammaT[:], a["q_gammaT"]), (betaT[:], a["q_betaT"])] +
                           [(bias_rows[:, b], on_all_partitions(a["q_bias"][b])) for b in range(3)])
                with nc.semaphore("l0_scaled") as scaled, nc.Block() as block:
                    @block.vector
                    def _(eng):
                        nc.vector.tensor_scalar(w["o"][:], w["o"][:], o_norm[:, 0:1], None, ALU.mult).then_inc(scaled, 1)
                norm_stage(nc, "l0n_", XT, XN, c["ones_mean"], (HT, Wba, GL))
                delta_gates(nc, "l0g_", GL, SCAL, a["A_log"], a["dt_bias"], masks)
                delta_stage(nc, "l0s_", HT, XN, SCAL, w, masks)
            relu_mlp_stage(nc, "l0m_", XT, HT, w_up, w_down, c["ones_mean"])
        qlora_weights(nc, "l0w_", a["q_weights"], a["q_scales"], a["q_lora_a"], a["q_lora_bT"], WQ, c["eye"])
        qlora_stage(nc, "l0q_", XT, XN, WQ, biasT, bias_rows, gammaT, betaT, c["eye"])

def layer1(nc, a, XT, XN, c):
    with ExitStack() as stack:
        m = Space(nc, "l1_", stack)
        Vh, head_rows = m.sb("Vh", [P, AN * QT * VW]), m.sb("head_rows", [AH, P])
        w, wv, w_out = [m.sb(f"w{k}", [P, P]) for k in range(4)], m.sb("wv", [P, P]), m.sb("w_out", [P, P])
        cos, sin = m.sb("cos", [P, SEQ]), m.sb("sin", [P, SEQ])
        q_dram = nc.dram_tensor("attn_q", [AN, 3, AD, SEQ], BF16).ap()
        k_dram = nc.dram_tensor("attn_k", [AN, 5, AD, SEQ], BF16).ap()
        ctx_dram = nc.dram_tensor("attn_ctx", [AN, AD, SEQ], F32).ap()
        sum_dram, rec_dram = (nc.dram_tensor(n, [AN, SEQ], F32).ap() for n in ("attn_sums", "attn_inverses"))
        load_stage(nc, "l1_load", [(w[k][:], a[f"rope_w{k}"]) for k in range(4)] + [(wv[:], a["attn_wv"]), (w_out[:], a["attn_wo"]), (cos[:], a["cos"]), (sin[:], a["sin"]), (head_rows[:], a["head_rows"])])
        norm_stage(nc, "l1n_", XT, XN, c["ones_mean"])
        attn_project(nc, "l1p_", XN, Vh, q_dram, k_dram, w, wv, cos, sin)
        attn_heads(nc, "l1h_", Vh, ctx_dram, sum_dram, q_dram, k_dram, c["eye16"])
        attn_output(nc, "l1o_", ctx_dram, sum_dram, rec_dram, XT, w_out, head_rows)
    clear_semaphores(nc)
    with ExitStack() as stack:
        m = Space(nc, "l1m_", stack)
        W1, W2 = m.sb("W1", [P, 8, 4 * P]), m.sb("W2", [P, 8, 4, P])
        B1, b2 = m.sb("B1", [P, 8, 4]), m.sb("b2", [8, P])
        RW, wr, br = m.sb("RW", [P, CHUNKS * 8]), m.sb("wr", [P, 8]), m.sb("br", [P, 8])
        gammaT, betaT = m.sb("gammaT", [P, 1]), m.sb("betaT", [P, 1])
        load_stage(nc, "l1m_load", [(W1[:], a["moe_W1"]), (W2[:], a["moe_W2"]), (B1[:], a["moe_B1"]), (b2[:], a["moe_b2"]), (wr[:], a["moe_wr"]),
                                    (br[:], on_all_partitions(a["moe_br"])), (gammaT[:], a["moe_gamma"]), (betaT[:], a["moe_beta"])])
        router_small(nc, "l1r_", XN, RW, wr, br, c["iota"], 8)
        dense_moe(nc, "l1e_", XN, XT, RW, W1, B1, W2, b2, gammaT, betaT, c["eye"], 8)

def layer2(nc, a, XT, XN, c):
    with ExitStack() as stack:
        m = Space(nc, "l2_", stack)
        wqkv, w1, w2 = m.sb("wqkv", [P, 3 * P]), m.sb("w1", [P, P]), m.sb("w2", [P, P])
        g1T, g2, g2row, g3row = m.sb("g1T", [P, 1]), m.sb("g2", [P, 8]), m.sb("g2row", [P, P]), m.sb("g3row", [P, P])
        coef, lam, prod, exps, lmb = m.sb("coef", [P, 64]), m.sb("lam", [P, 4]), m.sb("prod", [P, 2]), m.sb("exps", [P, 2]), m.sb("lmb", [P, 1])
        load_stage(nc, "l2_load", [(wqkv[:], a["lin_wqkv"]), (w1[:], a["lin_w1"]), (w2[:], a["lin_w2"]), (g1T[:], a["lin_g1"]), (g2[:], on_all_partitions(a["lin_g2"])),
                                   (g3row[:], on_all_partitions(a["lin_g3"])), (lam[:], on_all_partitions(a["lin_lambda"]))])
        with nc.semaphore("l2_dve") as dve_sem, nc.semaphore("l2_exp") as exp_done, nc.Block() as block:
            dve = Steps(dve_sem, "prod diff lmb fill coef")

            @block.scalar
            def _(eng):
                eng.wait_ge(*dve.did(0, "prod"))
                nc.scalar.activation(exps[:], prod[:], ACT.Exp).then_inc(exp_done, 1)

            @block.vector
            def _(eng):
                pairs = lam[:].rearrange("p (a b) -> p a b", b=2)
                nc.vector.tensor_tensor(prod[:], pairs[:, :, 0], pairs[:, :, 1], ALU.mult).then_inc(*dve.does("prod"))
                eng.wait_ge(exp_done, 1)
                nc.vector.tensor_tensor(lmb[:], exps[:, 0:1], exps[:, 1:2], ALU.subtract).then_inc(*dve.does("diff"))
                eng.wait_ge(*dve.did(0, "diff"))
                nc.vector.tensor_scalar(lmb[:], lmb[:], LAMBDA_INIT, None, ALU.add).then_inc(*dve.does("lmb"))
                nc.vector.memset(coef[:, 0:32], LIN_SCALE)
                nc.vector.memset(coef[:, 32:64], -LIN_SCALE).then_inc(*dve.does("fill"))
                nc.vector.tensor_scalar(g2row[:].rearrange("p (h d) -> p h d", d=8), over_heads(g2[:], 16), 1.0 - LAMBDA_INIT, None, ALU.mult)
                eng.wait_ge(*dve.did(0, "fill"))
                nc.vector.tensor_scalar(coef[:, 32:64], coef[:, 32:64], lmb[:, 0:1], None, ALU.mult).then_inc(*dve.does("coef"))
        norm_stage(nc, "l2n_", XT, XN, c["ones_mean"])
        linear_attn_stage(nc, "l2a_", XN, XT, wqkv, w1, w2, g1T, g2row, g3row, coef, c["eye"], c["ones_mean"])
    clear_semaphores(nc)
    with ExitStack() as stack:
        m = Space(nc, "l2s_", stack)
        w_gate, WT, SLOT = m.sb("w_gate", [P, EX]), m.sb("WT", [P, 2, CHUNKS]), m.sb("SLOT", [P, 2, CHUNKS], U32)
        BE, IDS = m.sb("BE", [1, BLOCKS], I32), m.sb("IDS", [P, BLOCKS], U32)
        x_dram = nc.dram_tensor("sparse_x", [TOK, D], F32).ap()
        y_dram = nc.dram_tensor("sparse_y", [SLOTS, D], F32).ap()
        ids_dram = nc.dram_tensor("sparse_ids", [SLOTS, 1], I32).ap()
        load_stage(nc, "l2s_load", [(w_gate[:], a["sparse_gate"])])
        with ExitStack() as scratch:
            HOT = Space(nc, "l2h_", scratch).sb("HOT", [P, 2 * CHUNKS * EX])
            sparse_route(nc, "l2r_", XN, HOT, WT, SLOT, BE, IDS, x_dram, ids_dram, w_gate, c["iota"], c["eye"], c)
        sparse_experts(nc, "l2e_", BE, IDS, x_dram, y_dram, a["sparse_w0"], a["sparse_w1"], a["sparse_wo"], c["eye"])
        sparse_combine(nc, "l2c_", SLOT, WT, XT, y_dram, c["eye"])

def layer3(nc, a, XT, XN, c):
    with ExitStack() as stack:
        m = Space(nc, "l3_", stack)
        GT, OT = m.sb("GT", [P, TOK]), m.sb("OT", [P, TOK])
        shapes = {"gk1": 16, "gb": 1, "wq": 1024, "wk": 1024, "wv": 1024, "pick": 1024, "fold": 1024, "wg": P, "wo": P, "gamma": 1, "beta": 1}
        t = {k: m.sb(k, [P, n]) for k, n in shapes.items()}
        t["gk2"] = m.sb("gk2", [16, P])
        load_stage(nc, "l3_load", [(tile[:], a["gla_" + k]) for k, tile in t.items()])
        norm_stage(nc, "l3n_", XT, XN, c["ones_mean"])
        gla_gates(nc, "l3g_", XN, GT, t["gk1"], t["gk2"], t["gb"])
        gla_states(nc, "l3s_", XN, GT, OT, t["wq"], t["wk"], t["wv"], t["pick"], t["fold"])
        gla_output(nc, "l3o_", XN, OT, XT, t["wg"], t["wo"], t["gamma"], t["beta"], c["ones_mean"])
    with ExitStack() as stack:
        m = Space(nc, "l3m_", stack)
        w1, w2, b1, b2 = m.sb("w1", [P, 4 * P]), m.sb("w2", [P, 4 * P]), m.sb("b1", [P, 4]), m.sb("b2", [P, 1])
        load_stage(nc, "l3m_load", [(b1[:], a["bin_b1"]), (b2[:], a["bin_b2"])])
        binary_weights(nc, "l3b_", a["bin_w1"], a["bin_w2"], w1, w2, c["eye"])
        gelu_mlp_stage(nc, "l3f_", XT, XN, w1, w2, b1, b2)

MASKS = "row_le_col row_gt_col row_ge_col row_lt_col ones eye".split()

def network(nc, a, out):
    with ExitStack() as stack:
        m = Space(nc, "net_", stack)
        XT, XN = m.sb("XT", [P, TOK]), m.sb("XN", [P, TOK])
        c = {k: m.sb(k, [P, P]) for k in MASKS}
        c["eye16"], c["iota"], c["ones_mean"] = m.sb("eye16", [P, P], BF16), m.sb("iota", [P, EX]), m.sb("ones_mean", [P, P])
        load_stage(nc, "net_load", [(XT[:], a["xT"])] + [(c[k][:], a[k]) for k in MASKS + ["iota", "ones_mean"]])
        with nc.semaphore("net_cast") as cast, nc.Block() as block:
            @block.vector
            def _(eng):
                nc.vector.tensor_copy(c["eye16"][:], c["eye"][:]).then_inc(cast, 1)
        for layer in (layer0, layer1, layer2, layer3):
            layer(nc, a, XT, XN, c)
            clear_semaphores(nc)
        with nc.semaphore("out_stored") as stored, nc.Block() as block:
            @block.sync
            def _(eng):
                eng.dma_start(out, XT[:]).then_inc(stored, 16)
                eng.wait_ge(stored, 16)

def shape_constants():
    i = np.arange(P)
    row, col = i[:, None], i[None]
    eye = np.eye(P, dtype=np.float32)
    levels = []
    for n in (1 << l for l in range(7)):
        levels.append(((row // (2 * n) == col // (2 * n)) & (row // n % 2 == 0) & (col // n % 2 == 1)).astype(np.float32) + eye)
    rates = (1.0 / 10000.0 ** (np.arange(0, 8, 2, dtype=np.float32) / np.float32(8))).astype(np.float32)
    angles = np.outer(np.arange(SEQ, dtype=np.float32), rates)
    cos, sin = np.repeat(np.cos(angles), 2, -1), np.repeat(np.sin(angles), 2, -1)
    sin[:, ::2] *= -1
    rows = np.arange(1024)
    head, value = rows // 64, rows // 8 % 8
    pick = np.zeros((P, 1024), np.float32)
    pick[head * 8 + value, rows] = 1
    return {
        "row_le_col": (row <= col), "row_gt_col": (row > col), "row_ge_col": (row >= col), "row_lt_col": (row < col), "ones": np.ones((P, P)), "eye": eye,
        "iota": np.tile(np.arange(EX), (P, 1)), "ones_mean": np.full((P, P), 1 / D), "head_rows": np.arange(16)[:, None] == col // 8, "level": np.concatenate(levels, 1),
        "cos": np.tile(cos.T, (16, 1)), "sin": np.tile(sin.T, (16, 1)), "gla_pick": pick, "gla_fold": pick.T.reshape(8, P, P).transpose(1, 0, 2).reshape(P, 1024),
    }

def layouts(x):
    rows = np.arange(1024)
    head, value, key = rows // 64, rows // 8 % 8, rows % 8
    swapped = np.arange(P) ^ 1
    l0 = lambda k: x["L0_attn_" + k]
    q = lambda k: x["L0_ffn_" + k]
    l1 = lambda k: x["L1_attn_" + k]
    moe = lambda k: x["L1_ffn_" + k]
    l2 = lambda k: x["L2_attn_" + k]
    l3 = lambda k: x["L3_attn_" + k]
    f3 = lambda k: x["L3_ffn_" + k]
    return {
        "xT": l0("x").reshape(TOK, D).T, "Wba": np.concatenate([l0("Wb"), l0("Wa")], 1), "Wq": l0("Wq"), "Wk": l0("Wk"), "Wv": l0("Wv"), "Wg": l0("Wg"),
        "Wo": l0("Wo").reshape(8, P, P).transpose(1, 0, 2).reshape(P, 1024), "o_norm_w": l0("o_norm_w")[:, None], "A_log": l0("A_log"), "dt_bias": l0("dt_bias"),
        "w_up": l0("W_fc"), "w_down": l0("W_proj").reshape(4, P, P).transpose(1, 0, 2).reshape(P, 4 * P),
        "q_weights": q("qweights"), "q_scales": q("scales"), "q_lora_a": q("lora_a"), "q_lora_bT": q("lora_b").transpose(0, 2, 1),
        "q_biasT": q("biases")[1::2].T, "q_bias": q("biases")[0::2], "q_gammaT": q("ln_gamma").T, "q_betaT": q("ln_beta").T,
        "rope_w0": l1("W_Q").T, "rope_w1": l1("W_Q")[swapped].T, "rope_w2": l1("W_K").T, "rope_w3": l1("W_K")[swapped].T, "attn_wv": l1("W_V").T, "attn_wo": l1("W_O").T,
        "moe_wr": moe("Wr").T, "moe_br": moe("br"), "moe_W1": moe("W1").transpose(2, 0, 1), "moe_B1": moe("b1").reshape(8, 4, P).transpose(2, 0, 1),
        "moe_W2": moe("W2").transpose(2, 0, 1).reshape(4, P, 8, P).transpose(1, 2, 0, 3), "moe_b2": moe("b2"), "moe_gamma": moe("gamma")[:, None], "moe_beta": moe("beta")[:, None],
        "lin_wqkv": np.concatenate([l2("Wq").T, l2("Wk").T, l2("Wv").T], 1), "lin_w1": l2("W1").T, "lin_w2": l2("W2").T,
        "lin_g1": l2("g1")[:, None], "lin_g2": l2("g2"), "lin_g3": l2("g3"), "lin_lambda": l2("lambda_params"),
        "sparse_gate": x["L2_ffn_gate_kernel"], "sparse_w0": x["L2_ffn_w0"], "sparse_w1": x["L2_ffn_w1"], "sparse_wo": x["L2_ffn_wo"],
        "gla_gk1": l3("Wgk1"), "gla_gk2": l3("Wgk2"), "gla_gb": l3("bgk2")[:, None], "gla_wq": l3("Wq")[:, head * 8 + key], "gla_wk": l3("Wk")[:, head * 8 + key],
        "gla_wv": l3("Wv")[:, head * 8 + value], "gla_wg": l3("Wg"), "gla_wo": l3("Wout"), "gla_gamma": l3("gamma")[:, None], "gla_beta": l3("beta")[:, None],
        "bin_w1": f3("w1"), "bin_b1": f3("b1").reshape(4, P).T, "bin_w2": f3("w2"), "bin_b2": f3("b2")[:, None],
    }

def kernel(**inputs):
    import concourse.bacc as bacc
    from concourse.bass_utils import run_bass_kernel_spmd

    arrays = {k: np.ascontiguousarray(v) for k, v in layouts({k: np.asarray(v) for k, v in inputs.items()}).items()}
    arrays.update({k: np.ascontiguousarray(v, dtype=np.float32) for k, v in shape_constants().items()})
    nc = bacc.Bacc("TRN2", target_bir_lowering=False, num_devices=1)
    a = {k: nc.dram_tensor("in_" + k, v.shape, mybir.dt.from_np(v.dtype), kind="ExternalInput").ap() for k, v in arrays.items()}
    out = nc.dram_tensor("out_T", [D, TOK], F32, kind="ExternalOutput").ap()
    network(nc, a, out)
    result = run_bass_kernel_spmd(nc, [{"in_" + k: v for k, v in arrays.items()}], core_ids=[0])
    return np.ascontiguousarray(result.results[0]["out_T"].T).reshape(BATCH, SEQ, D)
```

```python
from contextlib import ExitStack

import numpy as np

import concourse.bass as bass
from concourse import mybir

F32 = mybir.dt.float32
BF16 = mybir.dt.bfloat16
I32 = mybir.dt.int32
U32 = mybir.dt.uint32
ALU = mybir.AluOpType
ACT = mybir.ActivationFunctionType
AX = mybir.AxisListType.X

P = 128
BATCH, SEQ, D = 4, 1024, 128
TOK = BATCH * SEQ
GRP = 512
GROUPS = TOK // GRP
CHUNK = 128
CHUNKS = TOK // CHUNK

class Steps:

    def __init__(self, sem, names):
        self.sem, self.names, self.next = sem, names.split(), 0

    def does(self, name):
        assert self.names[self.next] == name, (self.names[self.next], name)
        self.next = (self.next + 1) % len(self.names)
        return self.sem, 1

    def did(self, tile, name):
        return self.sem, tile * len(self.names) + (self.names.index(name) + 1)

class Loads:

    def __init__(self, sem):
        self.sem, self.count = sem, 0

    def one(self):
        self.count += 16
        return self.sem, 16

    def all(self):
        return self.sem, self.count

def tiles(eng, n, depth, body):
    for i in range(depth):
        body(i, i, False)
    with eng.Fori(1, n // depth) as turn:
        for s in range(depth):
            body(turn * depth + s, s, True)

def lanes(eng, n, depth, body):
    def turn(k, again):
        parts = [body(k, s, k * depth + s, again) for s in range(depth)]
        while parts:
            parts = [part for part in parts if next(part, "done") != "done"]
    turn(0, False)
    with eng.Fori(1, n // depth) as k:
        turn(k, True)

def overlapped(eng, n, front, back, order):
    def turn(i, s, before, last=False):
        parts = {"F": iter(()) if last else front(i + 1, 1 - s, min(before + 1, 2)), "B": back(i, s, before)}
        for which in order:
            next(parts[which], None)
        for which in "FB":
            for _ in parts[which]:
                pass
    for _ in front(0, 0, 0):
        pass
    turn(0, 0, 0)
    turn(1, 1, 1)
    with eng.Fori(1, n // 2 - 1) as k:
        turn(k * 2, 0, 2)
        turn(k * 2 + 1, 1, 2)
    turn(n - 2, 0, 2)
    turn(n - 1, 1, 2, last=True)

class Space:

    def __init__(self, nc, prefix, stack):
        self.nc, self.prefix, self.stack = nc, prefix, stack

    def sb(self, name, shape, dt=F32):
        return self.stack.enter_context(self.nc.sbuf_tensor(self.prefix + name, shape, dt))

    def ps(self, name, shape=(P, 512), dt=F32):
        return self.stack.enter_context(self.nc.psum_tensor(self.prefix + name, list(shape), dt))

    def sem(self, name):
        return self.stack.enter_context(self.nc.semaphore(self.prefix + name))

def over_heads(ap, n):
    return ap.unsqueeze(1).to_broadcast([P, n, ap.shape[1]])

def along(ap, n):
    return ap.unsqueeze(2).to_broadcast([P, ap.shape[1], n])

def on_all_partitions(ap):
    flat = ap.rearrange("(a n) -> a n", a=1)
    return flat.to_broadcast([P, flat.shape[1]])

def rsqrt_names(k):
    return f"ln{k} rs{k} r2{k}", f"vr{k} nt{k} rn{k}"

def rsqrt_act(nc, eng, act, g, k, v, eps, ln, rs, r2):
    nc.scalar.activation(ln, v, ACT.Ln, bias=eps).then_inc(*act.does(f"ln{k}"))
    eng.wait_ge(*act.did(g, f"ln{k}"))
    nc.scalar.activation(rs, ln, ACT.Exp, scale=-0.5).then_inc(*act.does(f"rs{k}"))
    eng.wait_ge(*act.did(g, f"rs{k}"))
    nc.scalar.activation(r2, rs, ACT.Square).then_inc(*act.does(f"r2{k}"))

def rsqrt_dve(nc, eng, act, dve, g, k, v, eps, rs, r2):
    eng.wait_ge(*act.did(g, f"r2{k}"))
    nc.vector.scalar_tensor_tensor(r2, v, eps, r2, ALU.add, ALU.mult).then_inc(*dve.does(f"vr{k}"))
    eng.wait_ge(*dve.did(g, f"vr{k}"))
    nc.vector.tensor_scalar(r2, r2, -0.5, 1.5, ALU.mult, ALU.add).then_inc(*dve.does(f"nt{k}"))
    eng.wait_ge(*dve.did(g, f"nt{k}"))
    nc.vector.tensor_tensor(rs, rs, r2, ALU.mult).then_inc(*dve.does(f"rn{k}"))
    eng.wait_ge(*dve.did(g, f"rn{k}"))

def small_rsqrt_act(nc, eng, act, g, k, v, ln, rs, r2):
    nc.scalar.activation(ln, v, ACT.Ln).then_inc(*act.does(f"ln{k}"))
    eng.wait_ge(*act.did(g, f"ln{k}"))
    nc.scalar.activation(rs, ln, ACT.Exp, scale=-0.5).then_inc(*act.does(f"rs{k}"))
    eng.wait_ge(*act.did(g, f"rs{k}"))
    nc.scalar.activation(r2, rs, ACT.Square).then_inc(*act.does(f"r2{k}"))

def norm_stage(nc, name, XT, XN, ones_mean, rms=None):
    LANES = 2 if rms else 4
    with ExitStack() as stack:
        m = Space(nc, name, stack)
        xc, sq, ln, rs, r2 = (m.sb(n, [P, LANES, GRP]) for n in "xc sq ln rs r2".split())
        eps = m.sb("eps", [P, 2])
        mean = [m.ps(f"mean{s}") for s in range(LANES)]
        var = [m.ps(f"var{s}") for s in range(LANES)]
        pe_names, act_names, dve_names = "mean var", "sq " + rsqrt_names("v")[0], "xc " + rsqrt_names("v")[1] + " xn"
        if rms:
            HT, Wba, GL = rms
            hs = m.sb("hs", [P, LANES, GRP])
            ms = [m.ps(f"ms{s}") for s in range(LANES)]
            gl = [m.ps(f"gl{s}") for s in range(LANES)]
            pe_names, act_names, dve_names = pe_names + " ms gl", act_names + " sq2 " + rsqrt_names("m")[0] + " ht", dve_names + " " + rsqrt_names("m")[1] + " hs gl"
        pe_, act_, dve_ = ([Steps(m.sem(f"{e}{s}"), names) for s in range(LANES)] for e, names in (("pe", pe_names), ("act", act_names), ("dve", dve_names)))
        ready = m.sem("ready")

        def at(t, g):
            return t[:, bass.ds(g * GRP, GRP)]

        with nc.Block() as block:
            @block.tensor
            def _(eng):
                def body(k, s, g, again):
                    pe, act, dve = pe_[s], act_[s], dve_[s]
                    if again:
                        eng.wait_ge(*dve.did(k - 1, "xn"))
                    nc.tensor.matmul(mean[s][:], ones_mean[:], at(XT, g), start=True, stop=True).then_inc(*pe.does("mean"))
                    yield
                    eng.wait_ge(*act.did(k, "sq"))
                    nc.tensor.matmul(var[s][:], ones_mean[:], sq[:, s], start=True, stop=True).then_inc(*pe.does("var"))
                    yield
                    yield
                    if rms:
                        eng.wait_ge(*act.did(k, "sq2"))
                        nc.tensor.matmul(ms[s][:], ones_mean[:], sq[:, s], start=True, stop=True).then_inc(*pe.does("ms"))
                        yield
                        yield
                        eng.wait_ge(*dve.did(k, "hs"))
                        if again:
                            eng.wait_ge(*dve.did(k - 1, "gl"))
                        for t in range(4):
                            last = nc.tensor.matmul(gl[s][:, t * 16:t * 16 + 16], hs[:, s, t * P:t * P + P], Wba[:], start=True, stop=True)
                        last.then_inc(*pe.does("gl"))
                lanes(eng, GROUPS, LANES, body)

            @block.scalar
            def _(eng):
                nc.scalar.preload_act_table_set("natural_log_exp_and_others")
                eng.wait_ge(ready, 2)
                def body(k, s, g, again):
                    pe, act, dve = pe_[s], act_[s], dve_[s]
                    eng.wait_ge(*dve.did(k, "xc"))
                    nc.scalar.activation(sq[:, s], xc[:, s], ACT.Square).then_inc(*act.does("sq"))
                    yield
                    eng.wait_ge(*pe.did(k, "var"))
                    rsqrt_act(nc, eng, act, k, "v", var[s][:], eps[:, 0:1], ln[:, s], rs[:, s], r2[:, s])
                    yield
                    yield
                    if rms:
                        eng.wait_ge(*dve.did(k, "xn"))
                        nc.scalar.activation(sq[:, s], at(XN, g), ACT.Square).then_inc(*act.does("sq2"))
                        yield
                        eng.wait_ge(*pe.did(k, "ms"))
                        rsqrt_act(nc, eng, act, k, "m", ms[s][:], eps[:, 1:2], ln[:, s], rs[:, s], r2[:, s])
                        yield
                        eng.wait_ge(*dve.did(k, "hs"))
                        nc.scalar.activation(at(HT, g), hs[:, s], ACT.Copy).then_inc(*act.does("ht"))
                lanes(eng, GROUPS, LANES, body)

            @block.vector
            def _(eng):
                nc.vector.memset(eps[:, 0:1], 1e-5).then_inc(ready, 1)
                nc.vector.memset(eps[:, 1:2], 1e-6).then_inc(ready, 1)
                def body(k, s, g, again):
                    pe, act, dve = pe_[s], act_[s], dve_[s]
                    eng.wait_ge(*pe.did(k, "mean"))
                    nc.vector.tensor_tensor(xc[:, s], at(XT, g), mean[s][:], ALU.subtract).then_inc(*dve.does("xc"))
                    yield
                    yield
                    rsqrt_dve(nc, eng, act, dve, k, "v", var[s][:], 1e-5, rs[:, s], r2[:, s])
                    nc.vector.tensor_tensor(at(XN, g), xc[:, s], rs[:, s], ALU.mult).then_inc(*dve.does("xn"))
                    yield
                    if rms:
                        yield
                        rsqrt_dve(nc, eng, act, dve, k, "m", ms[s][:], 1e-6, rs[:, s], r2[:, s])
                        if again:
                            eng.wait_ge(*act.did(k - 1, "ht"))
                        nc.vector.tensor_tensor(hs[:, s], at(XN, g), rs[:, s], ALU.mult).then_inc(*dve.does("hs"))
                        yield
                        eng.wait_ge(*pe.did(k, "gl"))
                        nc.vector.tensor_copy(GL[:, bass.ds(g * 64, 64)], gl[s][:, 0:64]).then_inc(*dve.does("gl"))
                lanes(eng, GROUPS, LANES, body)

HEADS, DK = 8, 128
PAIR = 4 * P
SC = 48

def delta_gates(nc, name, GL, SCAL, A_log, dt_bias, masks):
    N = CHUNKS * HEADS
    with ExitStack() as stack:
        m = Space(nc, name, stack)
        la = m.sb("la", [P, HEADS])
        db = m.sb("db", [P, HEADS])
        ea = m.sb("ea", [P, HEADS])
        a, y, u, d, lu, g, eb = (m.sb(n, [P, N]) for n in "a y u d lu g eb".split())
        psum = [m.ps(f"sum{k}") for k in range(3)]
        loaded, act, dve, pe = Loads(m.sem("loaded")), Steps(m.sem("act"), "ea y lu eb e0 e1 e2"), \
            Steps(m.sem("dve"), "a na u d dm rd w1 is0 w2 w sp g ps b1 b2 b zero zc neg"), Steps(m.sem("pe"), "sums")
        before_incl, everyone, after = masks["row_le_col"], masks["ones"], masks["row_gt_col"]
        gl = GL[:].rearrange("p (c k) -> p c k", k=16)
        sc = SCAL[:].rearrange("p (c k) -> p c k", k=SC)

        def v3(t):
            return t[:].rearrange("p (c h) -> p c h", h=HEADS)

        def chunks(t):
            return t[:].unsqueeze(1).to_broadcast([P, CHUNKS, HEADS])

        with nc.Block() as block:
            @block.sync
            def _(eng):
                eng.dma_start(la[:], on_all_partitions(A_log)).then_inc(*loaded.one())
                eng.dma_start(db[:], on_all_partitions(dt_bias)).then_inc(*loaded.one())
                eng.wait_ge(*loaded.all())

            @block.scalar
            def _(eng):
                nc.scalar.preload_act_table_set("natural_log_exp_and_others")
                eng.wait_ge(*loaded.all())
                nc.scalar.activation(ea[:], la[:], ACT.Exp).then_inc(*act.does("ea"))
                eng.wait_ge(*dve.did(0, "na"))
                nc.scalar.activation(y[:], y[:], ACT.Exp).then_inc(*act.does("y"))
                eng.wait_ge(*dve.did(0, "u"))
                nc.scalar.activation(lu[:], u[:], ACT.Ln).then_inc(*act.does("lu"))
                nc.scalar.activation(v3(eb), gl[:, :, 0:HEADS], ACT.Exp, scale=-1.0).then_inc(*act.does("eb"))
                eng.wait_ge(*pe.did(0, "sums"))
                for k in range(3):
                    lo = (16, 32, 40)[k]
                    nc.scalar.activation(sc[:, :, lo:lo + HEADS], psum[k][:, 0:N].rearrange("p (c h) -> p c h", h=HEADS), ACT.Exp).then_inc(*act.does(f"e{k}"))

            @block.vector
            def _(eng):
                def step(ins, name_):
                    ins.then_inc(*dve.does(name_))
                    eng.wait_ge(*dve.did(0, name_))
                eng.wait_ge(*loaded.all())
                step(nc.vector.tensor_tensor(v3(a), gl[:, :, HEADS:16], chunks(db), ALU.add), "a")
                step(nc.vector.scalar_tensor_tensor(y[:], a[:], -1.0, a[:], ALU.mult, ALU.min), "na")
                eng.wait_ge(*act.did(0, "y"))
                step(nc.vector.tensor_scalar(u[:], y[:], 1.0, None, ALU.add), "u")
                step(nc.vector.tensor_scalar(d[:], u[:], -1.0, None, ALU.add), "d")
                step(nc.vector.tensor_scalar(g[:], d[:], 1e-30, None, ALU.max), "dm")
                step(nc.vector.reciprocal(g[:], g[:]), "rd")
                step(nc.vector.tensor_tensor(g[:], g[:], y[:], ALU.mult), "w1")
                step(nc.vector.tensor_scalar(d[:], d[:], 0.0, None, ALU.is_equal), "is0")
                eng.wait_ge(*act.did(0, "lu"))
                step(nc.vector.tensor_tensor(g[:], g[:], lu[:], ALU.mult), "w2")
                step(nc.vector.tensor_tensor(d[:], d[:], y[:], ALU.mult), "w")
                step(nc.vector.scalar_tensor_tensor(d[:], a[:], 0.0, d[:], ALU.max, ALU.add), "sp")
                step(nc.vector.tensor_tensor(g[:], g[:], d[:], ALU.add), "g")
                eng.wait_ge(*act.did(0, "ea"))
                step(nc.vector.scalar_tensor_tensor(sc[:, :, 0:HEADS], v3(g), -1.0, chunks(ea), ALU.mult, ALU.mult), "ps")
                eng.wait_ge(*act.did(0, "eb"))
                step(nc.vector.tensor_scalar(eb[:], eb[:], 1.0, None, ALU.add), "b1")
                step(nc.vector.reciprocal(eb[:], eb[:]), "b2")
                step(nc.vector.tensor_copy(sc[:, :, 8:16], v3(eb)), "b")
                eng.wait_ge(*act.did(0, "e2"))
                first = SCAL[:].rearrange("p (b c k) -> p b c k", b=BATCH, k=SC)[:, :, 0, :]
                step(nc.vector.memset(first[:, :, 16:24], 0.0), "zero")
                step(nc.vector.memset(first[:, :, 32:40], 0.0), "zc")
                step(nc.vector.tensor_scalar(sc[:, :, 24:32], sc[:, :, 16:24], -1.0, None, ALU.mult), "neg")

            @block.tensor
            def _(eng):
                eng.wait_ge(*dve.did(0, "ps"))
                for k, who in enumerate((before_incl, everyone, after)):
                    last = nc.tensor.matmul(psum[k][:, 0:N].rearrange("p (c h) -> p c h", h=HEADS), who[:], sc[:, :, 0:HEADS], start=True, stop=True)
                last.then_inc(*pe.does("sums"))

def delta_stage(nc, name, HT, XN, SCAL, w, masks):
    with ExitStack() as stack:
        m = Space(nc, name, stack)

        def heads(n):
            return m.sb(n, [P, HEADS, P])

        def heads2(n):
            return [heads(f"{n}{s}") for s in range(2)]

        hc = m.sb("hc", [P, P])
        q, k, E, Em, Gm = map(heads, "q k E Em Gm".split())
        v, sg, kd, kT, qT, An, PT, Al = map(heads2, "v sg kd kT qT An PT Al".split())
        U, T, W, r, dl, oP, o, S = map(heads, "U T W r dl oP o S".split())
        osq, oT = r, oP
        ss = m.sb("ss", [P, 16])
        rr = m.sb("rr", [P, 16])
        os_ = m.sb("os", [P, 8])
        ro = m.sb("ro", [P, 8])
        half = m.sb("half", [P, 16])
        sc = m.sb("sc", [P, 2, SC])
        nb = m.sb("nb", [P, 2, HEADS])
        A = [m.ps(f"A{j}") for j in range(2)]
        B = [m.ps(f"B{j}") for j in range(2)]
        C = [m.ps(f"C{j}") for j in range(2)]
        X = [m.ps(f"X{j}") for j in range(2)]
        LEVELS = 7

        SIDES = "T A T A T A T A T A A A A - A - -".split()

        inv_pe = "z00 z01 " + " ".join(f"z{l}0 z{l}1 u{l}0 t{l}0 u{l}1 t{l}1" for l in range(1, LEVELS - 1)) + " z60 z61 u60 u61"
        inv_act = " ".join(f"u{l}0 t{l}0 u{l}1 t{l}1" for l in range(1, LEVELS - 1)) + " u60 u61"
        pe_main = Steps(m.sem("pe_main"), inv_pe + " KS0 KS1 QS0 QS1 dl0 dl1 KD0 KD1 PD0 PD1")
        pe_ahead = Steps(m.sem("pe_ahead"), "q0 q1 k0 k1 v0 v1 g0 g1 D0 D1 kT0 kT1 qT0 qT1 KK0 KK1 QK0 QK1")
        pe_tail = Steps(m.sem("pe_tail"), "oT0 oT1 Y")
        act_main = Steps(m.sem("act_main"), inv_act + " oP0 oP1")
        act_ahead = Steps(m.sem("act_ahead"), "h sc q0 q1 k0 k1 v0 v1 g0 g1 E0 E1 kT0 kT1 qT0 qT1")
        act_tail = Steps(m.sem("act_tail"), "oT0 oT1")
        dve_main = Steps(m.sem("dve_main"), " ".join(f"w{l}0 w{l}1" for l in range(LEVELS)) + " r0 r1 dl0 dl1 S0 S1 o0 o1")
        dve_ahead = Steps(m.sem("dve_ahead"), "nb ssq ssk se sq kn0 kn1 qn0 qn1 A0 A1 P0 P1")
        dve_tail = Steps(m.sem("dve_tail"), "os0 os1 oe on0 on1 og0 og1 x1")
        pool_ahead = Steps(m.sem("pool_ahead"), "qq kk Gm rr kd Em0 Es0 Em1 Es1")
        pool_main = Steps(m.sem("pool_main"), "a00 T0 a01 T1 " + " ".join(f"a{l}0 a{l}1" for l in range(1, LEVELS)))
        pool_tail = Steps(m.sem("pool_tail"), "osq0 osq1 ro")
        cleared, half_set = m.sem("cleared"), m.sem("half_set")
        hs = [slice(4 * j, 4 * j + 4) for j in range(2)]

        def bank(t):
            return t[:].rearrange("p (h n) -> p h n", h=4)

        def tok(t, i):
            return t[:, bass.ds(i * CHUNK, CHUNK)]

        def run(eng, main, ahead, tail):
            def turn(i, s, has_ahead, has_tail, again):
                parts = {"A": ahead(i + 1, 1 - s, True, again) if has_ahead else iter(()), "T": tail(i - 1, 1 - s) if has_tail else iter(()), "-": iter(())}
                order = iter(SIDES)
                main(i, s, again, lambda: next(parts[next(order)], None))
                for which in "TA":
                    for _ in parts[which]:
                        pass
            for _ in ahead(0, 0, False, False):
                pass
            turn(0, 0, True, False, False)
            with eng.Fori(0, CHUNKS // 2 - 1) as kk:
                turn(kk * 2 + 1, 1, True, True, True)
                turn(kk * 2 + 2, 0, True, True, True)
            turn(CHUNKS - 1, 1, False, True, True)
            for _ in tail(CHUNKS - 1, 1):
                pass

        with nc.Block() as block:
            @block.tensor
            def _(eng):
                def mm(out, lhsT, rhs):
                    return nc.tensor.matmul(out, lhsT, rhs, start=True, stop=True)

                def ahead(i, s, again, again2):
                    eng.wait_ge(*act_ahead.did(i, "h"))
                    for n, before in (("q", "P"), ("k", "q"), ("v", "k"), ("g", "v")):
                        for j in range(2):
                            if n != "q":
                                eng.wait_ge(*act_ahead.did(i, f"{before}{j}"))
                            elif again:
                                eng.wait_ge(*dve_ahead.did(i - 1, f"{before}{j}"))
                            if n == "g" and again2:
                                eng.wait_ge(*act_tail.did(i - 2, f"oT{j}"))
                            mm(X[j][:], hc[:], w[n][:, j * PAIR:(j + 1) * PAIR]).then_inc(*pe_ahead.does(f"{n}{j}"))
                        yield
                    eng.wait_ge(*pool_ahead.did(i, "Gm"))
                    if again2:
                        eng.wait_ge(*dve_tail.did(i - 2, "x1"))
                    for j in range(2):
                        eng.wait_ge(*act_ahead.did(i, f"g{j}"))
                        mm(X[j][:], masks["row_gt_col"][:], Gm[:, hs[j], :].rearrange("p h n -> p (h n)")).then_inc(*pe_ahead.does(f"D{j}"))
                    yield
                    for n, src, before in (("kT", k, "E"), ("qT", q, "kT")):
                        for j in range(2):
                            eng.wait_ge(*act_ahead.did(i, f"{before}{j}"))
                            eng.wait_ge(*dve_ahead.did(i, f"{n[0]}n{j}"))
                            for h in range(4):
                                last = nc.tensor.transpose(bank(X[j])[:, h, :], src[:, 4 * j + h, :], masks["eye"][:])
                            last.then_inc(*pe_ahead.does(f"{n}{j}"))
                        yield
                    for j in range(2):
                        eng.wait_ge(*act_ahead.did(i, f"qT{j}"))
                        for h in range(4 * j, 4 * j + 4):
                            last = mm(bank(X[j])[:, h % 4, :], kT[s][:, h, :], kT[s][:, h, :])
                        last.then_inc(*pe_ahead.does(f"KK{j}"))
                    yield
                    for j in range(2):
                        eng.wait_ge(*dve_ahead.did(i, f"A{j}"))
                        for h in range(4 * j, 4 * j + 4):
                            last = mm(bank(X[j])[:, h % 4, :], kT[s][:, h, :], qT[s][:, h, :])
                        last.then_inc(*pe_ahead.does(f"QK{j}"))
                    yield

                def main(i, s, again, place):
                    def prev(who, step):
                        if again:
                            eng.wait_ge(*who.did(i - 1, step))
                    for l in range(LEVELS):
                        for j in range(2):
                            eng.wait_ge(*pool_main.did(i, f"a{l}{j}"))
                            if l:
                                eng.wait_ge(*dve_main.did(i, f"w{l - 1}{j}"))
                                if l > 1:
                                    eng.wait_ge(*act_main.did(i, f"u{l - 1}{j}"))
                            else:
                                prev(act_main, f"oP{j}")
                            for h in range(4 * j, 4 * j + 4):
                                last = mm(bank(B[j])[:, h % 4, :], Al[l % 2][:, h, :], U[:, h, :] if l else masks["eye"][:])
                            last.then_inc(*pe_main.does(f"z{l}{j}"))
                        place()
                        for j in range(2):
                            if l:
                                eng.wait_ge(*dve_main.did(i, f"w{l}{j}"))
                                if l == 1:
                                    eng.wait_ge(*pool_main.did(i, f"T{j}"))
                                    prev(dve_main, f"S{j}")
                                    prev(dve_main, f"o{j}")
                                else:
                                    eng.wait_ge(*(act_main.did(i, f"t{l - 1}{j}")))
                                for h in range(4 * j, 4 * j + 4):
                                    last = mm(bank(C[j])[:, h % 4, :], T[:, h, :], W[:, h, :]) if l < LEVELS - 1 else mm(bank(C[j])[:, h % 4, :], W[:, h, :], T[:, h, :])
                                last.then_inc(*pe_main.does(f"u{l}{j}"))
                            if 0 < l < LEVELS - 1:
                                for h in range(4 * j, 4 * j + 4):
                                    last = mm(bank(A[j])[:, h % 4, :], W[:, h, :], T[:, h, :])
                                last.then_inc(*pe_main.does(f"t{l}{j}"))
                        place()
                    if not again:
                        eng.wait_ge(cleared, 1)
                    for n, src, bk in (("KS", kT[s], B), ("QS", qT[s], A)):
                        for j in range(2):
                            prev(dve_main, f"S{j}")
                            for h in range(4 * j, 4 * j + 4):
                                last = mm(bank(bk[j])[:, h % 4, :], src[:, h, :], S[:, h, :])
                            last.then_inc(*pe_main.does(f"{n}{j}"))
                    place()
                    for j in range(2):
                        eng.wait_ge(*dve_main.did(i, f"r{j}"))
                        eng.wait_ge(*act_main.did(i, f"u6{j}"))
                        for h in range(4 * j, 4 * j + 4):
                            last = mm(bank(C[j])[:, h % 4, :], U[:, h, :], r[:, h, :])
                        last.then_inc(*pe_main.does(f"dl{j}"))
                    place()
                    for n, src, bk in (("KD", kd[s], C), ("PD", PT[s], B)):
                        for j in range(2):
                            eng.wait_ge(*dve_main.did(i, f"dl{j}"))
                            if n == "KD":
                                eng.wait_ge(*pool_ahead.did(i, "kd"))
                            else:
                                eng.wait_ge(*dve_ahead.did(i, f"P{j}"))
                            for h in range(4 * j, 4 * j + 4):
                                last = mm(bank(bk[j])[:, h % 4, :], src[:, h, :], dl[:, h, :])
                            last.then_inc(*pe_main.does(f"{n}{j}"))
                    place()

                def tail(i, s):
                    yield
                    yield
                    yield
                    for j in range(2):
                        eng.wait_ge(*dve_tail.did(i, f"og{j}"))
                        if not (isinstance(i, int) and i >= CHUNKS - 2):
                            eng.wait_ge(*act_ahead.did(i + 2, f"v{j}"))
                        for h in range(4 * j, 4 * j + 4):
                            last = nc.tensor.transpose(bank(X[j])[:, h % 4, :], o[:, h, :], masks["eye"][:])
                        last.then_inc(*pe_tail.does(f"oT{j}"))
                    yield
                    eng.wait_ge(*act_tail.did(i, "oT1"))
                    if not (isinstance(i, int) and i >= CHUNKS - 2):
                        eng.wait_ge(*act_ahead.did(i + 2, "g0"))
                    for h in range(HEADS):
                        last = nc.tensor.matmul(X[0][:, 0:P], w["o"][:, h * P:(h + 1) * P], oT[:, h, :], start=(h == 0), stop=(h == HEADS - 1))
                    last.then_inc(*pe_tail.does("Y"))
                    yield
                run(eng, main, ahead, tail)

            @block.scalar
            def _(eng):
                def ahead(i, s, again, again2):
                    def prev(who, step):
                        if again:
                            eng.wait_ge(*who.did(i - 1, step))

                    def prev2(who, step):
                        if again2:
                            eng.wait_ge(*who.did(i - 2, step))
                    prev(pe_ahead, "g1")
                    nc.scalar.activation(hc[:], tok(HT, i), ACT.Copy).then_inc(*act_ahead.does("h"))
                    prev2(dve_main, "o1")
                    prev2(pool_ahead, "kd")
                    nc.scalar.activation(sc[:, s], SCAL[:, bass.ds(i * SC, SC)], ACT.Copy).then_inc(*act_ahead.does("sc"))
                    for n, dst in (("q", q), ("k", k), ("v", v[s]), ("g", sg[s])):
                        for j in range(2):
                            eng.wait_ge(*pe_ahead.did(i, f"{n}{j}"))
                            if n == "q":
                                prev(pe_ahead, "qT1")
                            elif n == "k":
                                prev(pool_ahead, "kd")
                            elif n == "v":
                                prev2(dve_main, f"r{j}")
                            else:
                                prev2(dve_tail, f"og{j}")
                            nc.scalar.activation(dst[:, hs[j], :], bank(X[j]), ACT.Silu).then_inc(*act_ahead.does(f"{n}{j}"))
                        yield
                    for j in range(2):
                        eng.wait_ge(*pe_ahead.did(i, f"D{j}"))
                        prev(dve_ahead, f"A{j}")
                        nc.scalar.activation(E[:, hs[j], :], bank(X[j]), ACT.Exp).then_inc(*act_ahead.does(f"E{j}"))
                    yield
                    for n, dst, used in (("kT", kT[s], "KS"), ("qT", qT[s], "QS")):
                        for j in range(2):
                            eng.wait_ge(*pe_ahead.did(i, f"{n}{j}"))
                            prev2(pe_main, f"{used}{j}")
                            nc.scalar.activation(dst[:, hs[j], :], bank(X[j]), ACT.Copy).then_inc(*act_ahead.does(f"{n}{j}"))
                        yield
                    yield
                    yield

                def main(i, s, again, place):
                    for l in range(LEVELS):
                        place()
                        for j in range(2):
                            if l:
                                eng.wait_ge(*pe_main.did(i, f"u{l}{j}"))
                                nc.scalar.activation(U[:, hs[j], :], bank(C[j]), ACT.Copy).then_inc(*act_main.does(f"u{l}{j}"))
                            if 0 < l < LEVELS - 1:
                                eng.wait_ge(*pe_main.did(i, f"t{l}{j}"))
                                nc.scalar.activation(T[:, hs[j], :], bank(A[j]), ACT.Copy).then_inc(*act_main.does(f"t{l}{j}"))
                        place()
                    place()
                    place()
                    for j in range(2):
                        eng.wait_ge(*pe_main.did(i, f"PD{j}"))
                        if again:
                            eng.wait_ge(*pe_tail.did(i - 1, "Y"))
                        nc.scalar.activation(oP[:, hs[j], :], bank(B[j]), ACT.Copy).then_inc(*act_main.does(f"oP{j}"))
                    place()

                def tail(i, s):
                    yield
                    yield
                    yield
                    for j in range(2):
                        eng.wait_ge(*pe_tail.did(i, f"oT{j}"))
                        if j == 0:
                            eng.wait_ge(*dve_main.did(i, "o1"))
                        nc.scalar.activation(oT[:, hs[j], :], bank(X[j]), ACT.Copy).then_inc(*act_tail.does(f"oT{j}"))
                    yield
                    yield
                run(eng, main, ahead, tail)

            @block.vector
            def _(eng):
                nc.vector.memset(S[:], 0.0).then_inc(cleared, 1)

                def ahead(i, s, again, again2):
                    yield
                    yield
                    eng.wait_ge(*act_ahead.did(i, "sc"))
                    nc.vector.tensor_scalar(nb[:, s], sc[:, s, 8:16], -1.0, None, ALU.mult).then_inc(*dve_ahead.does("nb"))
                    eng.wait_ge(*pool_ahead.did(i, "qq"))
                    if again:
                        eng.wait_ge(*pool_ahead.did(i - 1, "rr"))
                    nc.vector.tensor_reduce(ss[:, 0:8], Gm[:], AX, ALU.add).then_inc(*dve_ahead.does("ssq"))
                    yield
                    eng.wait_ge(*pool_ahead.did(i, "kk"))
                    nc.vector.tensor_reduce(ss[:, 8:16], Em[:], AX, ALU.add).then_inc(*dve_ahead.does("ssk"))
                    eng.wait_ge(*dve_ahead.did(i, "ssk"))
                    nc.vector.tensor_scalar(ss[:], ss[:], 1e-6, None, ALU.add).then_inc(*dve_ahead.does("se"))
                    yield
                    eng.wait_ge(*pool_ahead.did(i, "rr"))
                    nc.vector.tensor_scalar(rr[:, 0:8], rr[:, 0:8], float(DK) ** -0.5, None, ALU.mult).then_inc(*dve_ahead.does("sq"))
                    eng.wait_ge(*dve_ahead.did(i, "sq"))
                    for n, t, lo in (("k", k, 8), ("q", q, 0)):
                        for j in range(2):
                            nc.vector.tensor_tensor(t[:, hs[j], :], t[:, hs[j], :], along(rr[:, lo + 4 * j:lo + 4 * j + 4], P), ALU.mult).then_inc(*dve_ahead.does(f"{n}n{j}"))
                        yield
                    yield
                    for j in range(2):
                        eng.wait_ge(*pe_ahead.did(i, f"KK{j}"))
                        eng.wait_ge(*pool_ahead.did(i, f"Es{j}"))
                        if again2:
                            eng.wait_ge(*pool_main.did(i - 2, f"a{LEVELS - 1}{j}"))
                        for h in range(4 * j, 4 * j + 4):
                            last = nc.vector.scalar_tensor_tensor(An[s][:, h, :], bank(X[j])[:, h % 4, :], nb[:, s, h:h + 1], E[:, h, :], ALU.mult, ALU.mult)
                        last.then_inc(*dve_ahead.does(f"A{j}"))
                    yield
                    for j in range(2):
                        eng.wait_ge(*pe_ahead.did(i, f"QK{j}"))
                        if again2:
                            eng.wait_ge(*pe_main.did(i - 2, f"PD{j}"))
                        nc.vector.tensor_tensor(PT[s][:, hs[j], :], bank(X[j]), Em[:, hs[j], :], ALU.mult).then_inc(*dve_ahead.does(f"P{j}"))
                    yield

                def main(i, s, again, place):
                    for l in range(LEVELS):
                        dst = W if l else U
                        for j in range(2):
                            eng.wait_ge(*pe_main.did(i, f"z{l}{j}"))
                            if l == 0 and again:
                                eng.wait_ge(*pe_main.did(i - 1, f"dl{j}"))
                            nc.vector.tensor_tensor(dst[:, hs[j], :], bank(B[j]), over_heads(masks["eye"][:], 4), ALU.add).then_inc(*dve_main.does(f"w{l}{j}"))
                        place()
                        place()
                    for j in range(2):
                        eng.wait_ge(*pe_main.did(i, f"KS{j}"))
                        eng.wait_ge(*act_ahead.did(i, f"v{j}"))
                        for h in range(4 * j, 4 * j + 4):
                            last = nc.vector.scalar_tensor_tensor(r[:, h, :], bank(B[j])[:, h % 4, :], sc[:, s, 24 + h:25 + h], v[s][:, h, :], ALU.mult, ALU.add)
                        last.then_inc(*dve_main.does(f"r{j}"))
                    place()
                    for j in range(2):
                        eng.wait_ge(*pe_main.did(i, f"dl{j}"))
                        nc.vector.tensor_tensor(dl[:, hs[j], :], bank(C[j]), along(sc[:, s, 8 + 4 * j:12 + 4 * j], P), ALU.mult).then_inc(*dve_main.does(f"dl{j}"))
                    place()
                    for j in range(2):
                        eng.wait_ge(*pe_main.did(i, f"KD{j}"))
                        for h in range(4 * j, 4 * j + 4):
                            last = nc.vector.scalar_tensor_tensor(S[:, h, :], S[:, h, :], sc[:, s, 32 + h:33 + h], bank(C[j])[:, h % 4, :], ALU.mult, ALU.add)
                        last.then_inc(*dve_main.does(f"S{j}"))
                    for j in range(2):
                        eng.wait_ge(*pe_main.did(i, f"QS{j}"))
                        eng.wait_ge(*act_main.did(i, f"oP{j}"))
                        if again:
                            eng.wait_ge(*pe_tail.did(i - 1, f"oT{j}"))
                        for h in range(4 * j, 4 * j + 4):
                            last = nc.vector.scalar_tensor_tensor(o[:, h, :], bank(A[j])[:, h % 4, :], sc[:, s, 16 + h:17 + h], oP[:, h, :], ALU.mult, ALU.add)
                        last.then_inc(*dve_main.does(f"o{j}"))
                    place()

                def tail(i, s):
                    yield
                    for j in range(2):
                        eng.wait_ge(*pool_tail.did(i, f"osq{j}"))
                        nc.vector.tensor_reduce(os_[:, 4 * j:4 * j + 4], osq[:, hs[j], :], AX, ALU.add).then_inc(*dve_tail.does(f"os{j}"))
                    eng.wait_ge(*dve_tail.did(i, "os1"))
                    nc.vector.tensor_scalar(os_[:], os_[:], 1.0 / DK, 1e-6, ALU.mult, ALU.add).then_inc(*dve_tail.does("oe"))
                    yield
                    eng.wait_ge(*pool_tail.did(i, "ro"))
                    for j in range(2):
                        nc.vector.tensor_tensor(o[:, hs[j], :], o[:, hs[j], :], along(ro[:, 4 * j:4 * j + 4], P), ALU.mult).then_inc(*dve_tail.does(f"on{j}"))
                    for j in range(2):
                        eng.wait_ge(*dve_tail.did(i, f"on{j}"))
                        nc.vector.tensor_tensor(o[:, hs[j], :], o[:, hs[j], :], sg[s][:, hs[j], :], ALU.mult).then_inc(*dve_tail.does(f"og{j}"))
                    yield
                    yield
                    eng.wait_ge(*pe_tail.did(i, "Y"))
                    nc.vector.tensor_tensor(tok(HT, i), X[0][:, 0:P], tok(XN, i), ALU.add).then_inc(*dve_tail.does("x1"))
                    yield
                run(eng, main, ahead, tail)

            @block.gpsimd
            def _(eng):
                nc.gpsimd.memset(half[:], -0.5).then_inc(half_set, 1)
                eng.wait_ge(half_set, 1)

                def ahead(i, s, again, again2):
                    def prev(who, step):
                        if again:
                            eng.wait_ge(*who.did(i - 1, step))
                    yield
                    eng.wait_ge(*act_ahead.did(i, "q1"))
                    prev(pe_ahead, "D1")
                    nc.gpsimd.tensor_tensor(Gm[:], q[:], q[:], ALU.mult).then_inc(*pool_ahead.does("qq"))
                    yield
                    eng.wait_ge(*act_ahead.did(i, "k1"))
                    prev(dve_ahead, "P1")
                    nc.gpsimd.tensor_tensor(Em[:], k[:], k[:], ALU.mult).then_inc(*pool_ahead.does("kk"))
                    eng.wait_ge(*dve_ahead.did(i, "ssq"))
                    nc.gpsimd.tensor_tensor(Gm[:], over_heads(masks["row_le_col"][:], HEADS), along(sc[:, s, 0:8], P), ALU.mult).then_inc(*pool_ahead.does("Gm"))
                    yield
                    eng.wait_ge(*dve_ahead.did(i, "se"))
                    prev(dve_ahead, "qn1")
                    nc.gpsimd.tensor_tensor(rr[:], ss[:], half[:], ALU.pow).then_inc(*pool_ahead.does("rr"))
                    yield
                    eng.wait_ge(*dve_ahead.did(i, "kn1"))
                    if again2:
                        eng.wait_ge(*pe_main.did(i - 2, "KD1"))
                    nc.gpsimd.tensor_tensor(kd[s][:], k[:], along(sc[:, s, 40:48], P), ALU.mult).then_inc(*pool_ahead.does("kd"))
                    yield
                    for j in range(2):
                        eng.wait_ge(*act_ahead.did(i, f"E{j}"))
                        nc.gpsimd.tensor_tensor(Em[:, hs[j], :], E[:, hs[j], :], over_heads(masks["row_le_col"][:], 4), ALU.mult).then_inc(*pool_ahead.does(f"Em{j}"))
                        eng.wait_ge(*pool_ahead.did(i, f"Em{j}"))
                        nc.gpsimd.tensor_tensor(E[:, hs[j], :], E[:, hs[j], :], over_heads(masks["row_lt_col"][:], 4), ALU.mult).then_inc(*pool_ahead.does(f"Es{j}"))
                    yield

                def main(i, s, again, place):
                    def level(l):
                        for j in range(2):
                            if l >= 2:
                                eng.wait_ge(*pe_main.did(i, f"z{l - 2}{j}"))
                                eng.wait_ge(*pool_main.did(i, f"T{j}"))
                            elif again:
                                eng.wait_ge(*pe_main.did(i - 1, f"z{LEVELS - 1 - l}{j}"))
                            if l == 0:
                                eng.wait_ge(*dve_ahead.did(i, f"A{j}"))
                            nc.gpsimd.tensor_tensor(Al[l % 2][:, hs[j], :], An[s][:, hs[j], :], over_heads(masks["level"][:, l * P:(l + 1) * P], 4), ALU.mult).then_inc(*pool_main.does(f"a{l}{j}"))
                            if l == 0:
                                eng.wait_ge(*pool_main.did(i, f"a0{j}"))
                                if again:
                                    eng.wait_ge(*pe_main.did(i - 1, f"u{LEVELS - 1}{j}"))
                                nc.gpsimd.tensor_tensor(T[:, hs[j], :], Al[0][:, hs[j], :], over_heads(masks["eye"][:], 4), ALU.add).then_inc(*pool_main.does(f"T{j}"))
                    level(0)
                    level(1)
                    for l in range(LEVELS):
                        place()
                        if l + 2 < LEVELS:
                            level(l + 2)
                        place()
                    for _ in range(3):
                        place()

                def tail(i, s):
                    for j in range(2):
                        eng.wait_ge(*dve_main.did(i, f"o{j}"))
                        eng.wait_ge(*pe_main.did(i, f"dl{j}"))
                        nc.gpsimd.tensor_tensor(osq[:, hs[j], :], o[:, hs[j], :], o[:, hs[j], :], ALU.mult).then_inc(*pool_tail.does(f"osq{j}"))
                    yield
                    eng.wait_ge(*dve_tail.did(i, "oe"))
                    nc.gpsimd.tensor_tensor(ro[:], os_[:], half[:, 0:8], ALU.pow).then_inc(*pool_tail.does("ro"))
                    yield
                run(eng, main, ahead, tail)

def at_group(t, g):
    return t[:, bass.ds(g * GRP, GRP)]

def relu_mlp_stage(nc, name, XT, X1, w_up, w_down, ones_mean):
    F = w_up.shape[1] // P
    with ExitStack() as stack:
        m = Space(nc, name, stack)
        sq, ln, rs, r2, xm = (m.sb(n, [P, 2, GRP]) for n in "sq ln rs r2 xm".split())
        r = m.sb("r", [P, F, GRP])
        hid = m.sb("hid", [P, F, GRP])
        xs = m.sb("xs", [P, 2, GRP])
        eps = m.sb("eps", [P, 1])
        ms = m.ps("ms")
        up = [m.ps(f"up{c}") for c in range(F)]
        down = m.ps("down")
        pe_f, pe = Steps(m.sem("pe_front"), "ms"), Steps(m.sem("pe"), " ".join(f"up{c}" for c in range(F)) + " down")
        act_f, act = Steps(m.sem("act_front"), "sq " + rsqrt_names("m")[0]), Steps(m.sem("act"), " ".join(f"r{c}" for c in range(F)))
        dve_f, dve = Steps(m.sem("dve_front"), rsqrt_names("m")[1] + " xm xs"), Steps(m.sem("dve"), " ".join(f"hid{c}" for c in range(F)) + " out")
        ready = m.sem("ready")
        with nc.Block() as block:
            @block.tensor
            def _(eng):
                def front(g, s, before):
                    eng.wait_ge(*act_f.did(g, "sq"))
                    if before:
                        eng.wait_ge(*dve_f.did(g - 1, "xm"))
                    nc.tensor.matmul(ms[:], ones_mean[:], sq[:, s], start=True, stop=True).then_inc(*pe_f.does("ms"))
                    yield
                    yield

                def back(g, s, before):
                    eng.wait_ge(*dve_f.did(g, "xm"))
                    for c in range(F):
                        if before:
                            eng.wait_ge(*dve.did(g - 1, f"hid{c}"))
                        nc.tensor.matmul(up[c][:], w_up[:, c * P:(c + 1) * P], xm[:, s], start=True, stop=True).then_inc(*pe.does(f"up{c}"))
                    yield
                    if before:
                        eng.wait_ge(*dve.did(g - 1, "out"))
                    for c in range(F):
                        eng.wait_ge(*dve.did(g, f"hid{c}"))
                        last = nc.tensor.matmul(down[:], w_down[:, c * P:(c + 1) * P], hid[:, c], start=(c == 0), stop=(c == F - 1))
                    last.then_inc(*pe.does("down"))
                    yield
                overlapped(eng, GROUPS, front, back, "FBFB")

            @block.scalar
            def _(eng):
                nc.scalar.preload_act_table_set("natural_log_exp_and_others")
                eng.wait_ge(ready, 1)
                def front(g, s, before):
                    nc.scalar.activation(sq[:, s], at_group(X1, g), ACT.Square).then_inc(*act_f.does("sq"))
                    yield
                    eng.wait_ge(*pe_f.did(g, "ms"))
                    rsqrt_act(nc, eng, act_f, g, "m", ms[:], eps[:], ln[:, s], rs[:, s], r2[:, s])
                    yield

                def back(g, s, before):
                    for c in range(F):
                        eng.wait_ge(*pe.did(g, f"up{c}"))
                        if before:
                            eng.wait_ge(*dve.did(g - 1, f"hid{c}"))
                        nc.scalar.activation(r[:, c], up[c][:], ACT.Relu).then_inc(*act.does(f"r{c}"))
                    yield
                overlapped(eng, GROUPS, front, back, "FBFB")

            @block.vector
            def _(eng):
                nc.vector.memset(eps[:], 1e-6).then_inc(ready, 1)
                def front(g, s, before):
                    yield
                    rsqrt_dve(nc, eng, act_f, dve_f, g, "m", ms[:], 1e-6, rs[:, s], r2[:, s])
                    nc.vector.tensor_tensor(xm[:, s], at_group(X1, g), rs[:, s], ALU.mult).then_inc(*dve_f.does("xm"))
                    nc.vector.tensor_tensor(xs[:, s], at_group(XT, g), at_group(X1, g), ALU.add).then_inc(*dve_f.does("xs"))
                    yield

                def back(g, s, before):
                    for c in range(F):
                        eng.wait_ge(*act.did(g, f"r{c}"))
                        if before:
                            eng.wait_ge(*pe.did(g - 1, "down"))
                        nc.vector.scalar_tensor_tensor(hid[:, c], up[c][:], 0.0, r[:, c], ALU.max, ALU.mult).then_inc(*dve.does(f"hid{c}"))
                    yield
                    eng.wait_ge(*pe.did(g, "down"))
                    eng.wait_ge(*dve_f.did(g, "xs"))
                    nc.vector.tensor_tensor(at_group(XT, g), down[:], xs[:, s], ALU.add).then_inc(*dve.does("out"))
                    yield
                overlapped(eng, GROUPS, front, back, "FBFB")

def gelu_mlp_stage(nc, name, XT, XN, w1, w2, bias1, bias2):
    F = w1.shape[1] // P
    with ExitStack() as stack:
        m = Space(nc, name, stack)
        hid = m.sb("hid", [P, 2, F, GRP])
        up = [m.ps(f"up{c}") for c in range(F)]
        down = [m.ps(f"down{s}") for s in range(2)]
        pe = Steps(m.sem("pe"), " ".join(f"up{c}" for c in range(F)) + " down")
        act = Steps(m.sem("act"), " ".join(f"hid{c}" for c in range(F)))
        dve = Steps(m.sem("dve"), "out")
        with nc.Block() as block:
            @block.tensor
            def _(eng):
                def body(g, s, again):
                    for c in range(F):
                        if s or again:
                            eng.wait_ge(*act.did(g - 1, f"hid{c}"))
                        nc.tensor.matmul(up[c][:], w1[:, c * P:(c + 1) * P], at_group(XN, g), start=True, stop=True).then_inc(*pe.does(f"up{c}"))
                    if again:
                        eng.wait_ge(*dve.did(g - 2, "out"))
                    for c in range(F):
                        eng.wait_ge(*act.did(g, f"hid{c}"))
                        last = nc.tensor.matmul(down[s][:], w2[:, c * P:(c + 1) * P], hid[:, s, c], start=(c == 0), stop=(c == F - 1))
                    last.then_inc(*pe.does("down"))
                tiles(eng, GROUPS, 2, body)

            @block.scalar
            def _(eng):
                def body(g, s, again):
                    if again:
                        eng.wait_ge(*pe.did(g - 2, "down"))
                    for c in range(F):
                        eng.wait_ge(*pe.did(g, f"up{c}"))
                        nc.scalar.activation(hid[:, s, c], up[c][:], ACT.Gelu, bias=bias1[:, c:c + 1]).then_inc(*act.does(f"hid{c}"))
                tiles(eng, GROUPS, 2, body)

            @block.vector
            def _(eng):
                def body(g, s, again):
                    eng.wait_ge(*pe.did(g, "down"))
                    nc.vector.scalar_tensor_tensor(at_group(XT, g), down[s][:], bias2[:, 0:1], at_group(XT, g), ALU.add, ALU.add).then_inc(*dve.does("out"))
                tiles(eng, GROUPS, 2, body)

def binary_weights(nc, name, w1_in, w2_in, w1, w2, eye):
    H = w1_in.shape[0]
    F = H // P
    with ExitStack() as stack:
        m = Space(nc, name, stack)
        raw = m.sb("raw", [P, 2, F, P])
        mag = m.sb("mag", [P, 2, F, P])
        sign = m.sb("sign", [P, 2, F, P])
        al = m.sb("al", [P, 2, F])
        turned = [m.ps(f"turned{k}") for k in range(2)]
        loaded = Loads(m.sem("loaded"))
        act, dve, pe = Steps(m.sem("act"), "mag sign w0 w1"), Steps(m.sem("dve"), "sum1 sum2 mean1 mean2 a1 a2 diff w"), Steps(m.sem("pe"), "t0 t1")
        with nc.Block() as block:
            @block.sync
            def _(eng):
                eng.dma_start(raw[:, 0], w1_in.rearrange("(c p) d -> p c d", p=P)).then_inc(*loaded.one())
                eng.dma_start(raw[:, 1], w2_in.rearrange("d (c p) -> d c p", p=P)).then_inc(*loaded.one())

            @block.scalar
            def _(eng):
                eng.wait_ge(*loaded.all())
                nc.scalar.activation(mag[:], raw[:], ACT.Abs).then_inc(*act.does("mag"))
                nc.scalar.activation(sign[:], raw[:], ACT.Sign).then_inc(*act.does("sign"))
                for k, dst in enumerate((w1, w2)):
                    eng.wait_ge(*pe.did(0, f"t{k}"))
                    nc.scalar.activation(dst[:], turned[k][:], ACT.Copy).then_inc(*act.does(f"w{k}"))

            @block.vector
            def _(eng):
                def step(ins, name_):
                    ins.then_inc(*dve.does(name_))
                    eng.wait_ge(*dve.did(0, name_))
                eng.wait_ge(*act.did(0, "mag"))
                step(nc.vector.tensor_reduce(al[:, 0], mag[:, 0], AX, ALU.add), "sum1")
                step(nc.vector.tensor_reduce(al[:, 1, 0:1], mag[:, 1].rearrange("p c n -> p (c n)"), AX, ALU.add), "sum2")
                step(nc.vector.tensor_scalar(al[:, 0], al[:, 0], 1.0 / P, None, ALU.mult), "mean1")
                step(nc.vector.tensor_scalar(al[:, 1, 0:1], al[:, 1, 0:1], 1.0 / H, None, ALU.mult), "mean2")
                eng.wait_ge(*act.did(0, "sign"))
                step(nc.vector.tensor_tensor(mag[:, 0], sign[:, 0], along(al[:, 0], P), ALU.mult), "a1")
                step(nc.vector.tensor_scalar(mag[:, 1], sign[:, 1], al[:, 1, 0:1], None, ALU.mult), "a2")
                step(nc.vector.tensor_tensor(mag[:], mag[:], raw[:], ALU.subtract), "diff")
                step(nc.vector.tensor_tensor(mag[:], mag[:], raw[:], ALU.add), "w")

            @block.tensor
            def _(eng):
                eng.wait_ge(*dve.did(0, "w"))
                for k in range(2):
                    for c in range(F):
                        last = nc.tensor.transpose(turned[k][:, c * P:(c + 1) * P], mag[:, k, c], eye[:])
                    last.then_inc(*pe.does(f"t{k}"))

def qlora_weights(nc, name, q_in, scales, lora_a, lora_bT, WQ, eye):
    L, GROUP = q_in.shape[0], 16
    R = lora_a.shape[1]
    with ExitStack() as stack:
        m = Space(nc, name, stack)
        qi = m.sb("qi", [P, L, P], q_in.dtype)
        wf = m.sb("wf", [P, L, P])
        sc = m.sb("sc", [P, L, P // GROUP])
        la = m.sb("la", [R, L, P])
        lb = m.sb("lb", [R, L, P])
        low = [m.ps(f"low{k}") for k in range(2)]
        turned = [m.ps(f"turned{k}") for k in range(2)]
        loaded = Loads(m.sem("loaded"))
        pe, dve = Steps(m.sem("pe"), "low turned"), Steps(m.sem("dve"), "float affine scaled sum0 sum1 w0 w1")
        parts = [slice(0, 4), slice(4, L)]

        def bank(t, n):
            return t[:, 0:n * P].rearrange("p (l n) -> p l n", n=P)
        with nc.Block() as block:
            @block.sync
            def _(eng):
                eng.dma_start(qi[:], q_in.rearrange("l o i -> o l i")).then_inc(*loaded.one())
                eng.dma_start(sc[:], scales.rearrange("l o g -> o l g")).then_inc(*loaded.one())
                eng.dma_start(la[:], lora_a.rearrange("l r i -> r l i")).then_inc(*loaded.one())
                eng.dma_start(lb[:], lora_bT.rearrange("l r o -> r l o")).then_inc(*loaded.one())

            @block.tensor
            def _(eng):
                eng.wait_ge(*loaded.all())
                for l in range(L):
                    last = nc.tensor.matmul(bank(low[l // 4], 4)[:, l % 4, :], lb[:, l], la[:, l], start=True, stop=True)
                last.then_inc(*pe.does("low"))
                eng.wait_ge(*dve.did(0, "sum1"))
                for l in range(L):
                    last = nc.tensor.transpose(bank(turned[l // 4], 4)[:, l % 4, :], wf[:, l], eye[:])
                last.then_inc(*pe.does("turned"))

            @block.vector
            def _(eng):
                def step(ins, name_):
                    ins.then_inc(*dve.does(name_))
                    eng.wait_ge(*dve.did(0, name_))
                eng.wait_ge(*loaded.all())
                step(nc.vector.tensor_copy(wf[:], qi[:]), "float")
                step(nc.vector.tensor_scalar(wf[:], wf[:], 1.0 / 7.5, -1.0, ALU.mult, ALU.add), "affine")
                w4 = wf[:].rearrange("p l (g k) -> p (l g) k", k=GROUP)
                step(nc.vector.tensor_tensor(w4, w4, along(sc[:].rearrange("p l g -> p (l g)"), GROUP), ALU.mult), "scaled")
                eng.wait_ge(*pe.did(0, "low"))
                for k, part in enumerate(parts):
                    step(nc.vector.tensor_tensor(wf[:, part], wf[:, part], bank(low[k], part.stop - part.start), ALU.add), f"sum{k}")
                eng.wait_ge(*pe.did(0, "turned"))
                for k, part in enumerate(parts):
                    nc.vector.tensor_copy(WQ[:, part], bank(turned[k], part.stop - part.start)).then_inc(*dve.does(f"w{k}"))

def qlora_stage(nc, name, XT, XN, WQ, biasT, bias_rows, gammaT, betaT, eye):
    L = 4
    with ExitStack() as stack:
        m = Space(nc, name, stack)
        h = m.sb("h", [P, L, GRP])
        y = m.sb("y", [P, L, 4, P])
        z = m.sb("z", [P, L, 4, P])
        yT = m.sb("yT", [P, L, GRP])
        st = m.sb("st", [P, L, 4, 6])
        ag = m.sb("ag", [P, L, 4, 2])
        rs = m.sb("rs", [P, L, 4])
        ve = m.sb("ve", [P, L, 4])
        half = m.sb("half", [P, 4])
        carrier = m.sb("carrier", [P, L])
        lin = [m.ps(f"lin{s}") for s in range(L)]
        turned = [m.ps(f"turned{s}") for s in range(L)]
        back = lin
        N = 3
        def steps(names):
            return " ".join(f"{n}{b}{s}" for b in range(N) for n in names.split() for s in range(L))
        def each(name_):
            return " ".join(f"{name_}{s}" for s in range(L))
        pe = Steps(m.sem("pe"), steps("lin turned back"))
        act = Steps(m.sem("act"), each("h") + " " + steps("gelu"))
        dve = Steps(m.sem("dve"), " ".join(" ".join([f"{n}{b}{s}" for n in ("y", "st") for s in range(L)] + [f"{n}{b}{s}" for s in range(L) for n in ("cr", "ag")] + [f"{n}{b}{s}" for n in ("ve", "z", "h") for s in range(L)]) for b in range(N)) + " " + each("out"))
        pool = Steps(m.sem("pool"), steps("rs"))
        half_set = m.sem("half_set")

        with nc.Block() as block:
            @block.tensor
            def _(eng):
                def body(i, _, again):
                    for b in range(N):
                        for s in range(L):
                            if b == 0:
                                eng.wait_ge(*act.did(i, f"h{s}"))
                                if again:
                                    eng.wait_ge(*dve.did(i - 1, f"h{N - 1}{s}"))
                            else:
                                eng.wait_ge(*dve.did(i, f"h{b - 1}{s}"))
                            for t in range(4):
                                last = nc.tensor.matmul(lin[s][:, t * P:(t + 1) * P], h[:, s, t * P:(t + 1) * P], WQ[:, 2 * b], start=True, stop=True)
                            last.then_inc(*pe.does(f"lin{b}{s}"))
                        for s in range(L):
                            eng.wait_ge(*dve.did(i, f"z{b}{s}"))
                            for t in range(4):
                                last = nc.tensor.transpose(turned[s][:, t * P:(t + 1) * P], z[:, s, t], eye[:])
                            last.then_inc(*pe.does(f"turned{b}{s}"))
                        for s in range(L):
                            eng.wait_ge(*act.did(i, f"gelu{b}{s}"))
                            nc.tensor.matmul(back[s][:], WQ[:, 2 * b + 1], yT[:, s], start=True, stop=True).then_inc(*pe.does(f"back{b}{s}"))
                tiles(eng, GROUPS // L, 1, body)

            @block.scalar
            def _(eng):
                def body(i, _, again):
                    for s in range(L):
                        if again:
                            eng.wait_ge(*dve.did(i - 1, f"out{s}"))
                        nc.scalar.activation(h[:, s], at_group(XN, i * L + s), ACT.Copy).then_inc(*act.does(f"h{s}"))
                    for b in range(N):
                        for s in range(L):
                            eng.wait_ge(*pe.did(i, f"turned{b}{s}"))
                            nc.scalar.activation(yT[:, s], turned[s][:], ACT.Gelu, scale=gammaT[:, b:b + 1], bias=betaT[:, b:b + 1]).then_inc(*act.does(f"gelu{b}{s}"))
                tiles(eng, GROUPS // L, 1, body)

            @block.vector
            def _(eng):
                def body(i, _, again):
                    for b in range(N):
                        for s in range(L):
                            eng.wait_ge(*pe.did(i, f"lin{b}{s}"))
                            nc.vector.tensor_tensor(y[:, s], lin[s][:].rearrange("p (t n) -> p t n", n=P), over_heads(bias_rows[:, b], 4), ALU.add).then_inc(*dve.does(f"y{b}{s}"))
                        for s in range(L):
                            eng.wait_ge(*dve.did(i, f"y{b}{s}"))
                            for t in range(4):
                                last = nc.vector.bn_stats(st[:, s, t], y[:, s, t])
                            last.then_inc(*dve.does(f"st{b}{s}"))
                        for s in range(L):
                            eng.wait_ge(*dve.did(i, f"st{b}{s}"))
                            nc.vector.memset(carrier[:, s:s + 1], 0.0).then_inc(*dve.does(f"cr{b}{s}"))
                            for t in range(4):
                                last = nc.vector.bn_aggr(ag[:, s, t], st[:, s, t])
                            last.then_inc(*dve.does(f"ag{b}{s}"))
                        for s in range(L):
                            eng.wait_ge(*dve.did(i, f"ag{b}{s}"))
                            nc.vector.tensor_scalar(ve[:, s], ag[:, s, :, 1], 1e-5, None, ALU.add).then_inc(*dve.does(f"ve{b}{s}"))
                        for s in range(L):
                            eng.wait_ge(*pool.did(i, f"rs{b}{s}"))
                            for t in range(4):
                                last = nc.vector.tensor_scalar(z[:, s, t], y[:, s, t], ag[:, s, t, 0:1], rs[:, s, t:t + 1], ALU.subtract, ALU.mult)
                            last.then_inc(*dve.does(f"z{b}{s}"))
                        for s in range(L):
                            eng.wait_ge(*pe.did(i, f"back{b}{s}"))
                            nc.vector.scalar_tensor_tensor(h[:, s], back[s][:], biasT[:, b:b + 1], h[:, s], ALU.add, ALU.add).then_inc(*dve.does(f"h{b}{s}"))
                    for s in range(L):
                        eng.wait_ge(*dve.did(i, f"h{N - 1}{s}"))
                        nc.vector.tensor_tensor(at_group(XT, i * L + s), at_group(XT, i * L + s), h[:, s], ALU.add).then_inc(*dve.does(f"out{s}"))
                tiles(eng, GROUPS // L, 1, body)

            @block.gpsimd
            def _(eng):
                nc.gpsimd.memset(half[:], -0.5).then_inc(half_set, 1)
                eng.wait_ge(half_set, 1)
                def body(i, _, again):
                    for b in range(N):
                        for s in range(L):
                            eng.wait_ge(*dve.did(i, f"ve{b}{s}"))
                            nc.gpsimd.tensor_tensor(rs[:, s], ve[:, s], half[:], ALU.pow).then_inc(*pool.does(f"rs{b}{s}"))
                tiles(eng, GROUPS // L, 1, body)

AH, AD = 16, 8
AN = BATCH * AH
PARTS = 3
STACK = PARTS * PARTS * AD
QT = SEQ // P
SHIFT = 96
VW = AD + 1

def attn_project(nc, name, XN, Vh, q_dram, k_dram, w, wv, cos, sin):
    with ExitStack() as stack:
        m = Space(nc, name, stack)
        xs = m.sb("xs", [P, GRP])
        a = m.sb("a", [P, 2, GRP])
        b = m.sb("b", [P, 2, GRP])
        part = m.sb("part", [P, 2, PARTS, GRP], BF16)
        banks = [m.ps(f"w{k}") for k in range(4)]
        vb = m.ps("vb")
        pe = Steps(m.sem("pe"), "w0 w1 w2 w3 v")
        act = Steps(m.sem("act"), "xs v " + " ".join(f"c{p}{k}" for p in range(PARTS) for k in range(2)))
        dve = Steps(m.sem("dve"), "c0 s0 c1 s1")
        pool = Steps(m.sem("pool"), "r0 r1 d10 d11 d20 d21")
        ones_set, stored = m.sem("ones"), m.sem("stored")
        vh = Vh[:].rearrange("p (b h t e) -> p b h t e", b=BATCH, h=AH, e=VW)

        def both(eng, body):
            body(0, 0, False)
            body(0, 1, True)
            with eng.Fori(1, BATCH) as seq:
                body(seq, 0, True)
                body(seq, 1, True)

        with nc.Block() as block:
            @block.tensor
            def _(eng):
                def body(seq, s, again):
                    g = seq * 2 + s
                    for k in range(4):
                        if again:
                            eng.wait_ge(*dve.did(g - 1, f"{'cs'[k % 2]}{k // 2}"))
                        nc.tensor.matmul(banks[k][:], w[k][:], at_group(XN, g), start=True, stop=True).then_inc(*pe.does(f"w{k}"))
                    eng.wait_ge(*act.did(g, "xs"))
                    if again:
                        eng.wait_ge(*act.did(g - 1, "v"))
                    for t in range(4):
                        last = nc.tensor.matmul(vb[:, t * P:(t + 1) * P], xs[:, t * P:(t + 1) * P], wv[:], start=True, stop=True)
                    last.then_inc(*pe.does("v"))
                both(eng, body)

            @block.scalar
            def _(eng):
                eng.wait_ge(ones_set, 1)
                def body(seq, s, again):
                    g = seq * 2 + s
                    if again:
                        eng.wait_ge(*pe.did(g - 1, "v"))
                    nc.scalar.activation(xs[:], at_group(XN, g), ACT.Copy).then_inc(*act.does("xs"))
                    eng.wait_ge(*pe.did(g, "v"))
                    for t in range(4):
                        last = nc.scalar.activation(vh[:, bass.ds(seq, 1), :, 4 * s + t, 0:AD].rearrange("p o h e -> p (o h) e"),
                                                    vb[:, t * P:(t + 1) * P].rearrange("p (h e) -> p h e", e=AD), ACT.Copy)
                    last.then_inc(*act.does("v"))
                    for p in range(PARTS):
                        for k in range(2):
                            eng.wait_ge(*pool.did(g, f"d{p}{k}" if p else f"r{k}"))
                            if again:
                                eng.wait_ge(stored, g * (5 + 3) * 16)
                            nc.scalar.activation(part[:, k, p], a[:, k], ACT.Copy).then_inc(*act.does(f"c{p}{k}"))
                both(eng, body)

            @block.vector
            def _(eng):
                def body(seq, s, again):
                    g = seq * 2 + s
                    for k in range(2):
                        if again:
                            eng.wait_ge(*act.did(g - 1, f"c{PARTS - 1}{k}"))
                        for n, dst, table in ((0, a, cos), (1, b, sin)):
                            eng.wait_ge(*pe.did(g, f"w{2 * k + n}"))
                            nc.vector.tensor_tensor(dst[:, k], banks[2 * k + n][:], table[:, s * GRP:(s + 1) * GRP], ALU.mult).then_inc(*dve.does(f"{'cs'[n]}{k}"))
                both(eng, body)

            @block.gpsimd
            def _(eng):
                nc.gpsimd.memset(Vh[:], 1.0).then_inc(ones_set, 1)
                def body(seq, s, again):
                    g = seq * 2 + s
                    for k in range(2):
                        eng.wait_ge(*dve.did(g, f"s{k}"))
                        nc.gpsimd.tensor_tensor(a[:, k], a[:, k], b[:, k], ALU.add).then_inc(*pool.does(f"r{k}"))
                    for p in range(1, PARTS):
                        for k in range(2):
                            eng.wait_ge(*act.did(g, f"c{p - 1}{k}"))
                            nc.gpsimd.tensor_tensor(a[:, k], a[:, k], part[:, k, p - 1], ALU.subtract).then_inc(*pool.does(f"d{p}{k}"))
                both(eng, body)

            @block.sync
            def _(eng):
                def body(seq, s, again):
                    g = seq * 2 + s
                    for p in range(PARTS):
                        for k, dram in enumerate((q_dram, k_dram)):
                            eng.wait_ge(*act.did(g, f"c{p}{k}"))
                            for row in [p] + ([p + PARTS] if k and p < 2 else []):
                                dst = dram.rearrange("(b h) r d t -> b h r d t", h=AH)[bass.ds(seq, 1), :, row, :, s * GRP:(s + 1) * GRP]
                                eng.dma_start(dst.rearrange("o h d t -> (o h) d t"), part[:, k, p]).then_inc(stored, 16)
                both(eng, body)
                eng.wait_ge(stored, GROUPS * 8 * 16)

def attn_heads(nc, name, Vh, ctx_dram, sum_dram, q_dram, k_dram, eye16):
    BANKS = 2
    UNITS = 2 * QT
    STEPS = 3
    PLAN = [0] * 3 + [1] * UNITS + [0] * 3 + [1, 0]
    with ExitStack() as stack:
        m = Space(nc, name, stack)
        qs = [m.sb(f"qs{s}", [P, SEQ], BF16) for s in range(2)]
        ks = [m.sb(f"ks{s}", [P, SEQ], BF16) for s in range(2)]
        vs = [m.sb(f"vs{s}", [P, QT * VW]) for s in range(2)]
        pt = m.sb("pt", [P, 2, SEQ])
        mx = m.sb("mx", [P, QT, 2])
        nm = m.sb("nm", [P, QT])
        d1 = m.sb("d1", [P, QT])
        d2 = m.sb("d2", [P, QT])
        mp = m.sb("mp", [P, QT, PARTS], BF16)
        out = m.sb("out", [VW, 2, 2, GRP])
        first = [m.ps(f"first{k}") for k in range(BANKS)]
        second = [m.ps(f"second{k}", [P, 2, GRP]) for k in range(2)]
        O = m.ps("O", [P, 2, GRP])
        loaded = [m.sem(f"loaded{s}") for s in range(2)]
        stored = [m.sem(f"stored{s}") for s in range(2)]
        ready = m.sem("ready")
        a_pe = Steps(m.sem("ape"), " ".join(f"n{u}" for u in range(UNITS)) + " row0 row1")
        b_pe = Steps(m.sem("bpe"), "s0 " + " ".join(f"s{t} v{t - 1}" for t in range(1, QT)) + f" v{QT - 1}")
        a_dve = Steps(m.sem("adve"), " ".join(f"m{u}" for u in range(UNITS)) + " nm p1 d1 p2 d2 p3")
        b_dve = Steps(m.sem("bdve"), "out")
        a_act = Steps(m.sem("aact"), "row0 row1")
        b_act = Steps(m.sem("bact"), " ".join(f"e{t}" for t in range(QT)))
        pool = Steps(m.sem("pool"), "v")
        LOADS = 6

        def run(eng, maxima, weights):
            def turn(n, s, wt, mx_, again2, again3, again4=False):
                units = maxima(n, s, again2) if mx_ else iter(())

                def step(i):
                    todo = PLAN[i] if i is not None else UNITS + 2
                    for _ in range(todo):
                        if next(units, None) is None:
                            return
                if wt:
                    weights(n - 1, 1 - s, again3, again4, step)
                else:
                    step(None)
            turn(0, 0, False, True, False, False)
            turn(1, 1, True, True, False, False)
            turn(2, 0, True, True, True, True)
            with eng.Fori(0, (AN - 4) // 2) as k:
                turn(k * 2 + 3, 1, True, True, True, True, True)
                turn(k * 2 + 4, 0, True, True, True, True, True)
            turn(AN - 1, 1, True, True, True, True, True)
            turn(AN, 0, True, False, True, True, True)

        with nc.Block() as block:
            @block.sync
            def _(eng):
                eng.wait_ge(ready, 6)

                def load(n, s):
                    for r in range(PARTS):
                        rows = slice(r * 24, r * 24 + 24)
                        eng.dma_start(qs[s][rows, :], q_dram[bass.ds(n, 1)].rearrange("o r d t -> (o r d) t")).then_inc(loaded[s], 16)
                        eng.dma_start(ks[s][rows, :], k_dram[bass.ds(n, 1), r:r + 3].rearrange("o r d t -> (o r d) t")).then_inc(loaded[s], 16)

                def store(n, s):
                    eng.wait_ge(*b_dve.did(n, "out"))
                    eng.dma_start(ctx_dram[bass.ds(n, 1)].rearrange("o d t -> (o d) t"), out[0:AD, s].rearrange("p a t -> p (a t)")).then_inc(stored[s], 16)
                    eng.dma_start(sum_dram[bass.ds(n, 1)], out[AD:VW, s].rearrange("p a t -> p (a t)")).then_inc(stored[s], 16)
                for s in range(2):
                    load(s, s)

                def body(n, s):
                    eng.wait_ge(*b_pe.did(n, f"s{QT - 1}"))
                    load(n + 2, s)
                    store(n, s)
                with eng.Fori(0, AN // 2 - 1) as k:
                    for s in range(2):
                        body(k * 2 + s, s)
                for s in range(2):
                    store(AN - 2 + s, s)
                for s in range(2):
                    eng.wait_ge(stored[s], AN // 2 * 32)

            @block.gpsimd
            def _(eng):
                fills = [(t[lo:hi, :], x) for s in range(2) for t, lo, hi, x in ((qs[s], 64, P, 0.0), (ks[s], 64, SHIFT, 0.0), (ks[s], SHIFT, P, 1.0))]
                for n, (rows, x) in enumerate(fills):
                    nc.gpsimd.memset(rows, x).then_inc(ready, 1)
                    eng.wait_ge(ready, n + 1)

                def values(n, s, again):
                    if again:
                        eng.wait_ge(*b_pe.did(n - 2, f"v{QT - 1}"))
                    nc.gpsimd.tensor_copy(vs[s][:], Vh[:, bass.ds(n * (QT * VW), QT * VW)]).then_inc(*pool.does("v"))
                tiles(eng, AN, 2, values)

            @block.tensor
            def _(eng):
                def maxima(n, s, again):
                    eng.wait_ge(loaded[s], (n // 2 + 1) * LOADS * 16 if isinstance(n, int) else (n - s) * (LOADS * 8) + LOADS * 16)
                    for u in range(UNITS):
                        k = u % BANKS
                        if u >= BANKS:
                            eng.wait_ge(*a_dve.did(n, f"m{u - BANKS}"))
                        elif again or (isinstance(n, int) and n):
                            eng.wait_ge(*a_act.did(n - 1, f"row{k}"))
                        qt, half = divmod(u, 2)
                        nc.tensor.matmul(first[k][:], qs[s][0:STACK, qt * P:(qt + 1) * P], ks[s][0:STACK, half * GRP:(half + 1) * GRP],
                                         start=True, stop=True).then_inc(*a_pe.does(f"n{u}"))
                        yield True
                    eng.wait_ge(*a_dve.did(n, "p3"))
                    for half in range(2):
                        for t in range(4):
                            last = nc.tensor.matmul(first[half][SHIFT:SHIFT + PARTS, t * P:(t + 1) * P], mp[:, 4 * half + t, :], eye16[:],
                                                    start=True, stop=True)
                        last.then_inc(*a_pe.does(f"row{half}"))
                    yield True

                def weights(n, s, again, again2, step):
                    eng.wait_ge(*a_act.did(n, "row1"))

                    def values(t):
                        eng.wait_ge(*b_act.did(n, f"e{t}"))
                        if t == 0:
                            eng.wait_ge(*pool.did(n, "v"))
                            if again:
                                eng.wait_ge(*b_dve.did(n - 1, "out"))
                        for half in range(2):
                            if half:
                                step(t * STEPS + 2)
                            last = nc.tensor.matmul(O[0:VW, half], vs[s][:, t * VW:(t + 1) * VW], pt[:, t % 2, half * GRP:(half + 1) * GRP],
                                                    start=(t == 0), stop=(t == QT - 1))
                        last.then_inc(*b_pe.does(f"v{t}"))
                    for t in range(QT):
                        step(t * STEPS)
                        if t >= 2:
                            eng.wait_ge(*b_act.did(n, f"e{t - 2}"))
                        elif again:
                            eng.wait_ge(*b_act.did(n - 1, f"e{QT - 2 + t}"))
                        for half in range(2):
                            last = nc.tensor.matmul(second[t % 2][:, half], ks[s][0:SHIFT + PARTS, t * P:(t + 1) * P], qs[s][0:SHIFT + PARTS, half * GRP:(half + 1) * GRP],
                                                    start=True, stop=True)
                        last.then_inc(*b_pe.does(f"s{t}"))
                        step(t * STEPS + 1)
                        if t:
                            values(t - 1)
                    values(QT - 1)
                    step(None)
                run(eng, maxima, weights)

            def other_steps(step, at):
                for t in range(QT):
                    step(t * STEPS)
                    at(t)
                    step(t * STEPS + 1)
                    if t:
                        step(t * STEPS - 1)
                step(QT * STEPS - 1)

            @block.scalar
            def _(eng):
                nc.scalar.preload_act_table_set("exp_and_others")
                eng.wait_ge(ready, 6)
                def maxima(n, s, again):
                    for u in range(UNITS):
                        yield True
                    for half in range(2):
                        eng.wait_ge(*a_pe.did(n, f"row{half}"))
                        if again:
                            eng.wait_ge(*b_pe.did(n - 2, f"s{QT - 1}"))
                        nc.scalar.activation(qs[s][SHIFT:SHIFT + PARTS, half * GRP:(half + 1) * GRP], first[half][SHIFT:SHIFT + PARTS, :],
                                             ACT.Copy).then_inc(*a_act.does(f"row{half}"))
                    yield True

                def weights(n, s, again, again2, step):
                    def exps(t):
                        eng.wait_ge(*b_pe.did(n, f"s{t}"))
                        if t >= 2:
                            eng.wait_ge(*b_pe.did(n, f"v{t - 2}"))
                        elif again:
                            eng.wait_ge(*b_pe.did(n - 1, f"v{QT - 2 + t}"))
                        nc.scalar.activation(pt[:, t % 2].rearrange("p (a b) -> p a b", a=2), second[t % 2][:], ACT.Exp, scale=float(AD) ** -0.5).then_inc(*b_act.does(f"e{t}"))
                    other_steps(step, exps)
                    step(None)
                run(eng, maxima, weights)

            @block.vector
            def _(eng):
                def maxima(n, s, again):
                    for u in range(UNITS):
                        eng.wait_ge(*a_pe.did(n, f"n{u}"))
                        nc.vector.tensor_reduce(mx[:, u // 2, u % 2:u % 2 + 1], first[u % BANKS][:], AX, ALU.max).then_inc(*a_dve.does(f"m{u}"))
                        yield True

                    def small(ins, name_):
                        ins.then_inc(*a_dve.does(name_))
                        eng.wait_ge(*a_dve.did(n, name_))
                    eng.wait_ge(*a_dve.did(n, f"m{UNITS - 1}"))
                    small(nc.vector.tensor_reduce(nm[:], mx[:], AX, ALU.max), "nm")
                    if again or (isinstance(n, int) and n):
                        eng.wait_ge(*a_pe.did(n - 1, "row1"))
                    small(nc.vector.tensor_scalar(mp[:, :, 0], nm[:], -1.0, None, ALU.mult), "p1")
                    small(nc.vector.scalar_tensor_tensor(d1[:], nm[:], -1.0, mp[:, :, 0], ALU.mult, ALU.subtract), "d1")
                    small(nc.vector.tensor_copy(mp[:, :, 1], d1[:]), "p2")
                    small(nc.vector.tensor_tensor(d2[:], d1[:], mp[:, :, 1], ALU.subtract), "d2")
                    small(nc.vector.tensor_copy(mp[:, :, 2], d2[:]), "p3")
                    yield True

                def weights(n, s, again, again2, step):
                    step(None)
                    eng.wait_ge(*b_pe.did(n, f"v{QT - 1}"))
                    if again2:
                        eng.wait_ge(stored[s], (n - s) * 16)
                    nc.vector.tensor_copy(out[:, s], O[0:VW]).then_inc(*b_dve.does("out"))
                run(eng, maxima, weights)

def attn_output(nc, name, ctx_dram, sum_dram, rec_dram, XT, w_out, head_rows):
    with ExitStack() as stack:
        m = Space(nc, name, stack)
        ctx = m.sb("ctx", [P, TOK])
        total, inverse = m.sb("total", [P, AN * SEQ // P]), m.sb("inverse", [P, AN * SEQ // P])
        rec = m.sb("rec", [AH, TOK])
        spread = [m.ps(f"spread{s}") for s in range(2)]
        proj = [m.ps(f"proj{s}") for s in range(2)]
        pe, dve = Steps(m.sem("pe"), "spread proj"), Steps(m.sem("dve"), "ctx x")
        sums_in, rec_out, rec_in, ctx_in, inverted = m.sem("sums_in"), m.sem("rec_out"), m.sem("rec_in"), m.sem("ctx_in"), m.sem("inverted")
        by_row = "n (a t) -> (n a) t"
        with nc.Block() as block:
            @block.sync
            def _(eng):
                eng.dma_start(total[:], sum_dram.rearrange(by_row, a=2)).then_inc(sums_in, 16)
                for b in range(BATCH):
                    eng.dma_start(ctx[:, b * SEQ:(b + 1) * SEQ], ctx_dram[b * AH:(b + 1) * AH].rearrange("h d t -> (h d) t")).then_inc(ctx_in, 16)
                eng.wait_ge(inverted, 1)
                eng.dma_start(rec_dram.rearrange(by_row, a=2), inverse[:]).then_inc(rec_out, 16)
                eng.wait_ge(rec_out, 16)
                eng.dma_start(rec[:].rearrange("h (b t) -> h b t", b=BATCH), rec_dram.rearrange("(b h) t -> h b t", b=BATCH)).then_inc(rec_in, 16)

            @block.tensor
            def _(eng):
                eng.wait_ge(rec_in, 16)

                def body(g, s, again):
                    if again:
                        eng.wait_ge(*dve.did(g - 2, "ctx"))
                    nc.tensor.matmul(spread[s][:], head_rows[0:AH, :], rec[:, bass.ds(g * GRP, GRP)], start=True, stop=True).then_inc(*pe.does("spread"))
                    eng.wait_ge(*dve.did(g, "ctx"))
                    if again:
                        eng.wait_ge(*dve.did(g - 2, "x"))
                    nc.tensor.matmul(proj[s][:], w_out[:], at_group(ctx, g), start=True, stop=True).then_inc(*pe.does("proj"))
                tiles(eng, GROUPS, 2, body)

            @block.vector
            def _(eng):
                eng.wait_ge(sums_in, 16)
                nc.vector.reciprocal(inverse[:], total[:]).then_inc(inverted, 1)
                eng.wait_ge(ctx_in, BATCH * 16)

                def body(g, s, again):
                    eng.wait_ge(*pe.did(g, "spread"))
                    nc.vector.tensor_tensor(at_group(ctx, g), at_group(ctx, g), spread[s][:], ALU.mult).then_inc(*dve.does("ctx"))
                    eng.wait_ge(*pe.did(g, "proj"))
                    nc.vector.tensor_tensor(at_group(XT, g), at_group(XT, g), proj[s][:], ALU.add).then_inc(*dve.does("x"))
                tiles(eng, GROUPS, 2, body)

def router_small(nc, name, XN, RW, w_router, bias_row, iota, E_):
    with ExitStack() as stack:
        m = Space(nc, name, stack)
        xs = m.sb("xs", [P, 2, GRP])
        lg = m.sb("lg", [P, 2, 4, E_])
        top = m.sb("top", [P, CHUNKS, 8])
        top4 = m.sb("top4", [P, 2, 4, 8])
        idx4 = m.sb("idx4", [P, 2, 4, 8], U32)
        fi8 = m.sb("fi8", [P, CHUNKS, 8])
        carrier = m.sb("carrier", [P, 2])
        fi = m.sb("fi", [P, 2, CHUNKS])
        ex = m.sb("ex", [P, CHUNKS])
        den = m.sb("den", [P, CHUNKS])
        wt = m.sb("wt", [P, 2, CHUNKS])
        hot = m.sb("hot", [P, 2, CHUNKS, E_])
        lp = [m.ps(f"lp{s}") for s in range(2)]
        pe, act = Steps(m.sem("pe"), "lg"), Steps(m.sem("act"), "xs")
        dve = Steps(m.sem("dve"), "lg cr0 max cr1 at top idx")
        end = Steps(m.sem("end"), "f0 f1 d den rec w1 h0 h1 s0 s1 rw")
        exped = m.sem("exped")
        with nc.Block() as block:
            @block.scalar
            def _(eng):
                def body(g, s, again):
                    if again:
                        eng.wait_ge(*pe.did(g - 2, "lg"))
                    nc.scalar.activation(xs[:, s], at_group(XN, g), ACT.Copy).then_inc(*act.does("xs"))
                tiles(eng, GROUPS, 2, body)
                eng.wait_ge(*end.did(0, "d"))
                nc.scalar.activation(ex[:], ex[:], ACT.Exp).then_inc(exped, 1)

            @block.tensor
            def _(eng):
                def body(g, s, again):
                    eng.wait_ge(*act.did(g, "xs"))
                    if again:
                        eng.wait_ge(*dve.did(g - 2, "lg"))
                    for t in range(4):
                        last = nc.tensor.matmul(lp[s][:, t * E_:(t + 1) * E_], xs[:, s, t * P:(t + 1) * P], w_router[:], start=True, stop=True)
                    last.then_inc(*pe.does("lg"))
                tiles(eng, GROUPS, 2, body)

            @block.vector
            def _(eng):
                def body(g, s, again):
                    eng.wait_ge(*pe.did(g, "lg"))
                    src = lp[s][:, 0:4 * E_].rearrange("p (t e) -> p t e", e=E_)
                    nc.vector.tensor_tensor(lg[:, s], src, over_heads(bias_row[:], 4), ALU.add).then_inc(*dve.does("lg"))
                    eng.wait_ge(*dve.did(g, "lg"))
                    nc.vector.memset(carrier[:, 0:1], 0.0).then_inc(*dve.does("cr0"))
                    for t in range(4):
                        last = nc.vector.max(top4[:, s, t], lg[:, s, t])
                    last.then_inc(*dve.does("max"))
                    eng.wait_ge(*dve.did(g, "max"))
                    nc.vector.memset(carrier[:, 1:2], 0.0).then_inc(*dve.does("cr1"))
                    for t in range(4):
                        last = nc.vector.max_index(idx4[:, s, t], top4[:, s, t], lg[:, s, t])
                    last.then_inc(*dve.does("at"))
                    nc.vector.tensor_copy(top[:, bass.ds(g * 4, 4), :], top4[:, s]).then_inc(*dve.does("top"))
                    eng.wait_ge(*dve.did(g, "at"))
                    nc.vector.tensor_copy(fi8[:, bass.ds(g * 4, 4), :], idx4[:, s]).then_inc(*dve.does("idx"))
                tiles(eng, GROUPS, 2, body)

                def step(ins, name_):
                    ins.then_inc(*end.does(name_))
                    eng.wait_ge(*end.did(0, name_))
                eng.wait_ge(*dve.did(GROUPS - 1, "idx"))
                for k in range(2):
                    step(nc.vector.tensor_copy(fi[:, k], fi8[:, :, k]), f"f{k}")
                step(nc.vector.tensor_tensor(ex[:], top[:, :, 1], top[:, :, 0], ALU.subtract), "d")
                eng.wait_ge(exped, 1)
                step(nc.vector.tensor_scalar(den[:], ex[:], 1.0, None, ALU.add), "den")
                step(nc.vector.reciprocal(wt[:, 0], den[:]), "rec")
                step(nc.vector.tensor_tensor(wt[:, 1], wt[:, 0], ex[:], ALU.mult), "w1")
                for k in range(2):
                    step(nc.vector.tensor_tensor(hot[:, k], iota[:, 0:E_].unsqueeze(1).to_broadcast([P, CHUNKS, E_]), along(fi[:, k], E_), ALU.is_equal), f"h{k}")
                for k in range(2):
                    step(nc.vector.tensor_tensor(hot[:, k], hot[:, k], along(wt[:, k], E_), ALU.mult), f"s{k}")
                step(nc.vector.tensor_tensor(RW[:].rearrange("p (c e) -> p c e", e=E_), hot[:, 0], hot[:, 1], ALU.add), "rw")

def dense_moe(nc, name, XN, XT, RW, W1, B1, W2, b2, gammaT, betaT, eye, E_):
    F = 4
    with ExitStack() as stack:
        m = Space(nc, name, stack)
        xs = m.sb("xs", [P, GRP])
        rw = m.sb("rw", [P, 4, E_])
        rwT = m.sb("rwT", [E_, GRP])
        hid = m.sb("hid", [P, 2, F, GRP])
        acc = m.sb("acc", [P, 4, P])
        z = m.sb("z", [P, 4, P])
        zT = m.sb("zT", [P, GRP])
        st, ag, rs, ve = m.sb("st", [P, 4, 6]), m.sb("ag", [P, 4, 2]), m.sb("rs", [P, 4]), m.sb("ve", [P, 4])
        half, carrier = m.sb("half", [P, 4]), m.sb("carrier", [P, 1])
        up = [m.ps(f"up{c}") for c in range(F)]
        down = [m.ps(f"down{k}") for k in range(2)]
        side = m.ps("side")
        small = m.ps("small")
        pe = Steps(m.sem("pe"), "rwT init " + " ".join(f"up{e}{c}" for e in range(1) for c in range(F)) + " " +
                   " ".join(" ".join(f"up{e + 1}{c}" for c in range(F) if e + 1 < E_) + f" down{e}" for e in range(E_)))
        pe_end, act_end, dve_end = Steps(m.sem("pe_end"), "zT"), Steps(m.sem("act_end"), "zT"), Steps(m.sem("dve_end"), "out")
        act = Steps(m.sem("act"), "xs rw rwT init " + " ".join(f"hid{e}{c}" for e in range(E_) for c in range(F)))
        dve = Steps(m.sem("dve"), " ".join(f"acc{e}" for e in range(E_)) + " st cr ag ve z")
        pool = Steps(m.sem("pool"), "rs")
        half_set = m.sem("half_set")

        def groups(eng, body, end):
            body(0, False, lambda: None)
            body(1, True, lambda: end(0, False))
            with eng.Fori(2, GROUPS) as g:
                body(g, True, lambda: end(g - 1, True))
            end(GROUPS - 1, True)

        def tiles4(t):
            return t[:].rearrange("p (t n) -> p t n", n=P)
        with nc.Block() as block:
            @block.tensor
            def _(eng):
                def body(g, again, end_before):
                    def prev(who, step):
                        if again:
                            eng.wait_ge(*who.did(g - 1, step))
                    eng.wait_ge(*act.did(g, "rw"))
                    prev(act, "init")
                    for t in range(4):
                        last = nc.tensor.transpose(side[0:E_, t * P:(t + 1) * P], rw[:, t], eye[:])
                    last.then_inc(*pe.does("rwT"))
                    eng.wait_ge(*act.did(g, "rwT"))
                    for t in range(4):
                        nc.tensor.matmul(side[:, t * P:(t + 1) * P], xs[:, t * P:(t + 1) * P], eye[:], start=True, stop=False)
                        last = nc.tensor.matmul(side[:, t * P:(t + 1) * P], rwT[:, t * P:(t + 1) * P], b2[:], start=False, stop=True)
                    last.then_inc(*pe.does("init"))

                    def hidden(e):
                        for c in range(F):
                            if e:
                                eng.wait_ge(*act.did(g, f"hid{e - 1}{c}"))
                            elif again:
                                eng.wait_ge(*act.did(g - 1, f"hid{E_ - 1}{c}"))
                            nc.tensor.matmul(up[c][:], W1[:, e, c * P:(c + 1) * P], xs[:], start=True, stop=True).then_inc(*pe.does(f"up{e}{c}"))
                    hidden(0)
                    end_before()
                    for e in range(E_):
                        if e + 1 < E_:
                            hidden(e + 1)
                        if e >= 2:
                            eng.wait_ge(*dve.did(g, f"acc{e - 2}"))
                        else:
                            prev(dve, f"acc{E_ - 2 + e}")
                        for t in range(4):
                            for c in range(F):
                                if t == 0:
                                    eng.wait_ge(*act.did(g, f"hid{e}{c}"))
                                last = nc.tensor.matmul(down[e % 2][:, t * P:(t + 1) * P], hid[:, e % 2, c, t * P:(t + 1) * P], W2[:, e, c], start=(c == 0), stop=(c == F - 1))
                        last.then_inc(*pe.does(f"down{e}"))

                def end(g, again):
                    eng.wait_ge(*dve.did(g, "z"))
                    if again:
                        eng.wait_ge(*act_end.did(g - 1, "zT"))
                    for t in range(4):
                        last = nc.tensor.transpose(small[:, t * P:(t + 1) * P], z[:, t], eye[:])
                    last.then_inc(*pe_end.does("zT"))
                groups(eng, body, end)

            @block.scalar
            def _(eng):
                def body(g, again, end_before):
                    def prev(who, step):
                        if again:
                            eng.wait_ge(*who.did(g - 1, step))
                    prev(pe, f"up{E_ - 1}{F - 1}")
                    nc.scalar.activation(xs[:], at_group(XN, g), ACT.Copy).then_inc(*act.does("xs"))
                    prev(dve, f"acc{E_ - 1}")
                    nc.scalar.activation(rw[:].rearrange("p t e -> p (t e)"), RW[:, bass.ds(g * (4 * E_), 4 * E_)], ACT.Copy).then_inc(*act.does("rw"))
                    eng.wait_ge(*pe.did(g, "rwT"))
                    nc.scalar.activation(rwT[:], side[0:E_, :], ACT.Copy).then_inc(*act.does("rwT"))
                    eng.wait_ge(*pe.did(g, "init"))
                    prev(dve, "z")
                    nc.scalar.activation(acc[:], tiles4(side), ACT.Copy).then_inc(*act.does("init"))
                    for e in range(E_):
                        if e == 1:
                            end_before()
                        for c in range(F):
                            eng.wait_ge(*pe.did(g, f"up{e}{c}"))
                            if c == 0:
                                if e >= 2:
                                    eng.wait_ge(*pe.did(g, f"down{e - 2}"))
                                else:
                                    prev(pe, f"down{E_ - 2 + e}")
                            nc.scalar.activation(hid[:, e % 2, c], up[c][:], ACT.Relu, bias=B1[:, e, c:c + 1]).then_inc(*act.does(f"hid{e}{c}"))

                def end(g, again):
                    eng.wait_ge(*pe_end.did(g, "zT"))
                    if again:
                        eng.wait_ge(*dve_end.did(g - 1, "out"))
                    nc.scalar.activation(zT[:], small[:], ACT.Identity, scale=gammaT[:, 0:1], bias=betaT[:, 0:1]).then_inc(*act_end.does("zT"))
                groups(eng, body, end)

            @block.vector
            def _(eng):
                def body(g, again, end_before):
                    end_before()
                    for e in range(E_):
                        eng.wait_ge(*pe.did(g, f"down{e}"))
                        if e == 0:
                            eng.wait_ge(*act.did(g, "init"))
                        else:
                            eng.wait_ge(*dve.did(g, f"acc{e - 1}"))
                        for t in range(4):
                            last = nc.vector.scalar_tensor_tensor(acc[:, t], tiles4(down[e % 2])[:, t], rw[:, t, e:e + 1], acc[:, t], ALU.mult, ALU.add)
                        last.then_inc(*dve.does(f"acc{e}"))
                    eng.wait_ge(*dve.did(g, f"acc{E_ - 1}"))
                    for t in range(4):
                        last = nc.vector.bn_stats(st[:, t], acc[:, t])
                    last.then_inc(*dve.does("st"))
                    eng.wait_ge(*dve.did(g, "st"))
                    nc.vector.memset(carrier[:], 0.0).then_inc(*dve.does("cr"))
                    for t in range(4):
                        last = nc.vector.bn_aggr(ag[:, t], st[:, t])
                    last.then_inc(*dve.does("ag"))
                    eng.wait_ge(*dve.did(g, "ag"))
                    nc.vector.tensor_scalar(ve[:], ag[:, :, 1], 1e-5, None, ALU.add).then_inc(*dve.does("ve"))
                    eng.wait_ge(*pool.did(g, "rs"))
                    for t in range(4):
                        last = nc.vector.tensor_scalar(z[:, t], acc[:, t], ag[:, t, 0:1], rs[:, t:t + 1], ALU.subtract, ALU.mult)
                    last.then_inc(*dve.does("z"))

                def end(g, again):
                    eng.wait_ge(*act_end.did(g, "zT"))
                    nc.vector.tensor_tensor(at_group(XT, g), at_group(XT, g), zT[:], ALU.add).then_inc(*dve_end.does("out"))
                groups(eng, body, end)

            @block.gpsimd
            def _(eng):
                nc.gpsimd.memset(half[:], -0.5).then_inc(half_set, 1)
                eng.wait_ge(half_set, 1)
                def body(g, _, again):
                    eng.wait_ge(*dve.did(g, "ve"))
                    nc.gpsimd.tensor_tensor(rs[:], ve[:], half[:], ALU.pow).then_inc(*pool.does("rs"))
                tiles(eng, GROUPS, 1, body)

GH, GD = 16, 8
STATES = GH * GD * GD
RT = STATES // P

def gla_gates(nc, name, XN, GT, w1, w2, bias):
    with ExitStack() as stack:
        m = Space(nc, name, stack)
        R = w1.shape[1]
        lo = m.sb("lo", [R, 2, GRP])
        z, y, u, d, lu, c = (m.sb(n, [P, 2, GRP]) for n in "z y u d lu c".split())
        lp = [m.ps(f"lp{s}") for s in range(2)]
        zp = [m.ps(f"zp{s}") for s in range(2)]
        pe_, act_, dve_ = ([Steps(m.sem(f"{e}{s}"), names) for s in range(2)] for e, names in (("pe", "lo z"), ("act", "lo y lu gate"), ("dve", "z na u d m ls")))
        with nc.Block() as block:
            @block.tensor
            def _(eng):
                def body(k, s, g, again):
                    pe, act, dve = pe_[s], act_[s], dve_[s]
                    if again:
                        eng.wait_ge(*act.did(k - 1, "lo"))
                    nc.tensor.matmul(lp[s][0:R, :], w1[:], at_group(XN, g), start=True, stop=True).then_inc(*pe.does("lo"))
                    yield
                    eng.wait_ge(*act.did(k, "lo"))
                    if again:
                        eng.wait_ge(*dve.did(k - 1, "z"))
                    nc.tensor.matmul(zp[s][:], w2[:], lo[:, s], start=True, stop=True).then_inc(*pe.does("z"))
                lanes(eng, GROUPS, 2, body)

            @block.scalar
            def _(eng):
                nc.scalar.preload_act_table_set("natural_log_exp_and_others")
                def body(k, s, g, again):
                    pe, act, dve = pe_[s], act_[s], dve_[s]
                    eng.wait_ge(*pe.did(k, "lo"))
                    if again:
                        eng.wait_ge(*pe.did(k - 1, "z"))
                    nc.scalar.activation(lo[:, s], lp[s][0:R, :], ACT.Copy).then_inc(*act.does("lo"))
                    yield
                    yield
                    eng.wait_ge(*dve.did(k, "na"))
                    nc.scalar.activation(y[:, s], y[:, s], ACT.Exp).then_inc(*act.does("y"))
                    yield
                    eng.wait_ge(*dve.did(k, "u"))
                    nc.scalar.activation(lu[:, s], u[:, s], ACT.Ln).then_inc(*act.does("lu"))
                    yield
                    eng.wait_ge(*dve.did(k, "ls"))
                    nc.scalar.activation(at_group(GT, g), d[:, s], ACT.Exp, scale=1.0 / 16).then_inc(*act.does("gate"))
                lanes(eng, GROUPS, 2, body)

            @block.vector
            def _(eng):
                def body(k, s, g, again):
                    pe, act, dve = pe_[s], act_[s], dve_[s]
                    def chain(name_):
                        eng.wait_ge(*dve.did(k, name_))
                    yield
                    eng.wait_ge(*pe.did(k, "z"))
                    nc.vector.tensor_scalar(z[:, s], zp[s][:], bias[:, 0:1], None, ALU.add).then_inc(*dve.does("z"))
                    chain("z")
                    nc.vector.scalar_tensor_tensor(y[:, s], z[:, s], -1.0, z[:, s], ALU.mult, ALU.min).then_inc(*dve.does("na"))
                    yield
                    eng.wait_ge(*act.did(k, "y"))
                    nc.vector.tensor_scalar(u[:, s], y[:, s], 1.0, None, ALU.add).then_inc(*dve.does("u"))
                    yield
                    chain("u")
                    if again:
                        eng.wait_ge(*act.did(k - 1, "gate"))
                    nc.vector.scalar_tensor_tensor(d[:, s], u[:, s], -1.0, y[:, s], ALU.add, ALU.subtract).then_inc(*dve.does("d"))
                    chain("d")
                    nc.vector.scalar_tensor_tensor(c[:, s], z[:, s], 0.0, d[:, s], ALU.min, ALU.add).then_inc(*dve.does("m"))
                    yield
                    eng.wait_ge(*act.did(k, "lu"))
                    chain("m")
                    nc.vector.tensor_tensor(d[:, s], c[:, s], lu[:, s], ALU.subtract).then_inc(*dve.does("ls"))
                lanes(eng, GROUPS, 2, body)

def gla_states(nc, name, XN, GT, OT, wq, wk, wv, pick, fold):
    with ExitStack() as stack:
        m = Space(nc, name, stack)
        k_sb = m.sb("k", [P, 2, GRP])
        kv = m.sb("kv", [P, 2, GRP])
        st = m.sb("st", [P, 2, GRP])
        y = m.sb("y", [P, 2, GRP])
        carry = m.sb("carry", [P, RT])
        K, V, G, Q = (m.ps(n) for n in "KVGQ")
        out = [m.ps(f"out{s}") for s in range(2)]
        pe = Steps(m.sem("pe"), "K0 V0 G0 Q0 " + " ".join(f"K{r} V{r} G{r} Q{r} f{r - 1}" for r in range(1, RT)) + f" f{RT - 1}")
        act = Steps(m.sem("act"), " ".join(f"k{r}" for r in range(RT)) + " o")
        dve = Steps(m.sem("dve"), " ".join(f"kv{r} st{r} ca{r} y{r}" for r in range(RT)))

        def halves(eng, body):
            body(0, 0, False)
            body(0, 1, True)
            with eng.Fori(1, BATCH) as seq:
                body(seq, 0, True)
                body(seq, 1, True)

        with nc.Block() as block:
            @block.tensor
            def _(eng):
                def body(seq, s, again):
                    g = seq * 2 + s

                    def prev(who, kind, r):
                        if r:
                            eng.wait_ge(*who.did(g, f"{kind}{r - 1}"))
                        elif again:
                            eng.wait_ge(*who.did(g - 1, f"{kind}{RT - 1}"))

                    def fold_rows(r):
                        eng.wait_ge(*dve.did(g, f"y{r}"))
                        if r == 0 and not isinstance(seq, int):
                            eng.wait_ge(*act.did(g - 2, "o"))
                        nc.tensor.matmul(out[s][:], fold[:, r * P:(r + 1) * P], y[:, r % 2], start=(r == 0), stop=(r == RT - 1)).then_inc(*pe.does(f"f{r}"))
                    for r in range(RT):
                        for n, bk, w, src, who, kind in (("K", K, wk, XN, act, "k"), ("V", V, wv, XN, dve, "kv"), ("G", G, pick, GT, dve, "st"), ("Q", Q, wq, XN, dve, "y")):
                            prev(who, kind, r)
                            nc.tensor.matmul(bk[:], w[:, r * P:(r + 1) * P], at_group(src, g), start=True, stop=True).then_inc(*pe.does(f"{n}{r}"))
                        if r:
                            fold_rows(r - 1)
                    fold_rows(RT - 1)
                halves(eng, body)

            @block.scalar
            def _(eng):
                def body(seq, s, again):
                    g = seq * 2 + s
                    for r in range(RT):
                        eng.wait_ge(*pe.did(g, f"K{r}"))
                        if r >= 2:
                            eng.wait_ge(*dve.did(g, f"kv{r - 2}"))
                        elif again:
                            eng.wait_ge(*dve.did(g - 1, f"kv{RT - 2 + r}"))
                        nc.scalar.activation(k_sb[:, r % 2], K[:], ACT.Copy).then_inc(*act.does(f"k{r}"))
                    eng.wait_ge(*pe.did(g, f"f{RT - 1}"))
                    nc.scalar.activation(at_group(OT, g), out[s][:], ACT.Copy).then_inc(*act.does("o"))
                halves(eng, body)

            @block.vector
            def _(eng):
                def body(seq, s, again):
                    g = seq * 2 + s
                    for r in range(RT):
                        eng.wait_ge(*pe.did(g, f"V{r}"))
                        eng.wait_ge(*act.did(g, f"k{r}"))
                        nc.vector.tensor_tensor(kv[:, r % 2], V[:], k_sb[:, r % 2], ALU.mult).then_inc(*dve.does(f"kv{r}"))
                        eng.wait_ge(*pe.did(g, f"G{r}"))
                        eng.wait_ge(*dve.did(g, f"kv{r}"))
                        nc.vector.tensor_tensor_scan(st[:, r % 2], G[:], kv[:, r % 2], carry[:, r:r + 1] if s else 0.0, ALU.mult, ALU.add).then_inc(*dve.does(f"st{r}"))
                        eng.wait_ge(*dve.did(g, f"st{r}"))
                        nc.vector.tensor_copy(carry[:, r:r + 1], st[:, r % 2, GRP - 1:GRP]).then_inc(*dve.does(f"ca{r}"))
                        eng.wait_ge(*pe.did(g, f"Q{r}"))
                        if r >= 2:
                            eng.wait_ge(*pe.did(g, f"f{r - 2}"))
                        elif again:
                            eng.wait_ge(*pe.did(g - 1, f"f{RT - 2 + r}"))
                        nc.vector.tensor_tensor(y[:, r % 2], Q[:], st[:, r % 2], ALU.mult).then_inc(*dve.does(f"y{r}"))
                halves(eng, body)

def gla_output(nc, name, XN, OT, XT, w_gate, w_out, gammaT, betaT, ones_mean):
    with ExitStack() as stack:
        m = Space(nc, name, stack)
        xc, sq, ln, rs, r2, on, sg, og = (m.sb(n, [P, 2, GRP]) for n in "xc sq ln rs r2 on sg og".split())
        eps = m.sb("eps", [P, 1])
        mean = [m.ps(f"mean{s}") for s in range(2)]
        var = [m.ps(f"var{s}") for s in range(2)]
        gate = [m.ps(f"gate{s}") for s in range(2)]
        out = [m.ps(f"out{s}") for s in range(2)]
        an, dn = rsqrt_names("v")
        pe_, act_, dve_ = ([Steps(m.sem(f"{e}{s}"), names) for s in range(2)] for e, names in (
            ("pe", "mean gate var out"), ("act", "sq " + an + " sg"), ("dve", "xc " + dn + " on af og xt")))
        ready = m.sem("ready")
        with nc.Block() as block:
            @block.tensor
            def _(eng):
                def body(k, s, g, again):
                    pe, act, dve = pe_[s], act_[s], dve_[s]
                    if again:
                        eng.wait_ge(*dve.did(k - 1, "xt"))
                    nc.tensor.matmul(mean[s][:], ones_mean[:], at_group(OT, g), start=True, stop=True).then_inc(*pe.does("mean"))
                    nc.tensor.matmul(gate[s][:], w_gate[:], at_group(XN, g), start=True, stop=True).then_inc(*pe.does("gate"))
                    yield
                    eng.wait_ge(*act.did(k, "sq"))
                    nc.tensor.matmul(var[s][:], ones_mean[:], sq[:, s], start=True, stop=True).then_inc(*pe.does("var"))
                    yield
                    yield
                    eng.wait_ge(*dve.did(k, "og"))
                    nc.tensor.matmul(out[s][:], w_out[:], og[:, s], start=True, stop=True).then_inc(*pe.does("out"))
                lanes(eng, GROUPS, 2, body)

            @block.scalar
            def _(eng):
                nc.scalar.preload_act_table_set("natural_log_exp_and_others")
                eng.wait_ge(ready, 1)
                def body(k, s, g, again):
                    pe, act, dve = pe_[s], act_[s], dve_[s]
                    eng.wait_ge(*dve.did(k, "xc"))
                    nc.scalar.activation(sq[:, s], xc[:, s], ACT.Square).then_inc(*act.does("sq"))
                    yield
                    eng.wait_ge(*pe.did(k, "var"))
                    rsqrt_act(nc, eng, act, k, "v", var[s][:], eps[:], ln[:, s], rs[:, s], r2[:, s])
                    yield
                    eng.wait_ge(*pe.did(k, "gate"))
                    nc.scalar.activation(sg[:, s], gate[s][:], ACT.Silu).then_inc(*act.does("sg"))
                lanes(eng, GROUPS, 2, body)

            @block.vector
            def _(eng):
                nc.vector.memset(eps[:], 1e-5).then_inc(ready, 1)
                def body(k, s, g, again):
                    pe, act, dve = pe_[s], act_[s], dve_[s]
                    eng.wait_ge(*pe.did(k, "mean"))
                    nc.vector.tensor_tensor(xc[:, s], at_group(OT, g), mean[s][:], ALU.subtract).then_inc(*dve.does("xc"))
                    yield
                    yield
                    rsqrt_dve(nc, eng, act, dve, k, "v", var[s][:], 1e-5, rs[:, s], r2[:, s])
                    nc.vector.tensor_tensor(on[:, s], xc[:, s], rs[:, s], ALU.mult).then_inc(*dve.does("on"))
                    eng.wait_ge(*dve.did(k, "on"))
                    nc.vector.tensor_scalar(on[:, s], on[:, s], gammaT[:, 0:1], betaT[:, 0:1], ALU.mult, ALU.add).then_inc(*dve.does("af"))
                    eng.wait_ge(*dve.did(k, "af"))
                    eng.wait_ge(*act.did(k, "sg"))
                    nc.vector.tensor_tensor(og[:, s], on[:, s], sg[:, s], ALU.mult).then_inc(*dve.does("og"))
                    yield
                    eng.wait_ge(*pe.did(k, "out"))
                    nc.vector.tensor_tensor(at_group(XT, g), out[s][:], at_group(XT, g), ALU.add).then_inc(*dve.does("xt"))
                lanes(eng, GROUPS, 2, body)

LH, LD = 16, 8

def linear_attn_stage(nc, name, XN, XT, wqkv, w1, w2, g1T, g2row, g3row, coef, eye, ones_mean):
    F3 = 3 * P
    HALF = LD // 2
    with ExitStack() as stack:
        m = Space(nc, name, stack)
        sq, ln, rs, r2 = (m.sb(n, [P, GRP]) for n in "sq ln rs r2".split())
        xm = m.sb("xm", [P, GRP])
        qk2 = m.sb("qk", [P, 2, 4, 2 * P])
        mn = m.sb("mn", [P, 4, 2 * P])
        v = m.sb("v", [P, 4, P])
        pr = m.sb("pr", [P, 2, LH * LD * LD])
        wr = m.sb("wr", [P, 2, LH * LD * LD])
        kv2 = m.sb("kv", [P, 2, 4, LD * LD])
        at = m.sb("at", [P, 4, P])
        t1 = m.sb("t1", [P, 4, P])
        hr = m.sb("hr", [P, 4 * LH])
        gr = m.sb("gr", [P, 4])
        aT = m.sb("aT", [P, GRP])
        hT = m.sb("hT", [P, GRP])
        lnh, rsh, r2h = (m.sb(n, [P, 4 * LH]) for n in "lnh rsh r2h".split())
        eps = m.sb("eps", [P, 1])
        ms = m.ps("ms")
        pj = [m.ps(f"pj{t}") for t in range(4)]
        turned, hid, out = m.ps("turned"), m.ps("hid"), m.ps("out")
        EPS = float(np.finfo(np.float32).eps)
        an, dn = rsqrt_names("m")
        pe_f, pe = Steps(m.sem("pe_front"), "ms p0 p1 p2 p3"), Steps(m.sem("pe"), "aT hid out")
        act_f, act = Steps(m.sem("act_front"), "sq " + an + " v0 v1 v2 v3 e"), Steps(m.sem("act"), "sq " + rsqrt_names("h")[0] + " sq2 " + rsqrt_names("g")[0] + " aT gelu")
        dve_f = Steps(m.sem("dve_front"), dn + " xm mn0 r0 mn1 r1 mn2 r2 mn3 r3 elu " + " ".join(f"kv{t} kc{t}" for t in range(4)))
        dve = Steps(m.sem("dve"), " ".join(f"at{t}" for t in range(4)) + " hs he " + rsqrt_names("h")[1] + " n1 n2 gs ge " + rsqrt_names("g")[1] + " a1 a2 a3 ha out")
        pool_f, pool = Steps(m.sem("pool_front"), " ".join(f"p{t}" for t in range(4))), Steps(m.sem("pool"), " ".join(f"w{t}" for t in range(4)))
        ready = m.sem("ready")
        ORDER = "FFBFBFBFBB"

        def flat(t):
            return t[:].rearrange("p a b -> p (a b)")
        with nc.Block() as block:
            @block.tensor
            def _(eng):
                def front(g, s, before):
                    eng.wait_ge(*act_f.did(g, "sq"))
                    if before:
                        eng.wait_ge(*dve_f.did(g - 1, "xm"))
                    nc.tensor.matmul(ms[:], ones_mean[:], sq[:], start=True, stop=True).then_inc(*pe_f.does("ms"))
                    yield
                    eng.wait_ge(*dve_f.did(g, "xm"))
                    for t in range(4):
                        if before:
                            eng.wait_ge(*act_f.did(g - 1, f"v{t}"))
                            eng.wait_ge(*dve_f.did(g - 1, f"r{t}"))
                        nc.tensor.matmul(pj[t][:, 0:F3], xm[:, t * P:(t + 1) * P], wqkv[:], start=True, stop=True).then_inc(*pe_f.does(f"p{t}"))
                    yield
                    yield
                    yield
                    yield

                def back(g, s, before):
                    yield
                    yield
                    yield
                    eng.wait_ge(*dve.did(g, "a3"))
                    if before:
                        eng.wait_ge(*act.did(g - 1, "aT"))
                    for t in range(4):
                        last = nc.tensor.transpose(turned[:, t * P:(t + 1) * P], at[:, t], eye[:])
                    last.then_inc(*pe.does("aT"))
                    yield
                    eng.wait_ge(*act.did(g, "aT"))
                    if before:
                        eng.wait_ge(*act.did(g - 1, "gelu"))
                    nc.tensor.matmul(hid[:], w1[:], aT[:], start=True, stop=True).then_inc(*pe.does("hid"))
                    eng.wait_ge(*act.did(g, "gelu"))
                    if before:
                        eng.wait_ge(*dve.did(g - 1, "out"))
                    nc.tensor.matmul(out[:], w2[:], hT[:], start=True, stop=True).then_inc(*pe.does("out"))
                    yield
                overlapped(eng, GROUPS, front, back, ORDER)

            @block.scalar
            def _(eng):
                eng.wait_ge(ready, 1)

                def front(g, s, before):
                    nc.scalar.preload_act_table_set("natural_log_exp_and_others")
                    if before:
                        eng.wait_ge(*pe_f.did(g - 1, "ms"))
                    nc.scalar.activation(sq[:], at_group(XN, g), ACT.Square).then_inc(*act_f.does("sq"))
                    yield
                    eng.wait_ge(*pe_f.did(g, "ms"))
                    rsqrt_act(nc, eng, act_f, g, "m", ms[:], eps[:], ln[:], rs[:], r2[:])
                    yield
                    for t in range(4):
                        eng.wait_ge(*dve_f.did(g, f"r{t}"))
                        if before:
                            eng.wait_ge(*pool_f.did(g - 1, f"p{t}"))
                        nc.scalar.activation(v[:, t], pj[t][:, 2 * P:F3], ACT.Copy).then_inc(*act_f.does(f"v{t}"))
                    nc.scalar.activation(mn[:], mn[:], ACT.Exp).then_inc(*act_f.does("e"))
                    yield
                    yield
                    yield

                def back(g, s, before):
                    yield
                    eng.wait_ge(*dve.did(g, "at3"))
                    nc.scalar.activation(t1[:], at[:], ACT.Square).then_inc(*act.does("sq"))
                    eng.wait_ge(*dve.did(g, "he"))
                    small_rsqrt_act(nc, eng, act, g, "h", hr[:], lnh[:], rsh[:], r2h[:])
                    yield
                    eng.wait_ge(*dve.did(g, "n2"))
                    nc.scalar.activation(t1[:], at[:], ACT.Square).then_inc(*act.does("sq2"))
                    eng.wait_ge(*dve.did(g, "ge"))
                    small_rsqrt_act(nc, eng, act, g, "g", gr[:], lnh[:, 0:4], rsh[:, 0:4], r2h[:, 0:4])
                    yield
                    eng.wait_ge(*pe.did(g, "aT"))
                    if before:
                        eng.wait_ge(*dve.did(g - 1, "ha"))
                    nc.scalar.activation(aT[:], turned[:], ACT.Copy).then_inc(*act.does("aT"))
                    yield
                    eng.wait_ge(*pe.did(g, "hid"))
                    nc.scalar.activation(hT[:], hid[:], ACT.Gelu).then_inc(*act.does("gelu"))
                    yield
                overlapped(eng, GROUPS, front, back, ORDER)

            @block.vector
            def _(eng):
                nc.vector.memset(eps[:], EPS).then_inc(ready, 1)

                def front(g, s, before):
                    qk, kv = qk2[:, s], kv2[:, s]
                    yield
                    rsqrt_dve(nc, eng, act_f, dve_f, g, "m", ms[:], EPS, rs[:], r2[:])
                    nc.vector.scalar_tensor_tensor(xm[:], at_group(XN, g), g1T[:, 0:1], rs[:], ALU.mult, ALU.mult).then_inc(*dve_f.does("xm"))
                    yield
                    for t in range(4):
                        eng.wait_ge(*pe_f.did(g, f"p{t}"))
                        if before:
                            eng.wait_ge(*dve_f.did(g - 1, "elu"))
                        nc.vector.tensor_scalar(mn[:, t], pj[t][:, 0:2 * P], 0.0, None, ALU.min).then_inc(*dve_f.does(f"mn{t}"))
                        if before == 2:
                            eng.wait_ge(*pool.did(g - 2, f"w{t}"))
                        nc.vector.tensor_scalar(qk[:, t], pj[t][:, 0:2 * P], 0.0, -1.0, ALU.max, ALU.add).then_inc(*dve_f.does(f"r{t}"))
                    eng.wait_ge(*act_f.did(g, "e"))
                    nc.vector.tensor_tensor(qk, qk, mn[:], ALU.add).then_inc(*dve_f.does("elu"))
                    yield
                    for t in range(4):
                        eng.wait_ge(*pool_f.did(g, f"p{t}"))
                        nc.vector.tensor_reduce(kv[:, t], pr[:, t % 2].rearrange("p (h f) -> p f h", h=LH), AX, ALU.add).then_inc(*dve_f.does(f"kv{t}"))
                        eng.wait_ge(*dve_f.did(g, f"kv{t}"))
                        nc.vector.tensor_tensor(kv[:, t], kv[:, t], coef[:], ALU.mult).then_inc(*dve_f.does(f"kc{t}"))
                        if t % 2:
                            yield

                def back(g, s, before):
                    def chain(name_):
                        eng.wait_ge(*dve.did(g, name_))
                    if before:
                        eng.wait_ge(*pe.did(g - 1, "aT"))
                    for t in range(4):
                        eng.wait_ge(*pool.did(g, f"w{t}"))
                        nc.vector.tensor_reduce(at[:, t], wr[:, t % 2].rearrange("p (f e) -> p f e", e=LD), AX, ALU.add).then_inc(*dve.does(f"at{t}"))
                    yield
                    eng.wait_ge(*act.did(g, "sq"))
                    nc.vector.tensor_reduce(hr[:], flat(t1).rearrange("p (h e) -> p h e", e=LD), AX, ALU.add).then_inc(*dve.does("hs"))
                    chain("hs")
                    nc.vector.tensor_scalar(hr[:], hr[:], 1.0 / LD, EPS, ALU.mult, ALU.add).then_inc(*dve.does("he"))
                    yield
                    rsqrt_dve(nc, eng, act, dve, g, "h", hr[:], 0.0, rsh[:], r2h[:])
                    at3 = flat(at).rearrange("p (h e) -> p h e", e=LD)
                    nc.vector.tensor_tensor(at3, at3, along(rsh[:], LD), ALU.mult).then_inc(*dve.does("n1"))
                    chain("n1")
                    nc.vector.tensor_tensor(at[:], at[:], over_heads(g2row[:], 4), ALU.mult).then_inc(*dve.does("n2"))
                    eng.wait_ge(*act.did(g, "sq2"))
                    nc.vector.tensor_reduce(gr[:], t1[:], AX, ALU.add).then_inc(*dve.does("gs"))
                    chain("gs")
                    nc.vector.tensor_scalar(gr[:], gr[:], 1.0 / P, EPS, ALU.mult, ALU.add).then_inc(*dve.does("ge"))
                    yield
                    rsqrt_dve(nc, eng, act, dve, g, "g", gr[:], 0.0, rsh[:, 0:4], r2h[:, 0:4])
                    nc.vector.tensor_tensor(t1[:], at[:], along(rsh[:, 0:4], P), ALU.mult).then_inc(*dve.does("a1"))
                    chain("a1")
                    nc.vector.tensor_tensor(t1[:], t1[:], over_heads(g3row[:], 4), ALU.mult).then_inc(*dve.does("a2"))
                    chain("a2")
                    nc.vector.tensor_tensor(at[:], at[:], t1[:], ALU.add).then_inc(*dve.does("a3"))
                    yield
                    eng.wait_ge(*act.did(g, "aT"))
                    nc.vector.tensor_tensor(at_group(XT, g), at_group(XT, g), aT[:], ALU.add).then_inc(*dve.does("ha"))
                    eng.wait_ge(*pe.did(g, "out"))
                    chain("ha")
                    nc.vector.tensor_tensor(at_group(XT, g), at_group(XT, g), out[:], ALU.add).then_inc(*dve.does("out"))
                    yield
                overlapped(eng, GROUPS, front, back, ORDER)

            @block.gpsimd
            def _(eng):
                def front(g, s, before):
                    qk = qk2[:, s]
                    yield
                    yield
                    yield
                    for t in range(4):
                        if t == 0:
                            eng.wait_ge(*dve_f.did(g, "elu"))
                        eng.wait_ge(*act_f.did(g, f"v{t}"))
                        if t >= 2:
                            eng.wait_ge(*dve_f.did(g, f"kv{t - 2}"))
                        elif before:
                            eng.wait_ge(*dve_f.did(g - 1, f"kv{t + 2}"))
                        k3 = qk[:, t, P:2 * P].rearrange("p (h e) -> p h e", e=LD).unsqueeze(3).to_broadcast([P, LH, LD, LD])
                        v3 = v[:, t].rearrange("p (h d) -> p h d", d=LD).unsqueeze(2).to_broadcast([P, LH, LD, LD])
                        nc.gpsimd.tensor_tensor(pr[:, t % 2].rearrange("p (h e d) -> p h e d", h=LH, e=LD), k3, v3, ALU.mult).then_inc(*pool_f.does(f"p{t}"))
                        if t % 2:
                            yield

                def back(g, s, before):
                    qk, kv = qk2[:, s], kv2[:, s]
                    for t in range(4):
                        eng.wait_ge(*dve_f.did(g, f"kc{t}"))
                        if t >= 2:
                            eng.wait_ge(*dve.did(g, f"at{t - 2}"))
                        elif before:
                            eng.wait_ge(*dve.did(g - 1, f"at{t + 2}"))
                        q3 = qk[:, t, 0:P].rearrange("p (h e) -> p h e", e=LD).unsqueeze(2).to_broadcast([P, LH, LD, LD])
                        kv3 = kv[:, t].rearrange("p (e d) -> p d e", d=LD).unsqueeze(1).to_broadcast([P, LH, LD, LD])
                        nc.gpsimd.tensor_tensor(wr[:, t % 2].rearrange("p (h d e) -> p h d e", h=LH, e=LD), q3, kv3, ALU.mult).then_inc(*pool.does(f"w{t}"))
                    for _ in range(5):
                        yield
                overlapped(eng, GROUPS, front, back, ORDER)

EX, MLP = 64, 256
BLOCKS = 2 * TOK // P + EX
SLOTS = BLOCKS * P

def sparse_route(nc, name, XN, HOT, WT, SLOT, BE, IDS, x_dram, ids_dram, w_gate, iota, eye, masks):
    C, E_ = CHUNKS, EX
    with ExitStack() as stack:
        m = Space(nc, name, stack)
        xs = m.sb("xs", [P, 2, GRP])
        xr = m.sb("xr", [P, 2, 4, P])
        lg = m.sb("lg", [P, 2, 4, E_])
        top4 = m.sb("top4", [P, 2, 4, 8])
        idx4 = m.sb("idx4", [P, 2, 4, 8], U32)
        top = m.sb("top", [P, C, 8])
        fi8 = m.sb("fi8", [P, C, 8])
        carrier = m.sb("carrier", [P, 2])
        fi = m.sb("fi", [P, 2, C])
        ex = m.sb("ex", [P, C])
        den = m.sb("den", [P, C])
        M = m.sb("M", [P, C * E_])
        rank = m.sb("rank", [P, C * E_])
        cnt = [m.sb(f"cnt{k}", [P, C * E_]) for k in range(2)]
        tot, incl, base, on1 = (m.sb(n, [P, E_]) for n in "tot incl base on1".split())
        ti = m.sb("ti", [P, E_], I32)
        sf = m.sb("sf", [P, 2, C])
        col = m.sb("col", [P, 1])
        ecol = m.sb("ecol", [P, 1])
        tokid = m.sb("tokid", [P, C], I32)
        zero = m.sb("zero", [P, BLOCKS], I32)
        si = m.sb("si", [P, 2, 2], U32)
        tk = m.sb("tk", [P, 2, 1], I32)
        back_i = m.sb("back_i", [BLOCKS, P], I32)
        back_f = m.sb("back_f", [BLOCKS, P])
        mark = m.sb("mark", [P, 3])
        zeroed, returned = m.sem("zeroed"), m.sem("returned")
        stored = [m.sem(f"stored{s}") for s in range(2)]
        scattered = [m.sem(f"scattered{s}") for s in range(2)]
        pe, act = Steps(m.sem("pe"), "lg xr"), Steps(m.sem("act"), "xs xr")
        dve = Steps(m.sem("dve"), "lg cr0 max cr1 at top idx")
        pe2 = Steps(m.sem("pe2"), "ranks be ids")
        end = Steps(m.sem("end"), "f0 f1 d den rec w1 h0 h1 M " + " ".join(f"rk{k} cn{k}" for k in range(4)) + " " + " ".join(f"px{k}" for k in range(5)) +
                    " ex rk tot t127 ti sh nb on1 incl excl base slot s0 r0 s1 r1 u le ej mn be bf ids")
        exped, consts = m.sem("exped"), m.sem("consts")
        pool = Steps(m.sem("pool"), "si tk carry")
        hot = HOT[:].rearrange("p (k c e) -> p k c e", k=2, e=E_)

        def ce(t):
            return t[:].rearrange("p (c e) -> p c e", e=E_)

        def pairs(eng, n, body):
            for s in range(2):
                body(s, s, 0)
            with eng.Fori(1, n // 2) as k:
                for s in range(2):
                    body(k * 2 + s, s, k)

        banks = [m.ps(f"bank{k}") for k in range(8)]
        with nc.Block() as block:
            @block.scalar
            def _(eng):
                def body(g, s, before):
                    again = not isinstance(g, int)
                    if again:
                        eng.wait_ge(*pe.did(g - 2, "xr"))
                    nc.scalar.activation(xs[:, s], at_group(XN, g), ACT.Copy).then_inc(*act.does("xs"))
                    eng.wait_ge(*pe.did(g, "xr"))
                    if again:
                        eng.wait_ge(stored[s], before * 16)
                    nc.scalar.activation(xr[:, s].rearrange("p t n -> p (t n)"), banks[2 + s][:], ACT.Copy).then_inc(*act.does("xr"))
                pairs(eng, GROUPS, body)
                eng.wait_ge(*end.did(0, "d"))
                nc.scalar.activation(ex[:], ex[:], ACT.Exp).then_inc(exped, 1)

            @block.sync
            def _(eng):
                def body(g, s, again):
                    eng.wait_ge(*act.did(g, "xr"))
                    eng.dma_start(x_dram.rearrange("(g t p) d -> g p t d", p=P, t=4)[bass.ds(g, 1)].rearrange("o p t d -> (o p) t d"), xr[:, s]).then_inc(stored[s], 16)
                tiles(eng, GROUPS, 2, body)
                eng.wait_ge(consts, 4)
                eng.dma_start(ids_dram.rearrange("(p n) o -> p (n o)", p=P), zero[:]).then_inc(zeroed, 16)
                for s in range(2):
                    eng.wait_ge(scattered[s], C * 16)
                eng.dma_start(back_i[:], ids_dram.rearrange("(b s) o -> b (s o)", s=P)).then_inc(returned, 16)
                eng.wait_ge(returned, 16)
                for s in range(2):
                    eng.wait_ge(stored[s], GROUPS // 2 * 16)

            @block.tensor
            def _(eng):
                def body(g, s, again):
                    eng.wait_ge(*act.did(g, "xs"))
                    if again:
                        eng.wait_ge(*dve.did(g - 2, "lg"))
                    for t in range(4):
                        last = nc.tensor.matmul(banks[s][:, t * E_:(t + 1) * E_], xs[:, s, t * P:(t + 1) * P], w_gate[:], start=True, stop=True)
                    last.then_inc(*pe.does("lg"))
                    if again:
                        eng.wait_ge(*act.did(g - 2, "xr"))
                    for t in range(4):
                        last = nc.tensor.transpose(banks[2 + s][:, t * P:(t + 1) * P], xs[:, s, t * P:(t + 1) * P], eye[:])
                    last.then_inc(*pe.does("xr"))
                tiles(eng, GROUPS, 2, body)
                eng.wait_ge(*end.did(0, "M"))
                eng.wait_ge(*act.did(GROUPS - 1, "xr"))
                for k in range(4):
                    nc.tensor.matmul(banks[k][:], masks["row_lt_col"][:], M[:, k * GRP:(k + 1) * GRP], start=True, stop=True)
                    last = nc.tensor.matmul(banks[4 + k][:], masks["ones"][:], M[:, k * GRP:(k + 1) * GRP], start=True, stop=True)
                last.then_inc(*pe2.does("ranks"))
                eng.wait_ge(*end.did(0, "mn"))
                nc.tensor.matmul(banks[0][0:1, 0:P], ecol[:], eye[:], start=True, stop=True).then_inc(*pe2.does("be"))
                eng.wait_ge(*end.did(0, "bf"))
                nc.tensor.transpose(banks[1][:, 0:BLOCKS], back_f[:], eye[:]).then_inc(*pe2.does("ids"))

            @block.vector
            def _(eng):
                def body(g, s, again):
                    eng.wait_ge(*pe.did(g, "lg"))
                    nc.vector.tensor_copy(lg[:, s].rearrange("p t e -> p (t e)"), banks[s][:, 0:4 * E_]).then_inc(*dve.does("lg"))
                    eng.wait_ge(*dve.did(g, "lg"))
                    nc.vector.memset(carrier[:, 0:1], 0.0).then_inc(*dve.does("cr0"))
                    for t in range(4):
                        last = nc.vector.max(top4[:, s, t], lg[:, s, t])
                    last.then_inc(*dve.does("max"))
                    eng.wait_ge(*dve.did(g, "max"))
                    nc.vector.memset(carrier[:, 1:2], 0.0).then_inc(*dve.does("cr1"))
                    for t in range(4):
                        last = nc.vector.max_index(idx4[:, s, t], top4[:, s, t], lg[:, s, t])
                    last.then_inc(*dve.does("at"))
                    nc.vector.tensor_copy(top[:, bass.ds(g * 4, 4), :], top4[:, s]).then_inc(*dve.does("top"))
                    eng.wait_ge(*dve.did(g, "at"))
                    nc.vector.tensor_copy(fi8[:, bass.ds(g * 4, 4), :], idx4[:, s]).then_inc(*dve.does("idx"))
                tiles(eng, GROUPS, 2, body)

                def step(ins, name_):
                    ins.then_inc(*end.does(name_))
                    eng.wait_ge(*end.did(0, name_))
                eng.wait_ge(*dve.did(GROUPS - 1, "idx"))
                for k in range(2):
                    step(nc.vector.tensor_copy(fi[:, k], fi8[:, :, k]), f"f{k}")
                step(nc.vector.tensor_tensor(ex[:], top[:, :, 1], top[:, :, 0], ALU.subtract), "d")
                eng.wait_ge(exped, 1)
                step(nc.vector.tensor_scalar(den[:], ex[:], 1.0, None, ALU.add), "den")
                step(nc.vector.reciprocal(WT[:, 0], den[:]), "rec")
                step(nc.vector.tensor_tensor(WT[:, 1], WT[:, 0], ex[:], ALU.mult), "w1")
                for k in range(2):
                    step(nc.vector.tensor_tensor(hot[:, k], iota[:, 0:E_].unsqueeze(1).to_broadcast([P, C, E_]), along(fi[:, k], E_), ALU.is_equal), f"h{k}")
                step(nc.vector.tensor_tensor(ce(M), hot[:, 0], hot[:, 1], ALU.add), "M")
                eng.wait_ge(*pe2.did(0, "ranks"))
                for k in range(4):
                    step(nc.vector.tensor_copy(rank[:, k * GRP:(k + 1) * GRP], banks[k][:]), f"rk{k}")
                    step(nc.vector.tensor_copy(cnt[0][:, k * GRP:(k + 1) * GRP], banks[4 + k][:]), f"cn{k}")
                for k in range(5):
                    a, b, n = cnt[k % 2], cnt[1 - k % 2], (1 << k) * E_
                    nc.vector.tensor_copy(b[:, 0:n], a[:, 0:n])
                    step(nc.vector.tensor_tensor(b[:, n:], a[:, n:], a[:, 0:C * E_ - n], ALU.add), f"px{k}")
                summed = cnt[1]
                step(nc.vector.tensor_copy(tot[:], summed[:, (C - 1) * E_:C * E_]), "ex")
                step(nc.vector.tensor_tensor(rank[:, E_:], rank[:, E_:], summed[:, 0:(C - 1) * E_], ALU.add), "rk")
                step(nc.vector.tensor_scalar(base[:], tot[:], float(P - 1), None, ALU.add), "tot")
                step(nc.vector.tensor_copy(ti[:], base[:]), "t127")
                step(nc.vector.tensor_scalar(ti[:], ti[:], 7, None, ALU.logical_shift_right), "ti")
                step(nc.vector.tensor_copy(tot[:], ti[:]), "sh")
                step(nc.vector.memset(on1[:], 1.0), "nb")
                step(nc.vector.tensor_tensor_scan(incl[:], on1[:], tot[:], 0.0, ALU.mult, ALU.add), "on1")
                step(nc.vector.tensor_tensor(base[:], incl[:], tot[:], ALU.subtract), "incl")
                step(nc.vector.tensor_scalar(base[:], base[:], float(P), None, ALU.mult), "excl")
                step(nc.vector.tensor_tensor(ce(rank), ce(rank), base[:].unsqueeze(1).to_broadcast([P, C, E_]), ALU.add), "base")
                eng.wait_ge(consts, 4)
                step(nc.vector.tensor_scalar(on1[:], incl[:], col[:, 0:1], None, ALU.is_le), "slot")
                for k in range(2):
                    step(nc.vector.tensor_tensor(hot[:, k], hot[:, k], ce(rank), ALU.mult), f"s{k}")
                    step(nc.vector.tensor_reduce(sf[:, k], hot[:, k], AX, ALU.add), f"r{k}")
                step(nc.vector.tensor_copy(SLOT[:], sf[:]), "u")
                step(nc.vector.tensor_reduce(ecol[:], on1[:], AX, ALU.add), "le")
                step(nc.vector.tensor_scalar(ecol[:], ecol[:], float(E_ - 1), None, ALU.min), "ej")
                step(nc.vector.tensor_copy(col[:], ecol[:]), "mn")
                eng.wait_ge(*pe2.did(0, "be"))
                step(nc.vector.tensor_copy(BE[:], banks[0][0:1, 0:BLOCKS]), "be")
                eng.wait_ge(returned, 16)
                step(nc.vector.tensor_copy(back_f[:], back_i[:]), "bf")
                eng.wait_ge(*pe2.did(0, "ids"))
                step(nc.vector.tensor_copy(IDS[:], banks[1][:, 0:BLOCKS]), "ids")

            @block.gpsimd
            def _(eng):
                nc.gpsimd.iota(tokid[:], pattern=[[P, C]], base=0, channel_multiplier=1).then_inc(consts, 1)
                nc.gpsimd.memset(zero[:], 0).then_inc(consts, 1)
                nc.gpsimd.memset(mark[:, 0:1], 0.0).then_inc(consts, 1)
                nc.gpsimd.iota(col[:], pattern=[[0, 1]], base=0, channel_multiplier=1, allow_small_or_imprecise_dtypes=True).then_inc(consts, 1)
                eng.wait_ge(*end.did(0, "u"))
                eng.wait_ge(consts, 4)
                eng.wait_ge(zeroed, 16)

                def carry(s):
                    nc.gpsimd.tensor_tensor(mark[:, 1 + s:2 + s], mark[:, 0:1], mark[:, 0:1], ALU.add).then_inc(*pool.does("carry"))

                def body(c, s, before):
                    if not isinstance(c, int):
                        eng.wait_ge(scattered[s], before * 32)
                    nc.gpsimd.tensor_copy(si[:, s], SLOT[:, :, bass.ds(c, 1)].rearrange("p k o -> p (k o)")).then_inc(*pool.does("si"))
                    nc.gpsimd.tensor_copy(tk[:, s], tokid[:, bass.ds(c, 1)]).then_inc(*pool.does("tk"))
                    eng.wait_ge(*pool.did(c, "tk"))
                    carry(s)
                    for k in range(2):
                        eng.indirect_dma_start(ids_dram, bass.IndirectOffsetOnAxis(ap=si[:, s, k:k + 1], axis=0), tk[:, s], None).then_inc(scattered[s], 16)
                pairs(eng, C, body)

def sparse_experts(nc, name, BE, IDS, x_dram, y_dram, w0_dram, w1_dram, wo_dram, eye):
    F = MLP // P
    with ExitStack() as stack:
        m = Space(nc, name, stack)
        W = 8
        w0 = m.sb("w0", [P, W, MLP])
        w1 = m.sb("w1", [P, W, MLP])
        wo = m.sb("wo", [P, W, F, P])
        ix = m.sb("ix", [P, W, 1], U32)
        xg = m.sb("xg", [P, W, P])
        xT = m.sb("xT", [P, 2, P])
        s0 = m.sb("s0", [P, 2, MLP])
        hid = m.sb("hid", [P, 2, MLP])
        y = m.sb("y", [P, W, P])
        mark, started = m.sb("mark", [P, 1 + W]), m.sem("started")
        xp = [m.ps(f"xp{k}") for k in range(2)]
        a = [m.ps(f"a{k}") for k in range(2)]
        b = [m.ps(f"b{k}") for k in range(2)]
        yp = [m.ps(f"yp{k}") for k in range(2)]
        wl = [m.sem(f"wl{k}") for k in range(W)]
        xl = [m.sem(f"xl{k}") for k in range(W)]
        ys = [m.sem(f"ys{k}") for k in range(W)]
        pe_x, pe_h, pe_y = (Steps(m.sem(f"pe_{n}"), n) for n in "xT h y".split())
        act_x, act_s = Steps(m.sem("act_x"), "xT"), Steps(m.sem("act_s"), "s0")
        dve_h, dve_y, pool = Steps(m.sem("dve_h"), "hid"), Steps(m.sem("dve_y"), "y"), Steps(m.sem("pool"), "ix carry")

        def slots(eng, body):
            for j in range(W):
                body(j, j, 1, False)
            with eng.Fori(1, BLOCKS // W) as k:
                for s in range(W):
                    body(k * W + s, s, k + 1, True)

        with nc.Block() as block:
            @block.sync
            def _(eng):
                def body(j, s, times, again):
                    e = eng.value_load(BE[0:1, bass.ds(j, 1)], min_val=0, max_val=EX - 1)
                    if again:
                        store(j - W, s)
                    eng.dma_start(w0[:, s], w0_dram[bass.ds(e, 1)].rearrange("o d f -> (o d) f")).then_inc(wl[s], 16)
                    eng.dma_start(w1[:, s], w1_dram[bass.ds(e, 1)].rearrange("o d f -> (o d) f")).then_inc(wl[s], 16)
                    eng.dma_start(wo[:, s], wo_dram[bass.ds(e, 1)].rearrange("o (c p) d -> (o p) c d", p=P)).then_inc(wl[s], 16)

                def store(j, s):
                    eng.wait_ge(*dve_y.did(j, "y"))
                    eng.dma_start(y_dram.rearrange("(b s) d -> b s d", s=P)[bass.ds(j, 1)].rearrange("o s d -> (o s) d"), y[:, s]).then_inc(ys[s], 16)
                slots(eng, body)
                for s in range(W):
                    store(BLOCKS - W + s, s)
                for s in range(W):
                    eng.wait_ge(ys[s], BLOCKS // W * 16)

            @block.gpsimd
            def _(eng):
                nc.gpsimd.memset(mark[:, 0:1], 0.0).then_inc(started, 1)
                eng.wait_ge(started, 1)

                def carry(s):
                    nc.gpsimd.tensor_tensor(mark[:, 1 + s:2 + s], mark[:, 0:1], mark[:, 0:1], ALU.add).then_inc(*pool.does("carry"))

                def body(j, s, times, again):
                    if again:
                        eng.wait_ge(*pe_x.did(j - W, "xT"))
                    nc.gpsimd.tensor_copy(ix[:, s], IDS[:, bass.ds(j, 1)]).then_inc(*pool.does("ix"))
                    eng.wait_ge(*pool.did(j, "ix"))
                    carry(s)
                    eng.indirect_dma_start(xg[:, s], None, x_dram, bass.IndirectOffsetOnAxis(ap=ix[:, s], axis=0)).then_inc(xl[s], 16)
                slots(eng, body)

            def lagged(eng, body):
                for j in range(2 * W):
                    body(j, j % W, j // W, [p for p in range(3) if j >= p])
                with eng.Fori(2, BLOCKS // W) as k:
                    for s in range(W):
                        body(k * W + s, s, k, [0, 1, 2])
                for e in range(2):
                    body(BLOCKS + e, e, BLOCKS // W, [p for p in range(3) if p > e])

            def fills(s, turn, back):
                return turn + 1 if s >= back else turn + 0

            def exists(j, back):
                return not isinstance(j, int) or j >= back

            @block.tensor
            def _(eng):
                def body(j, s, turn, parts):
                    if 0 in parts:
                        k = s % 2
                        eng.wait_ge(xl[s], fills(s, turn, 0) * 16)
                        if exists(j, 2):
                            eng.wait_ge(*act_x.did(j - 2, "xT"))
                        nc.tensor.transpose(xp[k][:, 0:P], xg[:, s], eye[:]).then_inc(*pe_x.does("xT"))
                    if 1 in parts:
                        z, k = (s - 1) % W, (s - 1) % 2
                        eng.wait_ge(wl[z], fills(s, turn, 1) * 48)
                        eng.wait_ge(*act_x.did(j - 1, "xT"))
                        if exists(j, 3):
                            eng.wait_ge(*dve_h.did(j - 3, "hid"))
                        for bank, w in ((a, w0), (b, w1)):
                            for c in range(F):
                                last = nc.tensor.matmul(bank[k][:, c * P:(c + 1) * P], w[:, z, c * P:(c + 1) * P], xT[:, k], start=True, stop=True)
                        last.then_inc(*pe_h.does("h"))
                    if 2 in parts:
                        z, k = (s - 2) % W, s % 2
                        eng.wait_ge(*dve_h.did(j - 2, "hid"))
                        if exists(j, 4):
                            eng.wait_ge(*dve_y.did(j - 4, "y"))
                        for c in range(F):
                            last = nc.tensor.matmul(yp[k][:, 0:P], hid[:, k, c * P:(c + 1) * P], wo[:, z, c], start=(c == 0), stop=(c == F - 1))
                        last.then_inc(*pe_y.does("y"))
                lagged(eng, body)

            @block.scalar
            def _(eng):
                def body(j, s, turn, parts):
                    if 0 in parts:
                        k = s % 2
                        eng.wait_ge(*pe_x.did(j, "xT"))
                        if exists(j, 2):
                            eng.wait_ge(*pe_h.did(j - 2, "h"))
                        nc.scalar.activation(xT[:, k], xp[k][:, 0:P], ACT.Copy).then_inc(*act_x.does("xT"))
                    if 1 in parts:
                        k = (s - 1) % 2
                        eng.wait_ge(*pe_h.did(j - 1, "h"))
                        if exists(j, 3):
                            eng.wait_ge(*dve_h.did(j - 3, "hid"))
                        nc.scalar.activation(s0[:, k], a[k][:, 0:MLP], ACT.Silu).then_inc(*act_s.does("s0"))
                lagged(eng, body)

            @block.vector
            def _(eng):
                def body(j, s, turn, parts):
                    if 1 in parts:
                        k = (s - 1) % 2
                        eng.wait_ge(*act_s.did(j - 1, "s0"))
                        if exists(j, 3):
                            eng.wait_ge(*pe_y.did(j - 3, "y"))
                        nc.vector.tensor_tensor(hid[:, k], s0[:, k], b[k][:, 0:MLP], ALU.mult).then_inc(*dve_h.does("hid"))
                    if 2 in parts:
                        z, k = (s - 2) % W, s % 2
                        eng.wait_ge(*pe_y.did(j - 2, "y"))
                        if exists(j, W + 2):
                            eng.wait_ge(ys[z], fills(s, turn, 2) * 16 - 16)
                        nc.vector.tensor_copy(y[:, z], yp[k][:, 0:P]).then_inc(*dve_y.does("y"))
                lagged(eng, body)

def sparse_combine(nc, name, SLOT, WT, XT, y_dram, eye):
    with ExitStack() as stack:
        m = Space(nc, name, stack)
        W = 4
        ix = m.sb("ix", [P, W, 2], U32)
        yg = m.sb("yg", [P, W, 2, P])
        wt = m.sb("wt", [P, W, 2])
        o = m.sb("o", [P, 2, P])
        mark, started = m.sb("mark", [P, 1 + W]), m.sem("started")
        turned = [m.ps(f"turned{k}") for k in range(2)]
        got = [m.sem(f"got{k}") for k in range(W)]
        pe, act, dve, pool = Steps(m.sem("pe"), "t"), Steps(m.sem("act"), "wt"), Steps(m.sem("dve"), "o0 o1 x"), Steps(m.sem("pool"), "ix carry")

        def slots(eng, body):
            for j in range(W):
                body(j, j, 1, False)
            with eng.Fori(1, CHUNKS // W) as k:
                for s in range(W):
                    body(k * W + s, s, k + 1, True)
        with nc.Block() as block:
            @block.gpsimd
            def _(eng):
                nc.gpsimd.memset(mark[:, 0:1], 0.0).then_inc(started, 1)
                eng.wait_ge(started, 1)

                def carry(s):
                    nc.gpsimd.tensor_tensor(mark[:, 1 + s:2 + s], mark[:, 0:1], mark[:, 0:1], ALU.add).then_inc(*pool.does("carry"))

                def body(c, s, times, again):
                    if again:
                        eng.wait_ge(*dve.did(c - W, "o1"))
                    nc.gpsimd.tensor_copy(ix[:, s], SLOT[:, :, bass.ds(c, 1)].rearrange("p k o -> p (k o)")).then_inc(*pool.does("ix"))
                    eng.wait_ge(*pool.did(c, "ix"))
                    carry(s)
                    for k in range(2):
                        eng.indirect_dma_start(yg[:, s, k], None, y_dram, bass.IndirectOffsetOnAxis(ap=ix[:, s, k:k + 1], axis=0)).then_inc(got[s], 16)
                slots(eng, body)

            @block.scalar
            def _(eng):
                def body(c, s, times, again):
                    if again:
                        eng.wait_ge(*dve.did(c - W, "o1"))
                    nc.scalar.activation(wt[:, s], WT[:, :, bass.ds(c, 1)].rearrange("p k o -> p (k o)"), ACT.Copy).then_inc(*act.does("wt"))
                slots(eng, body)

            @block.vector
            def _(eng):
                def body(c, s, times, again):
                    k = s % 2
                    eng.wait_ge(got[s], times * 32)
                    eng.wait_ge(*act.did(c, "wt"))
                    if again or s >= 2:
                        eng.wait_ge(*pe.did(c - 2, "t"))
                    nc.vector.tensor_scalar(o[:, k], yg[:, s, 0], wt[:, s, 0:1], None, ALU.mult).then_inc(*dve.does("o0"))
                    eng.wait_ge(*dve.did(c, "o0"))
                    nc.vector.scalar_tensor_tensor(o[:, k], yg[:, s, 1], wt[:, s, 1:2], o[:, k], ALU.mult, ALU.add).then_inc(*dve.does("o1"))
                    eng.wait_ge(*pe.did(c, "t"))
                    nc.vector.tensor_tensor(XT[:, bass.ds(c * P, P)], XT[:, bass.ds(c * P, P)], turned[k][:, 0:P], ALU.add).then_inc(*dve.does("x"))
                slots(eng, body)

            @block.tensor
            def _(eng):
                def body(c, s, times, again):
                    k = s % 2
                    eng.wait_ge(*dve.did(c, "o1"))
                    if again or s >= 2:
                        eng.wait_ge(*dve.did(c - 2, "x"))
                    nc.tensor.transpose(turned[k][:, 0:P], o[:, k], eye[:]).then_inc(*pe.does("t"))
                slots(eng, body)

LAMBDA_INIT = 0.8 - 0.6 * float(np.exp(-0.3 * 0))
LIN_SCALE = 1.0 / float(np.sqrt(D // 2))

def load_stage(nc, name, pairs):
    with nc.semaphore(name + "_a") as sem_a, nc.semaphore(name + "_b") as sem_b:
        first, second = Loads(sem_a), Loads(sem_b)
        with nc.Block() as block:
            @block.sync
            def _(eng):
                for tile, source in pairs[0::2]:
                    eng.dma_start(tile, source).then_inc(*first.one())
                eng.wait_ge(*first.all())

            @block.scalar
            def _(eng):
                for tile, source in pairs[1::2]:
                    eng.dma_start(tile, source).then_inc(*second.one())
                if second.count:
                    eng.wait_ge(*second.all())

def begin_load(nc, name, stack, pairs):
    first, second = (Loads(stack.enter_context(nc.semaphore(name + which))) for which in ("_a", "_b"))
    with nc.Block() as block:
        @block.sync
        def _(eng):
            for tile, source in pairs[0::2]:
                eng.dma_start(tile, source).then_inc(*first.one())

        @block.scalar
        def _(eng):
            for tile, source in pairs[1::2]:
                eng.dma_start(tile, source).then_inc(*second.one())
    return first, second

def finish_load(nc, loads):
    with nc.Block() as block:
        @block.sync
        def _(eng):
            for queue in loads:
                eng.wait_ge(*queue.all())

def clear_semaphores(nc):
    with nc.Block() as block:
        @block.gpsimd
        def _(eng):
            eng.sem_clear(range(FIRST_SEM, 256))

FIRST_SEM = 99

def layer0(nc, a, XT, XN, c):
    with ExitStack() as inner:
        m = Space(nc, "l0d_", inner)
        HT = m.sb("HT", [P, TOK])
        w_up, w_down = m.sb("w_up", [P, 4 * P]), m.sb("w_down", [P, 4 * P])
        with ExitStack() as delta:
            m = Space(nc, "l0e_", delta)
            GL, SCAL, Wba = m.sb("GL", [P, CHUNKS * 16]), m.sb("SCAL", [P, CHUNKS * SC]), m.sb("Wba", [P, 16])
            w = {k: m.sb("w_" + k, [P, 8 * P]) for k in "qkvgo"}
            o_norm = m.sb("o_norm", [P, 1])
            masks = dict(c)
            masks["level"] = m.sb("level", [P, 7 * P])
            load_stage(nc, "l0_gates", [(Wba[:], a["Wba"]), (o_norm[:], a["o_norm_w"])])
            weights = begin_load(nc, "l0_load", delta, [(masks["level"][:], a["level"])] + [(w[k][:], a["W" + k]) for k in "qkvgo"] +
                       [(w_up[:], a["w_up"]), (w_down[:], a["w_down"])])
            norm_stage(nc, "l0n_", XT, XN, c["ones_mean"], (HT, Wba, GL))
            finish_load(nc, weights)
            with nc.semaphore("l0_scaled") as scaled, nc.Block() as block:
                @block.vector
                def _(eng):
                    nc.vector.tensor_scalar(w["o"][:], w["o"][:], o_norm[:, 0:1], None, ALU.mult).then_inc(scaled, 1)
            delta_gates(nc, "l0g_", GL, SCAL, a["A_log"], a["dt_bias"], masks)
            delta_stage(nc, "l0s_", HT, XN, SCAL, w, masks)
        relu_mlp_stage(nc, "l0m_", XT, HT, w_up, w_down, c["ones_mean"])
    with ExitStack() as stack:
        m = Space(nc, "l0_", stack)
        biasT, gammaT, betaT = (m.sb(n, [P, 3]) for n in "biasT gammaT betaT".split())
        bias_rows, WQ = m.sb("bias_rows", [P, 3, P]), m.sb("WQ", [P, 6, P])
        load_stage(nc, "l0q_load", [(biasT[:], a["q_biasT"]), (gammaT[:], a["q_gammaT"]), (betaT[:], a["q_betaT"])] + [(bias_rows[:, b], on_all_partitions(a["q_bias"][b])) for b in range(3)])
        qlora_weights(nc, "l0w_", a["q_weights"], a["q_scales"], a["q_lora_a"], a["q_lora_bT"], WQ, c["eye"])
        qlora_stage(nc, "l0q_", XT, XN, WQ, biasT, bias_rows, gammaT, betaT, c["eye"])

def layer1(nc, a, XT, XN, c):
    with ExitStack() as stack:
        m = Space(nc, "l1m_", stack)
        W1, W2 = m.sb("W1", [P, 8, 4 * P]), m.sb("W2", [P, 8, 4, P])
        B1, b2 = m.sb("B1", [P, 8, 4]), m.sb("b2", [8, P])
        RW, wr, br = m.sb("RW", [P, CHUNKS * 8]), m.sb("wr", [P, 8]), m.sb("br", [P, 8])
        gammaT, betaT = m.sb("gammaT", [P, 1]), m.sb("betaT", [P, 1])
        with ExitStack() as attention:
            m = Space(nc, "l1_", attention)
            Vh, head_rows = m.sb("Vh", [P, AN * QT * VW]), m.sb("head_rows", [AH, P])
            w, wv, w_out = [m.sb(f"w{k}", [P, P]) for k in range(4)], m.sb("wv", [P, P]), m.sb("w_out", [P, P])
            cos, sin = m.sb("cos", [P, SEQ]), m.sb("sin", [P, SEQ])
            q_dram = nc.dram_tensor("attn_q", [AN, 3, AD, SEQ], BF16).ap()
            k_dram = nc.dram_tensor("attn_k", [AN, 5, AD, SEQ], BF16).ap()
            ctx_dram = nc.dram_tensor("attn_ctx", [AN, AD, SEQ], F32).ap()
            sum_dram, rec_dram = (nc.dram_tensor(n, [AN, SEQ], F32).ap() for n in ("attn_sums", "attn_inverses"))
            weights = begin_load(nc, "l1_load", attention, [(w[k][:], a[f"rope_w{k}"]) for k in range(4)] + [
                (wv[:], a["attn_wv"]), (w_out[:], a["attn_wo"]), (cos[:], a["cos"]), (sin[:], a["sin"]), (head_rows[:], a["head_rows"])])
            experts = begin_load(nc, "l1m_load", attention, [
                (W1[:], a["moe_W1"]), (W2[:], a["moe_W2"]), (B1[:], a["moe_B1"]), (b2[:], a["moe_b2"]), (wr[:], a["moe_wr"]),
                (br[:], on_all_partitions(a["moe_br"])), (gammaT[:], a["moe_gamma"]), (betaT[:], a["moe_beta"])])
            norm_stage(nc, "l1n_", XT, XN, c["ones_mean"])
            finish_load(nc, weights)
            attn_project(nc, "l1p_", XN, Vh, q_dram, k_dram, w, wv, cos, sin)
            attn_heads(nc, "l1h_", Vh, ctx_dram, sum_dram, q_dram, k_dram, c["eye16"])
            attn_output(nc, "l1o_", ctx_dram, sum_dram, rec_dram, XT, w_out, head_rows)
            finish_load(nc, experts)
        clear_semaphores(nc)
        router_small(nc, "l1r_", XN, RW, wr, br, c["iota"], 8)
        dense_moe(nc, "l1e_", XN, XT, RW, W1, B1, W2, b2, gammaT, betaT, c["eye"], 8)

def layer2(nc, a, XT, XN, c):
    with ExitStack() as stack:
        m = Space(nc, "l2_", stack)
        wqkv, w1, w2 = m.sb("wqkv", [P, 3 * P]), m.sb("w1", [P, P]), m.sb("w2", [P, P])
        g1T, g2, g2row, g3row = m.sb("g1T", [P, 1]), m.sb("g2", [P, 8]), m.sb("g2row", [P, P]), m.sb("g3row", [P, P])
        coef, lam, prod, exps, lmb = m.sb("coef", [P, 64]), m.sb("lam", [P, 4]), m.sb("prod", [P, 2]), m.sb("exps", [P, 2]), m.sb("lmb", [P, 1])
        load_stage(nc, "l2_load", [(wqkv[:], a["lin_wqkv"]), (w1[:], a["lin_w1"]), (w2[:], a["lin_w2"]), (g1T[:], a["lin_g1"]), (g2[:], on_all_partitions(a["lin_g2"])),
                                   (g3row[:], on_all_partitions(a["lin_g3"])), (lam[:], on_all_partitions(a["lin_lambda"]))])
        with nc.semaphore("l2_dve") as dve_sem, nc.semaphore("l2_exp") as exp_done, nc.Block() as block:
            dve = Steps(dve_sem, "prod diff lmb fill coef")

            @block.scalar
            def _(eng):
                eng.wait_ge(*dve.did(0, "prod"))
                nc.scalar.activation(exps[:], prod[:], ACT.Exp).then_inc(exp_done, 1)

            @block.vector
            def _(eng):
                pairs = lam[:].rearrange("p (a b) -> p a b", b=2)
                nc.vector.tensor_tensor(prod[:], pairs[:, :, 0], pairs[:, :, 1], ALU.mult).then_inc(*dve.does("prod"))
                eng.wait_ge(exp_done, 1)
                nc.vector.tensor_tensor(lmb[:], exps[:, 0:1], exps[:, 1:2], ALU.subtract).then_inc(*dve.does("diff"))
                eng.wait_ge(*dve.did(0, "diff"))
                nc.vector.tensor_scalar(lmb[:], lmb[:], LAMBDA_INIT, None, ALU.add).then_inc(*dve.does("lmb"))
                nc.vector.memset(coef[:, 0:32], LIN_SCALE)
                nc.vector.memset(coef[:, 32:64], -LIN_SCALE).then_inc(*dve.does("fill"))
                nc.vector.tensor_scalar(g2row[:].rearrange("p (h d) -> p h d", d=8), over_heads(g2[:], 16), 1.0 - LAMBDA_INIT, None, ALU.mult)
                eng.wait_ge(*dve.did(0, "fill"))
                nc.vector.tensor_scalar(coef[:, 32:64], coef[:, 32:64], lmb[:, 0:1], None, ALU.mult).then_inc(*dve.does("coef"))
        norm_stage(nc, "l2n_", XT, XN, c["ones_mean"])
        linear_attn_stage(nc, "l2a_", XN, XT, wqkv, w1, w2, g1T, g2row, g3row, coef, c["eye"], c["ones_mean"])
    clear_semaphores(nc)
    with ExitStack() as stack:
        m = Space(nc, "l2s_", stack)
        w_gate, WT, SLOT = m.sb("w_gate", [P, EX]), m.sb("WT", [P, 2, CHUNKS]), m.sb("SLOT", [P, 2, CHUNKS], U32)
        BE, IDS = m.sb("BE", [1, BLOCKS], I32), m.sb("IDS", [P, BLOCKS], U32)
        x_dram = nc.dram_tensor("sparse_x", [TOK, D], F32).ap()
        y_dram = nc.dram_tensor("sparse_y", [SLOTS, D], F32).ap()
        ids_dram = nc.dram_tensor("sparse_ids", [SLOTS, 1], I32).ap()
        load_stage(nc, "l2s_load", [(w_gate[:], a["sparse_gate"])])
        with ExitStack() as scratch:
            HOT = Space(nc, "l2h_", scratch).sb("HOT", [P, 2 * CHUNKS * EX])
            sparse_route(nc, "l2r_", XN, HOT, WT, SLOT, BE, IDS, x_dram, ids_dram, w_gate, c["iota"], c["eye"], c)
        sparse_experts(nc, "l2e_", BE, IDS, x_dram, y_dram, a["sparse_w0"], a["sparse_w1"], a["sparse_wo"], c["eye"])
        sparse_combine(nc, "l2c_", SLOT, WT, XT, y_dram, c["eye"])

def layer3(nc, a, XT, XN, c):
    with ExitStack() as stack:
        m = Space(nc, "l3_", stack)
        GT, OT = m.sb("GT", [P, TOK]), m.sb("OT", [P, TOK])
        shapes = {"gk1": 16, "gb": 1, "wq": 1024, "wk": 1024, "wv": 1024, "pick": 1024, "fold": 1024, "wg": P, "wo": P, "gamma": 1, "beta": 1}
        t = {k: m.sb(k, [P, n]) for k, n in shapes.items()}
        t["gk2"] = m.sb("gk2", [16, P])
        weights = begin_load(nc, "l3_load", stack, [(tile[:], a["gla_" + k]) for k, tile in t.items()])
        norm_stage(nc, "l3n_", XT, XN, c["ones_mean"])
        finish_load(nc, weights)
        gla_gates(nc, "l3g_", XN, GT, t["gk1"], t["gk2"], t["gb"])
        gla_states(nc, "l3s_", XN, GT, OT, t["wq"], t["wk"], t["wv"], t["pick"], t["fold"])
        gla_output(nc, "l3o_", XN, OT, XT, t["wg"], t["wo"], t["gamma"], t["beta"], c["ones_mean"])
    with ExitStack() as stack:
        m = Space(nc, "l3m_", stack)
        w1, w2, b1, b2 = m.sb("w1", [P, 4 * P]), m.sb("w2", [P, 4 * P]), m.sb("b1", [P, 4]), m.sb("b2", [P, 1])
        load_stage(nc, "l3m_load", [(b1[:], a["bin_b1"]), (b2[:], a["bin_b2"])])
        binary_weights(nc, "l3b_", a["bin_w1"], a["bin_w2"], w1, w2, c["eye"])
        gelu_mlp_stage(nc, "l3f_", XT, XN, w1, w2, b1, b2)

MASKS = "row_le_col row_gt_col row_lt_col ones eye".split()

def network(nc, a, out):
    with ExitStack() as stack:
        m = Space(nc, "net_", stack)
        XT, XN = m.sb("XT", [P, TOK]), m.sb("XN", [P, TOK])
        c = {k: m.sb(k, [P, P]) for k in MASKS}
        c["eye16"], c["iota"], c["ones_mean"] = m.sb("eye16", [P, P], BF16), m.sb("iota", [P, EX]), m.sb("ones_mean", [P, P])
        load_stage(nc, "net_load", [(XT[:], a["xT"])] + [(c[k][:], a[k]) for k in MASKS + ["iota", "ones_mean"]])
        with nc.semaphore("net_cast") as cast, nc.Block() as block:
            @block.vector
            def _(eng):
                nc.vector.tensor_copy(c["eye16"][:], c["eye"][:]).then_inc(cast, 1)
        for layer in (layer0, layer1, layer2, layer3):
            layer(nc, a, XT, XN, c)
            clear_semaphores(nc)
        with nc.semaphore("out_stored") as stored, nc.Block() as block:
            @block.sync
            def _(eng):
                eng.dma_start(out, XT[:]).then_inc(stored, 16)
                eng.wait_ge(stored, 16)

def shape_constants():
    i = np.arange(P)
    row, col = i[:, None], i[None]
    eye = np.eye(P, dtype=np.float32)
    levels = []
    for n in (1 << l for l in range(7)):
        levels.append((row // (2 * n) == col // (2 * n)) & (row // n % 2 == 0) & (col // n % 2 == 1))
    rates = (1.0 / 10000.0 ** (np.arange(0, 8, 2, dtype=np.float32) / np.float32(8))).astype(np.float32)
    angles = np.outer(np.arange(SEQ, dtype=np.float32), rates)
    cos, sin = np.repeat(np.cos(angles), 2, -1), np.repeat(np.sin(angles), 2, -1)
    sin[:, ::2] *= -1
    rows = np.arange(1024)
    head, value = rows // 64, rows // 8 % 8
    pick = np.zeros((P, 1024), np.float32)
    pick[head * 8 + value, rows] = 1
    return {
        "row_le_col": (row <= col), "row_gt_col": (row > col), "row_lt_col": (row < col), "ones": np.ones((P, P)), "eye": eye,
        "iota": np.tile(np.arange(EX), (P, 1)), "ones_mean": np.full((P, P), 1 / D), "head_rows": np.arange(16)[:, None] == col // 8, "level": np.concatenate(levels, 1),
        "cos": np.tile(cos.T, (16, 1)), "sin": np.tile(sin.T, (16, 1)), "gla_pick": pick, "gla_fold": pick.T.reshape(8, P, P).transpose(1, 0, 2).reshape(P, 1024),
    }

def layouts(x):
    rows = np.arange(1024)
    head, value, key = rows // 64, rows // 8 % 8, rows % 8
    swapped = np.arange(P) ^ 1
    l0 = lambda k: x["L0_attn_" + k]
    q = lambda k: x["L0_ffn_" + k]
    l1 = lambda k: x["L1_attn_" + k]
    moe = lambda k: x["L1_ffn_" + k]
    l2 = lambda k: x["L2_attn_" + k]
    l3 = lambda k: x["L3_attn_" + k]
    f3 = lambda k: x["L3_ffn_" + k]
    return {
        "xT": l0("x").reshape(TOK, D).T, "Wba": np.concatenate([l0("Wb"), l0("Wa")], 1), "Wq": l0("Wq"), "Wk": l0("Wk"), "Wv": l0("Wv"), "Wg": l0("Wg"),
        "Wo": l0("Wo").reshape(8, P, P).transpose(1, 0, 2).reshape(P, 1024), "o_norm_w": l0("o_norm_w")[:, None], "A_log": l0("A_log"), "dt_bias": l0("dt_bias"),
        "w_up": l0("W_fc"), "w_down": l0("W_proj").reshape(4, P, P).transpose(1, 0, 2).reshape(P, 4 * P),
        "q_weights": q("qweights"), "q_scales": q("scales"), "q_lora_a": q("lora_a"), "q_lora_bT": q("lora_b").transpose(0, 2, 1),
        "q_biasT": q("biases")[1::2].T, "q_bias": q("biases")[0::2], "q_gammaT": q("ln_gamma").T, "q_betaT": q("ln_beta").T,
        "rope_w0": l1("W_Q").T, "rope_w1": l1("W_Q")[swapped].T, "rope_w2": l1("W_K").T, "rope_w3": l1("W_K")[swapped].T, "attn_wv": l1("W_V").T, "attn_wo": l1("W_O").T,
        "moe_wr": moe("Wr").T, "moe_br": moe("br"), "moe_W1": moe("W1").transpose(2, 0, 1), "moe_B1": moe("b1").reshape(8, 4, P).transpose(2, 0, 1),
        "moe_W2": moe("W2").transpose(2, 0, 1).reshape(4, P, 8, P).transpose(1, 2, 0, 3), "moe_b2": moe("b2"), "moe_gamma": moe("gamma")[:, None], "moe_beta": moe("beta")[:, None],
        "lin_wqkv": np.concatenate([l2("Wq").T, l2("Wk").T, l2("Wv").T], 1), "lin_w1": l2("W1").T, "lin_w2": l2("W2").T,
        "lin_g1": l2("g1")[:, None], "lin_g2": l2("g2"), "lin_g3": l2("g3"), "lin_lambda": l2("lambda_params"),
        "sparse_gate": x["L2_ffn_gate_kernel"], "sparse_w0": x["L2_ffn_w0"], "sparse_w1": x["L2_ffn_w1"], "sparse_wo": x["L2_ffn_wo"],
        "gla_gk1": l3("Wgk1"), "gla_gk2": l3("Wgk2"), "gla_gb": l3("bgk2")[:, None], "gla_wq": l3("Wq")[:, head * 8 + key], "gla_wk": l3("Wk")[:, head * 8 + key],
        "gla_wv": l3("Wv")[:, head * 8 + value], "gla_wg": l3("Wg"), "gla_wo": l3("Wout"), "gla_gamma": l3("gamma")[:, None], "gla_beta": l3("beta")[:, None],
        "bin_w1": f3("w1"), "bin_b1": f3("b1").reshape(4, P).T, "bin_w2": f3("w2"), "bin_b2": f3("b2")[:, None],
    }

def kernel(**inputs):
    import concourse.bacc as bacc
    from concourse.bass_utils import run_bass_kernel_spmd

    arrays = {k: np.ascontiguousarray(v) for k, v in layouts({k: np.asarray(v) for k, v in inputs.items()}).items()}
    arrays.update({k: np.ascontiguousarray(v, dtype=np.float32) for k, v in shape_constants().items()})
    nc = bacc.Bacc("TRN2", target_bir_lowering=False, num_devices=1)
    a = {k: nc.dram_tensor("in_" + k, v.shape, mybir.dt.from_np(v.dtype), kind="ExternalInput").ap() for k, v in arrays.items()}
    out = nc.dram_tensor("out_T", [D, TOK], F32, kind="ExternalOutput").ap()
    network(nc, a, out)
    result = run_bass_kernel_spmd(nc, [{"in_" + k: v for k, v in arrays.items()}], core_ids=[0])
    return np.ascontiguousarray(result.results[0]["out_T"].T).reshape(BATCH, SEQ, D)
```
